# Optimizing a Trainium2 kernel written in Bass

```python
import numpy as np
import jax
import jax.numpy as jnp

def _softmax(x, axis=-1):
    return jax.nn.softmax(x, axis=axis)

def _gelu(x):
    return jax.nn.gelu(x, approximate=True)

def _silu(x):
    return jax.nn.silu(x)

def _sigmoid(x):
    return jax.nn.sigmoid(x)

def _layernorm(x, axis=-1, eps=1e-05):
    m = jnp.mean(x, axis=axis, keepdims=True)
    v = jnp.var(x, axis=axis, keepdims=True)
    return (x - m) / jnp.sqrt(v + eps)

def _scatter_add(tgt, idx, src, axis=0):
    return tgt.at[idx].add(src)

def _segment_sum(src, seg, n):
    return jax.ops.segment_sum(src, seg, n)
kernel_name = 'mk_decoder_preln_d4_seqx_r8_b48d2e'

def setup_inputs(seed: int=0):
    np.random.seed(seed)
    _w = jnp.asarray

    def _rec_inputs():
        import jax
        import jax.numpy as jnp
        _rk = jax.random.key(seed)
        x = -0.001547 + 1.001 * jax.random.normal(jax.random.fold_in(_rk, 1), (64, 128, 128), jnp.float32)
        _lenS = 128 - jax.random.randint(jax.random.fold_in(_rk, 7), (64,), 0, max(1, 128 // 4) + 1, jnp.int32)
        _lenS2 = 77 - jax.random.randint(jax.random.fold_in(_rk, 8), (64,), 0, max(1, 77 // 4) + 1, jnp.int32)
        _ctx_1024P = jax.random.normal(jax.random.fold_in(_rk, 11), (64, 16, 128), jnp.float32)
        _ctx_1024c = jax.random.dirichlet(jax.random.fold_in(_rk, 511), 0.3 * jnp.ones((16,), jnp.float32), (64, 77))
        _ctx_1024t = jnp.einsum('bsk,bkd->bsd', _ctx_1024c, _ctx_1024P)
        _ctx_1024t = _ctx_1024t * jax.lax.rsqrt(jnp.mean(jnp.square(_ctx_1024t)) + 1e-12) * 0.953939
        ctx_1024 = -0.00010331 + 0.999899 * (_ctx_1024t + 0.3 * jax.random.normal(jax.random.fold_in(_rk, 611), (64, 77, 128), jnp.float32))
        _validS = jnp.arange(128)[None, :] < _lenS[:, None]
        _validS2 = jnp.arange(77)[None, :] < _lenS2[:, None]
        _causal = jnp.tril(jnp.ones((128, 128), dtype=bool))
        mask_BxS2_bf1 = jnp.ones((64, 77), dtype=bool)
        return (x, ctx_1024, _lenS2, mask_BxS2_bf1)
    x, ctx_1024, _lenS2, mask_BxS2_bf1 = _rec_inputs()

    def _L0_attn_setup():
        import math
        import jax, jax.numpy as jnp
        import numpy as np
        DIM = 128
        N_HEADS = 16
        HEAD_DIM = DIM // N_HEADS
        SEQ_LEN = 256
        BASE = 10000.0
        EPS = 1e-05

        def rope_cache(seq_len, dim):
            pos = jnp.arange(seq_len, dtype=jnp.float32)[:, None]
            di = jnp.arange(0, dim, 2, dtype=jnp.float32) / dim
            theta = pos * jnp.exp(-di * math.log(BASE))
            cos = jnp.repeat(jnp.cos(theta), 2, axis=1)
            sin = jnp.repeat(jnp.sin(theta), 2, axis=1)
            return (cos, sin)

        def rotate_half(x):
            x1 = x[..., ::2]
            x2 = x[..., 1::2]
            return jnp.concatenate((-x2, x1), axis=-1)

        def layernorm(x, gamma, beta):
            mu = jnp.mean(x, axis=-1, keepdims=True)
            var = jnp.var(x, axis=-1, keepdims=True)
            return (x - mu) * jax.lax.rsqrt(var + EPS) * gamma + beta
        key = jax.random.key(seed)
        ks = jax.random.split(key, 7)
        s = 1.0 / math.sqrt(DIM)
        return {'x': jax.random.normal(ks[0], (2, SEQ_LEN, DIM), dtype=jnp.float32), 'Wq': jax.random.normal(ks[1], (DIM, DIM), dtype=jnp.float32) * s, 'Wk': jax.random.normal(ks[2], (DIM, DIM), dtype=jnp.float32) * s, 'Wv': jax.random.normal(ks[3], (DIM, DIM), dtype=jnp.float32) * s, 'q_gamma': jnp.ones((HEAD_DIM,), jnp.float32), 'q_beta': jnp.zeros((HEAD_DIM,), jnp.float32), 'k_gamma': jnp.ones((HEAD_DIM,), jnp.float32), 'k_beta': jnp.zeros((HEAD_DIM,), jnp.float32), 'Wo': jax.random.normal(ks[4], (DIM, DIM), dtype=jnp.float32) * s, 'bo': jnp.zeros((DIM,), jnp.float32)}
    _L0_attn_all = _L0_attn_setup()
    _L0_attn_in = {k: v for k, v in _L0_attn_all.items() if k in ('Wq', 'Wk', 'Wv', 'q_gamma', 'q_beta', 'k_gamma', 'k_beta', 'Wo', 'bo')}
    del _L0_attn_all

    def _L0_xattn_setup():
        import jax, jax.numpy as jnp
        import numpy as np
        N_HEADS = 16
        key = jax.random.key(seed)
        ks = jax.random.split(key, 9)
        B, T, C, S = (32, 8, 128, 512)
        w_scale = 1.0 / np.sqrt(C).astype(np.float32)
        return {'x': jax.random.normal(ks[0], (B, T, C), jnp.float32), 'cache_k': jax.random.normal(ks[1], (B, S, C), jnp.float32), 'cache_v': jax.random.normal(ks[2], (B, S, C), jnp.float32), 'cache_len': jax.random.randint(ks[3], (B,), 0, S - T, jnp.int32), 'wq': jax.random.normal(ks[4], (C, C), jnp.float32) * w_scale, 'wk': jax.random.normal(ks[5], (C, C), jnp.float32) * w_scale, 'wv': jax.random.normal(ks[6], (C, C), jnp.float32) * w_scale, 'wo': jax.random.normal(ks[7], (C, C), jnp.float32) * w_scale, 'bo': jnp.zeros((C,), jnp.float32)}
    _L0_xattn_all = _L0_xattn_setup()
    _L0_xattn_in = {k: v for k, v in _L0_xattn_all.items() if k in ('wq', 'wk', 'wv', 'wo', 'bo')}
    del _L0_xattn_all

    def _L0_ffn_setup():
        import jax, jax.numpy as jnp
        import numpy as np
        N_EXPERTS = 32
        TOP_K = 8
        N_GROUP = 4
        TOPK_GROUP = 2
        ROUTED_SCALING = 2.5

        def _gate(x, gate_w, gate_bias):
            T, E = (x.shape[0], gate_w.shape[0])
            logits = jnp.einsum('th,eh->te', x, gate_w)
            scores = jax.nn.sigmoid(logits)
            scores_choice = scores + gate_bias[None, :]
            grp = scores_choice.reshape(T, N_GROUP, E // N_GROUP)
            top2, _ = jax.lax.top_k(grp, 2)
            group_scores = top2.sum(-1)
            _, grp_idx = jax.lax.top_k(group_scores, TOPK_GROUP)
            group_mask = jax.nn.one_hot(grp_idx, N_GROUP, dtype=scores.dtype).sum(1)
            expert_mask = jnp.repeat(group_mask, E // N_GROUP, axis=1)
            masked = jnp.where(expert_mask > 0, scores_choice, 0.0)
            _, topk_idx = jax.lax.top_k(masked, TOP_K)
            topk_w = jnp.take_along_axis(scores, topk_idx, axis=1)
            topk_w = topk_w / (topk_w.sum(-1, keepdims=True) + 1e-20)
            topk_w = topk_w * ROUTED_SCALING
            return (topk_idx, topk_w)

        def _mlp(x, wg, wu, wd):
            return jnp.einsum('...i,hi->...h', jax.nn.silu(jnp.einsum('...h,ih->...i', x, wg)) * jnp.einsum('...h,ih->...i', x, wu), wd)
        key = jax.random.key(seed)
        ks = jax.random.split(key, 9)
        B, S, H, I = (2, 64, 128, 64)
        w = 0.02
        return {'hidden_states': jax.random.normal(ks[0], (B, S, H), jnp.float32), 'gate_w': jax.random.normal(ks[1], (N_EXPERTS, H), jnp.float32) * w, 'gate_bias': jax.random.normal(ks[2], (N_EXPERTS,), jnp.float32) * w, 'expert_gate': jax.random.normal(ks[3], (N_EXPERTS, I, H), jnp.float32) * w, 'expert_up': jax.random.normal(ks[4], (N_EXPERTS, I, H), jnp.float32) * w, 'expert_down': jax.random.normal(ks[5], (N_EXPERTS, H, I), jnp.float32) * w, 'shared_gate': jax.random.normal(ks[6], (2 * I, H), jnp.float32) * w, 'shared_up': jax.random.normal(ks[7], (2 * I, H), jnp.float32) * w, 'shared_down': jax.random.normal(ks[8], (H, 2 * I), jnp.float32) * w}
    _L0_ffn_all = _L0_ffn_setup()
    _L0_ffn_in = {k: v for k, v in _L0_ffn_all.items() if k in ('gate_w', 'gate_bias', 'expert_gate', 'expert_up', 'expert_down', 'shared_gate', 'shared_up', 'shared_down')}
    del _L0_ffn_all

    def _L1_attn_setup():
        import jax, jax.numpy as jnp
        import numpy as np
        B, L, C = (2, 256, 128)
        H, POS = (8, 16)
        D = C // H
        MAXS = 32
        S = MAXS + 1
        MAX_FREQ, MIN_FREQ = (16.0, 1.0)
        SCALE = POS ** (-0.5)
        key = jax.random.key(seed)
        ks = jax.random.split(key, 12)

        def w(k, shape, s=0.02):
            return jax.random.normal(k, shape, dtype=jnp.float32) * s
        return {'x': jax.random.normal(ks[0], (B, L, C), dtype=jnp.float32), 'w_wave': w(ks[1], (C, 3 * H)), 'b_wave': w(ks[2], (3 * H,)), 'w_query': w(ks[3], (C, H * POS)), 'b_query': w(ks[4], (H * POS,)), 'key_weight': w(ks[5], (POS,)), 'w_se1': w(ks[6], (C, C // 4)), 'b_se1': w(ks[7], (C // 4,)), 'w_se2': w(ks[8], (C // 4, C)), 'b_se2': w(ks[9], (C,)), 'w_out': w(ks[10], (C, C))}
    _L1_attn_all = _L1_attn_setup()
    _L1_attn_in = {k: v for k, v in _L1_attn_all.items() if k in ('w_wave', 'b_wave', 'w_query', 'b_query', 'key_weight', 'w_se1', 'b_se1', 'w_se2', 'b_se2', 'w_out')}
    del _L1_attn_all

    def _L1_xattn_setup():
        import jax, jax.numpy as jnp
        import numpy as np
        N_HEADS = 16
        D_MODEL = 128
        HEAD_DIM = D_MODEL // N_HEADS
        MASK_FILL = -100000000.0

        def _split_heads(x):
            B, S, _ = x.shape
            return x.reshape(B, S, N_HEADS, HEAD_DIM).transpose(0, 2, 1, 3)
        key = jax.random.key(seed)
        ks = jax.random.split(key, 12)
        B, L, P = (2, 256, 256)
        s = 1.0 / np.sqrt(D_MODEL).astype(np.float32)
        inp = {'q': jax.random.normal(ks[0], (B, L, D_MODEL), dtype=jnp.float32), 'k': jax.random.normal(ks[1], (B, P, D_MODEL), dtype=jnp.float32), 'v': jax.random.normal(ks[2], (B, P, D_MODEL), dtype=jnp.float32), 'attention_mask': jnp.ones((B, P), dtype=bool), 'Wq': jax.random.normal(ks[3], (D_MODEL, D_MODEL), dtype=jnp.float32) * s, 'bq': jnp.zeros((D_MODEL,), dtype=jnp.float32), 'Wk': jax.random.normal(ks[4], (D_MODEL, D_MODEL), dtype=jnp.float32) * s, 'bk': jnp.zeros((D_MODEL,), dtype=jnp.float32), 'Wv': jax.random.normal(ks[5], (D_MODEL, D_MODEL), dtype=jnp.float32) * s, 'bv': jnp.zeros((D_MODEL,), dtype=jnp.float32), 'Wo': jax.random.normal(ks[6], (D_MODEL, D_MODEL), dtype=jnp.float32) * s, 'bo': jnp.zeros((D_MODEL,), dtype=jnp.float32)}
        return inp
    _L1_xattn_all = _L1_xattn_setup()
    _L1_xattn_in = {k: v for k, v in _L1_xattn_all.items() if k in ('Wq', 'bq', 'Wk', 'bk', 'Wv', 'bv', 'Wo', 'bo')}
    del _L1_xattn_all

    def _L1_ffn_setup():
        import jax, jax.numpy as jnp
        import numpy as np
        BLOCK = 32
        W_BITS = 4
        ACT_BITS = 16

        def act_qdq(x):
            qmax = 2.0 ** (ACT_BITS - 1) - 1.0
            scale = jnp.maximum(jnp.max(jnp.abs(x)) / qmax, 1e-12)
            return jnp.clip(jnp.round(x / scale), -qmax - 1.0, qmax) * scale

        def fixed_qdq_u16(x):
            scale = 1.0 / 65536.0
            return jnp.clip(jnp.round(x / scale), 0.0, 65535.0) * scale

        def lpbq_dequant(w):
            O, I = w.shape
            qmax = 2.0 ** (W_BITS - 1) - 1.0
            wb = w.reshape(O, I // BLOCK, BLOCK)
            s = jnp.maximum(jnp.max(jnp.abs(wb), axis=-1, keepdims=True) / qmax, 1e-12)
            wq = jnp.clip(jnp.round(wb / s), -qmax - 1.0, qmax) * s
            return wq.reshape(O, I)
        key = jax.random.key(seed)
        k1, k2, k3, k4 = jax.random.split(key, 4)
        B, S, H, I = (2, 512, 128, 384)
        x = jax.random.normal(k1, (B, S, H), jnp.float32)
        w_gate = jax.random.normal(k2, (I, H), jnp.float32) * 0.02
        w_up = jax.random.normal(k3, (I, H), jnp.float32) * 0.02
        w_down = jax.random.normal(k4, (H, I), jnp.float32) * 0.02
        return {'x': x, 'w_gate': w_gate, 'w_up': w_up, 'w_down': w_down}
    _L1_ffn_all = _L1_ffn_setup()
    _L1_ffn_in = {k: v for k, v in _L1_ffn_all.items() if k in ('w_gate', 'w_up', 'w_down')}
    del _L1_ffn_all

    def _L2_attn_setup():
        import jax, jax.numpy as jnp
        import numpy as np
        B, L, D, H = (8, 256, 128, 16)
        HD = D // H
        K = 4
        EPS = 1e-06

        def _short_conv(x, w, b):
            xp = jnp.pad(x, ((0, 0), (K - 1, 0), (0, 0)))
            y = b
            for i in range(K):
                y = y + w[:, i] * xp[:, i:i + x.shape[1], :]
            return y

        def _delta_rule(q, k, v, beta):
            qT = jnp.moveaxis(q, 1, 0)
            kT = jnp.moveaxis(k, 1, 0)
            vT = jnp.moveaxis(v, 1, 0)
            bT = jnp.moveaxis(beta, 1, 0)

            def step(S, inp):
                q_t, k_t, v_t, b_t = inp
                pred = jnp.einsum('bhk,bhkv->bhv', k_t, S)
                S = S + b_t[..., None, None] * (k_t[..., None] * (v_t - pred)[..., None, :])
                o_t = jnp.einsum('bhk,bhkv->bhv', q_t, S)
                return (S, o_t)
            S0 = jnp.zeros((q.shape[0], H, HD, HD), q.dtype)
            _, o = jax.lax.scan(step, S0, (qT, kT, vT, bT))
            return jnp.moveaxis(o, 0, 1)

        def _rmsnorm(x, w):
            return x * jax.lax.rsqrt(jnp.mean(x * x, axis=-1, keepdims=True) + EPS) * w
        key = jax.random.key(seed)
        ks = jax.random.split(key, 12)
        s = 0.02
        inp = {'x': jax.random.normal(ks[0], (B, L, D), jnp.float32), 'Wq': jax.random.normal(ks[1], (D, D), jnp.float32) * s, 'bq': jnp.zeros((D,), jnp.float32), 'Wk': jax.random.normal(ks[2], (D, D), jnp.float32) * s, 'bk': jnp.zeros((D,), jnp.float32), 'Wv': jax.random.normal(ks[3], (D, D), jnp.float32) * s, 'bv': jnp.zeros((D,), jnp.float32), 'Wbeta': jax.random.normal(ks[4], (H, D), jnp.float32) * s, 'bbeta': jnp.zeros((H,), jnp.float32), 'Wo': jax.random.normal(ks[5], (D, D), jnp.float32) * s, 'bo': jnp.zeros((D,), jnp.float32), 'wq_conv': jax.random.normal(ks[6], (D, K), jnp.float32) * 0.2, 'bq_conv': jnp.zeros((D,), jnp.float32), 'wk_conv': jax.random.normal(ks[7], (D, K), jnp.float32) * 0.2, 'bk_conv': jnp.zeros((D,), jnp.float32), 'wv_conv': jax.random.normal(ks[8], (D, K), jnp.float32) * 0.2, 'bv_conv': jnp.zeros((D,), jnp.float32), 'norm_w': jnp.ones((HD,), jnp.float32)}
        return inp
    _L2_attn_all = _L2_attn_setup()
    _L2_attn_in = {k: v for k, v in _L2_attn_all.items() if k in ('Wq', 'bq', 'Wk', 'bk', 'Wv', 'bv', 'Wbeta', 'bbeta', 'Wo', 'bo', 'wq_conv', 'bq_conv', 'wk_conv', 'bk_conv', 'wv_conv', 'bv_conv', 'norm_w')}
    del _L2_attn_all

    def _L2_xattn_setup():
        import jax, jax.numpy as jnp
        import numpy as np
        DIM = 128
        H = 16
        DH = DIM // H
        LN_EPS = 1e-05

        def _linear_params(key, din, dout):
            kw, kb = jax.random.split(key)
            bound = 1.0 / np.sqrt(din)
            W = jax.random.uniform(kw, (din, dout), jnp.float32, -bound, bound)
            b = jax.random.uniform(kb, (dout,), jnp.float32, -bound, bound)
            return (W, b)

        def _layernorm(x, g, b):
            m = jnp.mean(x, axis=-1, keepdims=True)
            v = jnp.mean(jnp.square(x - m), axis=-1, keepdims=True)
            return (x - m) * jax.lax.rsqrt(v + LN_EPS) * g + b

        def _split_heads(x):
            B, N, _ = x.shape
            return x.reshape(B, N, H, DH).transpose(2, 0, 1, 3).reshape(H * B, N, DH)

        def _merge_heads(x, B):
            _, N, _ = x.shape
            return x.reshape(H, B, N, DH).transpose(1, 2, 0, 3).reshape(B, N, DIM)
        key = jax.random.key(seed)
        ks = jax.random.split(key, 10)
        inp = {'Q': jax.random.normal(ks[0], (8, 64, DIM), jnp.float32), 'K1': jax.random.normal(ks[1], (8, 128, DIM), jnp.float32), 'K2': jax.random.normal(ks[2], (8, 128, DIM), jnp.float32)}
        for name, k in zip(['q', 'k1', 'k2', 'v1', 'v2', 'o'], ks[3:9]):
            W, b = _linear_params(k, DIM, DIM)
            inp['W' + name] = W
            inp['b' + name] = b
        inp['g0'] = jnp.ones((DIM,), jnp.float32)
        inp['beta0'] = jnp.zeros((DIM,), jnp.float32)
        inp['g1'] = jnp.ones((DIM,), jnp.float32)
        inp['beta1'] = jnp.zeros((DIM,), jnp.float32)
        return inp
    _L2_xattn_all = _L2_xattn_setup()
    _L2_xattn_in = {k: v for k, v in _L2_xattn_all.items() if k in ('Wq', 'bq', 'Wk1', 'bk1', 'Wk2', 'bk2', 'Wv1', 'bv1', 'Wv2', 'bv2', 'Wo', 'bo', 'g0', 'beta0', 'g1', 'beta1')}
    del _L2_xattn_all

    def _L2_ffn_setup():
        import jax, jax.numpy as jnp
        import numpy as np
        B, S, H, F, G = (8, 256, 128, 512, 128)
        EPS = 1e-05

        def _dequant(q, scales, g):
            K, N = q.shape
            w = (q.astype(jnp.float32) - 128.0).reshape(K // g, g, N) * scales[:, None, :]
            return w.reshape(K, N)
        key = jax.random.key(seed)
        ks = jax.random.split(key, 8)
        x = jax.random.normal(ks[0], (B, S, H), dtype=jnp.float32)
        ln_gamma = jnp.ones((H,), jnp.float32)
        ln_beta = jnp.zeros((H,), jnp.float32)
        fc1_q = jax.random.randint(ks[1], (H, F), 0, 32, dtype=jnp.int32)
        fc2_q = jax.random.randint(ks[2], (F, H), 0, 32, dtype=jnp.int32)
        fc1_scales = jax.random.uniform(ks[3], (H // G, F), jnp.float32) * 0.02 + 0.001
        fc2_scales = jax.random.uniform(ks[4], (F // G, H), jnp.float32) * 0.02 + 0.001
        fc1_bias = jax.random.normal(ks[5], (F,), jnp.float32) * 0.02
        fc2_bias = jax.random.normal(ks[6], (H,), jnp.float32) * 0.02
        return {'x': x, 'ln_gamma': ln_gamma, 'ln_beta': ln_beta, 'fc1_q': fc1_q, 'fc1_scales': fc1_scales, 'fc1_bias': fc1_bias, 'fc2_q': fc2_q, 'fc2_scales': fc2_scales, 'fc2_bias': fc2_bias}
    _L2_ffn_all = _L2_ffn_setup()
    _L2_ffn_in = {k: v for k, v in _L2_ffn_all.items() if k in ('ln_gamma', 'ln_beta', 'fc1_q', 'fc1_scales', 'fc1_bias', 'fc2_q', 'fc2_scales', 'fc2_bias')}
    del _L2_ffn_all

    def _L3_attn_setup():
        import jax, jax.numpy as jnp
        import numpy as np
        D_MODEL = 128
        N_HEADS = 16
        HEAD_DIM = D_MODEL // N_HEADS
        D_LATENT = 32
        LAMBDA_DECAY = 0.01
        TIME_STEP = 0.01
        CLAMP = 10000.0

        def _reference_tuple_inner(x, Wq, Wk, Wv, Wo, W_down_kv, W_up_k, W_up_v):
            B, S, _ = x.shape
            q = x @ Wq
            k = x @ Wk
            v = x @ Wv
            latent_kv = (k + v) @ W_down_kv
            k_rec = latent_kv @ W_up_k
            v_rec = latent_kv @ W_up_v

            def heads(t):
                return t.reshape(B, S, N_HEADS, HEAD_DIM).transpose(0, 2, 1, 3)
            qh, kh, vh = (heads(q), heads(k_rec), heads(v_rec))
            scale = 1.0 / (jnp.sqrt(jnp.float32(D_MODEL)) + 1e-08)
            scores = jnp.einsum('bhqd,bhkd->bhqk', qh, kh) * scale
            scores = jnp.clip(jnp.nan_to_num(scores, nan=-1000000000.0), -CLAMP, CLAMP)
            idx = jnp.arange(S, dtype=jnp.float32)
            decay = jnp.exp(-LAMBDA_DECAY * TIME_STEP * jnp.abs(idx[:, None] - idx[None, :]))
            scores = scores * decay[None, None, :, :]
            scores = jnp.clip(jnp.nan_to_num(scores, nan=-1000000000.0), -CLAMP, CLAMP)
            attn = jax.nn.softmax(scores, axis=-1)
            out = jnp.einsum('bhqk,bhkd->bhqd', attn, vh)
            out = out.transpose(0, 2, 1, 3).reshape(B, S, D_MODEL)
            return (out @ Wo, latent_kv)
        key = jax.random.key(seed)
        ks = jax.random.split(key, 8)
        B, S = (2, 256)

        def w(k, i, o):
            return jax.random.normal(k, (i, o), dtype=jnp.float32) * 0.02
        return {'x': jax.random.normal(ks[0], (B, S, D_MODEL), dtype=jnp.float32), 'Wq': w(ks[1], D_MODEL, D_MODEL), 'Wk': w(ks[2], D_MODEL, D_MODEL), 'Wv': w(ks[3], D_MODEL, D_MODEL), 'Wo': w(ks[4], D_MODEL, D_MODEL), 'W_down_kv': w(ks[5], D_MODEL, D_LATENT), 'W_up_k': w(ks[6], D_LATENT, D_MODEL), 'W_up_v': w(ks[7], D_LATENT, D_MODEL)}
    _L3_attn_all = _L3_attn_setup()
    _L3_attn_in = {k: v for k, v in _L3_attn_all.items() if k in ('Wq', 'Wk', 'Wv', 'Wo', 'W_down_kv', 'W_up_k', 'W_up_v')}
    del _L3_attn_all

    def _L3_xattn_setup():
        import jax, jax.numpy as jnp
        import numpy as np
        DIM = 128
        CTX_DIM = 128
        HEADS = 8
        DIM_HEAD = 64
        INNER = HEADS * DIM_HEAD
        EPS = 1e-05

        def _layer_norm(x, gamma, beta):
            mu = jnp.mean(x, axis=-1, keepdims=True)
            var = jnp.mean(jnp.square(x - mu), axis=-1, keepdims=True)
            return (x - mu) * jax.lax.rsqrt(var + EPS) * gamma + beta
        key = jax.random.key(seed)
        ks = jax.random.split(key, 8)
        b, n, m = (4, 256, 256)
        x = jax.random.normal(ks[0], (b, n, DIM), dtype=jnp.float32)
        context = jax.random.normal(ks[1], (b, m, CTX_DIM), dtype=jnp.float32)
        Wq = jax.random.normal(ks[2], (DIM, INNER), dtype=jnp.float32) / np.sqrt(DIM)
        Wkv = jax.random.normal(ks[3], (CTX_DIM, 2 * INNER), dtype=jnp.float32) / np.sqrt(CTX_DIM)
        Wout = jax.random.normal(ks[4], (INNER, DIM), dtype=jnp.float32) / np.sqrt(INNER)
        bout = jnp.zeros((DIM,), dtype=jnp.float32)
        g1 = jnp.ones((DIM,), dtype=jnp.float32)
        b1 = jnp.zeros((DIM,), dtype=jnp.float32)
        g2 = jnp.ones((CTX_DIM,), dtype=jnp.float32)
        b2 = jnp.zeros((CTX_DIM,), dtype=jnp.float32)
        return {'x': x, 'context': context, 'g1': g1, 'b1': b1, 'g2': g2, 'b2': b2, 'Wq': Wq, 'Wkv': Wkv, 'Wout': Wout, 'bout': bout}
    _L3_xattn_all = _L3_xattn_setup()
    _L3_xattn_in = {k: v for k, v in _L3_xattn_all.items() if k in ('g1', 'b1', 'g2', 'b2', 'Wq', 'Wkv', 'Wout', 'bout')}
    del _L3_xattn_all

    def _L3_ffn_setup():
        import jax, jax.numpy as jnp
        import numpy as np
        HIDDEN = 128
        N_EXPERTS = 32
        MOE_I = 64
        N_GROUP = 4
        TOPK_GROUP = 2
        TOP_K = 6
        N_LOCAL_GROUPS = 16
        ANCHOR_I = 32
        SHARED_I = 64
        ROUTED_SCALE = 0.2
        ANCHOR_ALPHA = 0.1
        BATCH, SEQ = (1, 128)

        def _moe_forward(hidden_states, gate_weight, gate_bias, w_gate, w_up, w_down, shared_w_gate, shared_w_up, shared_w_down, anchor_w_gate, anchor_w_up, anchor_w_down):
            B, S, H = hidden_states.shape
            x = hidden_states.reshape(-1, H)
            T = x.shape[0]
            E = gate_weight.shape[0]
            L = anchor_w_gate.shape[0]
            logits = x @ gate_weight.T
            scores = jax.nn.sigmoid(logits)
            sc = scores + gate_bias
            grp = sc.reshape(T, N_GROUP, E // N_GROUP)
            group_scores = jax.lax.top_k(grp, 2)[0].sum(-1)
            _, gidx = jax.lax.top_k(group_scores, TOPK_GROUP)
            gmask = jax.nn.one_hot(gidx, N_GROUP, dtype=sc.dtype).sum(1)
            emask = jnp.repeat(gmask, E // N_GROUP, axis=1)
            masked = jnp.where(emask > 0, sc, -jnp.inf)
            _, topidx = jax.lax.top_k(masked, TOP_K)
            tw = jnp.take_along_axis(scores, topidx, axis=-1)
            tw = tw / (tw.sum(-1, keepdims=True) + 1e-20) * ROUTED_SCALE
            g = jnp.einsum('th,ehi->tei', x, w_gate)
            u = jnp.einsum('th,ehi->tei', x, w_up)
            eo = jnp.einsum('tei,eih->teh', jax.nn.silu(g) * u, w_down)
            cw = (jax.nn.one_hot(topidx, E, dtype=x.dtype) * tw[..., None]).sum(1)
            routed = jnp.einsum('te,teh->th', cw, eo)
            shared = jax.nn.silu(x @ shared_w_gate) * (x @ shared_w_up) @ shared_w_down
            lg = topidx[:, 0] // (E // L)
            ag = jnp.einsum('th,lhi->tli', x, anchor_w_gate)
            au = jnp.einsum('th,lhi->tli', x, anchor_w_up)
            ao = jnp.einsum('tli,lih->tlh', jax.nn.silu(ag) * au, anchor_w_down)
            acw = jax.nn.one_hot(lg, L, dtype=x.dtype)
            anchor = jnp.einsum('tl,tlh->th', acw, ao)
            out = routed + shared + ANCHOR_ALPHA * anchor
            return out.reshape(B, S, H)
        key = jax.random.key(seed)
        ks = jax.random.split(key, 13)
        s = 0.02
        return {'hidden_states': jax.random.normal(ks[0], (BATCH, SEQ, HIDDEN), jnp.float32), 'gate_weight': s * jax.random.normal(ks[1], (N_EXPERTS, HIDDEN), jnp.float32), 'gate_bias': s * jax.random.normal(ks[2], (N_EXPERTS,), jnp.float32), 'w_gate': s * jax.random.normal(ks[3], (N_EXPERTS, HIDDEN, MOE_I), jnp.float32), 'w_up': s * jax.random.normal(ks[4], (N_EXPERTS, HIDDEN, MOE_I), jnp.float32), 'w_down': s * jax.random.normal(ks[5], (N_EXPERTS, MOE_I, HIDDEN), jnp.float32), 'shared_w_gate': s * jax.random.normal(ks[6], (HIDDEN, SHARED_I), jnp.float32), 'shared_w_up': s * jax.random.normal(ks[7], (HIDDEN, SHARED_I), jnp.float32), 'shared_w_down': s * jax.random.normal(ks[8], (SHARED_I, HIDDEN), jnp.float32), 'anchor_w_gate': s * jax.random.normal(ks[9], (N_LOCAL_GROUPS, HIDDEN, ANCHOR_I), jnp.float32), 'anchor_w_up': s * jax.random.normal(ks[10], (N_LOCAL_GROUPS, HIDDEN, ANCHOR_I), jnp.float32), 'anchor_w_down': s * jax.random.normal(ks[11], (N_LOCAL_GROUPS, ANCHOR_I, HIDDEN), jnp.float32)}
    _L3_ffn_all = _L3_ffn_setup()
    _L3_ffn_in = {k: v for k, v in _L3_ffn_all.items() if k in ('gate_weight', 'gate_bias', 'w_gate', 'w_up', 'w_down', 'shared_w_gate', 'shared_w_up', 'shared_w_down', 'anchor_w_gate', 'anchor_w_up', 'anchor_w_down')}
    del _L3_ffn_all
    return {'x': x, 'ctx_1024': ctx_1024, '_lenS2': _lenS2, 'mask_BxS2_bf1': mask_BxS2_bf1, 'L0_attn_Wq': _L0_attn_in['Wq'], 'L0_attn_Wk': _L0_attn_in['Wk'], 'L0_attn_Wv': _L0_attn_in['Wv'], 'L0_attn_q_gamma': _L0_attn_in['q_gamma'], 'L0_attn_q_beta': _L0_attn_in['q_beta'], 'L0_attn_k_gamma': _L0_attn_in['k_gamma'], 'L0_attn_k_beta': _L0_attn_in['k_beta'], 'L0_attn_Wo': _L0_attn_in['Wo'], 'L0_attn_bo': _L0_attn_in['bo'], 'L0_xattn_wq': _L0_xattn_in['wq'], 'L0_xattn_wk': _L0_xattn_in['wk'], 'L0_xattn_wv': _L0_xattn_in['wv'], 'L0_xattn_wo': _L0_xattn_in['wo'], 'L0_xattn_bo': _L0_xattn_in['bo'], 'L0_ffn_gate_w': _L0_ffn_in['gate_w'], 'L0_ffn_gate_bias': _L0_ffn_in['gate_bias'], 'L0_ffn_expert_gate': _L0_ffn_in['expert_gate'], 'L0_ffn_expert_up': _L0_ffn_in['expert_up'], 'L0_ffn_expert_down': _L0_ffn_in['expert_down'], 'L0_ffn_shared_gate': _L0_ffn_in['shared_gate'], 'L0_ffn_shared_up': _L0_ffn_in['shared_up'], 'L0_ffn_shared_down': _L0_ffn_in['shared_down'], 'L1_attn_w_wave': _L1_attn_in['w_wave'], 'L1_attn_b_wave': _L1_attn_in['b_wave'], 'L1_attn_w_query': _L1_attn_in['w_query'], 'L1_attn_b_query': _L1_attn_in['b_query'], 'L1_attn_key_weight': _L1_attn_in['key_weight'], 'L1_attn_w_se1': _L1_attn_in['w_se1'], 'L1_attn_b_se1': _L1_attn_in['b_se1'], 'L1_attn_w_se2': _L1_attn_in['w_se2'], 'L1_attn_b_se2': _L1_attn_in['b_se2'], 'L1_attn_w_out': _L1_attn_in['w_out'], 'L1_xattn_Wq': _L1_xattn_in['Wq'], 'L1_xattn_bq': _L1_xattn_in['bq'], 'L1_xattn_Wk': _L1_xattn_in['Wk'], 'L1_xattn_bk': _L1_xattn_in['bk'], 'L1_xattn_Wv': _L1_xattn_in['Wv'], 'L1_xattn_bv': _L1_xattn_in['bv'], 'L1_xattn_Wo': _L1_xattn_in['Wo'], 'L1_xattn_bo': _L1_xattn_in['bo'], 'L1_ffn_w_gate': _L1_ffn_in['w_gate'], 'L1_ffn_w_up': _L1_ffn_in['w_up'], 'L1_ffn_w_down': _L1_ffn_in['w_down'], 'L2_attn_Wq': _L2_attn_in['Wq'], 'L2_attn_bq': _L2_attn_in['bq'], 'L2_attn_Wk': _L2_attn_in['Wk'], 'L2_attn_bk': _L2_attn_in['bk'], 'L2_attn_Wv': _L2_attn_in['Wv'], 'L2_attn_bv': _L2_attn_in['bv'], 'L2_attn_Wbeta': _L2_attn_in['Wbeta'], 'L2_attn_bbeta': _L2_attn_in['bbeta'], 'L2_attn_Wo': _L2_attn_in['Wo'], 'L2_attn_bo': _L2_attn_in['bo'], 'L2_attn_wq_conv': _L2_attn_in['wq_conv'], 'L2_attn_bq_conv': _L2_attn_in['bq_conv'], 'L2_attn_wk_conv': _L2_attn_in['wk_conv'], 'L2_attn_bk_conv': _L2_attn_in['bk_conv'], 'L2_attn_wv_conv': _L2_attn_in['wv_conv'], 'L2_attn_bv_conv': _L2_attn_in['bv_conv'], 'L2_attn_norm_w': _L2_attn_in['norm_w'], 'L2_xattn_Wq': _L2_xattn_in['Wq'], 'L2_xattn_bq': _L2_xattn_in['bq'], 'L2_xattn_Wk1': _L2_xattn_in['Wk1'], 'L2_xattn_bk1': _L2_xattn_in['bk1'], 'L2_xattn_Wk2': _L2_xattn_in['Wk2'], 'L2_xattn_bk2': _L2_xattn_in['bk2'], 'L2_xattn_Wv1': _L2_xattn_in['Wv1'], 'L2_xattn_bv1': _L2_xattn_in['bv1'], 'L2_xattn_Wv2': _L2_xattn_in['Wv2'], 'L2_xattn_bv2': _L2_xattn_in['bv2'], 'L2_xattn_Wo': _L2_xattn_in['Wo'], 'L2_xattn_bo': _L2_xattn_in['bo'], 'L2_xattn_g0': _L2_xattn_in['g0'], 'L2_xattn_beta0': _L2_xattn_in['beta0'], 'L2_xattn_g1': _L2_xattn_in['g1'], 'L2_xattn_beta1': _L2_xattn_in['beta1'], 'L2_ffn_ln_gamma': _L2_ffn_in['ln_gamma'], 'L2_ffn_ln_beta': _L2_ffn_in['ln_beta'], 'L2_ffn_fc1_q': _L2_ffn_in['fc1_q'], 'L2_ffn_fc1_scales': _L2_ffn_in['fc1_scales'], 'L2_ffn_fc1_bias': _L2_ffn_in['fc1_bias'], 'L2_ffn_fc2_q': _L2_ffn_in['fc2_q'], 'L2_ffn_fc2_scales': _L2_ffn_in['fc2_scales'], 'L2_ffn_fc2_bias': _L2_ffn_in['fc2_bias'], 'L3_attn_Wq': _L3_attn_in['Wq'], 'L3_attn_Wk': _L3_attn_in['Wk'], 'L3_attn_Wv': _L3_attn_in['Wv'], 'L3_attn_Wo': _L3_attn_in['Wo'], 'L3_attn_W_down_kv': _L3_attn_in['W_down_kv'], 'L3_attn_W_up_k': _L3_attn_in['W_up_k'], 'L3_attn_W_up_v': _L3_attn_in['W_up_v'], 'L3_xattn_g1': _L3_xattn_in['g1'], 'L3_xattn_b1': _L3_xattn_in['b1'], 'L3_xattn_g2': _L3_xattn_in['g2'], 'L3_xattn_b2': _L3_xattn_in['b2'], 'L3_xattn_Wq': _L3_xattn_in['Wq'], 'L3_xattn_Wkv': _L3_xattn_in['Wkv'], 'L3_xattn_Wout': _L3_xattn_in['Wout'], 'L3_xattn_bout': _L3_xattn_in['bout'], 'L3_ffn_gate_weight': _L3_ffn_in['gate_weight'], 'L3_ffn_gate_bias': _L3_ffn_in['gate_bias'], 'L3_ffn_w_gate': _L3_ffn_in['w_gate'], 'L3_ffn_w_up': _L3_ffn_in['w_up'], 'L3_ffn_w_down': _L3_ffn_in['w_down'], 'L3_ffn_shared_w_gate': _L3_ffn_in['shared_w_gate'], 'L3_ffn_shared_w_up': _L3_ffn_in['shared_w_up'], 'L3_ffn_shared_w_down': _L3_ffn_in['shared_w_down'], 'L3_ffn_anchor_w_gate': _L3_ffn_in['anchor_w_gate'], 'L3_ffn_anchor_w_up': _L3_ffn_in['anchor_w_up'], 'L3_ffn_anchor_w_down': _L3_ffn_in['anchor_w_down']}

def reference(x, ctx_1024, _lenS2, mask_BxS2_bf1, L0_attn_Wq, L0_attn_Wk, L0_attn_Wv, L0_attn_q_gamma, L0_attn_q_beta, L0_attn_k_gamma, L0_attn_k_beta, L0_attn_Wo, L0_attn_bo, L0_xattn_wq, L0_xattn_wk, L0_xattn_wv, L0_xattn_wo, L0_xattn_bo, L0_ffn_gate_w, L0_ffn_gate_bias, L0_ffn_expert_gate, L0_ffn_expert_up, L0_ffn_expert_down, L0_ffn_shared_gate, L0_ffn_shared_up, L0_ffn_shared_down, L1_attn_w_wave, L1_attn_b_wave, L1_attn_w_query, L1_attn_b_query, L1_attn_key_weight, L1_attn_w_se1, L1_attn_b_se1, L1_attn_w_se2, L1_attn_b_se2, L1_attn_w_out, L1_xattn_Wq, L1_xattn_bq, L1_xattn_Wk, L1_xattn_bk, L1_xattn_Wv, L1_xattn_bv, L1_xattn_Wo, L1_xattn_bo, L1_ffn_w_gate, L1_ffn_w_up, L1_ffn_w_down, L2_attn_Wq, L2_attn_bq, L2_attn_Wk, L2_attn_bk, L2_attn_Wv, L2_attn_bv, L2_attn_Wbeta, L2_attn_bbeta, L2_attn_Wo, L2_attn_bo, L2_attn_wq_conv, L2_attn_bq_conv, L2_attn_wk_conv, L2_attn_bk_conv, L2_attn_wv_conv, L2_attn_bv_conv, L2_attn_norm_w, L2_xattn_Wq, L2_xattn_bq, L2_xattn_Wk1, L2_xattn_bk1, L2_xattn_Wk2, L2_xattn_bk2, L2_xattn_Wv1, L2_xattn_bv1, L2_xattn_Wv2, L2_xattn_bv2, L2_xattn_Wo, L2_xattn_bo, L2_xattn_g0, L2_xattn_beta0, L2_xattn_g1, L2_xattn_beta1, L2_ffn_ln_gamma, L2_ffn_ln_beta, L2_ffn_fc1_q, L2_ffn_fc1_scales, L2_ffn_fc1_bias, L2_ffn_fc2_q, L2_ffn_fc2_scales, L2_ffn_fc2_bias, L3_attn_Wq, L3_attn_Wk, L3_attn_Wv, L3_attn_Wo, L3_attn_W_down_kv, L3_attn_W_up_k, L3_attn_W_up_v, L3_xattn_g1, L3_xattn_b1, L3_xattn_g2, L3_xattn_b2, L3_xattn_Wq, L3_xattn_Wkv, L3_xattn_Wout, L3_xattn_bout, L3_ffn_gate_weight, L3_ffn_gate_bias, L3_ffn_w_gate, L3_ffn_w_up, L3_ffn_w_down, L3_ffn_shared_w_gate, L3_ffn_shared_w_up, L3_ffn_shared_w_down, L3_ffn_anchor_w_gate, L3_ffn_anchor_w_up, L3_ffn_anchor_w_down):
    import jax
    import jax.numpy as jnp

    def _L0_attn_ref(x, Wq, Wk, Wv, q_gamma, q_beta, k_gamma, k_beta, Wo, bo):
        import math
        import jax, jax.numpy as jnp
        import numpy as np
        DIM = 128
        N_HEADS = 16
        HEAD_DIM = DIM // N_HEADS
        SEQ_LEN = 256
        BASE = 10000.0
        EPS = 1e-05

        def rope_cache(seq_len, dim):
            pos = jnp.arange(seq_len, dtype=jnp.float32)[:, None]
            di = jnp.arange(0, dim, 2, dtype=jnp.float32) / dim
            theta = pos * jnp.exp(-di * math.log(BASE))
            cos = jnp.repeat(jnp.cos(theta), 2, axis=1)
            sin = jnp.repeat(jnp.sin(theta), 2, axis=1)
            return (cos, sin)

        def rotate_half(x):
            x1 = x[..., ::2]
            x2 = x[..., 1::2]
            return jnp.concatenate((-x2, x1), axis=-1)

        def layernorm(x, gamma, beta):
            mu = jnp.mean(x, axis=-1, keepdims=True)
            var = jnp.var(x, axis=-1, keepdims=True)
            return (x - mu) * jax.lax.rsqrt(var + EPS) * gamma + beta
        B, S, D = x.shape
        H, hd = (N_HEADS, HEAD_DIM)
        q = (x @ Wq.T).reshape(B, S, H, hd).transpose(0, 2, 1, 3)
        k = (x @ Wk.T).reshape(B, S, H, hd).transpose(0, 2, 1, 3)
        v = (x @ Wv.T).reshape(B, S, H, hd).transpose(0, 2, 1, 3)
        q = layernorm(q, q_gamma, q_beta)
        k = layernorm(k, k_gamma, k_beta)
        cos, sin = rope_cache(S, hd)
        cos = cos[None, None]
        sin = sin[None, None]
        q = q * cos + rotate_half(q) * sin
        k = k * cos + rotate_half(k) * sin
        scale = 1.0 / math.sqrt(hd)
        scores = scale * jnp.einsum('bhqd,bhkd->bhqk', q, k)
        mask = jnp.tril(jnp.ones((S, S), dtype=bool))
        scores = jnp.where(mask, scores, -jnp.inf)
        attn = jax.nn.softmax(scores, axis=-1)
        out = jnp.einsum('bhqk,bhkd->bhqd', attn, v)
        out = out.transpose(0, 2, 1, 3).reshape(B, S, D)
        return out @ Wo.T + bo

    def _L0_xattn_ref(x, cache_k, cache_v, cache_len, wq, wk, wv, wo, bo):
        import jax, jax.numpy as jnp
        import numpy as np
        N_HEADS = 16
        B, T, C = x.shape
        S = cache_k.shape[1]
        H = N_HEADS
        hd = C // H
        q = x @ wq.T
        k_new = x @ wk.T
        v_new = x @ wv.T
        pos = jnp.arange(S)
        past_mask = (pos[None, :] < cache_len[:, None])[..., None]
        past_k = jnp.where(past_mask, cache_k, 0.0)
        past_v = jnp.where(past_mask, cache_v, 0.0)
        k = jnp.concatenate([past_k, k_new], axis=1)
        v = jnp.concatenate([past_v, v_new], axis=1)

        def to_heads(t):
            return t.reshape(B, t.shape[1], H, hd).transpose(0, 2, 1, 3)
        qh, kh, vh = (to_heads(q), to_heads(k), to_heads(v))
        scores = jnp.einsum('bhqd,bhkd->bhqk', qh, kh) / np.sqrt(hd).astype(np.float32)
        max_cl = jnp.max(cache_len)
        key_valid = jnp.concatenate([pos < max_cl, jnp.ones((T,), bool)])
        NEG = jnp.float32(-1e+30)
        scores = jnp.where(key_valid[None, None, None, :], scores, NEG)
        attn = jax.nn.softmax(scores, axis=-1)
        out = jnp.einsum('bhqk,bhkd->bhqd', attn, vh)
        out = out.transpose(0, 2, 1, 3).reshape(B, T, C)
        return out @ wo.T + bo

    def _L0_ffn_ref(hidden_states, gate_w, gate_bias, expert_gate, expert_up, expert_down, shared_gate, shared_up, shared_down):
        import jax, jax.numpy as jnp
        import numpy as np
        N_EXPERTS = 32
        TOP_K = 8
        N_GROUP = 4
        TOPK_GROUP = 2
        ROUTED_SCALING = 2.5

        def _gate(x, gate_w, gate_bias):
            T, E = (x.shape[0], gate_w.shape[0])
            logits = jnp.einsum('th,eh->te', x, gate_w)
            scores = jax.nn.sigmoid(logits)
            scores_choice = scores + gate_bias[None, :]
            grp = scores_choice.reshape(T, N_GROUP, E // N_GROUP)
            top2, _ = jax.lax.top_k(grp, 2)
            group_scores = top2.sum(-1)
            _, grp_idx = jax.lax.top_k(group_scores, TOPK_GROUP)
            group_mask = jax.nn.one_hot(grp_idx, N_GROUP, dtype=scores.dtype).sum(1)
            expert_mask = jnp.repeat(group_mask, E // N_GROUP, axis=1)
            masked = jnp.where(expert_mask > 0, scores_choice, 0.0)
            _, topk_idx = jax.lax.top_k(masked, TOP_K)
            topk_w = jnp.take_along_axis(scores, topk_idx, axis=1)
            topk_w = topk_w / (topk_w.sum(-1, keepdims=True) + 1e-20)
            topk_w = topk_w * ROUTED_SCALING
            return (topk_idx, topk_w)

        def _mlp(x, wg, wu, wd):
            return jnp.einsum('...i,hi->...h', jax.nn.silu(jnp.einsum('...h,ih->...i', x, wg)) * jnp.einsum('...h,ih->...i', x, wu), wd)
        orig_shape = hidden_states.shape
        H = orig_shape[-1]
        residuals = hidden_states
        x = hidden_states.reshape(-1, H)
        topk_idx, topk_w = _gate(x, gate_w, gate_bias)
        g = jnp.einsum('th,eih->eti', x, expert_gate)
        u = jnp.einsum('th,eih->eti', x, expert_up)
        outs = jnp.einsum('eti,ehi->eth', jax.nn.silu(g) * u, expert_down)
        outs_t = jnp.transpose(outs, (1, 0, 2))
        gathered = jnp.take_along_axis(outs_t, topk_idx[:, :, None], axis=1)
        final = (gathered * topk_w[:, :, None]).sum(1)
        shared = _mlp(residuals, shared_gate, shared_up, shared_down)
        return final.reshape(orig_shape) + shared

    def _L1_attn_ref(x, w_wave, b_wave, w_query, b_query, key_weight, w_se1, b_se1, w_se2, b_se2, w_out):
        import jax, jax.numpy as jnp
        import numpy as np
        B, L, C = (2, 256, 128)
        H, POS = (8, 16)
        D = C // H
        MAXS = 32
        S = MAXS + 1
        MAX_FREQ, MIN_FREQ = (16.0, 1.0)
        SCALE = POS ** (-0.5)
        b, l, c = x.shape
        stride_grid = jnp.arange(-MAXS // 2, MAXS // 2 + 1, dtype=x.dtype)
        wp = jax.nn.silu(x @ w_wave + b_wave).reshape(b, l, 3, H)
        freq = jax.nn.sigmoid(wp[:, :, 0, :]) * (MAX_FREQ - MIN_FREQ) + MIN_FREQ
        phase = jnp.tanh(wp[:, :, 1, :]) * MAX_FREQ
        decay = jax.nn.sigmoid(wp[:, :, 2, :]) * 9.5 + 0.5
        freq_avg = freq.mean(-1)
        phase_avg = phase.mean(-1)
        decay_avg = decay.mean(-1)
        q = jax.nn.silu(x @ w_query + b_query).reshape(b, l, H, POS)
        centers = jnp.arange(l, dtype=x.dtype)
        sample_pos = centers[None, :, None] + stride_grid[None, None, :] * freq_avg[..., None] + phase_avg[..., None]
        valid = (sample_pos >= 0) & (sample_pos < l)
        idx = jnp.clip(sample_pos.astype(jnp.int32), 0, l - 1)
        values = jnp.take_along_axis(x[:, :, None, :], idx[:, :, :, None], axis=1)
        values = values.reshape(b, l, S, H, D).transpose(0, 1, 3, 2, 4)
        rel = jnp.abs(stride_grid)[None, None, None, :] * freq_avg[:, :, None, None]
        qk = jnp.einsum('blhd,d->blh', q, key_weight)
        scores = qk[..., None] * rel * SCALE
        env = jnp.exp(-rel / jnp.clip(decay_avg, 0.1, None)[:, :, None, None])
        mask = valid[:, :, None, :]
        scores = jnp.where(mask, scores, -jnp.inf)
        attn = jax.nn.softmax(scores, axis=-1) * env * mask.astype(x.dtype)
        attn = attn / (attn.sum(-1, keepdims=True) + 1e-08)
        out = jnp.einsum('blhsd,blhs->blhd', values, attn).reshape(b, l, c)
        se = jax.nn.sigmoid(jax.nn.silu(out @ w_se1 + b_se1) @ w_se2 + b_se2)
        out = out * se
        out = jax.nn.silu(out @ w_out)
        return out

    def _L1_xattn_ref(q, k, v, attention_mask, Wq, bq, Wk, bk, Wv, bv, Wo, bo):
        import jax, jax.numpy as jnp
        import numpy as np
        N_HEADS = 16
        D_MODEL = 128
        HEAD_DIM = D_MODEL // N_HEADS
        MASK_FILL = -100000000.0

        def _split_heads(x):
            B, S, _ = x.shape
            return x.reshape(B, S, N_HEADS, HEAD_DIM).transpose(0, 2, 1, 3)
        qm = _split_heads(q @ Wq.T + bq)
        km = _split_heads(k @ Wk.T + bk)
        vm = _split_heads(v @ Wv.T + bv)
        scores = jnp.einsum('bnlh,bnph->bnlp', qm, km) / np.sqrt(HEAD_DIM).astype(np.float32)
        mask = attention_mask[:, None, None, :]
        scores = jnp.where(mask, scores, MASK_FILL)
        attn = jax.nn.softmax(scores, axis=-1)
        out = jnp.einsum('bnlp,bnph->bnlh', attn, vm)
        B, _, L, _ = out.shape
        out = out.transpose(0, 2, 1, 3).reshape(B, L, D_MODEL)
        return out @ Wo.T + bo

    def _L1_ffn_ref(x, w_gate, w_up, w_down):
        import jax, jax.numpy as jnp
        import numpy as np
        BLOCK = 32
        W_BITS = 4
        ACT_BITS = 16

        def act_qdq(x):
            qmax = 2.0 ** (ACT_BITS - 1) - 1.0
            scale = jnp.maximum(jnp.max(jnp.abs(x)) / qmax, 1e-12)
            return jnp.clip(jnp.round(x / scale), -qmax - 1.0, qmax) * scale

        def fixed_qdq_u16(x):
            scale = 1.0 / 65536.0
            return jnp.clip(jnp.round(x / scale), 0.0, 65535.0) * scale

        def lpbq_dequant(w):
            O, I = w.shape
            qmax = 2.0 ** (W_BITS - 1) - 1.0
            wb = w.reshape(O, I // BLOCK, BLOCK)
            s = jnp.maximum(jnp.max(jnp.abs(wb), axis=-1, keepdims=True) / qmax, 1e-12)
            wq = jnp.clip(jnp.round(wb / s), -qmax - 1.0, qmax) * s
            return wq.reshape(O, I)
        x = act_qdq(x)
        up = act_qdq(x @ lpbq_dequant(w_up).T)
        gate = act_qdq(x @ lpbq_dequant(w_gate).T)
        sig = fixed_qdq_u16(jax.nn.sigmoid(gate))
        gate = act_qdq(gate * sig)
        o = act_qdq(gate * up)
        return o @ lpbq_dequant(w_down).T

    def _L2_attn_ref(x, Wq, bq, Wk, bk, Wv, bv, Wbeta, bbeta, Wo, bo, wq_conv, bq_conv, wk_conv, bk_conv, wv_conv, bv_conv, norm_w):
        import jax, jax.numpy as jnp
        import numpy as np
        B, L, D, H = (8, 256, 128, 16)
        HD = D // H
        K = 4
        EPS = 1e-06

        def _short_conv(x, w, b):
            xp = jnp.pad(x, ((0, 0), (K - 1, 0), (0, 0)))
            y = b
            for i in range(K):
                y = y + w[:, i] * xp[:, i:i + x.shape[1], :]
            return y

        def _delta_rule(q, k, v, beta):
            qT = jnp.moveaxis(q, 1, 0)
            kT = jnp.moveaxis(k, 1, 0)
            vT = jnp.moveaxis(v, 1, 0)
            bT = jnp.moveaxis(beta, 1, 0)

            def step(S, inp):
                q_t, k_t, v_t, b_t = inp
                pred = jnp.einsum('bhk,bhkv->bhv', k_t, S)
                S = S + b_t[..., None, None] * (k_t[..., None] * (v_t - pred)[..., None, :])
                o_t = jnp.einsum('bhk,bhkv->bhv', q_t, S)
                return (S, o_t)
            S0 = jnp.zeros((q.shape[0], H, HD, HD), q.dtype)
            _, o = jax.lax.scan(step, S0, (qT, kT, vT, bT))
            return jnp.moveaxis(o, 0, 1)

        def _rmsnorm(x, w):
            return x * jax.lax.rsqrt(jnp.mean(x * x, axis=-1, keepdims=True) + EPS) * w
        Bx, Lx, Dx = x.shape
        k = _short_conv(x @ Wk.T + bk, wk_conv, bk_conv)
        q = _short_conv(x @ Wq.T + bq, wq_conv, bq_conv)
        v = _short_conv(x @ Wv.T + bv, wv_conv, bv_conv)
        beta = jax.nn.sigmoid(x @ Wbeta.T + bbeta)
        k = k.reshape(Bx, Lx, H, HD)
        q = q.reshape(Bx, Lx, H, HD)
        v = v.reshape(Bx, Lx, H, HD)
        v = jax.nn.silu(v)
        knorm = jnp.linalg.norm(k, axis=-1, keepdims=True)
        qnorm = jnp.linalg.norm(q, axis=-1, keepdims=True)
        k = k / (knorm + EPS)
        v = v / (knorm + EPS)
        q = q / (qnorm + EPS)
        o = _delta_rule(q, k, v, beta)
        o = _rmsnorm(o, norm_w)
        o = o.reshape(Bx, Lx, Dx)
        return o @ Wo.T + bo

    def _L2_xattn_ref(Q, K1, K2, Wq, bq, Wk1, bk1, Wk2, bk2, Wv1, bv1, Wv2, bv2, Wo, bo, g0, beta0, g1, beta1):
        import jax, jax.numpy as jnp
        import numpy as np
        DIM = 128
        H = 16
        DH = DIM // H
        LN_EPS = 1e-05

        def _linear_params(key, din, dout):
            kw, kb = jax.random.split(key)
            bound = 1.0 / np.sqrt(din)
            W = jax.random.uniform(kw, (din, dout), jnp.float32, -bound, bound)
            b = jax.random.uniform(kb, (dout,), jnp.float32, -bound, bound)
            return (W, b)

        def _layernorm(x, g, b):
            m = jnp.mean(x, axis=-1, keepdims=True)
            v = jnp.mean(jnp.square(x - m), axis=-1, keepdims=True)
            return (x - m) * jax.lax.rsqrt(v + LN_EPS) * g + b

        def _split_heads(x):
            B, N, _ = x.shape
            return x.reshape(B, N, H, DH).transpose(2, 0, 1, 3).reshape(H * B, N, DH)

        def _merge_heads(x, B):
            _, N, _ = x.shape
            return x.reshape(H, B, N, DH).transpose(1, 2, 0, 3).reshape(B, N, DIM)
        B = Q.shape[0]
        Qp = Q @ Wq + bq
        K1p = K1 @ Wk1 + bk1
        K2p = K2 @ Wk2 + bk2
        V1p = K1p @ Wv1 + bv1
        V2p = K2p @ Wv2 + bv2
        Q_ = _split_heads(Qp)
        K_ = jnp.concatenate([_split_heads(K1p), _split_heads(K2p)], axis=1)
        V_ = jnp.concatenate([_split_heads(V1p), _split_heads(V2p)], axis=1)
        scores = jnp.einsum('bqd,bkd->bqk', Q_, K_) / np.sqrt(DIM).astype(np.float32)
        A = jax.nn.softmax(scores, axis=1)
        out = Q_ + jnp.einsum('bqk,bkd->bqd', A, V_)
        out = _merge_heads(out, B)
        out = _layernorm(out, g0, beta0)
        out = out + jax.nn.relu(out @ Wo + bo)
        out = _layernorm(out, g1, beta1)
        return out

    def _L2_ffn_ref(x, ln_gamma, ln_beta, fc1_q, fc1_scales, fc1_bias, fc2_q, fc2_scales, fc2_bias):
        import jax, jax.numpy as jnp
        import numpy as np
        B, S, H, F, G = (8, 256, 128, 512, 128)
        EPS = 1e-05

        def _dequant(q, scales, g):
            K, N = q.shape
            w = (q.astype(jnp.float32) - 128.0).reshape(K // g, g, N) * scales[:, None, :]
            return w.reshape(K, N)
        residual = x
        mu = jnp.mean(x, axis=-1, keepdims=True)
        var = jnp.mean(jnp.square(x - mu), axis=-1, keepdims=True)
        h = (x - mu) * jax.lax.rsqrt(var + EPS) * ln_gamma + ln_beta
        hf = h.reshape(-1, H)
        w1 = _dequant(fc1_q, fc1_scales, G)
        y = hf @ w1 + fc1_bias
        y = jax.nn.silu(y)
        w2 = _dequant(fc2_q, fc2_scales, G)
        z = y @ w2 + fc2_bias
        return residual + 0.5 * z.reshape(residual.shape)

    def _L3_attn_ref(x, Wq, Wk, Wv, Wo, W_down_kv, W_up_k, W_up_v):
        import jax, jax.numpy as jnp
        import numpy as np
        D_MODEL = 128
        N_HEADS = 16
        HEAD_DIM = D_MODEL // N_HEADS
        D_LATENT = 32
        LAMBDA_DECAY = 0.01
        TIME_STEP = 0.01
        CLAMP = 10000.0

        def _reference_tuple_inner(x, Wq, Wk, Wv, Wo, W_down_kv, W_up_k, W_up_v):
            B, S, _ = x.shape
            q = x @ Wq
            k = x @ Wk
            v = x @ Wv
            latent_kv = (k + v) @ W_down_kv
            k_rec = latent_kv @ W_up_k
            v_rec = latent_kv @ W_up_v

            def heads(t):
                return t.reshape(B, S, N_HEADS, HEAD_DIM).transpose(0, 2, 1, 3)
            qh, kh, vh = (heads(q), heads(k_rec), heads(v_rec))
            scale = 1.0 / (jnp.sqrt(jnp.float32(D_MODEL)) + 1e-08)
            scores = jnp.einsum('bhqd,bhkd->bhqk', qh, kh) * scale
            scores = jnp.clip(jnp.nan_to_num(scores, nan=-1000000000.0), -CLAMP, CLAMP)
            idx = jnp.arange(S, dtype=jnp.float32)
            decay = jnp.exp(-LAMBDA_DECAY * TIME_STEP * jnp.abs(idx[:, None] - idx[None, :]))
            scores = scores * decay[None, None, :, :]
            scores = jnp.clip(jnp.nan_to_num(scores, nan=-1000000000.0), -CLAMP, CLAMP)
            attn = jax.nn.softmax(scores, axis=-1)
            out = jnp.einsum('bhqk,bhkd->bhqd', attn, vh)
            out = out.transpose(0, 2, 1, 3).reshape(B, S, D_MODEL)
            return (out @ Wo, latent_kv)
        return _reference_tuple_inner(x, Wq, Wk, Wv, Wo, W_down_kv, W_up_k, W_up_v)[0]

    def _L3_xattn_ref(x, context, g1, b1, g2, b2, Wq, Wkv, Wout, bout):
        import jax, jax.numpy as jnp
        import numpy as np
        DIM = 128
        CTX_DIM = 128
        HEADS = 8
        DIM_HEAD = 64
        INNER = HEADS * DIM_HEAD
        EPS = 1e-05

        def _layer_norm(x, gamma, beta):
            mu = jnp.mean(x, axis=-1, keepdims=True)
            var = jnp.mean(jnp.square(x - mu), axis=-1, keepdims=True)
            return (x - mu) * jax.lax.rsqrt(var + EPS) * gamma + beta
        b, n, _ = x.shape
        m = context.shape[1]
        scale = DIM_HEAD ** (-0.5)
        xn = _layer_norm(x, g1, b1)
        cn = _layer_norm(context, g2, b2)
        q = xn @ Wq
        kv = cn @ Wkv
        k, v = jnp.split(kv, 2, axis=-1)
        q = q.reshape(b, n, HEADS, DIM_HEAD).transpose(0, 2, 1, 3)
        k = k.reshape(b, m, HEADS, DIM_HEAD).transpose(0, 2, 1, 3)
        v = v.reshape(b, m, HEADS, DIM_HEAD).transpose(0, 2, 1, 3)
        sim = jnp.einsum('bhid,bhjd->bhij', q, k) * scale
        attn = jax.nn.softmax(sim, axis=-1)
        out = jnp.einsum('bhij,bhjd->bhid', attn, v)
        out = out.transpose(0, 2, 1, 3).reshape(b, n, INNER)
        return out @ Wout + bout

    def _L3_ffn_ref(hidden_states, gate_weight, gate_bias, w_gate, w_up, w_down, shared_w_gate, shared_w_up, shared_w_down, anchor_w_gate, anchor_w_up, anchor_w_down):
        import jax, jax.numpy as jnp
        import numpy as np
        HIDDEN = 128
        N_EXPERTS = 32
        MOE_I = 64
        N_GROUP = 4
        TOPK_GROUP = 2
        TOP_K = 6
        N_LOCAL_GROUPS = 16
        ANCHOR_I = 32
        SHARED_I = 64
        ROUTED_SCALE = 0.2
        ANCHOR_ALPHA = 0.1
        BATCH, SEQ = (1, 128)

        def _moe_forward(hidden_states, gate_weight, gate_bias, w_gate, w_up, w_down, shared_w_gate, shared_w_up, shared_w_down, anchor_w_gate, anchor_w_up, anchor_w_down):
            B, S, H = hidden_states.shape
            x = hidden_states.reshape(-1, H)
            T = x.shape[0]
            E = gate_weight.shape[0]
            L = anchor_w_gate.shape[0]
            logits = x @ gate_weight.T
            scores = jax.nn.sigmoid(logits)
            sc = scores + gate_bias
            grp = sc.reshape(T, N_GROUP, E // N_GROUP)
            group_scores = jax.lax.top_k(grp, 2)[0].sum(-1)
            _, gidx = jax.lax.top_k(group_scores, TOPK_GROUP)
            gmask = jax.nn.one_hot(gidx, N_GROUP, dtype=sc.dtype).sum(1)
            emask = jnp.repeat(gmask, E // N_GROUP, axis=1)
            masked = jnp.where(emask > 0, sc, -jnp.inf)
            _, topidx = jax.lax.top_k(masked, TOP_K)
            tw = jnp.take_along_axis(scores, topidx, axis=-1)
            tw = tw / (tw.sum(-1, keepdims=True) + 1e-20) * ROUTED_SCALE
            g = jnp.einsum('th,ehi->tei', x, w_gate)
            u = jnp.einsum('th,ehi->tei', x, w_up)
            eo = jnp.einsum('tei,eih->teh', jax.nn.silu(g) * u, w_down)
            cw = (jax.nn.one_hot(topidx, E, dtype=x.dtype) * tw[..., None]).sum(1)
            routed = jnp.einsum('te,teh->th', cw, eo)
            shared = jax.nn.silu(x @ shared_w_gate) * (x @ shared_w_up) @ shared_w_down
            lg = topidx[:, 0] // (E // L)
            ag = jnp.einsum('th,lhi->tli', x, anchor_w_gate)
            au = jnp.einsum('th,lhi->tli', x, anchor_w_up)
            ao = jnp.einsum('tli,lih->tlh', jax.nn.silu(ag) * au, anchor_w_down)
            acw = jax.nn.one_hot(lg, L, dtype=x.dtype)
            anchor = jnp.einsum('tl,tlh->th', acw, ao)
            out = routed + shared + ANCHOR_ALPHA * anchor
            return out.reshape(B, S, H)
        return _moe_forward(hidden_states, gate_weight, gate_bias, w_gate, w_up, w_down, shared_w_gate, shared_w_up, shared_w_down, anchor_w_gate, anchor_w_up, anchor_w_down)
    x = x + _L0_attn_ref(_layernorm(x, axis=-1), L0_attn_Wq, L0_attn_Wk, L0_attn_Wv, L0_attn_q_gamma, L0_attn_q_beta, L0_attn_k_gamma, L0_attn_k_beta, L0_attn_Wo, L0_attn_bo)
    x = x + _L0_xattn_ref(_layernorm(x, axis=-1), ctx_1024, ctx_1024, _lenS2, L0_xattn_wq, L0_xattn_wk, L0_xattn_wv, L0_xattn_wo, L0_xattn_bo)
    x = x + _L0_ffn_ref(_layernorm(x, axis=-1), L0_ffn_gate_w, L0_ffn_gate_bias, L0_ffn_expert_gate, L0_ffn_expert_up, L0_ffn_expert_down, L0_ffn_shared_gate, L0_ffn_shared_up, L0_ffn_shared_down)
    x = x + _L1_attn_ref(_layernorm(x, axis=-1), L1_attn_w_wave, L1_attn_b_wave, L1_attn_w_query, L1_attn_b_query, L1_attn_key_weight, L1_attn_w_se1, L1_attn_b_se1, L1_attn_w_se2, L1_attn_b_se2, L1_attn_w_out)
    x = x + _L1_xattn_ref(_layernorm(x, axis=-1), ctx_1024, ctx_1024, mask_BxS2_bf1, L1_xattn_Wq, L1_xattn_bq, L1_xattn_Wk, L1_xattn_bk, L1_xattn_Wv, L1_xattn_bv, L1_xattn_Wo, L1_xattn_bo)
    x = x + _L1_ffn_ref(_layernorm(x, axis=-1), L1_ffn_w_gate, L1_ffn_w_up, L1_ffn_w_down)
    x = x + _L2_attn_ref(_layernorm(x, axis=-1), L2_attn_Wq, L2_attn_bq, L2_attn_Wk, L2_attn_bk, L2_attn_Wv, L2_attn_bv, L2_attn_Wbeta, L2_attn_bbeta, L2_attn_Wo, L2_attn_bo, L2_attn_wq_conv, L2_attn_bq_conv, L2_attn_wk_conv, L2_attn_bk_conv, L2_attn_wv_conv, L2_attn_bv_conv, L2_attn_norm_w)
    x = x + _L2_xattn_ref(_layernorm(x, axis=-1), ctx_1024, ctx_1024, L2_xattn_Wq, L2_xattn_bq, L2_xattn_Wk1, L2_xattn_bk1, L2_xattn_Wk2, L2_xattn_bk2, L2_xattn_Wv1, L2_xattn_bv1, L2_xattn_Wv2, L2_xattn_bv2, L2_xattn_Wo, L2_xattn_bo, L2_xattn_g0, L2_xattn_beta0, L2_xattn_g1, L2_xattn_beta1)
    x = x + _L2_ffn_ref(_layernorm(x, axis=-1), L2_ffn_ln_gamma, L2_ffn_ln_beta, L2_ffn_fc1_q, L2_ffn_fc1_scales, L2_ffn_fc1_bias, L2_ffn_fc2_q, L2_ffn_fc2_scales, L2_ffn_fc2_bias)
    x = x + _L3_attn_ref(_layernorm(x, axis=-1), L3_attn_Wq, L3_attn_Wk, L3_attn_Wv, L3_attn_Wo, L3_attn_W_down_kv, L3_attn_W_up_k, L3_attn_W_up_v)
    x = x + _L3_xattn_ref(_layernorm(x, axis=-1), ctx_1024, L3_xattn_g1, L3_xattn_b1, L3_xattn_g2, L3_xattn_b2, L3_xattn_Wq, L3_xattn_Wkv, L3_xattn_Wout, L3_xattn_bout)
    x = x + _L3_ffn_ref(_layernorm(x, axis=-1), L3_ffn_gate_weight, L3_ffn_gate_bias, L3_ffn_w_gate, L3_ffn_w_up, L3_ffn_w_down, L3_ffn_shared_w_gate, L3_ffn_shared_w_up, L3_ffn_shared_w_down, L3_ffn_anchor_w_gate, L3_ffn_anchor_w_up, L3_ffn_anchor_w_down)
    return x

_drawn_inputs = setup_inputs


def setup_inputs(seed=0):
    import zlib

    import numpy as np

    out = dict(_drawn_inputs(seed))
    spreads = {'L0_attn_q_gamma': (1.0, 0.2),
     'L0_attn_q_beta': (0.0, 0.572),
     'L0_attn_k_gamma': (1.0, 0.6),
     'L0_attn_k_beta': (0.0, 0.784),
     'L0_attn_bo': (0.0, 0.286),
     'L0_xattn_bo': (0.0, 0.1),
     'L1_xattn_bq': (0.0, 1.961),
     'L1_xattn_bk': (0.0, 2.0),
     'L1_xattn_bv': (0.0, 0.506),
     'L1_xattn_bo': (0.0, 0.493),
     'L2_attn_bq': (0.0, 0.8),
     'L2_attn_bk': (0.0, 0.799),
     'L2_attn_bv': (0.0, 0.8),
     'L2_attn_bbeta': (0.0, 2.0),
     'L2_attn_bo': (0.0, 2.0),
     'L2_attn_bq_conv': (0.0, 0.41),
     'L2_attn_bk_conv': (0.0, 0.429),
     'L2_attn_bv_conv': (0.0, 0.487),
     'L2_attn_norm_w': (1.0, 0.6),
     'L2_xattn_g0': (1.0, 0.6),
     'L2_xattn_beta0': (0.0, 2.0),
     'L2_xattn_g1': (1.0, 0.6),
     'L2_xattn_beta1': (0.0, 2.0),
     'L2_ffn_ln_gamma': (1.0, 0.2),
     'L2_ffn_ln_beta': (0.0, 0.1),
     'L3_xattn_g1': (1.0, 0.6),
     'L3_xattn_b1': (0.0, 2.0),
     'L3_xattn_g2': (1.0, 0.6),
     'L3_xattn_b2': (0.0, 2.0),
     'L3_xattn_bout': (0.0, 2.0)}
    factors = {'L0_ffn_gate_w': 8.0,
     'L0_ffn_gate_bias': 8.0,
     'L0_ffn_expert_gate': 8.0,
     'L0_ffn_expert_up': 8.0,
     'L0_ffn_expert_down': 8.0,
     'L0_ffn_shared_gate': 8.0,
     'L0_ffn_shared_up': 8.0,
     'L0_ffn_shared_down': 8.0,
     'L1_attn_w_wave': 24.912,
     'L1_attn_b_wave': 64.0,
     'L1_attn_w_query': 64.0,
     'L1_attn_b_query': 64.0,
     'L1_attn_key_weight': 64.0,
     'L1_attn_w_se1': 64.0,
     'L1_attn_b_se1': 64.0,
     'L1_attn_w_se2': 64.0,
     'L1_attn_b_se2': 64.0,
     'L1_ffn_w_gate': 8.0,
     'L1_ffn_w_up': 8.0,
     'L1_ffn_w_down': 8.0,
     'L2_attn_Wbeta': 32.432,
     'L2_xattn_bq': 23.383,
     'L2_xattn_bk2': 29.2,
     'L2_xattn_bv2': 64.0,
     'L2_xattn_bo': 21.601,
     'L2_ffn_fc1_scales': 18.354,
     'L2_ffn_fc1_bias': 64.0,
     'L2_ffn_fc2_bias': 64.0,
     'L3_attn_Wq': 64.0,
     'L3_attn_Wk': 64.0,
     'L3_attn_Wv': 64.0,
     'L3_attn_Wo': 64.0,
     'L3_attn_W_down_kv': 64.0,
     'L3_attn_W_up_k': 64.0,
     'L3_attn_W_up_v': 64.0,
     'L3_xattn_Wq': 34.249,
     'L3_xattn_Wkv': 26.95,
     'L3_xattn_Wout': 26.477,
     'L3_ffn_gate_weight': 200.0,
     'L3_ffn_gate_bias': 200.0,
     'L3_ffn_w_gate': 200.0,
     'L3_ffn_w_up': 200.0,
     'L3_ffn_w_down': 200.0,
     'L3_ffn_shared_w_gate': 64.0,
     'L3_ffn_shared_w_up': 64.0,
     'L3_ffn_shared_w_down': 64.0,
     'L3_ffn_anchor_w_gate': 200.0,
     'L3_ffn_anchor_w_up': 200.0,
     'L3_ffn_anchor_w_down': 200.0,
     'L1_attn_w_out': 8.0,
     'L2_attn_Wq': 4.052,
     'L2_attn_Wk': 3.335,
     'L2_attn_Wv': 3.207,
     'L2_attn_wq_conv': 3.908,
     'L2_attn_wk_conv': 3.131,
     'L2_attn_wv_conv': 3.459,
     'L2_xattn_Wk1': 5.91,
     'L2_xattn_bk1': 8.0,
     'L2_xattn_Wk2': 6.585,
     'L2_xattn_Wv1': 6.883,
     'L2_xattn_bv1': 8.0,
     'L2_xattn_Wv2': 4.528}
    for name, (base, spread) in spreads.items():
        noise = np.random.default_rng([zlib.crc32(name.encode()), seed]).standard_normal(out[name].shape)
        drawn = base * np.exp(spread * noise) if base else spread * noise
        out[name] = jnp.asarray(drawn.astype(out[name].dtype))
    for name, factor in factors.items():
        out[name] = (out[name] * factor).astype(out[name].dtype)
    return out
```

```python
from contextlib import ExitStack

import concourse.bass as bass
import numpy as np
from concourse import mybir

F32 = mybir.dt.float32
BF16 = mybir.dt.bfloat16
I32 = mybir.dt.int32
I16 = mybir.dt.int16
U8 = mybir.dt.uint8
ALU = mybir.AluOpType
ACT = mybir.ActivationFunctionType
AX = mybir.AxisListType

P = 128
SC = 77
UNITS = 2
HEADS = 16
HD = 8
SLOT = 32
GROUPS = HEADS * SLOT // P
BANK = 512
LN_EPS = 1e-5


def spread(ap, axis, size):
    shape = list(ap.shape)
    return ap.unsqueeze(axis).broadcast_to(shape[:axis] + [size] + shape[axis:])


class Chain:

    def __init__(self, eng, sem, i=0, per_iteration=0):
        self.eng, self.sem, self.base, self.per, self.k = eng, sem, i * per_iteration, per_iteration, 0

    def link(self, ins):
        self.k += 1
        ins.then_inc(self.sem, 1)
        self.eng.wait_ge(self.sem, self.base + self.k)

    def close(self):
        assert self.k == self.per, (self.k, self.per)


class Stage:

    def __init__(self, nc, ctx, tag):
        self.nc, self.ctx, self.tag, self.sems = nc, ctx, tag, []
        ctx.callback(self.clear)

    def clear(self):
        self.nc.clear_and_free_semaphores(self.sems)
        self.nc.all_engine_barrier()

    def sb(self, name, shape, dt=F32):
        return self.ctx.enter_context(self.nc.sbuf_tensor(f"{self.tag}_{name}", shape, dt))

    def ps(self, name, shape, dt=F32):
        return self.ctx.enter_context(self.nc.psum_tensor(f"{self.tag}_{name}", shape, dt))

    def sem(self, name):
        self.sems.append(self.nc.alloc_semaphore(f"{self.tag}_{name}"))
        return self.sems[-1]


class Core:

    def __init__(self, nc, ctx, batch):
        def sb(name, shape, dt=F32):
            return ctx.enter_context(nc.sbuf_tensor(name, shape, dt))

        self.nc, self.batch = nc, batch
        self.x = sb("x_all", [P, batch, P])
        self.stat = sb("stat_all", [P, batch, 2])
        self.rstd = sb("rstd_all", [P, batch, 1])
        self.rstd2 = sb("rstd2_all", [P, batch, 1])
        self.nmr2 = sb("nmr2_all", [P, batch, 1])
        self.nmr = sb("nmr_all", [P, batch, 1])
        self.ctxT = sb("ctxT", [P, batch, SC])
        self.ident = sb("ident", [P, P])
        self.beat = sb("beat", [1, 1])
        self.ones = sb("ones", [1, P])


def load_everything(nc, core, dram):
    with ExitStack() as ctx:
        st = Stage(nc, ctx, "load")
        x_in, c_in, stats_step = st.sem("x_in"), st.sem("c_in"), st.sem("stats_step")
        bn = st.sb("bn", [P, 6])
        mv = st.sb("mv", [P, 2])
        block = ctx.enter_context(nc.Block())

        @block.sync
        def _(sp):
            sp.dma_start(core.x[:, :, :], dram["x"].rearrange("b t d -> t b d")).then_inc(x_in, 16)
            sp.wait_ge(x_in, 16)

        @block.scalar
        def _(act):
            act.dma_start(core.ctxT[:, :, :], dram["ctxT"]).then_inc(c_in, 16)
            act.dma_start(core.ident[:, :], dram["ident"]).then_inc(c_in, 16)
            act.dma_start(core.ones[:, :], dram["ident"][0:1, :]).then_inc(c_in, 16)
            act.wait_ge(c_in, 48)

        @block.vector
        def _(dve):
            dve.wait_ge(c_in, 48)
            nc.vector.memset(core.ones[:, :], 1.0)
            dve.wait_ge(x_in, 16)
            with dve.Fori(0, core.batch) as i:
                chain = Chain(dve, stats_step, i, 3)
                chain.link(take_stats(dve, chain, core, i, bn, mv))
                chain.close()


def store_everything(nc, core, dram):
    with ExitStack() as ctx:
        st = Stage(nc, ctx, "store")
        x_out = st.sem("x_out")
        block = ctx.enter_context(nc.Block())

        @block.sync
        def _(sp):
            sp.dma_start(dram["out"].rearrange("b t d -> t b d"), core.x[:, :, :]).then_inc(x_out, 16)
            sp.wait_ge(x_out, 16)


def take_stats(dve, chain, core, b, bn, mv):
    dve.memset(core.beat[:, :], 0.0)
    chain.link(dve.bn_stats(bn[:, :], core.x[:, b, :]))
    dve.memset(core.beat[:, :], 0.0)
    chain.link(dve.bn_aggr(mv[:, :], bn[:, :]))
    return dve.tensor_copy(core.stat[:, b, :], mv[:, :])


def norm_scalars(nc, core, tag, second_eps=None):
    with ExitStack() as ctx:
        st = Stage(nc, ctx, tag + "_ln")
        var_ready, std_ready, step, var2_ready, std2_ready = (
            st.sem(n) for n in ("var_ready", "std_ready", "step", "var2_ready", "std2_ready"))
        std = st.sb("std", [P, core.batch])
        var = st.sb("var", [P, core.batch])
        rstd, nmr, rstd2, nmr2 = (a[:, :, 0] for a in (core.rstd, core.nmr, core.rstd2, core.nmr2))
        block = ctx.enter_context(nc.Block())

        @block.scalar
        def _(act):
            act.wait_ge(var_ready, 1)
            act.activation(std[:, :], var[:, :], ACT.Sqrt).then_inc(std_ready, 1)
            if second_eps is not None:
                act.wait_ge(var2_ready, 1)
                act.activation(std[:, :], var[:, :], ACT.Sqrt).then_inc(std2_ready, 1)

        @block.vector
        def _(dve):
            chain = Chain(dve, step)
            dve.tensor_scalar(var[:, :], core.stat[:, :, 1], LN_EPS, None, ALU.add).then_inc(var_ready, 1)
            dve.wait_ge(std_ready, 1)
            chain.link(dve.reciprocal(rstd, std[:, :]))
            chain.link(dve.scalar_tensor_tensor(nmr, core.stat[:, :, 0], -1.0, rstd, ALU.mult, ALU.mult))
            if second_eps is not None:
                chain.link(dve.tensor_tensor(var[:, :], core.stat[:, :, 1], rstd, ALU.mult))
                chain.link(dve.tensor_tensor(var[:, :], var[:, :], rstd, ALU.mult))
                dve.tensor_scalar(var[:, :], var[:, :], second_eps, None, ALU.add).then_inc(var2_ready, 1)
                dve.wait_ge(std2_ready, 1)
                chain.link(dve.reciprocal(std[:, :], std[:, :]))
                dve.tensor_tensor(rstd2, rstd, std[:, :], ALU.mult)
                dve.tensor_tensor(nmr2, nmr, std[:, :], ALU.mult)


def softmax_attention(nc, core, dram, tag, heads_norm=False, context=None, latent=False):
    batch = core.batch
    own = context != "only"
    key_tiles = ([(SC, "ctx")] if context else []) + ([(P, "own")] if own else [])
    NK = sum(n for n, _ in key_tiles)
    CHUNK = min(BANK // NK, 4)
    NCH = HEADS // CHUNK
    K = HD + 1 if context else HD
    blocks = [(h, t) for h in range(CHUNK) for t in range(len(key_tiles))]
    scale = 1.0 if latent else float(HD) ** -0.5

    with ExitStack() as ctx:
        st = Stage(nc, ctx, tag)
        U = UNITS

        def unit_sb(name, shape, dt=F32):
            return [st.sb(f"{name}{u}", shape, dt) for u in range(U)]

        names = [n for n in (tag + "_w_qkv", tag + "_w_q", tag + "_b_q", tag + "_w_k", tag + "_w_kc", tag + "_w_v",
                             tag + "_w_vc", tag + "_aux", tag + "_w_o", tag + "_b_o", tag + "_b_v",
                             tag + "_w_kv", tag + "_w_down", tag + "_w_up_v", tag + "_gb") if n in dram]
        shared = (["rope"] if heads_norm else []) + (["decay"] if latent else [])
        w = {n: st.sb(n + "_s", list(dram[n].shape)) for n in names + shared}

        def W(n):
            return w[f"{tag}_{n}"]

        xn, xT = unit_sb("xn", [P, P]), unit_sb("xT", [P, P])
        qT, kT = unit_sb("qT", [P, GROUPS, P]), unit_sb("kT", [P, GROUPS, NK])
        v = [unit_sb(f"v_{kind}", [n, HEADS, HD + 1]) for n, kind in key_tiles]
        probs = [unit_sb(f"probs{j}_", [P, CHUNK, NK]) for j in range(2)]
        pT = [unit_sb(f"pT{j}_", [P, 4, P]) for j in range(2)]
        top = unit_sb("top", [P, HEADS])
        rz = unit_sb("rz", [P, HEADS])
        o, oT = unit_sb("o", [P, P]), unit_sb("oT", [P, P])
        bn, mv = unit_sb("bn", [P, 6]), unit_sb("mv", [P, 2])
        if heads_norm:
            qk = unit_sb("qk", [P, 2, HEADS, HD])
            sq = unit_sb("sq", [P, 2, HEADS, HD])
            rot = unit_sb("rot", [P, 2, HEADS, HD])
            hstat = unit_sb("hstat", [P, 2 * HEADS])
            hvar = unit_sb("hvar", [P, 2 * HEADS])
            hrstd = unit_sb("hrstd", [P, 2 * HEADS])
            minus_half = st.sb("minus_half", [P, 2 * HEADS])
            padded = unit_sb("padded", [P, 2, GROUPS, 4, SLOT])
            ident_b = st.sb("ident_b", [P, P], BF16)
            causal_b = st.sb("causal_b", [P, 4, P], BF16)
        if context:
            rows = st.sb("rows", [2, batch, SC])
            ctxm, ctxu = unit_sb("ctxm", [P, SC]), unit_sb("ctxu", [P, SC])
        if latent:
            kvT, latT = unit_sb("kvT", [P, P]), unit_sb("latT", [SLOT, P])

        scores = [st.ps(f"scores{u}", [P, 2, BANK]) for u in range(U)]
        ptp = [st.ps(f"ptp{j}", [P, 4, P]) for j in range(2)]
        misc = [st.ps(f"misc{u}", [P, BANK]) for u in range(U)]
        A, O, B2 = slice(0, P), slice(P, P + HEADS * (HD + 1)), slice(3 * P, 4 * P)

        s = {n: st.sem(n) for n in (
            "loaded", "consts", "rows_step", "rows_ready", "xn_ready", "xt_done", "xt_ready", "vec_step",
            "first_step", "last_step", "scores_done", "shifted", "probs_ready",
            "pt_done", "pt_copied", "pv_done", "o_ready", "ot_done", "ot_ready",
            "y_done", "y_added", "q_done", "q_ready", "k_done", "k_ready", "v_done", "v_ready")}
        if heads_norm:
            s |= {n: st.sem(n) for n in ("proj_done", "var_ready", "square_ready", "centred", "hrstd_ready",
                                         "padded_ready")}
        if context:
            s |= {n: st.sem(n) for n in ("mask_done", "ctxm_ready", "ctxu_ready", "kc_done", "kc_ready",
                                         "vc_done", "vc_ready")}
        if latent:
            s |= {n: st.sem(n) for n in ("kv_done", "kv_ready", "lat_done", "lat_ready")}
        n_loads = len(names) + len(shared) + (2 if context else 0) + (2 if heads_norm else 0)
        mask_raw = st.sb("mask_raw", [2, batch, SC], U8) if context == "only" else None
        len_raw = st.sb("len_raw", [2, batch], I32) if context == "past" else None
        row_c = st.sb("row_c", [2, 2 + SC]) if context else None
        stage_f = st.sb("stage_f", [P, 5 * P]) if heads_norm else None
        len_f = st.sb("len_f", [2, batch]) if context == "past" else None
        len_max = st.sb("len_max", [2, 1]) if context == "past" else None
        keep_less_fill = st.sb("keep_less_fill", [2, 1]) if context == "only" else None
        beyond = st.sb("beyond", [2, SC]) if context == "past" else None
        block = ctx.enter_context(nc.Block())

        def head_of(c, j):
            return (4 * c + j) if CHUNK == 4 else (8 * (c // 4) + 4 * (c % 2) + 2 * (c // 2 % 2) + j)

        def count(b, per=1, extra=1):
            i, at = b
            return at * per + extra if i is None else i * (U * per) + (at * per + extra)

        def number(b):
            return count(b, 1, 0)

        def neighbour(b, d):
            return (b[0], b[1] + d)

        def step_of(k):
            return k * 4 // NCH if k * 4 % NCH == 0 else None

        @block.sync
        def _(sp):
            for n in names + shared:
                sp.dma_start(w[n][tuple(slice(None) for _ in dram[n].shape)], dram[n]).then_inc(s["loaded"], 16)
            if context:
                sp.dma_start(row_c[:, :], dram["row_c"]).then_inc(s["loaded"], 16)
                if context == "only":
                    src = dram["key_mask"].rearrange("(a b) t -> a b t", a=1).broadcast_to([2, batch, SC])
                    sp.dma_start(mask_raw[:, :, :], src).then_inc(s["loaded"], 16)
                else:
                    src = dram["lens"].rearrange("(a b) -> a b", a=1).broadcast_to([2, batch])
                    sp.dma_start(len_raw[:, :], src).then_inc(s["loaded"], 16)
            if heads_norm:
                sp.dma_start(stage_f[:, 0:P], dram["ident"]).then_inc(s["loaded"], 16)
                sp.dma_start(stage_f[:, P:5 * P], dram["causal"]).then_inc(s["loaded"], 16)
            sp.wait_ge(s["loaded"], 16 * n_loads)

        @block.gpsimd
        def _(pool):
            if not heads_norm:
                return
            pool.wait_ge(s["consts"], 1)
            with pool.Fori(0, batch // U) as i:
                for u in range(U):
                    pool.wait_ge(s["var_ready"], i * U + (u + 1))
                    pool.tensor_tensor(hrstd[u][:, :], hvar[u][:, :], minus_half[:, :], ALU.pow)\
                        .then_inc(s["hrstd_ready"], 1)

        @block.vector
        def _(dve):
            once = Chain(dve, s["rows_step"])
            for tile in v:
                for u in range(U):
                    dve.memset(tile[u][:, :, HD:HD + 1], 1.0)
            dve.wait_ge(s["loaded"], 16 * n_loads)
            if heads_norm:
                for u in range(U):
                    dve.memset(padded[u][:, :, :, :, :], 0.0)
                dve.memset(minus_half[:, :], -0.5)
                dve.tensor_copy(ident_b[:, :], stage_f[:, 0:P])
                once.link(dve.tensor_copy(causal_b[:, :, :].rearrange("p a b -> p (a b)"), stage_f[:, P:5 * P]))
            if context == "only":
                once.link(dve.tensor_tensor(keep_less_fill[:, :], row_c[:, 0:1], row_c[:, 1:2], ALU.subtract))
                once.link(dve.tensor_copy(rows[:, :, :], mask_raw[:, :, :]))
                once.link(dve.tensor_scalar(rows[:, :, :], rows[:, :, :], keep_less_fill[:, :], row_c[:, 1:2],
                                            ALU.mult, ALU.add))
            if context == "past":
                pos = row_c[:, 2:2 + SC]
                once.link(dve.tensor_copy(len_f[:, :], len_raw[:, :]))
                once.link(dve.tensor_reduce(len_max[:, :], len_f[:, :], AX.X, ALU.max))
                once.link(dve.tensor_scalar(beyond[:, :], pos, len_max[:, :], row_c[:, 1:2], ALU.is_ge, ALU.mult))
                once.link(dve.tensor_tensor(rows[:, :, :], spread(pos, 1, batch), spread(len_f[:, :], 2, SC), ALU.is_lt))
                once.link(dve.tensor_scalar(rows[:, :, :], rows[:, :, :], row_c[:, 0:1], None, ALU.mult))
                once.link(dve.tensor_tensor(rows[:, :, :], rows[:, :, :], spread(beyond[:, :], 1, batch), ALU.add))
            dve.sem_inc(s["rows_ready"], 1)
            dve.drain().then_inc(s["consts"], 1)

            def shift(chain, b, c, u):
                dve.wait_ge(s["scores_done"], count(b, NCH, c + 1))
                S = scores[u][:, c % 2, 0:CHUNK * NK].rearrange("p (h k) -> p h k", h=CHUNK)
                tp = top[u][:, c * CHUNK:(c + 1) * CHUNK]
                dst = probs[c % 2][u][:, :, :]
                if latent:
                    chain.link(dve.tensor_scalar(dst, S, -1e4, 1e4, ALU.max, ALU.min))
                    chain.link(dve.tensor_tensor(dst, dst, spread(w["decay"][:, :], 1, CHUNK), ALU.mult))
                    S = dst
                chain.link(dve.tensor_reduce(tp, S, AX.X, ALU.max))
                dve.tensor_tensor(dst, S, spread(tp, 2, NK), ALU.subtract).then_inc(s["shifted"], 1)

            def finish(chain, b, u):
                dve.wait_ge(s["pv_done"], count(b, NCH, NCH))
                acc = misc[u][:, O].rearrange("p (h f) -> p h f", h=HEADS)
                chain.link(dve.reciprocal(rz[u][:, :], acc[:, :, HD]))
                dve.tensor_tensor(o[u][:, :].rearrange("p (h f) -> p h f", h=HEADS), acc[:, :, 0:HD],
                                  spread(rz[u][:, :], 2, HD), ALU.mult).then_inc(s["o_ready"], 1)

            def head_norm(chain, b, u):
                acc = scores[u][:, 0, 0:2 * P].rearrange("p (a h f) -> p a h f", a=2, h=HEADS)
                hs = hstat[u][:, :].rearrange("p (a h) -> p a h", a=2)
                dve.wait_ge(s["proj_done"], count(b))
                chain.link(dve.tensor_reduce(hs, acc, AX.X, ALU.add))
                chain.link(dve.tensor_scalar(hstat[u][:, :], hstat[u][:, :], 1.0 / HD, None, ALU.mult))
                chain.link(dve.tensor_tensor(qk[u][:, :, :, :], acc, spread(hs, 3, HD), ALU.subtract))
                chain.link(dve.tensor_tensor(sq[u][:, :, :, :], qk[u][:, :, :, :], qk[u][:, :, :, :], ALU.mult))
                chain.link(dve.tensor_reduce(hs, sq[u][:, :, :, :], AX.X, ALU.add))
                dve.tensor_scalar(hvar[u][:, :], hstat[u][:, :], 1.0 / HD, LN_EPS, ALU.mult, ALU.add)\
                   .then_inc(s["var_ready"], 1)

            def rotate(chain, b, u):
                flat = qk[u][:, :, :, :].rearrange("p a h f -> p (a h) f")
                gb = W("gb")[:, :].rearrange("p (s a f) -> p s a f", s=2, a=2)
                dve.wait_ge(s["hrstd_ready"], count(b))
                chain.link(dve.tensor_tensor(flat, flat, spread(hrstd[u][:, :], 2, HD), ALU.mult))
                for a in range(2):
                    chain.link(dve.tensor_tensor(qk[u][:, a, :, :], qk[u][:, a, :, :],
                                                 spread(gb[:, 0, a, :], 1, HEADS), ALU.mult))
                    chain.link(dve.tensor_tensor(qk[u][:, a, :, :], qk[u][:, a, :, :],
                                                 spread(gb[:, 1, a, :], 1, HEADS), ALU.add))
                cos, sin = w["rope"][:, 0:HD], w["rope"][:, HD:2 * HD]
                r = rot[u][:, :, :, :].rearrange("p a h f -> p (a h) f")
                dve.tensor_tensor(r[:, :, 0:HD // 2], flat[:, :, 1:HD:2], spread(sin[:, 0:HD // 2], 1, 2 * HEADS), ALU.mult)
                dve.tensor_tensor(r[:, :, HD // 2:HD], flat[:, :, 0:HD:2], spread(sin[:, HD // 2:HD], 1, 2 * HEADS), ALU.mult)
                chain.link(dve.tensor_tensor(sq[u][:, :, :, :].rearrange("p a h f -> p (a h) f"), flat,
                                             spread(cos, 1, 2 * HEADS), ALU.mult))
                for a in range(2):
                    last = dve.tensor_tensor(padded[u][:, a, :, :, 0:HD].rearrange("p g r f -> p r g f"),
                                             sq[u][:, a, :, :].rearrange("p (r g) f -> p r g f", g=GROUPS),
                                             rot[u][:, a, :, :].rearrange("p (r g) f -> p r g f", g=GROUPS), ALU.add)
                last.then_inc(s["padded_ready"], 1)

            def residual(chain, b, u):
                dve.wait_ge(s["y_done"], count(b))
                n = number(b)
                chain.link(dve.tensor_tensor(core.x[:, n, :], core.x[:, n, :], misc[u][:, B2], ALU.add))
                take_stats(dve, chain, core, n, bn[u], mv[u]).then_inc(s["y_added"], 1)

            def mask_context(b, u):
                dve.wait_ge(s["mask_done"], count(b))
                dve.tensor_tensor(ctxm[u][:, :], scores[u][:, 1, 0:SC], core.ctxT[:, number(b), :], ALU.mult)\
                   .then_inc(s["ctxm_ready"], 1)

            def copy_q(b, u):
                dve.wait_ge(s["q_done"], count(b))
                acc = scores[u][:, 0, :].rearrange("p (g t) -> p g t", g=GROUPS)
                if context:
                    last = dve.tensor_tensor(qT[u][:, :, :], acc, spread(W("b_q")[:, :], 2, P), ALU.add)
                elif latent:
                    last = dve.tensor_scalar(qT[u][:, :, :], acc, 1.0 / (float(np.sqrt(np.float32(P))) + 1e-8), None,
                                             ALU.mult)
                else:
                    last = dve.tensor_copy(qT[u][:, :, :], acc)
                last.then_inc(s["q_ready"], 1)

            def front(chain, b, u, step):
                if step == 0 and context:
                    mask_context(b, u)
                if step == 0 and heads_norm:
                    head_norm(chain, b, u)
                if step == 1 and not heads_norm:
                    copy_q(b, u)
                if step == 3 and heads_norm:
                    rotate(chain, b, u)
                    copy_q(b, u)

            def attend(chain, b, u, tail=True, start_next=True):
                before, behind, other = neighbour(b, -1), neighbour(b, 1), 1 - u
                if tail:
                    finish(chain, before, other)
                for c in range(NCH):
                    shift(chain, b, c, u)
                    if tail and step_of(c) == 1:
                        residual(chain, before, other)
                    if start_next:
                        front(chain, behind, other, step_of(c))

            once = Chain(dve, s["first_step"])
            for step in range(4):
                front(once, (None, 0), 0, step)
            attend(once, (None, 0), 0, tail=False)
            per_sequence = (11 if heads_norm else 0) + (3 if latent else 1) * NCH + 1 + 3
            with dve.Fori(0, batch // U - 1) as i:
                chain = Chain(dve, s["vec_step"], i, per_sequence * U)
                attend(chain, (i, 1), 1)
                attend(chain, (i, 2), 0)
                chain.close()
            once = Chain(dve, s["last_step"])
            attend(once, (None, batch - 1), 1, start_next=False)
            finish(once, (None, batch - 1), 1)
            residual(once, (None, batch - 1), 1)

        @block.scalar
        def _(act):
            act.wait_ge(s["consts"], 1)

            def begin(b, u):
                n = number(b)
                act.activation(xn[u][:, :], core.x[:, n, :], ACT.Identity, bias=core.nmr[:, n, :],
                               scale=core.rstd[:, n, :]).then_inc(s["xn_ready"], 1)
                if context:
                    act.activation(ctxu[u][:, :], core.ctxT[:, n, :], ACT.Copy).then_inc(s["ctxu_ready"], 1)
                act.wait_ge(s["xt_done"], count(b))
                act.activation(xT[u][:, :], scores[u][:, 0, A], ACT.Copy).then_inc(s["xt_ready"], 1)

            def copy_k(b, u):
                act.wait_ge(s["k_done"], count(b))
                act.activation(kT[u][:, :, NK - P:NK], scores[u][:, 1, :].rearrange("p (g t) -> p g t", g=GROUPS),
                               ACT.Copy).then_inc(s["k_ready"], 1)

            def copy_v(b, u, src):
                act.wait_ge(s["v_done"], count(b))
                act.activation(v[-1][u][:, :, 0:HD], src.rearrange("p (h f) -> p h f", h=HEADS), ACT.Copy)\
                   .then_inc(s["v_ready"], 1)

            def front(b, u, step):
                if heads_norm and step == 0:
                    copy_v(b, u, scores[u][:, 1, 0:P])
                if heads_norm and step == 3:
                    copy_k(b, u)
                if latent and step == 0:
                    act.wait_ge(s["kv_done"], count(b))
                    act.activation(kvT[u][:, :], scores[u][:, 1, 0:P], ACT.Copy).then_inc(s["kv_ready"], 1)
                if latent and step == 1:
                    act.wait_ge(s["lat_done"], count(b))
                    act.activation(latT[u][:, :], scores[u][0:SLOT, 1, P:2 * P], ACT.Copy).then_inc(s["lat_ready"], 1)
                if own and not heads_norm and step == (2 if latent else 1):
                    copy_k(b, u)
                if context and step == 2:
                    act.wait_ge(s["kc_done"], count(b))
                    act.activation(kT[u][:, :, 0:SC], misc[u][:, 0:GROUPS * SC].rearrange("p (g t) -> p g t", g=GROUPS),
                                   ACT.Copy).then_inc(s["kc_ready"], 1)
                if own and not heads_norm and step == 2:
                    copy_v(b, u, misc[u][:, B2])
                if context and step == 3:
                    act.wait_ge(s["vc_done"], count(b))
                    act.activation(v[0][u][:, :, 0:HD], scores[u][0:SC, 1, 0:P].rearrange("p (h f) -> p h f", h=HEADS),
                                   ACT.Copy).then_inc(s["vc_ready"], 1)

            def tail(b, u):
                act.wait_ge(s["ot_done"], count(b))
                act.activation(oT[u][:, :], misc[u][:, A], ACT.Copy).then_inc(s["ot_ready"], 1)

            def exps(b, c, u):
                act.wait_ge(s["shifted"], count(b, NCH, c + 1))
                act.activation(probs[c % 2][u][:, :, :], probs[c % 2][u][:, :, :], ACT.Exp, scale=scale)\
                   .then_inc(s["probs_ready"], 1)

            def copies(b, c, u):
                act.wait_ge(s["pt_done"], count(b, NCH, c + 1))
                src, dst = ptp[c % 2], pT[c % 2][u]
                if len(key_tiles) == 1:
                    m = key_tiles[0][0]
                    act.activation(dst[0:m, :, :], src[0:m, :, :], ACT.Copy).then_inc(s["pt_copied"], 1)
                else:
                    act.activation(dst[0:SC, 0:4:2, :], src[0:SC, 0:4:2, :], ACT.Copy)
                    act.activation(dst[:, 1:4:2, :], src[:, 1:4:2, :], ACT.Copy).then_inc(s["pt_copied"], 1)

            def attend(b, u, with_tail=True, start_next=True):
                if start_next:
                    begin(neighbour(b, 1), 1 - u)
                for c in range(NCH):
                    exps(b, c, u)
                    if c:
                        copies(b, c - 1, u)
                    if with_tail and step_of(c) == 0:
                        tail(neighbour(b, -1), 1 - u)
                    if start_next and step_of(c) != 3:
                        front(neighbour(b, 1), 1 - u, step_of(c))
                copies(b, NCH - 1, u)
                if start_next:
                    front(neighbour(b, 1), 1 - u, 3)

            begin((None, 0), 0)
            for step in range(4):
                front((None, 0), 0, step)
            attend((None, 0), 0, with_tail=False)
            with act.Fori(0, batch // U - 1) as i:
                attend((i, 1), 1)
                attend((i, 2), 0)
            attend((None, batch - 1), 1, start_next=False)
            tail((None, batch - 1), 1)

        @block.tensor
        def _(pe):
            pe.wait_ge(s["consts"], 1)

            def mm(out, lhsT, rhs, start=True, stop=True, skip=False):
                return pe.matmul(out, lhsT, rhs, start=start, stop=stop, skip_group_check=skip)

            def begin(b, u):
                pe.wait_ge(s["xn_ready"], count(b))
                pe.transpose(scores[u][:, 0, A], xn[u][:, :], core.ident[:, :]).then_inc(s["xt_done"], 1)
                if context:
                    mm(scores[u][:, 1, 0:SC], core.ones[0:1, :], rows[0:1, number(b), :]).then_inc(s["mask_done"], 1)

            def front_0(b, u):
                pe.wait_ge(s["xt_ready"], count(b))
                if heads_norm:
                    mm(scores[u][:, 0, 0:2 * P], xT[u][:, :], W("w_qkv")[:, 0:2 * P]).then_inc(s["proj_done"], 1)
                    mm(scores[u][:, 1, 0:P], xT[u][:, :], W("w_qkv")[:, 2 * P:3 * P]).then_inc(s["v_done"], 1)
                    return
                if latent:
                    mm(scores[u][:, 1, 0:P], W("w_kv")[:, 0:P], xT[u][:, :], stop=False)
                    mm(scores[u][:, 1, 0:P], W("w_kv")[:, P:2 * P], xT[u][:, :], start=False).then_inc(s["kv_done"], 1)
                for g in range(GROUPS):
                    last = mm(scores[u][:, 0, g * P:(g + 1) * P], W("w_q")[:, g * P:(g + 1) * P], xT[u][:, :])
                last.then_inc(s["q_done"], 1)
                if context:
                    pe.wait_ge(s["ctxm_ready"], count(b))
                if own and not latent:
                    for g in range(GROUPS):
                        last = mm(scores[u][:, 1, g * P:(g + 1) * P], W("w_k")[:, g * P:(g + 1) * P], xT[u][:, :])
                    last.then_inc(s["k_done"], 1)

            def front_1(b, u):
                if latent:
                    pe.wait_ge(s["kv_ready"], count(b))
                    mm(scores[u][0:SLOT, 1, P:2 * P], W("w_down")[:, :], kvT[u][:, :]).then_inc(s["lat_done"], 1)

            def front_2(b, u):
                if latent:
                    pe.wait_ge(s["lat_ready"], count(b))
                    for g in range(GROUPS):
                        last = mm(scores[u][:, 1, g * P:(g + 1) * P], W("w_k")[:, g * P:(g + 1) * P], latT[u][:, :])
                    last.then_inc(s["k_done"], 1)
                    mm(misc[u][:, B2], latT[u][:, :], W("w_up_v")[:, :]).then_inc(s["v_done"], 1)
                if context:
                    if own:
                        mm(misc[u][:, B2], xT[u][:, :], W("w_v")[:, :]).then_inc(s["v_done"], 1)
                    for g in range(GROUPS):
                        out = misc[u][:, g * SC:(g + 1) * SC]
                        mm(out, W("w_kc")[:, g * P:(g + 1) * P], ctxm[u][:, :], stop=False)
                        last = mm(out, W("aux")[:, g * P:(g + 1) * P], rows[:, number(b), :], start=False)
                    last.then_inc(s["kc_done"], 1)

            def front_3(b, u):
                if context:
                    pe.wait_ge(s["k_ready" if own else "q_ready"], count(b))
                    src = ctxm[u] if own else ctxu[u]
                    if not own:
                        pe.wait_ge(s["ctxu_ready"], count(b))
                    out = scores[u][0:SC, 1, 0:P]
                    last = mm(out, src[:, :], W("w_vc")[:, :], stop=own)
                    if not own:
                        last = mm(out, core.ones[0:1, 0:SC], W("b_v")[0:1, :], start=False)
                    last.then_inc(s["vc_done"], 1)
                if heads_norm:
                    pe.wait_ge(s["padded_ready"], count(b))
                    pe.wait_ge(s["v_ready"], count(b))
                    for a, sem in ((0, "q_done"), (1, "k_done")):
                        for g in range(GROUPS):
                            last = pe.transpose(scores[u][:, a, g * P:(g + 1) * P],
                                                padded[u][:, a, g, :, :].rearrange("p h f -> p (h f)"), core.ident[:, :])
                        last.then_inc(s[sem], 1)

            def tail_turn(b, u):
                pe.wait_ge(s["o_ready"], count(b))
                pe.transpose(misc[u][:, A], o[u][:, :], core.ident[:, :]).then_inc(s["ot_done"], 1)

            def tail_project(b, u):
                pe.wait_ge(s["ot_ready"], count(b))
                last = mm(misc[u][:, B2], oT[u][:, :], W("w_o")[:, :], stop=latent)
                if not latent:
                    last = mm(misc[u][:, B2], core.ones[0:1, :], W("b_o")[0:1, :], start=False)
                last.then_inc(s["y_done"], 1)

            def scoring(b, c, u):
                if c == 0:
                    pe.wait_ge(s["q_ready"], count(b))
                    if own:
                        pe.wait_ge(s["k_ready"], count(b))
                        if not heads_norm:
                            pe.wait_ge(s["v_ready"], count(b))
                    if context:
                        pe.wait_ge(s["kc_ready"], count(b))
                        pe.wait_ge(s["vc_ready"], count(b))
                if c >= 2:
                    pe.wait_ge(s["shifted"], count(b, NCH, c - 1))
                if heads_norm:
                    mm(scores[u][:, c % 2, :], ident_b[:, :], causal_b[:, :, :].rearrange("p a b -> p (a b)"),
                       stop=False, skip=True)
                for j in range(CHUNK):
                    r, g = divmod(head_of(c, j), GROUPS)
                    at = r * SLOT
                    last = mm(scores[u][:, c % 2, j * NK:(j + 1) * NK], qT[u][at:at + K, g, :], kT[u][at:at + K, g, :],
                              start=not heads_norm, skip=heads_norm)
                last.then_inc(s["scores_done"], 1)

            def turn(b, c, u):
                pe.wait_ge(s["probs_ready"], count(b, NCH, c + 1))
                for at, (h, t) in enumerate(blocks):
                    k0 = sum(key_tiles[x][0] for x in range(t))
                    nk = key_tiles[t][0]
                    last = pe.transpose(ptp[c % 2][0:nk, at, :], probs[c % 2][u][:, h, k0:k0 + nk], core.ident[:, :])
                last.then_inc(s["pt_done"], 1)

            def weigh(b, c, u):
                pe.wait_ge(s["pt_copied"], count(b, NCH, c + 1))
                for at, (h, t) in enumerate(blocks):
                    hh = head_of(c, h)
                    nk = key_tiles[t][0]
                    out = misc[u][:, P + hh * (HD + 1):P + (hh + 1) * (HD + 1)]
                    last = mm(out, pT[c % 2][u][0:nk, at, :], v[t][u][:, hh, :], start=t == 0,
                              stop=t == len(key_tiles) - 1)
                last.then_inc(s["pv_done"], 1)

            def beside(b, u, step, tail, start_next):
                before, behind = neighbour(b, -1), neighbour(b, 1)
                if step == 0:
                    if start_next:
                        front_0(behind, u)
                    if tail:
                        tail_turn(before, u)
                if step == 1:
                    if tail:
                        tail_project(before, u)
                    if start_next:
                        front_1(behind, u)
                if step == 2 and start_next:
                    if tail:
                        pe.wait_ge(s["y_added"], count(before))
                    front_2(behind, u)

            def attend(b, u, tail=True, start_next=True):
                scoring(b, 0, u)
                if start_next:
                    begin(neighbour(b, 1), 1 - u)
                for c in range(NCH):
                    if c + 1 < NCH:
                        scoring(b, c + 1, u)
                    beside(b, 1 - u, step_of(c), tail, start_next)
                    turn(b, c, u)
                    if c:
                        weigh(b, c - 1, u)
                if start_next and not heads_norm:
                    front_3(neighbour(b, 1), 1 - u)
                weigh(b, NCH - 1, u)
                if start_next and heads_norm:
                    front_3(neighbour(b, 1), 1 - u)

            begin((None, 0), 0)
            for front in (front_0, front_1, front_2, front_3):
                front((None, 0), 0)
            attend((None, 0), 0, tail=False)
            with pe.Fori(0, batch // U - 1) as i:
                attend((i, 1), 1)
                attend((i, 2), 0)
            attend((None, batch - 1), 1, start_next=False)
            tail_turn((None, batch - 1), 1)
            tail_project((None, batch - 1), 1)


TILE = 4


def mlp_stage(nc, core, dram, tag, kind):
    batch, T, NT = core.batch, TILE, TILE * P
    gated = kind != "plain"
    NCHK = dram[tag + "_w_d"].shape[1]
    E, EG = 32, 4
    NW = E + (16 if kind == "moe3" else 0)
    routed = [k for k in range(NCHK) if gated and k != NCHK - 1]
    with ExitStack() as ctx:
        st = Stage(nc, ctx, tag)
        s = {n: st.sem(n) for n in (
            "loaded", "consts", "once_step", "xn_ready", "xt_done", "xt_ready", "up_done", "act_ready",
            "hidden_ready", "down_done", "y_done", "y_added", "vec_step", "spread_done",
            "logits_done", "logits_ready", "clamped", "exp_ready", "route_ready", "rt_done", "rt_ready")}
        if gated:
            names = ["w_g", "w_u", "w_d", "w_r", "b_r", "pick"]
        else:
            names = ["w_g", "w_d", "b_g", "b_d", "ln_g", "ln_b"]
        w = {n: st.sb(n, list(dram[f"{tag}_{n}"].shape)) for n in names}
        if not gated:
            raw = {n: st.sb("raw_" + n, list(dram[f"{tag}_q_{n}"].shape), I32) for n in ("w_g", "w_d")}
            xres = st.sb("xres", [P, T, P])
            hb = st.sb("half_bias", [P, NCHK])
        xn = st.sb("xn", [P, T, P])
        xT = st.sb("xT", [P, NT])
        act_t = [st.sb(f"act{j}", [P, NT]) for j in range(2)]
        hid = [st.sb(f"hid{j}", [P, NT]) for j in range(2)] if gated else act_t
        bn, mv = st.sb("bn", [P, 6]), st.sb("mv", [P, 2])
        gp = [st.ps(f"g{j}", [P, NT]) for j in range(2)]
        up = [st.ps(f"u{j}", [P, NT]) for j in range(2)] if gated else None
        wb = [st.ps(f"wb{j}", [P, NT]) for j in range(2)] if gated else None
        yp = st.ps("y", [P, T, P])
        misc = st.ps("misc", [P, NT])
        if gated:
            sig = st.sb("sig", [P, T, E])
            choice = st.sb("choice", [P, T, EG, E // EG])
            best = st.sb("best", [P, T, EG, 8])
            gs = st.sb("gs", [P, T, EG])
            gt = st.sb("gt", [P, T, EG, EG])
            eq = st.sb("eq", [P, T, EG, EG])
            keep = st.sb("keep", [P, T, EG])
            top8 = st.sb("top8", [P, T, 8])
            first8 = st.sb("first8", [P, T, 8])
            marked = st.sb("marked", [P, T, E])
            tot = st.sb("tot", [P, T])
            route = st.sb("route", [P, T, P])
            rT = st.sb("rT", [NW, NT])
            lower = st.sb("lower", [P, EG, EG])
        n_loads = 16 * (len(names) + (0 if gated else 2) + (1 if gated else 0))
        block = ctx.enter_context(nc.Block())

        @block.sync
        def _(sp):
            for n in names:
                sp.dma_start(w[n][tuple(slice(None) for _ in w[n].shape)], dram[f"{tag}_{n}"]).then_inc(s["loaded"], 16)
            if gated:
                sp.dma_start(lower[:, :, :], dram["lower"]).then_inc(s["loaded"], 16)
            else:
                for n in raw:
                    sp.dma_start(raw[n][tuple(slice(None) for _ in raw[n].shape)], dram[f"{tag}_q_{n}"])\
                      .then_inc(s["loaded"], 16)
            sp.wait_ge(s["loaded"], n_loads)

        @block.vector
        def _(dve):
            dve.sem_inc(s["y_added"], 1)
            dve.wait_ge(s["loaded"], n_loads)
            once = Chain(dve, s["once_step"])
            if gated:
                once.link(dve.memset(route[:, :, :], 0.0))
                once.link(dve.memset(first8[:, :, :], -1e30))
            else:
                for n in raw:
                    dst = w[n][tuple(slice(None) for _ in w[n].shape)]
                    src = raw[n][tuple(slice(None) for _ in raw[n].shape)]
                    once.link(dve.scalar_tensor_tensor(dst, src, -128.0, dst, ALU.add, ALU.mult))
            dve.sem_inc(s["consts"], 1)

            def beat():
                dve.memset(core.beat[:, :], 0.0)

            def route_tokens(i):
                flat = choice[:, :, :, :].rearrange("p t g e -> p t (g e)")
                dve.wait_ge(s["logits_ready"], i + 1)
                dve.tensor_scalar(sig[:, :, :], sig[:, :, :], -1.0, 88.0, ALU.mult, ALU.min).then_inc(s["clamped"], 1)
                dve.wait_ge(s["exp_ready"], i + 1)
                chain.link(dve.tensor_scalar(sig[:, :, :], sig[:, :, :], 1.0, None, ALU.add))
                chain.link(dve.reciprocal(sig[:, :, :], sig[:, :, :]))
                chain.link(dve.tensor_tensor(flat, sig[:, :, :], spread(w["b_r"][:, :], 1, T), ALU.add))
                beat()
                for t in range(T):
                    for g in range(EG):
                        last = dve.max(best[:, t, g, :], choice[:, t, g, :])
                chain.link(last)
                chain.link(dve.tensor_tensor(gs[:, :, :], best[:, :, :, 0], best[:, :, :, 1], ALU.add))
                for t in range(T):
                    ahead, behind = spread(gs[:, t, :], 1, EG), spread(gs[:, t, :], 2, EG)
                    dve.tensor_tensor(gt[:, t, :, :], ahead, behind, ALU.is_gt)
                    last = dve.tensor_tensor(eq[:, t, :, :], ahead, behind, ALU.is_equal)
                chain.link(last)
                chain.link(dve.tensor_tensor(eq[:, :, :, :], eq[:, :, :, :], spread(lower[:, :, :], 1, T), ALU.mult))
                chain.link(dve.tensor_tensor(gt[:, :, :, :], gt[:, :, :, :], eq[:, :, :, :], ALU.add))
                chain.link(dve.tensor_reduce(keep[:, :, :], gt[:, :, :, :], AX.X, ALU.add))
                chain.link(dve.tensor_scalar(keep[:, :, :], keep[:, :, :], 2.0, None, ALU.is_lt))
                chain.link(dve.tensor_tensor(choice[:, :, :, :], choice[:, :, :, :], spread(keep[:, :, :], 3, E // EG), ALU.mult))
                if kind == "moe3":
                    chain.link(dve.tensor_scalar(keep[:, :, :], keep[:, :, :], -1.0, 1e30, ALU.add, ALU.mult))
                    chain.link(dve.tensor_tensor(choice[:, :, :, :], choice[:, :, :, :],
                                                 spread(keep[:, :, :], 3, E // EG), ALU.add))
                beat()
                for t in range(T):
                    last = dve.max(top8[:, t, :], flat[:, t, :])
                chain.link(last)
                if kind == "moe3":
                    chain.link(dve.tensor_copy(first8[:, :, 0:1], top8[:, :, 0:1]))
                    chain.link(dve.memset(top8[:, :, 6:8], -1e30))
                    beat()
                    for t in range(T):
                        last = dve.match_replace(marked[:, t, :], first8[:, t, :], flat[:, t, :], 1e30)
                    chain.link(last)
                    chain.link(dve.tensor_scalar(marked[:, :, :], marked[:, :, :], 1e30, None, ALU.is_equal))
                    chain.link(dve.scalar_tensor_tensor(marked[:, :, :], flat, -1e29, marked[:, :, :], ALU.is_gt, ALU.mult))
                    chain.link(dve.tensor_tensor(route[:, :, E:NW], marked[:, :, 0:E:2], marked[:, :, 1:E:2], ALU.add))
                    chain.link(dve.tensor_scalar(route[:, :, E:NW], route[:, :, E:NW], 0.1, None, ALU.mult))
                beat()
                for t in range(T):
                    last = dve.match_replace(marked[:, t, :], top8[:, t, :], flat[:, t, :], 1e30)
                chain.link(last)
                chain.link(dve.tensor_scalar(marked[:, :, :], marked[:, :, :], 1e30, None, ALU.is_equal))
                if kind == "moe3":
                    chain.link(dve.scalar_tensor_tensor(marked[:, :, :], flat, -1e29, marked[:, :, :], ALU.is_gt, ALU.mult))
                chain.link(dve.tensor_tensor(marked[:, :, :], marked[:, :, :], sig[:, :, :], ALU.mult))
                chain.link(dve.tensor_reduce(tot[:, :], marked[:, :, :], AX.X, ALU.add))
                chain.link(dve.tensor_scalar(tot[:, :], tot[:, :], 1e-20, None, ALU.add))
                chain.link(dve.reciprocal(tot[:, :], tot[:, :]))
                chain.link(dve.tensor_scalar(tot[:, :], tot[:, :], 2.5 if kind == "moe0" else 0.2, None, ALU.mult))
                dve.tensor_tensor(route[:, :, 0:E], marked[:, :, :], spread(tot[:, :], 2, E), ALU.mult)\
                   .then_inc(s["route_ready"], 1)

            def hidden(i, k):
                j, n = k % 2, i * NCHK + (k + 1)
                dve.wait_ge(s["act_ready"], n)
                if k >= 2:
                    dve.wait_ge(s["down_done"], n - 2)
                if k in routed:
                    chain.link(dve.tensor_tensor(hid[j][:, :], act_t[j][:, :], up[j][:, :], ALU.mult))
                    dve.wait_ge(s["spread_done"], i * len(routed) + (k + 1))
                    dve.tensor_tensor(hid[j][:, :], hid[j][:, :], wb[j][:, :], ALU.mult).then_inc(s["hidden_ready"], 1)
                else:
                    dve.tensor_tensor(hid[j][:, :], act_t[j][:, :], up[j][:, :], ALU.mult).then_inc(s["hidden_ready"], 1)

            per = ((29 if kind == "moe3" else 19) + len(routed) if gated else T) + 3 * T
            with dve.Fori(0, batch // T) as i:
                chain = Chain(dve, s["vec_step"], i, per)
                if gated:
                    route_tokens(i)
                    for k in range(NCHK):
                        hidden(i, k)
                if gated:
                    dve.wait_ge(s["down_done"], (i + 1) * NCHK)
                else:
                    dve.wait_ge(s["y_done"], i + 1)
                for t in range(T):
                    b = i * T + t
                    if gated:
                        chain.link(dve.tensor_tensor(core.x[:, b, :], core.x[:, b, :], yp[:, t, :], ALU.add))
                    else:
                        chain.link(dve.tensor_tensor(core.x[:, b, :], core.x[:, b, :], xres[:, t, :], ALU.add))
                        chain.link(dve.scalar_tensor_tensor(core.x[:, b, :], yp[:, t, :], 0.5, core.x[:, b, :],
                                                            ALU.mult, ALU.add))
                    last = take_stats(dve, chain, core, b, bn, mv)
                last.then_inc(s["y_added"], 1)
                chain.close()

        @block.scalar
        def _(act):
            act.wait_ge(s["consts"], 1)
            with act.Fori(0, batch // T) as i:
                act.wait_ge(s["y_added"], i + 1)
                for t in range(T):
                    b = i * T + t
                    if not gated:
                        act.activation(xres[:, t, :], core.x[:, b, :], ACT.Identity, bias=core.nmr[:, b, :],
                                       scale=core.rstd[:, b, :])
                        last = act.activation(xn[:, t, :], core.x[:, b, :], ACT.Identity, bias=core.nmr2[:, b, :],
                                              scale=core.rstd2[:, b, :])
                    else:
                        last = act.activation(xn[:, t, :], core.x[:, b, :], ACT.Identity, bias=core.nmr[:, b, :],
                                              scale=core.rstd[:, b, :])
                last.then_inc(s["xn_ready"], 1)
                act.wait_ge(s["xt_done"], i + 1)
                if gated:
                    act.activation(xT[:, :], misc[:, :], ACT.Copy).then_inc(s["xt_ready"], 1)
                    act.wait_ge(s["logits_done"], i + 1)
                    act.activation(sig[:, :, :], misc[:, 0:T * E].rearrange("p (t e) -> p t e", t=T), ACT.Copy)\
                       .then_inc(s["logits_ready"], 1)
                    act.wait_ge(s["clamped"], i + 1)
                    act.activation(sig[:, :, :], sig[:, :, :], ACT.Exp).then_inc(s["exp_ready"], 1)
                    act.wait_ge(s["rt_done"], i + 1)
                    act.activation(rT[:, :], misc[0:NW, :], ACT.Copy).then_inc(s["rt_ready"], 1)
                else:
                    act.activation(xT[:, :], misc[:, :], ACT.Identity, bias=w["ln_b"][:, :], scale=w["ln_g"][:, :])\
                       .then_inc(s["xt_ready"], 1)
                for k in range(NCHK):
                    j, n = k % 2, i * NCHK + (k + 1)
                    act.wait_ge(s["up_done"], n)
                    if k >= 2:
                        act.wait_ge(s["hidden_ready" if gated else "down_done"], n - 2)
                    if gated:
                        act.activation(act_t[j][:, :], gp[j][:, :], ACT.Silu).then_inc(s["act_ready"], 1)
                    else:
                        act.activation(act_t[j][:, :], gp[j][:, :], ACT.Silu, bias=w["b_g"][:, k:k + 1])\
                           .then_inc(s["act_ready"], 1)

        @block.tensor
        def _(pe):
            pe.wait_ge(s["consts"], 1)

            def down(i, k):
                j = k % 2
                pe.wait_ge(s["hidden_ready" if gated else "act_ready"], i * NCHK + (k + 1))
                for t in range(T):
                    last = pe.matmul(yp[:, t, :], hid[j][:, t * P:(t + 1) * P], w["w_d"][:, k, :],
                                     start=(k == 0 and t == 0), stop=(gated and k == NCHK - 1), skip_group_check=True)
                last.then_inc(s["down_done"], 1)

            with pe.Fori(0, batch // T) as i:
                pe.wait_ge(s["xn_ready"], i + 1)
                for t in range(T):
                    last = pe.transpose(misc[:, t * P:(t + 1) * P], xn[:, t, :], core.ident[:, :])
                last.then_inc(s["xt_done"], 1)
                pe.wait_ge(s["xt_ready"], i + 1)
                if gated:
                    for t in range(T):
                        last = pe.matmul(misc[:, t * E:(t + 1) * E], xT[:, t * P:(t + 1) * P], w["w_r"][:, :],
                                         start=True, stop=True)
                    last.then_inc(s["logits_done"], 1)
                    pe.wait_ge(s["route_ready"], i + 1)
                    for t in range(T):
                        last = pe.transpose(misc[:, t * P:(t + 1) * P], route[:, t, :], core.ident[:, :])
                    last.then_inc(s["rt_done"], 1)
                for k in range(NCHK):
                    j, n = k % 2, i * NCHK + (k + 1)
                    if k >= 2:
                        pe.wait_ge(s["hidden_ready" if gated else "act_ready"], n - 2)
                    last = pe.matmul(gp[j][:, :], w["w_g"][:, k, :], xT[:, :], start=True, stop=True)
                    if gated:
                        last = pe.matmul(up[j][:, :], w["w_u"][:, k, :], xT[:, :], start=True, stop=True)
                    last.then_inc(s["up_done"], 1)
                    if k in routed:
                        if k == 0:
                            pe.wait_ge(s["rt_ready"], i + 1)
                        pe.matmul(wb[j][:, :], w["pick"][:, k, :], rT[:, :], start=True, stop=True)\
                          .then_inc(s["spread_done"], 1)
                    if k:
                        down(i, k - 1)
                down(i, NCHK - 1)
                if not gated:
                    for t in range(T):
                        last = pe.matmul(yp[:, t, :], core.ones[0:1, :], w["b_d"][0:1, :], start=False, stop=True,
                                         skip_group_check=True)
                    last.then_inc(s["y_done"], 1)


MAGIC = 1.5 * 2.0 ** 23
QMAX = 32767.0


def quantised_mlp(nc, core, dram, tag):
    batch, T, NT, CH = core.batch, TILE, TILE * P, 3
    NI = batch // T
    with ExitStack() as ctx:
        st = Stage(nc, ctx, tag)
        wn = st.sb("w_natural", [P, 3 * CH, P])
        wT = st.sb("w", [P, 3 * CH, P])
        ws, wr = st.sb("w_scale", [P, 3 * CH * 4]), st.sb("w_inverse", [P, 3 * CH * 4])
        xi = st.sb("x_int", [P, NI, NT], I16)
        ui = st.sb("up_int", [P, NI, CH * NT], I16)
        gi = st.sb("gate_int", [P, NI, CH * NT], I16)
        high = st.sb("high", [P, 2, NI])
        top, most = st.sb("top", [P, 2]), st.sb("most", [P, 2])
        unit, scale, ratio = (st.sb(n, [P, 5]) for n in ("unit", "scale", "ratio"))
        X, G, UP, G2, OUT = range(5)
        xn = st.sb("xn", [P, T, P])
        f0, f1 = st.sb("f0", [P, CH * NT]), st.sb("f1", [P, CH * NT])
        xT = st.sb("xT", [P, NT])
        bn, mv = st.sb("bn", [P, 6]), st.sb("mv", [P, 2])
        misc = st.ps("misc", [P, NT])
        gu = [st.ps(n, [P, CH, NT]) for n in ("g", "u")]

        def col(tile, c):
            return tile[:, c:c + 1]

        def rounded(dve, chain, dst, src, mult, tmp):
            chain.link(dve.tensor_scalar(tmp, src, mult, MAGIC, ALU.mult, ALU.add))
            return dve.tensor_scalar(dst, tmp, -MAGIC, None, ALU.add)

        with ExitStack() as c2:
            st2 = Stage(nc, c2, tag + "_weights")
            loaded, step, quantised, turned, copied = (st2.sem(n) for n in ("loaded", "step", "quantised", "turned", "copied"))
            block = c2.enter_context(nc.Block())

            @block.sync
            def _(sp):
                sp.dma_start(wn[:, :, :], dram[tag + "_w"]).then_inc(loaded, 16)
                sp.wait_ge(loaded, 16)

            @block.vector
            def _(dve):
                chain = Chain(dve, step)
                blocks = wn[:, :, :].rearrange("p c (k i) -> p (c k) i", i=32)
                dve.wait_ge(loaded, 16)
                chain.link(dve.tensor_reduce(ws[:, :], blocks, AX.X, ALU.max, apply_absolute_value=True))
                chain.link(dve.tensor_scalar(ws[:, :], ws[:, :], 1.0 / 7.0, 1e-12, ALU.mult, ALU.max))
                chain.link(dve.reciprocal(wr[:, :], ws[:, :]))
                chain.link(dve.tensor_tensor(blocks, blocks, spread(wr[:, :], 2, 32), ALU.mult))
                chain.link(dve.tensor_scalar(wn[:, :, :], wn[:, :, :], MAGIC, None, ALU.add))
                chain.link(dve.tensor_scalar(wn[:, :, :], wn[:, :, :], -MAGIC, None, ALU.add))
                dve.tensor_tensor(blocks, blocks, spread(ws[:, :], 2, 32), ALU.mult).then_inc(quantised, 1)

            @block.tensor
            def _(pe):
                pe.wait_ge(quantised, 1)
                for k in range(3 * CH):
                    last = pe.transpose(gu[k // 6][:, k % 6 // 2, k % 2 * P:(k % 2 + 1) * P], wn[:, k, :], core.ident[:, :])
                last.then_inc(turned, 1)

            @block.scalar
            def _(act):
                act.wait_ge(turned, 1)
                for k in range(3 * CH):
                    act.activation(wT[:, k, :], gu[k // 6][:, k % 6 // 2, k % 2 * P:(k % 2 + 1) * P], ACT.Copy)

        def measured(name, first, n, units):
            with ExitStack() as c2:
                st2 = Stage(nc, c2, f"{tag}_{name}")
                step, top_ready, most_ready = st2.sem("step"), st2.sem("top_ready"), st2.sem("most_ready")
                block = c2.enter_context(nc.Block())

                @block.vector
                def _(dve):
                    chain = Chain(dve, step)
                    dve.tensor_reduce(top[:, 0:n], high[:, 0:n, :], AX.X, ALU.max).then_inc(top_ready, 1)
                    units(dve, chain)
                    sc, ra, un = (a[:, first:first + n] for a in (scale, ratio, unit))
                    dve.wait_ge(most_ready, 1)
                    chain.link(dve.tensor_tensor(sc, most[:, 0:n], un, ALU.mult))
                    chain.link(dve.tensor_scalar(sc, sc, 1.0 / QMAX, 1e-12, ALU.mult, ALU.max))
                    chain.link(dve.reciprocal(ra, sc))
                    dve.tensor_tensor(ra, ra, un, ALU.mult)

                @block.gpsimd
                def _(pool):
                    pool.wait_ge(top_ready, 1)
                    pool.partition_all_reduce(most[:, 0:n], top[:, 0:n], P, bass.bass_isa.ReduceOp.max)\
                        .then_inc(most_ready, 1)

        def run_pass(name, sems, vector, scalar=None, tensor=None, per=0):
            with ExitStack() as c2:
                st2 = Stage(nc, c2, f"{tag}_{name}")
                s = {n: st2.sem(n) for n in sems + ["vec_step", "tile_done"]}
                block = c2.enter_context(nc.Block())

                @block.vector
                def _(dve):
                    dve.sem_inc(s["tile_done"], 1)
                    with dve.Fori(0, NI) as i:
                        chain = Chain(dve, s["vec_step"], i, per)
                        vector(dve, s, i, chain).then_inc(s["tile_done"], 1)
                        chain.close()

                if scalar:
                    @block.scalar
                    def _(act):
                        with act.Fori(0, NI) as i:
                            scalar(act, s, i)

                if tensor:
                    @block.tensor
                    def _(pe):
                        with pe.Fori(0, NI) as i:
                            tensor(pe, s, i)

        def normalise(act, s, i):
            act.wait_ge(s["tile_done"], i + 1)
            for t in range(T):
                b = i * T + t
                last = act.activation(xn[:, t, :], core.x[:, b, :], ACT.Identity, bias=core.nmr[:, b, :],
                                      scale=core.rstd[:, b, :])
            last.then_inc(s["xn_ready"], 1)

        def max_x(dve, s, i, chain):
            dve.wait_ge(s["xn_ready"], i + 1)
            return dve.tensor_reduce(high[:, 0, i:i + 1] if isinstance(i, int) else high[:, 0, i].unsqueeze(1),
                                     xn[:, :, :], AX.XY, ALU.max, apply_absolute_value=True)

        run_pass("max_x", ["xn_ready"], max_x, scalar=normalise)
        measured("scale_x", X, 1, lambda dve, chain: chain.link(dve.memset(col(unit, X), 1.0)))

        def quantise_x(dve, s, i, chain):
            dve.wait_ge(s["xn_ready"], i + 1)
            chain.link(dve.tensor_scalar(xn[:, :, :], xn[:, :, :], col(ratio, X), MAGIC, ALU.mult, ALU.add))
            dve.tensor_scalar(xn[:, :, :], xn[:, :, :], -MAGIC, None, ALU.add).then_inc(s["xq_ready"], 1)
            dve.wait_ge(s["gu_done"], i + 1)
            for a in range(2):
                last = dve.tensor_reduce(high[:, a, i].unsqueeze(1), gu[a][:, :, :], AX.XY, ALU.max,
                                         apply_absolute_value=True)
            return last

        def copy_x(act, s, i):
            normalise(act, s, i)
            act.wait_ge(s["xt_done"], i + 1)
            act.activation(xi[:, i, :], misc[:, :], ACT.Copy)
            act.activation(xT[:, :], misc[:, :], ACT.Copy).then_inc(s["xt_ready"], 1)

        def gate_up(pe, s, i):
            pe.wait_ge(s["tile_done"], i + 1)
            pe.wait_ge(s["xt_ready"], i + 1)
            for a in range(2):
                for k in range(CH):
                    last = pe.matmul(gu[a][:, k, :], wT[:, a * CH + k, :], xT[:, :], start=True, stop=True)
            last.then_inc(s["gu_done"], 1)

        def turn_x(pe, s, i):
            pe.wait_ge(s["xq_ready"], i + 1)
            for t in range(T):
                last = pe.transpose(misc[:, t * P:(t + 1) * P], xn[:, t, :], core.ident[:, :])
            last.then_inc(s["xt_done"], 1)
            gate_up(pe, s, i)

        run_pass("max_gu", ["xn_ready", "xq_ready", "xt_done", "xt_ready", "gu_done"], quantise_x, copy_x, turn_x, per=1)

        def unit_gu(dve, chain):
            dve.tensor_copy(col(unit, G), col(scale, X))
            chain.link(dve.tensor_copy(col(unit, UP), col(scale, X)))

        measured("scale_gu", G, 2, unit_gu)

        def quantise_sigmoid(dve, s, i, chain):
            dve.wait_ge(s["sig_ready"], i + 1)
            chain.link(dve.tensor_scalar(f1[:, :], f1[:, :], 65536.0, MAGIC, ALU.mult, ALU.add))
            chain.link(dve.tensor_scalar(f1[:, :], f1[:, :], -MAGIC, 65535.0, ALU.add, ALU.min))
            chain.link(dve.tensor_tensor(f1[:, :], f1[:, :], gi[:, i, :], ALU.mult))

        def quantise_gu(dve, s, i, chain):
            dve.wait_ge(s["gu_done"], i + 1)
            g, u = (gu[a][:, :, :].rearrange("p c t -> p (c t)") for a in range(2))
            rounded(dve, chain, gi[:, i, :], g, col(ratio, G), f0[:, :]).then_inc(s["gate_ready"], 1)
            dve.wait_ge(s["gate_ready"], i + 1)
            chain.link(rounded(dve, chain, ui[:, i, :], u, col(ratio, UP), f0[:, :]))
            quantise_sigmoid(dve, s, i, chain)
            return dve.tensor_reduce(high[:, 0, i].unsqueeze(1), f1[:, :], AX.X, ALU.max, apply_absolute_value=True)

        def sigmoid(act, s, i):
            act.activation(f1[:, :], gi[:, i, :], ACT.Sigmoid, scale=col(scale, G)).then_inc(s["sig_ready"], 1)

        def widen_x(act, s, i):
            act.wait_ge(s["tile_done"], i + 1)
            act.activation(xT[:, :], xi[:, i, :], ACT.Copy).then_inc(s["xt_ready"], 1)
            act.wait_ge(s["gate_ready"], i + 1)
            sigmoid(act, s, i)

        run_pass("max_g2", ["xt_ready", "gu_done", "gate_ready", "sig_ready"], quantise_gu, widen_x, gate_up, per=6)
        measured("scale_g2", G2, 1, lambda dve, chain: chain.link(
            dve.tensor_scalar(col(unit, G2), col(scale, G), 1.0 / 65536.0, None, ALU.mult)))

        def quantise_g2(dve, s, i, chain):
            quantise_sigmoid(dve, s, i, chain)
            chain.link(rounded(dve, chain, gi[:, i, :], f1[:, :], col(ratio, G2), f1[:, :]))
            chain.link(dve.tensor_tensor(f1[:, :], gi[:, i, :], ui[:, i, :], ALU.mult))
            return dve.tensor_reduce(high[:, 0, i].unsqueeze(1), f1[:, :], AX.X, ALU.max, apply_absolute_value=True)

        def sigmoid_again(act, s, i):
            act.wait_ge(s["tile_done"], i + 1)
            sigmoid(act, s, i)

        run_pass("max_out", ["sig_ready"], quantise_g2, sigmoid_again, per=6)
        measured("scale_out", OUT, 1, lambda dve, chain: chain.link(
            dve.tensor_tensor(col(unit, OUT), col(scale, G2), col(scale, UP), ALU.mult)))

        def finish(dve, s, i, chain):
            chain.link(dve.tensor_tensor(f0[:, :], gi[:, i, :], ui[:, i, :], ALU.mult))
            rounded(dve, chain, f0[:, :], f0[:, :], col(ratio, OUT), f0[:, :]).then_inc(s["out_ready"], 1)
            dve.wait_ge(s["y_done"], i + 1)
            for t in range(T):
                b = i * T + t
                chain.link(dve.scalar_tensor_tensor(core.x[:, b, :], misc[:, t * P:(t + 1) * P], col(scale, OUT),
                                                    core.x[:, b, :], ALU.mult, ALU.add))
                last = take_stats(dve, chain, core, b, bn, mv)
            return last

        def down(pe, s, i):
            pe.wait_ge(s["out_ready"], i + 1)
            for t in range(T):
                for k in range(CH):
                    last = pe.matmul(misc[:, t * P:(t + 1) * P], f0[:, k * NT + t * P:k * NT + (t + 1) * P],
                                     wT[:, 2 * CH + k, :], start=(k == 0), stop=(k == CH - 1))
            last.then_inc(s["y_done"], 1)

        run_pass("down", ["out_ready", "y_done"], finish, None, down, per=2 + 3 * T)


def wide_cross_attention(nc, core, dram, tag):
    batch, U, H, DH, CH = core.batch, UNITS, 8, 64, 4
    INNER = H * DH
    with ExitStack() as ctx:
        st = Stage(nc, ctx, tag)

        def unit_sb(name, shape, dt=F32):
            return [st.sb(f"{name}{u}", shape, dt) for u in range(U)]

        names = ["w_q", "w_kv", "w_o", "b_o", "ln"]
        w = {n: st.sb(n, list(dram[f"{tag}_{n}"].shape)) for n in names}
        c_all = st.sb("c_all", [SC, batch, P])
        cstat = st.sb("cstat", [SC, batch, 2])
        crstd, cnmr = st.sb("crstd", [SC, batch, 1]), st.sb("cnmr", [SC, batch, 1])
        cbn, cmv = st.sb("cbn", [SC, 6]), st.sb("cmv", [SC, 2])
        xn, xT, cn, cT = unit_sb("xn", [P, P]), unit_sb("xT", [P, P]), unit_sb("cn", [SC, P]), unit_sb("cT", [P, SC])
        qT, kT, v = unit_sb("qT", [P, CH, P]), unit_sb("kT", [P, CH, SC]), unit_sb("v", [SC, INNER])
        probs = unit_sb("probs", [P, 2, CH, SC])
        pT = unit_sb("pT", [SC, 2, CH, P])
        top, z = unit_sb("top", [P, 2, CH]), unit_sb("z", [P, 2, CH])
        o, oT = unit_sb("o", [P, INNER]), unit_sb("oT", [P, CH, P])
        bn, mv = unit_sb("bn", [P, 6]), unit_sb("mv", [P, 2])
        scores = [st.ps(f"scores{u}", [P, 2, BANK]) for u in range(U)]
        ptp = [st.ps(f"ptp{a}", [P, CH, P]) for a in range(2)]
        misc = [st.ps(f"misc{u}", [P, BANK]) for u in range(U)]
        s = {n: st.sem(n) for n in (
            "loaded", "once_step", "cvar_ready", "cstd_ready", "consts", "xn_ready", "cn_ready", "xt_done", "xt_ready",
            "ct_done", "ct_ready", "q_done", "q_ready", "k_done", "k_ready", "v_done", "v_ready", "scores_done",
            "shifted", "probs_ready", "pt_done0", "pt_done1", "pt_copied0", "pt_copied1", "pv_done", "o_ready",
            "ot_done", "ot_ready", "y_done", "y_added", "vec_step")}
        n_loads = 16 * (len(names) + 1)
        block = ctx.enter_context(nc.Block())

        @block.sync
        def _(sp):
            sp.dma_start(c_all[:, :, :], dram["ctx"].rearrange("b t d -> t b d")).then_inc(s["loaded"], 16)
            for n in names:
                sp.dma_start(w[n][tuple(slice(None) for _ in w[n].shape)], dram[f"{tag}_{n}"]).then_inc(s["loaded"], 16)
            sp.wait_ge(s["loaded"], n_loads)

        @block.vector
        def _(dve):
            dve.sem_inc(s["y_added"], U)
            dve.wait_ge(s["loaded"], n_loads)
            with dve.Fori(0, batch) as b:
                once = Chain(dve, s["once_step"], b, 3)
                once.link(dve.bn_stats(cbn[:, :], c_all[:, b, :]))
                dve.memset(core.beat[:, :], 0.0)
                once.link(dve.bn_aggr(cmv[:, :], cbn[:, :]))
                once.link(dve.tensor_copy(cstat[:, b, :], cmv[:, :]))
            dve.tensor_scalar(crstd[:, :, 0], cstat[:, :, 1], LN_EPS, None, ALU.add).then_inc(s["cvar_ready"], 1)
            dve.wait_ge(s["cstd_ready"], 1)
            dve.reciprocal(crstd[:, :, 0], crstd[:, :, 0]).then_inc(s["once_step"], 1)
            dve.wait_ge(s["once_step"], 3 * batch + 1)
            dve.scalar_tensor_tensor(cnmr[:, :, 0], cstat[:, :, 0], -1.0, crstd[:, :, 0], ALU.mult, ALU.mult)\
               .then_inc(s["consts"], 1)
            with dve.Fori(0, batch // U) as i:
                chain = Chain(dve, s["vec_step"], i, 6 * U)
                for u in range(U):
                    dve.wait_ge(s["q_done"], i * U + (u + 1))
                    dve.tensor_copy(qT[u][:, :, :], scores[u][:, 0, :].rearrange("p (c t) -> p c t", c=CH))\
                       .then_inc(s["q_ready"], 1)
                for u in range(U):
                    S = scores[u][:, :, 0:CH * SC].rearrange("p a (c k) -> p a c k", c=CH)
                    dve.wait_ge(s["scores_done"], i * U + (u + 1))
                    chain.link(dve.tensor_reduce(top[u][:, :, :], S, AX.X, ALU.max))
                    dve.tensor_tensor(probs[u][:, :, :, :], S, spread(top[u][:, :, :], 3, SC), ALU.subtract)\
                       .then_inc(s["shifted"], 1)
                for u in range(U):
                    dve.wait_ge(s["probs_ready"], i * U + (u + 1))
                    chain.link(dve.tensor_reduce(z[u][:, :, :], probs[u][:, :, :, :], AX.X, ALU.add))
                    chain.link(dve.reciprocal(z[u][:, :, :], z[u][:, :, :]))
                for u in range(U):
                    dve.wait_ge(s["pv_done"], i * U + (u + 1))
                    dve.tensor_tensor(o[u][:, :].rearrange("p (c a f) -> p a c f", a=2, f=DH),
                                      misc[u][:, :].rearrange("p (c a f) -> p a c f", a=2, f=DH),
                                      spread(z[u][:, :, :], 3, DH), ALU.mult).then_inc(s["o_ready"], 1)
                for u in range(U):
                    b = i * U + u
                    dve.wait_ge(s["y_done"], i * U + (u + 1))
                    chain.link(dve.tensor_tensor(core.x[:, b, :], core.x[:, b, :], scores[u][:, 1, 0:P], ALU.add))
                    take_stats(dve, chain, core, b, bn[u], mv[u]).then_inc(s["y_added"], 1)
                chain.close()

        @block.scalar
        def _(act):
            act.wait_ge(s["cvar_ready"], 1)
            act.activation(crstd[:, :, 0], crstd[:, :, 0], ACT.Sqrt).then_inc(s["cstd_ready"], 1)
            act.wait_ge(s["consts"], 1)
            with act.Fori(0, batch // U) as i:
                def n_of(u):
                    return i * U + (u + 1)

                for u in range(U):
                    b = i * U + u
                    act.activation(xn[u][:, :], core.x[:, b, :], ACT.Identity, bias=core.nmr2[:, b, :],
                                   scale=core.rstd2[:, b, :]).then_inc(s["xn_ready"], 1)
                    act.activation(cn[u][:, :], c_all[:, b, :], ACT.Identity, bias=cnmr[:, b, :],
                                   scale=crstd[:, b, :]).then_inc(s["cn_ready"], 1)
                for u in range(U):
                    act.wait_ge(s["xt_done"], n_of(u))
                    act.activation(xT[u][:, :], misc[u][:, 0:P], ACT.Identity, bias=w["ln"][:, 1:2], scale=w["ln"][:, 0:1])\
                       .then_inc(s["xt_ready"], 1)
                    act.wait_ge(s["ct_done"], n_of(u))
                    act.activation(cT[u][:, :], scores[u][:, 1, 0:SC], ACT.Identity, bias=w["ln"][:, 3:4],
                                   scale=w["ln"][:, 2:3]).then_inc(s["ct_ready"], 1)
                for u in range(U):
                    act.wait_ge(s["v_done"], n_of(u))
                    act.activation(v[u][:, :], misc[u][0:SC, :], ACT.Copy).then_inc(s["v_ready"], 1)
                    act.wait_ge(s["k_done"], n_of(u))
                    act.activation(kT[u][:, :, :], scores[u][:, 1, 0:CH * SC].rearrange("p (c t) -> p c t", c=CH),
                                   ACT.Copy).then_inc(s["k_ready"], 1)
                for u in range(U):
                    act.wait_ge(s["shifted"], n_of(u))
                    act.activation(probs[u][:, :, :, :], probs[u][:, :, :, :], ACT.Exp, scale=float(DH) ** -0.5)\
                       .then_inc(s["probs_ready"], 1)
                for u in range(U):
                    for a in range(2):
                        act.wait_ge(s[f"pt_done{a}"], n_of(u))
                        act.activation(pT[u][:, a, :, :], ptp[a][0:SC, :, :], ACT.Copy).then_inc(s[f"pt_copied{a}"], 1)
                for u in range(U):
                    act.wait_ge(s["ot_done"], n_of(u))
                    act.activation(oT[u][:, :, :], scores[u][:, 0, :].rearrange("p (c t) -> p c t", c=CH), ACT.Copy)\
                       .then_inc(s["ot_ready"], 1)

        @block.tensor
        def _(pe):
            pe.sem_inc(s["pt_copied0"], 1)
            pe.sem_inc(s["pt_copied1"], 1)
            pe.wait_ge(s["consts"], 1)

            def mm(out, lhsT, rhs, start=True, stop=True):
                return pe.matmul(out, lhsT, rhs, start=start, stop=stop)

            with pe.Fori(0, batch // U) as i:
                def n_of(u):
                    return i * U + (u + 1)

                for u in range(U):
                    pe.wait_ge(s["y_added"], n_of(u))
                    pe.wait_ge(s["xn_ready"], n_of(u))
                    pe.transpose(misc[u][:, 0:P], xn[u][:, :], core.ident[:, :]).then_inc(s["xt_done"], 1)
                    pe.wait_ge(s["cn_ready"], n_of(u))
                    pe.transpose(scores[u][:, 1, 0:SC], cn[u][:, :], core.ident[0:SC, 0:SC]).then_inc(s["ct_done"], 1)
                for u in range(U):
                    pe.wait_ge(s["xt_ready"], n_of(u))
                    for c in range(CH):
                        last = mm(scores[u][:, 0, c * P:(c + 1) * P], w["w_q"][:, c * P:(c + 1) * P], xT[u][:, :])
                    last.then_inc(s["q_done"], 1)
                    pe.wait_ge(s["ct_ready"], n_of(u))
                    mm(misc[u][0:SC, :], cT[u][:, :], w["w_kv"][:, INNER:2 * INNER]).then_inc(s["v_done"], 1)
                    for c in range(CH):
                        last = mm(scores[u][:, 1, c * SC:(c + 1) * SC], w["w_kv"][:, c * P:(c + 1) * P], cT[u][:, :])
                    last.then_inc(s["k_done"], 1)
                for u in range(U):
                    pe.wait_ge(s["q_ready"], n_of(u))
                    pe.wait_ge(s["k_ready"], n_of(u))
                    for c in range(CH):
                        for a in range(2):
                            last = mm(scores[u][:, a, c * SC:(c + 1) * SC], qT[u][a * DH:(a + 1) * DH, c, :],
                                      kT[u][a * DH:(a + 1) * DH, c, :])
                    last.then_inc(s["scores_done"], 1)
                for u in range(U):
                    pe.wait_ge(s["probs_ready"], n_of(u))
                    for a in range(2):
                        pe.wait_ge(s[f"pt_copied{a}"], n_of(u))
                        for c in range(CH):
                            last = pe.transpose(ptp[a][0:SC, c, :], probs[u][:, a, c, :], core.ident[:, :])
                        last.then_inc(s[f"pt_done{a}"], 1)
                for u in range(U):
                    pe.wait_ge(s["v_ready"], n_of(u))
                    for a in range(2):
                        pe.wait_ge(s[f"pt_copied{a}"], n_of(u) + 1)
                        for c in range(CH):
                            h = 2 * c + a
                            last = mm(misc[u][:, h * DH:(h + 1) * DH], pT[u][:, a, c, :], v[u][:, h * DH:(h + 1) * DH])
                    last.then_inc(s["pv_done"], 1)
                for u in range(U):
                    pe.wait_ge(s["o_ready"], n_of(u))
                    for c in range(CH):
                        last = pe.transpose(scores[u][:, 0, c * P:(c + 1) * P], o[u][:, c * P:(c + 1) * P], core.ident[:, :])
                    last.then_inc(s["ot_done"], 1)
                for u in range(U):
                    pe.wait_ge(s["ot_ready"], n_of(u))
                    for c in range(CH):
                        mm(scores[u][:, 1, 0:P], oT[u][:, c, :], w["w_o"][:, c, :], start=c == 0, stop=False)
                    mm(scores[u][:, 1, 0:P], core.ones[0:1, :], w["b_o"][0:1, :], start=False).then_inc(s["y_done"], 1)


def query_softmax_attention(nc, core, dram, tag):
    batch, U = core.batch, UNITS
    CHUNKS = [(half, src) for half in range(2) for src in range(2)]
    NCH = len(CHUNKS)
    with ExitStack() as ctx:
        st = Stage(nc, ctx, tag)

        def unit_sb(name, shape, dt=F32):
            return [st.sb(f"{name}{u}", shape, dt) for u in range(U)]

        names = ["w_q", "b_q", "w_k", "b_k", "w_slot", "w_v", "b_v", "w_qt", "b_qt", "w_o", "b_o", "gb"]
        w = {n: st.sb(n, list(dram[f"{tag}_{n}"].shape)) for n in names}
        xn, xT = unit_sb("xn", [P, P]), unit_sb("xT", [P, P])
        k12, kT = unit_sb("k12", [P, 2, SC]), unit_sb("kT", [P, GROUPS, 2 * SC])
        qT, v = unit_sb("qT", [P, GROUPS, P]), unit_sb("v", [SC, 2, HEADS, HD])
        vs = unit_sb("vs", [SC, 8, HD])
        probs = unit_sb("probs", [SC, 8, P])
        top, z = unit_sb("top", [SC, 8]), unit_sb("z", [SC, 8])
        bn, mv, var, rs = (unit_sb(n, [P, k]) for n, k in (("bn", 6), ("mv", 2), ("var", 1), ("rs", 1)))
        o1, o1T, o2 = unit_sb("o1", [P, P]), unit_sb("o1T", [P, P]), unit_sb("o2", [P, P])
        minus_half = st.sb("minus_half", [P, 1])
        scores = [st.ps(f"scores{u}", [P, 2, BANK]) for u in range(U)]
        misc = [st.ps(f"misc{u}", [P, BANK]) for u in range(U)]
        extra = [st.ps(f"extra{u}", [P, BANK]) for u in range(U)]
        s = {n: st.sem(n) for n in (
            "loaded", "consts", "xn_ready", "xt_done", "xt_ready", "q_done", "q_ready", "k12_done", "k12_ready",
            "k_done", "k_ready", "v_done", "v_ready", "scores_done", "shifted", "probs_ready", "vs_ready", "pv_done",
            "var_ready", "rs_ready", "o1_ready", "o1t_done", "o1t_ready", "y_done", "y_added", "vec_step")}
        block = ctx.enter_context(nc.Block())

        @block.sync
        def _(sp):
            for n in names:
                sp.dma_start(w[n][tuple(slice(None) for _ in w[n].shape)], dram[f"{tag}_{n}"]).then_inc(s["loaded"], 16)
            sp.wait_ge(s["loaded"], 16 * len(names))

        @block.gpsimd
        def _(pool):
            pool.wait_ge(s["consts"], 1)
            with pool.Fori(0, batch // U) as i:
                for r in range(2):
                    for u in range(U):
                        pool.wait_ge(s["var_ready"], i * (2 * U) + (r * U + u + 1))
                        pool.tensor_tensor(rs[u][:, :], var[u][:, :], minus_half[:, :], ALU.pow).then_inc(s["rs_ready"], 1)

        @block.vector
        def _(dve):
            dve.sem_inc(s["y_added"], U)
            dve.wait_ge(s["loaded"], 16 * len(names))
            dve.memset(minus_half[:, :], -0.5).then_inc(s["consts"], 1)

            def shift(i, c, u):
                n = i * (NCH * U) + (c * U + u + 1)
                S = scores[u][0:SC, :, :].rearrange("p a (h t) -> p (a h) t", t=P)
                dve.wait_ge(s["scores_done"], n)
                dve.wait_ge(s["pv_done"], n)
                chain.link(dve.tensor_reduce(top[u][:, :], S, AX.X, ALU.max))
                dve.tensor_tensor(probs[u][:, :, :], S, spread(top[u][:, :], 2, P), ALU.subtract).then_inc(s["shifted"], 1)

            def divide(i, c, u):
                half, src = CHUNKS[c]
                dve.wait_ge(s["probs_ready"], i * (NCH * U) + (c * U + u + 1))
                chain.link(dve.tensor_reduce(z[u][:, :], probs[u][:, :, :], AX.X, ALU.add))
                chain.link(dve.reciprocal(z[u][:, :], z[u][:, :]))
                dve.tensor_tensor(vs[u][:, :, :], v[u][:, src, 8 * half:8 * half + 8, :], spread(z[u][:, :], 2, HD), ALU.mult)\
                   .then_inc(s["vs_ready"], 1)

            def moments(i, r, u, src):
                dve.memset(core.beat[:, :], 0.0)
                chain.link(dve.bn_stats(bn[u][:, :], src))
                dve.memset(core.beat[:, :], 0.0)
                chain.link(dve.bn_aggr(mv[u][:, :], bn[u][:, :]))
                dve.tensor_scalar(var[u][:, :], mv[u][:, 1:2], LN_EPS, None, ALU.add).then_inc(s["var_ready"], 1)

            def norm(i, r, u, dst, src):
                dve.wait_ge(s["rs_ready"], i * (2 * U) + (r * U + u + 1))
                chain.link(dve.tensor_scalar(dst, src, mv[u][:, 0:1], rs[u][:, :], ALU.subtract, ALU.mult))
                chain.link(dve.tensor_tensor(dst, dst, w["gb"][:, 2 * r, :], ALU.mult))
                return dve.tensor_tensor(dst, dst, w["gb"][:, 2 * r + 1, :], ALU.add)

            with dve.Fori(0, batch // U) as i:
                chain = Chain(dve, s["vec_step"], i, U * (3 * NCH + 2 + 2 + 1 + 2 + 3 + 1 + 2))
                for u in range(U):
                    dve.wait_ge(s["q_done"], i * U + (u + 1))
                    acc = scores[u][:, 0, :].rearrange("p (g t) -> p g t", g=GROUPS)
                    dve.tensor_tensor(qT[u][:, :, :], acc, spread(w["b_q"][:, :], 2, P), ALU.add).then_inc(s["q_ready"], 1)
                for c in range(NCH):
                    for u in range(U):
                        shift(i, c, u)
                    for u in range(U):
                        divide(i, c, u)
                for u in range(U):
                    dve.wait_ge(s["pv_done"], i * (NCH * U) + ((NCH - 1) * U + u + 1 + U))
                    moments(i, 0, u, extra[u][:, 0:P])
                for u in range(U):
                    norm(i, 0, u, o1[u][:, :], extra[u][:, 0:P]).then_inc(s["o1_ready"], 1)
                for u in range(U):
                    dve.wait_ge(s["o1_ready"], i * U + (u + 1))
                    dve.wait_ge(s["y_done"], i * U + (u + 1))
                    chain.link(dve.scalar_tensor_tensor(o2[u][:, :], misc[u][:, P:2 * P], 0.0, o1[u][:, :], ALU.max, ALU.add))
                    moments(i, 1, u, o2[u][:, :])
                for u in range(U):
                    b = i * U + u
                    chain.link(norm(i, 1, u, o2[u][:, :], o2[u][:, :]))
                    chain.link(dve.tensor_tensor(core.x[:, b, :], core.x[:, b, :], o2[u][:, :], ALU.add))
                    take_stats(dve, chain, core, b, bn[u], mv[u]).then_inc(s["y_added"], 1)
                chain.close()

        @block.scalar
        def _(act):
            act.wait_ge(s["consts"], 1)
            with act.Fori(0, batch // U) as i:
                def n_of(u):
                    return i * U + (u + 1)

                for u in range(U):
                    b = i * U + u
                    act.activation(xn[u][:, :], core.x[:, b, :], ACT.Identity, bias=core.nmr[:, b, :],
                                   scale=core.rstd[:, b, :]).then_inc(s["xn_ready"], 1)
                for u in range(U):
                    act.wait_ge(s["xt_done"], n_of(u))
                    act.activation(xT[u][:, :], misc[u][:, 0:P], ACT.Copy).then_inc(s["xt_ready"], 1)
                for u in range(U):
                    act.wait_ge(s["k12_done"], n_of(u))
                    for src in range(2):
                        last = act.activation(k12[u][:, src, :], extra[u][:, src * SC:(src + 1) * SC], ACT.Identity,
                                              bias=w["b_k"][:, src:src + 1])
                    last.then_inc(s["k12_ready"], 1)
                for u in range(U):
                    act.wait_ge(s["k_done"], n_of(u))
                    for a, bank in enumerate((misc[u], extra[u])):
                        last = act.activation(kT[u][:, 2 * a:2 * a + 2, :],
                                              bank[:, 0:4 * SC].rearrange("p (g t) -> p g t", g=2), ACT.Copy)
                    last.then_inc(s["k_ready"], 1)
                    act.wait_ge(s["v_done"], n_of(u))
                    act.activation(v[u][:, :, :, :].rearrange("p s h f -> p (s h f)"), scores[u][0:SC, 1, 0:2 * P], ACT.Copy)\
                       .then_inc(s["v_ready"], 1)
                for c in range(NCH):
                    for u in range(U):
                        act.wait_ge(s["shifted"], i * (NCH * U) + (c * U + u + 1))
                        act.activation(probs[u][:, :, :], probs[u][:, :, :], ACT.Exp, scale=float(P) ** -0.5)\
                           .then_inc(s["probs_ready"], 1)
                for u in range(U):
                    act.wait_ge(s["o1t_done"], n_of(u))
                    act.activation(o1T[u][:, :], misc[u][:, 0:P], ACT.Copy).then_inc(s["o1t_ready"], 1)

        @block.tensor
        def _(pe):
            pe.sem_inc(s["pv_done"], U)
            pe.wait_ge(s["consts"], 1)

            def mm(out, lhsT, rhs, start=True, stop=True, skip=False):
                return pe.matmul(out, lhsT, rhs, start=start, stop=stop, skip_group_check=skip)

            with pe.Fori(0, batch // U) as i:
                def n_of(u):
                    return i * U + (u + 1)

                for u in range(U):
                    b = i * U + u
                    pe.wait_ge(s["y_added"], n_of(u))
                    for src in range(2):
                        last = mm(extra[u][:, src * SC:(src + 1) * SC], w["w_k"][:, src, :], core.ctxT[:, b, :])
                    last.then_inc(s["k12_done"], 1)
                    pe.wait_ge(s["xn_ready"], n_of(u))
                    pe.transpose(misc[u][:, 0:P], xn[u][:, :], core.ident[:, :]).then_inc(s["xt_done"], 1)
                for u in range(U):
                    pe.wait_ge(s["xt_ready"], n_of(u))
                    for g in range(GROUPS):
                        last = mm(scores[u][:, 0, g * P:(g + 1) * P], w["w_q"][:, g * P:(g + 1) * P], xT[u][:, :])
                    last.then_inc(s["q_done"], 1)
                    pe.wait_ge(s["k12_ready"], n_of(u))
                    for src in range(2):
                        out = scores[u][0:SC, 1, src * P:(src + 1) * P]
                        mm(out, k12[u][:, src, :], w["w_v"][:, src, :], stop=False)
                        last = mm(out, core.ones[0:1, 0:SC], w["b_v"][0:1, src * P:(src + 1) * P], start=False)
                    last.then_inc(s["v_done"], 1)
                    keys = k12[u][:, :, :].rearrange("p s t -> p (s t)")
                    for g in range(GROUPS):
                        bank = (misc[u], extra[u])[g // 2]
                        last = mm(bank[:, g % 2 * 2 * SC:(g % 2 + 1) * 2 * SC], w["w_slot"][:, g * P:(g + 1) * P], keys)
                    last.then_inc(s["k_done"], 1)
                for u in range(U):
                    pe.wait_ge(s["k_ready"], n_of(u))
                    mm(extra[u][:, 0:P], xT[u][:, :], w["w_qt"][:, :], stop=False, skip=True)
                    mm(extra[u][:, 0:P], core.ones[0:1, :], w["b_qt"][0:1, :], start=False, stop=False, skip=True)

                def scoring(c, u):
                    n = i * (NCH * U) + (c * U + u + 1)
                    half, src = CHUNKS[c]
                    if c == 0:
                        pe.wait_ge(s["q_ready"], n_of(u))
                        pe.wait_ge(s["v_ready"], n_of(u))
                    else:
                        pe.wait_ge(s["shifted"], n - U)
                    for a in range(2):
                        for g in range(4):
                            at = (2 * half + a) * SLOT
                            last = mm(scores[u][0:SC, a, g * P:(g + 1) * P], kT[u][at:at + HD, g, src * SC:(src + 1) * SC],
                                      qT[u][at:at + HD, g, :])
                    last.then_inc(s["scores_done"], 1)

                def weigh(c, u):
                    half, src = CHUNKS[c]
                    pe.wait_ge(s["vs_ready"], i * (NCH * U) + (c * U + u + 1))
                    for h in range(8):
                        hh = 8 * half + h
                        last = mm(extra[u][:, hh * HD:(hh + 1) * HD], probs[u][:, h, :], vs[u][:, h, :], start=False,
                                  stop=(c == NCH - 1), skip=True)
                    last.then_inc(s["pv_done"], 1)

                order = [(c, u) for c in range(NCH) for u in range(U)]
                scoring(*order[0])
                scoring(*order[1])
                for k, cu in enumerate(order):
                    if k + 2 < len(order):
                        scoring(*order[k + 2])
                    weigh(*cu)
                for u in range(U):
                    pe.wait_ge(s["o1_ready"], n_of(u))
                    pe.transpose(misc[u][:, 0:P], o1[u][:, :], core.ident[:, :]).then_inc(s["o1t_done"], 1)
                for u in range(U):
                    pe.wait_ge(s["o1t_ready"], n_of(u))
                    mm(misc[u][:, P:2 * P], o1T[u][:, :], w["w_o"][:, :], stop=False)
                    mm(misc[u][:, P:2 * P], core.ones[0:1, :], w["b_o"][0:1, :], start=False).then_inc(s["y_done"], 1)


def delta_rule_attention(nc, core, dram, tag):
    batch, T, NT = core.batch, TILE, TILE * P
    NI, NJ, KC, EPS = batch // TILE, batch // 8, 4, 1e-6
    STORES = 6 * 16
    TR = KC - 1
    scratch = {n: nc.dram_tensor(f"{tag}_scratch_{n}", [batch, P, P], F32, kind="Internal").ap() for n in "qkvo"}
    small_d = nc.dram_tensor(f"{tag}_scratch_small", [3, batch, HEADS, P], F32, kind="Internal").ap()

    with ExitStack() as ctx:
        st = Stage(nc, ctx, tag + "_in")
        names = ["w_in", "b_in", "conv", "w_beta", "b_beta", "head_sum"]
        w = {n: st.sb(n, list(dram[f"{tag}_{n}"].shape)) for n in names}
        xn, xT = st.sb("xn", [P, T, P]), st.sb("xT", [P, NT])
        raw = [st.sb(f"raw_{n}", [P, T, TR + P]) for n in "qkv"]
        cv = [st.sb(f"conv_{n}", [P, T, P]) for n in "qkv"]
        sq = [st.sb(f"square_{n}", [P, NT]) for n in "qk"]
        small = st.sb("small", [HEADS, 3, NT])
        misc = st.ps("misc", [P, NT])
        proj = [st.ps(f"proj_{n}", [P, NT]) for n in "qkv"]
        sm = [st.ps(f"small{n}", [HEADS, NT]) for n in range(3)]
        s = {n: st.sem(n) for n in ("loaded", "consts", "xn_ready", "xt_done", "xt_ready", "proj_done", "raw_ready",
                                    "conv_ready", "conv_step", "square_ready", "sums_done", "small_ready", "v_ready", "stored")}
        block = ctx.enter_context(nc.Block())

        @block.sync
        def _(sp):
            for n in names:
                sp.dma_start(w[n][tuple(slice(None) for _ in w[n].shape)], dram[f"{tag}_{n}"]).then_inc(s["loaded"], 16)
            sp.wait_ge(s["loaded"], 16 * len(names))
            sp.sem_inc(s["stored"], STORES)
            with sp.Fori(0, NI) as i:
                for k, n in enumerate("qk"):
                    if k == 0:
                        sp.wait_ge(s["conv_ready"], i + 1)
                    dst = scratch[n].rearrange("(i b) p t -> i p b t", b=T)[i]
                    sp.dma_start(dst, cv[k][:, :, :]).then_inc(s["stored"], 16)
                sp.wait_ge(s["v_ready"], i + 1)
                sp.dma_start(scratch["v"].rearrange("(i b) p t -> i p b t", b=T)[i], cv[2][:, :, :]).then_inc(s["stored"], 16)
                sp.wait_ge(s["small_ready"], i + 1)
                for k in range(3):
                    dst = small_d[k].rearrange("(i b) h t -> i h b t", b=T)[i]
                    sp.dma_start(dst, small[:, k, :].rearrange("h (b t) -> h b t", b=T)).then_inc(s["stored"], 16)
            sp.wait_ge(s["stored"], STORES * (NI + 1))

        @block.vector
        def _(dve):
            dve.wait_ge(s["loaded"], 16 * len(names))
            for r in raw:
                last = dve.memset(r[:, :, 0:TR], 0.0)
            last.then_inc(s["consts"], 1)
            with dve.Fori(0, NI) as i:
                chain = Chain(dve, s["conv_step"], i, 3 * (KC - 1))
                dve.wait_ge(s["stored"], STORES * (i + 1))
                for k in range(3):
                    dve.wait_ge(s["raw_ready"], i * 3 + (k + 1))
                    c = w["conv"][:, k, :]
                    chain.link(dve.tensor_scalar(cv[k][:, :, :], raw[k][:, :, 0:P], c[:, 0:1], c[:, KC:KC + 1],
                                                 ALU.mult, ALU.add))
                    for tap in range(1, KC):
                        last = dve.scalar_tensor_tensor(cv[k][:, :, :], raw[k][:, :, tap:tap + P], c[:, tap:tap + 1],
                                                        cv[k][:, :, :], ALU.mult, ALU.add)
                        if tap < KC - 1:
                            chain.link(last)
                last.then_inc(s["conv_ready"], 1)
                chain.close()

        @block.scalar
        def _(act):
            act.wait_ge(s["consts"], 1)
            with act.Fori(0, NI) as i:
                for t in range(T):
                    b = i * T + t
                    last = act.activation(xn[:, t, :], core.x[:, b, :], ACT.Identity, bias=core.nmr[:, b, :],
                                          scale=core.rstd[:, b, :])
                last.then_inc(s["xn_ready"], 1)
                act.wait_ge(s["xt_done"], i + 1)
                act.activation(xT[:, :], misc[:, :], ACT.Copy).then_inc(s["xt_ready"], 1)
                act.wait_ge(s["proj_done"], i + 1)
                for k in range(3):
                    act.activation(raw[k][:, :, TR:], proj[k][:, :].rearrange("p (b t) -> p b t", b=T), ACT.Identity,
                                   bias=w["b_in"][:, k:k + 1]).then_inc(s["raw_ready"], 1)
                act.wait_ge(s["conv_ready"], i + 1)
                act.activation(cv[2][:, :, :], cv[2][:, :, :], ACT.Silu).then_inc(s["v_ready"], 1)
                for k in range(2):
                    last = act.activation(sq[k][:, :], cv[k][:, :, :].rearrange("p b t -> p (b t)"), ACT.Square)
                last.then_inc(s["square_ready"], 1)
                act.wait_ge(s["sums_done"], i + 1)
                for k in range(3):
                    last = act.activation(small[:, k, :], sm[k][:, :], ACT.Identity, bias=w["b_beta"][:, k:k + 1])
                last.then_inc(s["small_ready"], 1)

        @block.tensor
        def _(pe):
            pe.wait_ge(s["consts"], 1)
            with pe.Fori(0, NI) as i:
                pe.wait_ge(s["xn_ready"], i + 1)
                for t in range(T):
                    last = pe.transpose(misc[:, t * P:(t + 1) * P], xn[:, t, :], core.ident[:, :])
                last.then_inc(s["xt_done"], 1)
                pe.wait_ge(s["xt_ready"], i + 1)
                for k in range(3):
                    last = pe.matmul(proj[k][:, :], w["w_in"][:, k, :], xT[:, :], start=True, stop=True)
                last.then_inc(s["proj_done"], 1)
                pe.matmul(sm[0][:, :], w["w_beta"][:, :], xT[:, :], start=True, stop=True)
                pe.wait_ge(s["square_ready"], i + 1)
                for k in range(2):
                    last = pe.matmul(sm[1 + k][:, :], w["head_sum"][:, :], sq[k][:, :], start=True, stop=True)
                last.then_inc(s["sums_done"], 1)

    with ExitStack() as ctx:
        st = Stage(nc, ctx, tag + "_rec")
        q, k, v = (st.sb(n, [P, NJ, HD, P]) for n in "qkv")
        beta, qq, kk = (st.sb(n, [P, NJ, P]) for n in ("beta", "q_sq", "k_sq"))
        S = st.sb("S", [P, NJ, HD, HD])
        m0, m1 = st.sb("m0", [P, NJ, HD, HD]), st.sb("m1", [P, NJ, HD, HD])
        d = st.sb("d", [P, NJ, HD])
        osq = st.sb("osq", [P, HD, P])
        s = {n: st.sem(n) for n in ("loaded", "step", "clamped", "exp_ready", "norms_ready", "rms_ready", "root_ready",
                                    "rec", "token_done", "post", "o_ready", "stored")}
        block = ctx.enter_context(nc.Block())

        @block.sync
        def _(sp):
            for n, t in (("k", k), ("v", v), ("q", q)):
                sp.dma_start(t[:, :, :, :].rearrange("p j d t -> p j (d t)"),
                             scratch[n].rearrange("(j l) (h d) t -> (l h) j (d t)", l=8, h=HEADS)).then_inc(s["loaded"], 16)
            for n, t in ((0, beta), (1, qq), (2, kk)):
                sp.dma_start(t[:, :, :], small_d[n].rearrange("(j l) h t -> (l h) j t", l=8)).then_inc(s["loaded"], 16)
            sp.wait_ge(s["o_ready"], 1)
            sp.dma_start(scratch["o"].rearrange("(j l) (h d) t -> (l h) j (d t)", l=8, h=HEADS),
                         v[:, :, :, :].rearrange("p j d t -> p j (d t)")).then_inc(s["stored"], 16)
            sp.wait_ge(s["stored"], 16)

        @block.scalar
        def _(act):
            act.wait_ge(s["clamped"], 1)
            act.activation(beta[:, :, :], beta[:, :, :], ACT.Exp).then_inc(s["exp_ready"], 1)
            act.activation(kk[:, :, :], kk[:, :, :], ACT.Sqrt)
            act.activation(qq[:, :, :], qq[:, :, :], ACT.Sqrt).then_inc(s["norms_ready"], 1)
            act.wait_ge(s["rms_ready"], 1)
            act.activation(kk[:, :, :], kk[:, :, :], ACT.Sqrt).then_inc(s["root_ready"], 1)

        @block.vector
        def _(dve):
            pre = Chain(dve, s["step"])
            dve.wait_ge(s["loaded"], 16 * 6)
            dve.tensor_scalar(beta[:, :, :], beta[:, :, :], -1.0, 88.0, ALU.mult, ALU.min).then_inc(s["clamped"], 1)
            dve.memset(S[:, :, :, :], 0.0)
            dve.wait_ge(s["exp_ready"], 1)
            pre.link(dve.tensor_scalar(beta[:, :, :], beta[:, :, :], 1.0, None, ALU.add))
            pre.link(dve.reciprocal(beta[:, :, :], beta[:, :, :]))
            dve.wait_ge(s["norms_ready"], 1)
            for a in (kk, qq):
                pre.link(dve.tensor_scalar(a[:, :, :], a[:, :, :], EPS, None, ALU.add))
                pre.link(dve.reciprocal(a[:, :, :], a[:, :, :]))
            pre.link(dve.tensor_tensor(beta[:, :, :], beta[:, :, :], kk[:, :, :], ALU.mult))
            pre.link(dve.tensor_tensor(beta[:, :, :], beta[:, :, :], kk[:, :, :], ALU.mult))
            with dve.Fori(0, P) as t:
                chain = Chain(dve, s["rec"], t, 7)
                kt, qt = spread(k[:, :, :, t], 2, HD), spread(q[:, :, :, t], 2, HD)
                chain.link(dve.tensor_tensor(m0[:, :, :, :], S[:, :, :, :], kt, ALU.mult))
                chain.link(dve.tensor_reduce(d[:, :, :], m0[:, :, :, :], AX.X, ALU.add))
                chain.link(dve.tensor_tensor(d[:, :, :], v[:, :, :, t], d[:, :, :], ALU.subtract))
                chain.link(dve.tensor_tensor(d[:, :, :], d[:, :, :], spread(beta[:, :, t], 2, HD), ALU.mult))
                chain.link(dve.tensor_tensor(m1[:, :, :, :], spread(d[:, :, :], 3, HD), kt, ALU.mult))
                chain.link(dve.tensor_tensor(S[:, :, :, :], S[:, :, :, :], m1[:, :, :, :], ALU.add))
                chain.link(dve.tensor_tensor(m1[:, :, :, :], S[:, :, :, :], qt, ALU.mult))
                dve.memset(core.beat[:, :], 0.0)
                dve.tensor_reduce(v[:, :, :, t], m1[:, :, :, :], AX.X, ALU.add).then_inc(s["token_done"], 1)
                chain.close()
                dve.wait_ge(s["token_done"], t + 1)
            post = Chain(dve, s["post"])
            for j in range(NJ):
                post.link(dve.tensor_tensor(osq[:, :, :], v[:, j, :, :], v[:, j, :, :], ALU.mult))
                post.link(dve.tensor_reduce(kk[:, j, :], osq[:, :, :].rearrange("p d t -> p t d"), AX.X, ALU.add))
            post.link(dve.tensor_tensor(kk[:, :, :], kk[:, :, :], qq[:, :, :], ALU.mult))
            post.link(dve.tensor_tensor(kk[:, :, :], kk[:, :, :], qq[:, :, :], ALU.mult))
            dve.tensor_scalar(kk[:, :, :], kk[:, :, :], 1.0 / HD, 1e-6, ALU.mult, ALU.add).then_inc(s["rms_ready"], 1)
            dve.wait_ge(s["root_ready"], 1)
            post.link(dve.reciprocal(kk[:, :, :], kk[:, :, :]))
            post.link(dve.tensor_tensor(kk[:, :, :], kk[:, :, :], qq[:, :, :], ALU.mult))
            dve.tensor_tensor(v[:, :, :, :], v[:, :, :, :], spread(kk[:, :, :], 2, HD), ALU.mult).then_inc(s["o_ready"], 1)

    with ExitStack() as ctx:
        st = Stage(nc, ctx, tag + "_out")
        oT = st.sb("oT", [P, batch, P])
        ot = [st.sb(f"ot{j}", [P, T, P]) for j in range(1)]
        w_o, b_o, nw = st.sb("w_o", [P, P]), st.sb("b_o", [1, P]), st.sb("norm_w", [P, 1])
        bn, mv = st.sb("bn", [P, 6]), st.sb("mv", [P, 2])
        yp = st.ps("y", [P, T, P])
        s = {n: st.sem(n) for n in ("loaded", "consts", "ot_ready", "y_done", "y_added", "vec_step")}
        block = ctx.enter_context(nc.Block())

        @block.sync
        def _(sp):
            sp.dma_start(oT[:, :, :], scratch["o"].rearrange("b p t -> p b t")).then_inc(s["loaded"], 16)
            sp.dma_start(w_o[:, :], dram[tag + "_w_o"]).then_inc(s["loaded"], 16)
            sp.dma_start(b_o[:, :], dram[tag + "_b_o"]).then_inc(s["loaded"], 16)
            sp.dma_start(nw[:, :], dram[tag + "_norm_w"]).then_inc(s["loaded"], 16)
            sp.wait_ge(s["loaded"], 64)

        @block.scalar
        def _(act):
            act.wait_ge(s["consts"], 1)
            with act.Fori(0, NI) as i:
                act.wait_ge(s["y_added"], i + 1)
                for t in range(T):
                    last = act.activation(ot[0][:, t, :], oT[:, i * T + t, :], ACT.Copy)
                last.then_inc(s["ot_ready"], 1)

        @block.tensor
        def _(pe):
            pe.wait_ge(s["consts"], 1)
            with pe.Fori(0, NI) as i:
                pe.wait_ge(s["ot_ready"], i + 1)
                for t in range(T):
                    pe.matmul(yp[:, t, :], ot[0][:, t, :], w_o[:, :], start=True, stop=False)
                    last = pe.matmul(yp[:, t, :], core.ones[0:1, :], b_o[0:1, :], start=False, stop=True)
                last.then_inc(s["y_done"], 1)

        @block.vector
        def _(dve):
            dve.sem_inc(s["y_added"], 1)
            dve.wait_ge(s["loaded"], 64)
            dve.tensor_scalar(w_o[:, :], w_o[:, :], nw[:, :], None, ALU.mult).then_inc(s["consts"], 1)
            with dve.Fori(0, NI) as i:
                chain = Chain(dve, s["vec_step"], i, 3 * T)
                dve.wait_ge(s["y_done"], i + 1)
                for t in range(T):
                    b = i * T + t
                    chain.link(dve.tensor_tensor(core.x[:, b, :], core.x[:, b, :], yp[:, t, :], ALU.add))
                    last = take_stats(dve, chain, core, b, bn, mv)
                last.then_inc(s["y_added"], 1)
                chain.close()


def wave_attention(nc, core, dram, tag):
    batch, T, NT = core.batch, TILE, TILE * P
    NI, H, PD, NS, DH = batch // T, 8, 16, 33, 16
    W3 = 3 * H
    LINKS = 34 + 14 * T
    with ExitStack() as ctx:
        st = Stage(nc, ctx, tag)
        names = ["w_wave", "b_wave", "w_query", "b_query", "kw", "w_se1", "b_se1", "w_se2", "b_se2", "w_out"]
        w = {n: st.sb(n, list(dram[f"{tag}_{n}"].shape)) for n in names}
        tab = st.sb("tables", list(dram["wave_tables"].shape))
        grid, absgrid, J = tab[:, 0:NS], tab[:, NS:2 * NS], tab[:, 2 * NS:2 * NS + P]
        cent, half_less, A3, B3 = (tab[:, 2 * NS + P + a:2 * NS + P + b] for a, b in ((0, 1), (1, 2), (2, 5), (5, 8)))
        hb1, hb2 = st.sb("half_b_se1", [P // 4, 1]), st.sb("half_b_se2", [P, 1])
        xn, xT = st.sb("xn", [P, T, P]), st.sb("xT", [P, NT])
        th_w, th_q = st.sb("th_wave", [P, T, W3]), st.sb("th_query", [P, T, P])
        wave, wt = st.sb("wave2", [P, T, W3]), st.sb("wave_tanh", [P, T, W3])
        qk = st.sb("qk", [P, T, H])
        fpd, inv = st.sb("fpd", [P, T, 3]), st.sb("inverse", [P, T, 3])
        place, valid, hole, rel, rd, far = (st.sb(n, [P, T, NS]) for n in ("place", "valid", "hole", "rel", "rd", "far"))
        e1, e2 = st.sb("e1", [P, T, H, NS]), st.sb("e2", [P, T, H, NS])
        top, z, norm, slope, bias = (st.sb(n, [P, T, H]) for n in ("top", "z", "norm", "slope", "bias"))
        near, shift = st.sb("near", [P, T, 1]), st.sb("shift", [P, T, 1])
        smp = [st.sb(f"sample{j}", [P, 2, P]) for j in range(2)]
        off = [st.sb(f"off{j}", [P, 2, P]) for j in range(2)]
        flag = [st.sb(f"flag{j}", [P, 2, P]) for j in range(2)]
        dist = [st.sb(f"dist{j}", [P, 2, P]) for j in range(2)]
        E = [st.sb(f"E{j}", [P, H, 2, P]) for j in range(2)]
        A = [st.sb(f"A{j}", [P, H, P]) for j in range(2)]
        AT = [st.sb(f"AT{j}", [P, H, P]) for j in range(2)]
        o, oT = st.sb("o", [P, T, P]), st.sb("oT", [P, NT])
        s1, s1t = st.sb("s1", [P // 4, NT]), st.sb("s1t", [P // 4, NT])
        s2t, yt = st.sb("s2t", [P, NT]), st.sb("yt", [P, T, P])
        bn, mv = st.sb("bn", [P, 6]), st.sb("mv", [P, 2])
        misc, zw, zq, op, s1p = st.ps("misc", [P, NT]), st.ps("zw", [P, T, W3]), st.ps("zq", [P, T, P]), \
            st.ps("op", [P, T, P]), st.ps("s1p", [P // 4, NT])
        yp = st.ps("yp", [P, T, P])
        ptp = [st.ps(f"ptp{a}", [P, 4, P]) for a in range(2)]
        s = {n: st.sem(n) for n in (
            "loaded", "once", "consts", "xn_ready", "xt_done", "xt_ready", "z_done", "th_ready", "wave_ready", "wt_ready",
            "e1_ready", "e1_exp", "dist_ready", "E_ready", "A_ready", "at_done", "at_ready", "pv_done",
            "o_ready", "ot_done", "ot_ready", "s1_done", "s1_ready", "s1_used", "s2_done", "s2_ready", "g_ready",
            "y_done", "yt_ready", "y_added", "vec_step")}
        n_loads = 16 * (len(names) + 1)
        block = ctx.enter_context(nc.Block())

        @block.sync
        def _(sp):
            for n in names:
                sp.dma_start(w[n][tuple(slice(None) for _ in w[n].shape)], dram[f"{tag}_{n}"]).then_inc(s["loaded"], 16)
            sp.dma_start(tab[:, :], dram["wave_tables"]).then_inc(s["loaded"], 16)
            sp.wait_ge(s["loaded"], n_loads)

        @block.vector
        def _(dve):
            dve.sem_inc(s["y_added"], 1)
            dve.wait_ge(s["loaded"], n_loads)
            dve.tensor_scalar(hb1[:, :], w["b_se1"][:, :], 0.5, None, ALU.mult)
            dve.tensor_scalar(hb2[:, :], w["b_se2"][:, :], 0.5, None, ALU.mult).then_inc(s["consts"], 1)

            def tt(out, a, b, op):
                chain.link(dve.tensor_tensor(out, a, b, op))

            def ts(out, a, s1_, s2_, op0, op1=ALU.bypass):
                chain.link(dve.tensor_scalar(out, a, s1_, s2_, op0, op1))

            def stt(out, a, sc, b, op0, op1):
                chain.link(dve.scalar_tensor_tensor(out, a, sc, b, op0, op1))

            def flat(a):
                return a[:, :, :].rearrange("p a b -> p (a b)")

            def waves(i):
                dve.wait_ge(s["th_ready"], i + 1)
                dve.scalar_tensor_tensor(flat(wave), flat(th_w), 1.0, zw[:, :, :].rearrange("p a b -> p (a b)"),
                                         ALU.add, ALU.mult).then_inc(s["wave_ready"], 1)
                stt(flat(th_q), flat(th_q), 1.0, zq[:, :, :].rearrange("p a b -> p (a b)"), ALU.add, ALU.mult)
                q = flat(th_q).rearrange("p (x d) -> p x d", d=PD)
                tt(q, q, spread(w["kw"][:, :], 1, T * H), ALU.mult)
                chain.link(dve.tensor_reduce(flat(qk), q, AX.X, ALU.add))
                ts(qk[:, :, :], qk[:, :, :], 0.5 * PD ** -0.5, None, ALU.mult)
                dve.wait_ge(s["wt_ready"], i + 1)
                chain.link(dve.tensor_reduce(fpd[:, :, :], wt[:, :, :].rearrange("p t (a h) -> p t a h", a=3), AX.X, ALU.add))
                tt(fpd[:, :, :], fpd[:, :, :], spread(A3, 1, T), ALU.mult)
                tt(fpd[:, :, :], fpd[:, :, :], spread(B3, 1, T), ALU.add)
                ts(fpd[:, :, 2:3], fpd[:, :, 2:3], 0.1, None, ALU.max)
                chain.link(dve.reciprocal(inv[:, :, 0:3:2], fpd[:, :, 0:3:2]))

            def samples(i):
                f, ph, rdec = (spread(a, 2, NS) for a in (fpd[:, :, 0], fpd[:, :, 1], inv[:, :, 2]))
                tt(place[:, :, :], spread(grid, 1, T), f, ALU.mult)
                ts(place[:, :, :], place[:, :, :], cent, None, ALU.add)
                tt(place[:, :, :], place[:, :, :], ph, ALU.add)
                ts(hole[:, :, :], place[:, :, :], 0.0, None, ALU.is_ge)
                stt(flat(valid), flat(place), float(P), flat(hole), ALU.is_lt, ALU.mult)
                ts(hole[:, :, :], valid[:, :, :], -1.0, 1e30, ALU.add, ALU.mult)
                tt(rel[:, :, :], spread(absgrid, 1, T), f, ALU.mult)
                tt(rd[:, :, :], rel[:, :, :], rdec, ALU.mult)
                tt(far[:, :, :], rel[:, :, :], hole[:, :, :], ALU.subtract)
                chain.link(dve.tensor_reduce(near[:, :, 0], far[:, :, :], AX.X, ALU.min))
                tt(e1[:, :, :, :], spread(qk[:, :, :], 3, NS), spread(rel[:, :, :], 2, H), ALU.mult)
                tt(e1[:, :, :, :], e1[:, :, :, :], spread(hole[:, :, :], 2, H), ALU.add)
                chain.link(dve.tensor_reduce(top[:, :, :], e1[:, :, :, :], AX.X, ALU.max))
                tt(e1[:, :, :, :], e1[:, :, :, :], spread(top[:, :, :], 3, NS), ALU.subtract)
                dve.tensor_tensor(e2[:, :, :, :], e1[:, :, :, :], spread(rd[:, :, :], 2, H), ALU.subtract)\
                   .then_inc(s["e1_ready"], 1)
                tt(slope[:, :, :], qk[:, :, :], spread(inv[:, :, 2], 2, H), ALU.subtract)
                tt(bias[:, :, :], slope[:, :, :], spread(near[:, :, 0], 2, H), ALU.mult)
                tt(bias[:, :, :], bias[:, :, :], top[:, :, :], ALU.subtract)
                ts(shift[:, :, 0], fpd[:, :, 1], -1.0, half_less, ALU.mult, ALU.add)
                tt(shift[:, :, 0], shift[:, :, 0], inv[:, :, 0], ALU.mult)
                ts(shift[:, :, 0], shift[:, :, 0], -0.5, None, ALU.add)

            def sums(i):
                dve.wait_ge(s["e1_exp"], i + 1)
                chain.link(dve.tensor_reduce(z[:, :, :], e1[:, :, :, :], AX.X, ALU.add))
                chain.link(dve.tensor_reduce(norm[:, :, :], e2[:, :, :, :], AX.X, ALU.add))
                stt(flat(norm), flat(z), 1e-8, flat(norm), ALU.mult, ALU.add)
                chain.link(dve.reciprocal(norm[:, :, :], norm[:, :, :]))

            def spots(i, t):
                j = t % 2
                f, ph = fpd[:, t, 0:1], fpd[:, t, 1:2]
                ts(smp[j][:, 0, :], J, inv[:, t, 0:1], shift[:, t, :], ALU.mult, ALU.add)
                ts(smp[j][:, 0, :], smp[j][:, 0, :], MAGIC, -MAGIC, ALU.add, ALU.add)
                ts(smp[j][:, 1, :], smp[j][:, 0, :], 1.0, None, ALU.add)
                ts(off[j][:, :, :], smp[j][:, :, :], f, cent, ALU.mult, ALU.add)
                for k in range(2):
                    last = dve.scalar_tensor_tensor(off[j][:, k, :], off[j][:, k, :], ph, J, ALU.add, ALU.subtract)
                chain.link(last)
                stt(smp[j][:, :, :], smp[j][:, :, :], -1.0, smp[j][:, :, :], ALU.mult, ALU.max)
                if t >= 2:
                    dve.wait_ge(s["A_ready"], i * T + (t - 1))
                ts(flag[j][:, :, :], off[j][:, :, :], 0.0, None, ALU.is_ge)
                stt(flag[j][:, :, :], off[j][:, :, :], 1.0, flag[j][:, :, :], ALU.is_lt, ALU.mult)
                stt(flag[j][:, :, :], smp[j][:, :, :], float(NS // 2), flag[j][:, :, :], ALU.is_le, ALU.mult)
                ts(smp[j][:, :, :], smp[j][:, :, :], f, near[:, t, :], ALU.mult, ALU.subtract)
                if t >= 2:
                    dve.wait_ge(s["E_ready"], i * T + (t - 1))
                dve.tensor_tensor(dist[j][:, :, :], smp[j][:, :, :], flag[j][:, :, :], ALU.mult).then_inc(s["dist_ready"], 1)

            def matrix(i, t):
                j = t % 2
                dve.wait_ge(s["E_ready"], i * T + (t + 1))
                tt(E[j][:, :, :, :].rearrange("p h k j -> p h (k j)"), E[j][:, :, :, :].rearrange("p h k j -> p h (k j)"),
                   spread(flag[j][:, :, :].rearrange("p k j -> p (k j)"), 1, H), ALU.mult)
                if t >= 2:
                    dve.wait_ge(s["at_done"], (i * T + (t - 1)) * 2)
                dve.tensor_tensor(A[j][:, :, :], E[j][:, :, 0, :], E[j][:, :, 1, :], ALU.add).then_inc(s["A_ready"], 1)

            with dve.Fori(0, NI) as i:
                chain = Chain(dve, s["vec_step"], i, LINKS)
                waves(i)
                samples(i)
                spots(i, 0)
                spots(i, 1)
                sums(i)
                for t in range(T):
                    matrix(i, t)
                    if t + 2 < T:
                        spots(i, t + 2)
                dve.wait_ge(s["pv_done"], i * T + T)
                dve.tensor_tensor(o[:, :, :].rearrange("p t (h d) -> p (t h) d", h=H),
                                  op[:, :, :].rearrange("p t (h d) -> p (t h) d", h=H), spread(flat(norm), 2, DH), ALU.mult)\
                   .then_inc(s["o_ready"], 1)
                dve.wait_ge(s["s1_ready"], i + 1)
                dve.scalar_tensor_tensor(s1[:, :], s1t[:, :], 1.0, s1[:, :], ALU.add, ALU.mult).then_inc(s["s1_used"], 1)
                dve.wait_ge(s["s2_ready"], i + 1)
                dve.scalar_tensor_tensor(oT[:, :], s2t[:, :], 1.0, oT[:, :], ALU.add, ALU.mult).then_inc(s["g_ready"], 1)
                dve.wait_ge(s["yt_ready"], i + 1)
                stt(flat(yt), flat(yt), 1.0, yp[:, :, :].rearrange("p a b -> p (a b)"), ALU.add, ALU.mult)
                for t in range(T):
                    b = i * T + t
                    stt(core.x[:, b, :], yt[:, t, :], 0.25, core.x[:, b, :], ALU.mult, ALU.add)
                    last = take_stats(dve, chain, core, b, bn, mv)
                last.then_inc(s["y_added"], 1)
                chain.close()

        @block.scalar
        def _(act):
            act.wait_ge(s["consts"], 1)
            with act.Fori(0, NI) as i:
                act.wait_ge(s["y_added"], i + 1)
                for t in range(T):
                    b = i * T + t
                    last = act.activation(xn[:, t, :], core.x[:, b, :], ACT.Identity, bias=core.nmr[:, b, :],
                                          scale=core.rstd[:, b, :])
                last.then_inc(s["xn_ready"], 1)
                act.wait_ge(s["xt_done"], i + 1)
                act.activation(xT[:, :], misc[:, :], ACT.Copy).then_inc(s["xt_ready"], 1)
                act.wait_ge(s["z_done"], i + 1)
                act.activation(th_w[:, :, :], zw[:, :, :], ACT.Tanh, scale=0.5)
                act.activation(th_q[:, :, :], zq[:, :, :], ACT.Tanh, scale=0.5).then_inc(s["th_ready"], 1)
                act.wait_ge(s["wave_ready"], i + 1)
                w3, t3 = (a[:, :, :].rearrange("p t (a h) -> p t a h", a=3) for a in (wave, wt))
                for a, sc in ((0, 0.25), (2, 0.25), (1, 0.5)):
                    last = act.activation(t3[:, :, a, :], w3[:, :, a, :], ACT.Tanh, scale=sc)
                last.then_inc(s["wt_ready"], 1)
                act.wait_ge(s["e1_ready"], i + 1)
                act.activation(e1[:, :, :, :], e1[:, :, :, :], ACT.Exp)
                act.activation(e2[:, :, :, :], e2[:, :, :, :], ACT.Exp).then_inc(s["e1_exp"], 1)

                def exps(t):
                    j = t % 2
                    act.wait_ge(s["dist_ready"], i * T + (t + 1))
                    if t >= 2:
                        act.wait_ge(s["A_ready"], i * T + (t - 1))
                    for h in range(H):
                        last = act.activation(E[j][:, h, :, :], dist[j][:, :, :], ACT.Exp, bias=bias[:, t, h:h + 1],
                                              scale=slope[:, t, h:h + 1])
                    last.then_inc(s["E_ready"], 1)

                def copies(t):
                    j = t % 2
                    for a in range(2):
                        act.wait_ge(s["at_done"], (i * T + t) * 2 + (a + 1))
                        act.activation(AT[j][:, 4 * a:4 * a + 4, :], ptp[a][:, :, :], ACT.Copy).then_inc(s["at_ready"], 1)

                exps(0)
                for t in range(T):
                    if t + 1 < T:
                        exps(t + 1)
                    copies(t)
                act.wait_ge(s["ot_done"], i + 1)
                act.activation(oT[:, :], misc[:, :], ACT.Copy).then_inc(s["ot_ready"], 1)
                act.wait_ge(s["s1_done"], i + 1)
                act.activation(s1t[:, :], s1p[:, :], ACT.Tanh, scale=0.5, bias=hb1[:, :])
                act.activation(s1[:, :], s1p[:, :], ACT.Identity, bias=w["b_se1"][:, :]).then_inc(s["s1_ready"], 1)
                act.wait_ge(s["s2_done"], i + 1)
                act.activation(s2t[:, :], yp[:, :, :].rearrange("p a b -> p (a b)"), ACT.Tanh, scale=0.25, bias=hb2[:, :])\
                   .then_inc(s["s2_ready"], 1)
                act.wait_ge(s["y_done"], i + 1)
                act.activation(yt[:, :, :], yp[:, :, :], ACT.Tanh, scale=0.25).then_inc(s["yt_ready"], 1)

        @block.tensor
        def _(pe):
            pe.wait_ge(s["consts"], 1)

            def mm(out, lhsT, rhs, start=True, stop=True):
                return pe.matmul(out, lhsT, rhs, start=start, stop=stop)

            with pe.Fori(0, NI) as i:
                pe.wait_ge(s["xn_ready"], i + 1)
                for t in range(T):
                    last = pe.transpose(misc[:, t * P:(t + 1) * P], xn[:, t, :], core.ident[:, :])
                last.then_inc(s["xt_done"], 1)
                pe.wait_ge(s["xt_ready"], i + 1)
                for t in range(T):
                    mm(zw[:, t, :], xT[:, t * P:(t + 1) * P], w["w_wave"][:, :], stop=False)
                    mm(zw[:, t, :], core.ones[0:1, :], w["b_wave"][0:1, :], start=False)
                    mm(zq[:, t, :], xT[:, t * P:(t + 1) * P], w["w_query"][:, :], stop=False)
                    last = mm(zq[:, t, :], core.ones[0:1, :], w["b_query"][0:1, :], start=False)
                last.then_inc(s["z_done"], 1)
                for t in range(T):
                    j = t % 2
                    pe.wait_ge(s["A_ready"], i * T + (t + 1))
                    for a in range(2):
                        if t:
                            pe.wait_ge(s["at_ready"], (i * T + (t - 1)) * 2 + (a + 1))
                        for h in range(4):
                            last = pe.transpose(ptp[a][:, h, :], A[j][:, 4 * a + h, :], core.ident[:, :])
                        last.then_inc(s["at_done"], 1)
                    pe.wait_ge(s["at_ready"], (i * T + t) * 2 + 2)
                    for h in range(H):
                        last = mm(op[:, t, h * DH:(h + 1) * DH], AT[j][:, h, :], xn[:, t, h * DH:(h + 1) * DH])
                    last.then_inc(s["pv_done"], 1)
                pe.wait_ge(s["o_ready"], i + 1)
                for t in range(T):
                    last = pe.transpose(misc[:, t * P:(t + 1) * P], o[:, t, :], core.ident[:, :])
                last.then_inc(s["ot_done"], 1)
                pe.wait_ge(s["ot_ready"], i + 1)
                mm(s1p[:, :], w["w_se1"][:, :], oT[:, :]).then_inc(s["s1_done"], 1)
                pe.wait_ge(s["s1_used"], i + 1)
                mm(yp[:, :, :].rearrange("p a b -> p (a b)"), w["w_se2"][:, :], s1[:, :]).then_inc(s["s2_done"], 1)
                pe.wait_ge(s["g_ready"], i + 1)
                for t in range(T):
                    last = mm(yp[:, t, :], oT[:, t * P:(t + 1) * P], w["w_out"][:, :])
                last.then_inc(s["y_done"], 1)


STAGES = ["L0_attn", "L0_xattn", "L0_ffn", "L1_attn", "L1_xattn", "L1_ffn",
          "L2_attn", "L2_xattn", "L2_ffn", "L3_attn", "L3_xattn", "L3_ffn"]

MLP_KINDS = {"L0_ffn": "moe0", "L2_ffn": "plain", "L3_ffn": "moe3"}


def decoder_kernel(nc, dram, batch, stages=STAGES):
    with ExitStack() as ctx:
        core = Core(nc, ctx, batch)
        load_everything(nc, core, dram)
        for tag in stages:
            norm_scalars(nc, core, tag, LN_EPS if tag in ("L2_ffn", "L3_xattn") else None)
            if tag == "L0_attn":
                softmax_attention(nc, core, dram, tag, heads_norm=True)
            elif tag == "L0_xattn":
                softmax_attention(nc, core, dram, tag, context="past")
            elif tag == "L1_xattn":
                softmax_attention(nc, core, dram, tag, context="only")
            elif tag == "L3_attn":
                softmax_attention(nc, core, dram, tag, latent=True)
            elif tag == "L1_ffn":
                quantised_mlp(nc, core, dram, tag)
            elif tag == "L2_xattn":
                query_softmax_attention(nc, core, dram, tag)
            elif tag == "L3_xattn":
                wide_cross_attention(nc, core, dram, tag)
            elif tag == "L2_attn":
                delta_rule_attention(nc, core, dram, tag)
            elif tag == "L1_attn":
                wave_attention(nc, core, dram, tag)
            elif tag in MLP_KINDS:
                mlp_stage(nc, core, dram, tag, MLP_KINDS[tag])
        store_everything(nc, core, dram)


def head_slots(w):
    out = np.zeros((w.shape[0], GROUPS, 4, SLOT), w.dtype)
    out[..., :HD] = w.reshape(w.shape[0], 4, GROUPS, HD).transpose(0, 2, 1, 3)
    return out.reshape(w.shape[0], HEADS * SLOT)


def slot_column(value):
    out = np.zeros((HEADS, SLOT), np.float32)
    out[:, HD] = value
    return out.reshape(HEADS * SLOT)


def layout(x):
    a = {"x": x["x"], "ctxT": x["ctx_1024"].transpose(2, 0, 1), "ident": np.eye(P, dtype=np.float32)}
    pos, di = np.arange(P, dtype=np.float32)[:, None], np.arange(0, HD, 2, dtype=np.float32) / HD
    theta = pos * np.exp(-di * np.float32(np.log(10000.0)))
    sin = np.repeat(np.sin(theta), 2, axis=1)
    sin[:, :HD // 2] *= -1
    a["rope"] = np.concatenate([np.repeat(np.cos(theta), 2, axis=1), sin], axis=1).astype(np.float32)
    a["causal"] = np.tile(np.triu(np.full((P, P), -1e30, np.float32), 1), (1, 4))
    a["decay"] = np.exp(-0.01 * 0.01 * np.abs(pos - pos.T)).astype(np.float32)
    a["row_c"] = np.concatenate([np.eye(2, dtype=np.float32), np.tile(np.arange(SC, dtype=np.float32), (2, 1))], axis=1)
    a["lens"] = x["_lenS2"]
    a["key_mask"] = x["mask_BxS2_bf1"].view(np.uint8)

    t = "L0_attn_"
    a[t + "w_qkv"] = np.concatenate([x[t + n].T for n in ("Wq", "Wk", "Wv")], axis=1)
    a[t + "gb"] = np.tile(np.concatenate([x[t + n] for n in ("q_gamma", "k_gamma", "q_beta", "k_beta")]), (P, 1))
    a[t + "w_o"], a[t + "b_o"] = x[t + "Wo"].T, x[t + "bo"][None]

    t = "L0_xattn_"
    a[t + "w_q"], a[t + "w_k"] = head_slots(x[t + "wq"].T), head_slots(x[t + "wk"].T)
    a[t + "b_q"] = slot_column(1.0).reshape(GROUPS, P).T
    a[t + "w_kc"] = head_slots(a["ident"])
    a[t + "aux"] = np.stack([slot_column(0.0), slot_column(-1e30)])
    a[t + "w_v"], a[t + "w_vc"] = x[t + "wv"].T, a["ident"]
    a[t + "w_o"], a[t + "b_o"] = x[t + "wo"].T, x[t + "bo"][None]

    t = "L1_xattn_"
    a[t + "w_q"], a[t + "w_kc"] = head_slots(x[t + "Wq"].T), head_slots(x[t + "Wk"].T)
    bq = head_slots(x[t + "bq"][None])[0]
    bq.reshape(HEADS, SLOT)[:, HD] = 1.0
    a[t + "b_q"] = bq.reshape(GROUPS, P).T
    a[t + "aux"] = np.stack([head_slots(x[t + "bk"][None])[0], slot_column(-1e8 * HD ** 0.5)])
    a[t + "w_vc"], a[t + "b_v"] = x[t + "Wv"].T, x[t + "bv"][None]
    a[t + "w_o"], a[t + "b_o"] = x[t + "Wo"].T, x[t + "bo"][None]

    t = "L3_attn_"
    a[t + "w_q"] = head_slots(x[t + "Wq"])
    a[t + "w_kv"] = np.concatenate([x[t + "Wk"], x[t + "Wv"]], axis=1)
    a[t + "w_down"], a[t + "w_k"], a[t + "w_up_v"] = x[t + "W_down_kv"], head_slots(x[t + "W_up_k"]), x[t + "W_up_v"]
    a[t + "w_o"] = x[t + "Wo"]

    def chunks_in(*ws):
        return np.concatenate(ws, axis=1).reshape(P, -1, P)

    def chunks_out(*ws):
        return np.concatenate(ws, axis=0).reshape(-1, P, P).transpose(1, 0, 2)

    def pick(rows, groups):
        owner = np.concatenate([first + np.arange(n * width) // width for first, n, width in groups])
        return (np.arange(rows)[:, None] == owner[None, :]).astype(np.float32).reshape(rows, -1, P)

    t = "L3_xattn_"
    a["ctx"] = x["ctx_1024"]
    a[t + "w_q"], a[t + "w_kv"] = x[t + "Wq"], x[t + "Wkv"]
    a[t + "w_o"], a[t + "b_o"] = x[t + "Wout"].reshape(-1, P, P).transpose(1, 0, 2), x[t + "bout"][None]
    a[t + "ln"] = np.stack([x[t + n] for n in ("g1", "b1", "g2", "b2")], axis=1)

    t = "L2_xattn_"
    a[t + "w_q"], a[t + "b_q"] = head_slots(x[t + "Wq"]), head_slots(x[t + "bq"][None]).reshape(GROUPS, P).T
    a[t + "w_k"] = np.stack([x[t + "Wk1"], x[t + "Wk2"]], axis=1)
    a[t + "b_k"] = np.stack([x[t + "bk1"], x[t + "bk2"]], axis=1)
    a[t + "w_slot"] = head_slots(a["ident"])
    a[t + "w_v"] = np.stack([x[t + "Wv1"], x[t + "Wv2"]], axis=1)
    a[t + "b_v"] = np.concatenate([x[t + "bv1"], x[t + "bv2"]])[None]
    a[t + "w_qt"], a[t + "b_qt"] = x[t + "Wq"], x[t + "bq"][None]
    a[t + "w_o"], a[t + "b_o"] = x[t + "Wo"], x[t + "bo"][None]
    a[t + "gb"] = np.tile(np.stack([x[t + n] for n in ("g0", "beta0", "g1", "beta1")]), (P, 1, 1))

    t = "L2_attn_"
    a[t + "w_in"] = np.stack([x[t + n].T for n in ("Wq", "Wk", "Wv")], axis=1)
    a[t + "b_in"] = np.stack([x[t + n] for n in ("bq", "bk", "bv")], axis=1)
    a[t + "conv"] = np.stack([np.concatenate([x[f"{t}w{n}_conv"], x[f"{t}b{n}_conv"][:, None]], axis=1) for n in "qkv"], axis=1)
    a[t + "w_beta"] = x[t + "Wbeta"].T
    a[t + "b_beta"] = np.stack([x[t + "bbeta"], np.zeros(HEADS, np.float32), np.zeros(HEADS, np.float32)], axis=1)
    a[t + "head_sum"] = np.repeat(np.eye(HEADS, dtype=np.float32), HD, axis=0)
    a[t + "w_o"], a[t + "b_o"], a[t + "norm_w"] = x[t + "Wo"].T, x[t + "bo"][None], np.tile(x[t + "norm_w"], HEADS)[:, None]

    t = "L1_attn_"
    grid = np.arange(-16, 17, dtype=np.float32)
    tok = np.arange(P, dtype=np.float32)
    a["wave_tables"] = np.concatenate(
        [np.tile(np.concatenate([grid, np.abs(grid), tok]), (P, 1)), tok[:, None], 0.5 - tok[:, None],
         np.tile(np.float32([7.5 / 8, 2.0, 4.75 / 8, 8.5, 0.0, 5.25]), (P, 1))], axis=1).astype(np.float32)
    for n in ("w_wave", "w_query", "w_se1", "w_se2", "w_out"):
        a[t + n] = x[t + n]
    a[t + "b_wave"], a[t + "b_query"] = x[t + "b_wave"][None], x[t + "b_query"][None]
    a[t + "b_se1"], a[t + "b_se2"] = x[t + "b_se1"][:, None], x[t + "b_se2"][:, None]
    a[t + "kw"] = np.tile(x[t + "key_weight"], (P, 1))

    a["lower"] = np.tile(np.tril(np.ones((4, 4), np.float32), -1), (P, 1, 1))
    t = "L0_ffn_"
    for dst, e, sh in (("w_g", "expert_gate", "shared_gate"), ("w_u", "expert_up", "shared_up")):
        a[t + dst] = chunks_in(x[t + e].transpose(2, 0, 1).reshape(P, -1), x[t + sh].T)
    a[t + "w_d"] = chunks_out(x[t + "expert_down"].transpose(0, 2, 1).reshape(-1, P), x[t + "shared_down"].T)
    a[t + "w_r"], a[t + "b_r"] = x[t + "gate_w"].T, np.tile(x[t + "gate_bias"], (P, 1))
    a[t + "pick"] = pick(32, [(0, 32, 64)])

    t = "L3_ffn_"
    pad = np.zeros((P, P // 2), np.float32)
    for n in ("g", "u"):
        full = {"g": "gate", "u": "up"}[n]
        a[t + "w_" + n] = chunks_in(x[t + "w_" + full].transpose(1, 0, 2).reshape(P, -1),
                                    x[t + "anchor_w_" + full].transpose(1, 0, 2).reshape(P, -1),
                                    x[t + "shared_w_" + full], pad)
    a[t + "w_d"] = chunks_out(x[t + "w_down"].reshape(-1, P), x[t + "anchor_w_down"].reshape(-1, P),
                              x[t + "shared_w_down"], pad.T)
    a[t + "w_r"], a[t + "b_r"] = x[t + "gate_weight"].T, np.tile(x[t + "gate_bias"], (P, 1))
    a[t + "pick"] = pick(48, [(0, 32, 64), (32, 16, 32)])

    t = "L1_ffn_"
    a[t + "w"] = np.concatenate([x[t + "w_gate"].reshape(3, P, P).transpose(1, 0, 2),
                                 x[t + "w_up"].reshape(3, P, P).transpose(1, 0, 2), x[t + "w_down"].reshape(P, 3, P)], axis=1)

    t = "L2_ffn_"
    a[t + "q_w_g"], a[t + "q_w_d"] = chunks_in(x[t + "fc1_q"]), chunks_out(x[t + "fc2_q"])
    a[t + "w_g"] = np.tile(x[t + "fc1_scales"].reshape(1, -1, P), (P, 1, 1))
    a[t + "w_d"] = np.tile(x[t + "fc2_scales"].reshape(1, -1, P), (P, 1, 1))
    a[t + "b_g"], a[t + "b_d"] = x[t + "fc1_bias"].reshape(-1, P).T, x[t + "fc2_bias"][None]
    a[t + "ln_g"], a[t + "ln_b"] = x[t + "ln_gamma"][:, None], x[t + "ln_beta"][:, None]
    return a


def kernel(**inputs):
    import concourse.bacc as bacc
    from concourse.bass_utils import run_bass_kernel_spmd

    arrays = {n: np.ascontiguousarray(v) for n, v in layout({n: np.asarray(v) for n, v in inputs.items()}).items()}
    nc = bacc.Bacc("TRN2", target_bir_lowering=False, num_devices=1)
    dram = {n: nc.dram_tensor("in_" + n, v.shape, mybir.dt.from_np(v.dtype), kind="ExternalInput").ap()
            for n, v in arrays.items()}
    shape = inputs["x"].shape
    dram["out"] = nc.dram_tensor("out", shape, F32, kind="ExternalOutput").ap()
    decoder_kernel(nc, dram, shape[0])
    r = run_bass_kernel_spmd(nc, [{"in_" + n: v for n, v in arrays.items()}], core_ids=[0])
    return r.results[0]["out"]
```

```python
from contextlib import ExitStack

import concourse.bass as bass
import numpy as np
from concourse import mybir

F32 = mybir.dt.float32
BF16 = mybir.dt.bfloat16
I32 = mybir.dt.int32
I16 = mybir.dt.int16
U8 = mybir.dt.uint8
ALU = mybir.AluOpType
ACT = mybir.ActivationFunctionType
AX = mybir.AxisListType

P = 128
SC = 77
UNITS = 2
HEADS = 16
HD = 8
SLOT = 32
GROUPS = HEADS * SLOT // P
BANK = 512
LN_EPS = 1e-5


def spread(ap, axis, size):
    shape = list(ap.shape)
    return ap.unsqueeze(axis).broadcast_to(shape[:axis] + [size] + shape[axis:])


class Chain:

    def __init__(self, eng, sem, i=0, per_iteration=0):
        self.eng, self.sem, self.base, self.per, self.k = eng, sem, i * per_iteration, per_iteration, 0

    def link(self, ins):
        self.k += 1
        ins.then_inc(self.sem, 1)
        self.eng.wait_ge(self.sem, self.base + self.k)

    def close(self):
        assert self.k == self.per, (self.k, self.per)


class Stage:

    def __init__(self, nc, ctx, tag):
        self.nc, self.ctx, self.tag, self.sems = nc, ctx, tag, []
        ctx.callback(self.clear)

    def clear(self):
        self.nc.clear_and_free_semaphores(self.sems)
        self.nc.all_engine_barrier()

    def sb(self, name, shape, dt=F32):
        return self.ctx.enter_context(self.nc.sbuf_tensor(f"{self.tag}_{name}", shape, dt))

    def ps(self, name, shape, dt=F32):
        return self.ctx.enter_context(self.nc.psum_tensor(f"{self.tag}_{name}", shape, dt))

    def sem(self, name):
        self.sems.append(self.nc.alloc_semaphore(f"{self.tag}_{name}"))
        return self.sems[-1]


class Core:

    def __init__(self, nc, ctx, batch):
        def sb(name, shape, dt=F32):
            return ctx.enter_context(nc.sbuf_tensor(name, shape, dt))

        self.nc, self.batch = nc, batch
        self.x = sb("x_all", [P, batch, P])
        self.stat = sb("stat_all", [P, batch, 2])
        self.rstd = sb("rstd_all", [P, batch, 1])
        self.rstd2 = sb("rstd2_all", [P, batch, 1])
        self.nmr2 = sb("nmr2_all", [P, batch, 1])
        self.nmr = sb("nmr_all", [P, batch, 1])
        self.ctxT = sb("ctxT", [P, batch, SC])
        self.ident = sb("ident", [P, P])
        self.beat = sb("beat", [1, 1])
        self.ones = sb("ones", [1, P])


def load_everything(nc, core, dram):
    with ExitStack() as ctx:
        st = Stage(nc, ctx, "load")
        x_in, c_in, stats_step = st.sem("x_in"), st.sem("c_in"), st.sem("stats_step")
        bn = st.sb("bn", [P, 6])
        mv = st.sb("mv", [P, 2])
        block = ctx.enter_context(nc.Block())

        @block.sync
        def _(sp):
            sp.dma_start(core.x[:, :, :], dram["x"].rearrange("b t d -> t b d")).then_inc(x_in, 16)
            sp.wait_ge(x_in, 16)

        @block.scalar
        def _(act):
            act.dma_start(core.ctxT[:, :, :], dram["ctxT"]).then_inc(c_in, 16)
            act.dma_start(core.ident[:, :], dram["ident"]).then_inc(c_in, 16)
            act.dma_start(core.ones[:, :], dram["ident"][0:1, :]).then_inc(c_in, 16)
            act.wait_ge(c_in, 48)

        @block.vector
        def _(dve):
            dve.wait_ge(c_in, 48)
            nc.vector.memset(core.ones[:, :], 1.0)
            dve.wait_ge(x_in, 16)
            with dve.Fori(0, core.batch) as i:
                chain = Chain(dve, stats_step, i, 3)
                chain.link(take_stats(dve, chain, core, i, bn, mv))
                chain.close()


def store_everything(nc, core, dram):
    with ExitStack() as ctx:
        st = Stage(nc, ctx, "store")
        x_out = st.sem("x_out")
        block = ctx.enter_context(nc.Block())

        @block.sync
        def _(sp):
            sp.dma_start(dram["out"].rearrange("b t d -> t b d"), core.x[:, :, :]).then_inc(x_out, 16)
            sp.wait_ge(x_out, 16)


def take_stats(dve, chain, core, b, bn, mv):
    dve.memset(core.beat[:, :], 0.0)
    chain.link(dve.bn_stats(bn[:, :], core.x[:, b, :]))
    dve.memset(core.beat[:, :], 0.0)
    chain.link(dve.bn_aggr(mv[:, :], bn[:, :]))
    return dve.tensor_copy(core.stat[:, b, :], mv[:, :])


def norm_scalars(nc, core, tag, second_eps=None):
    with ExitStack() as ctx:
        st = Stage(nc, ctx, tag + "_ln")
        var_ready, std_ready, step, var2_ready, std2_ready = (
            st.sem(n) for n in ("var_ready", "std_ready", "step", "var2_ready", "std2_ready"))
        std = st.sb("std", [P, core.batch])
        var = st.sb("var", [P, core.batch])
        rstd, nmr, rstd2, nmr2 = (a[:, :, 0] for a in (core.rstd, core.nmr, core.rstd2, core.nmr2))
        block = ctx.enter_context(nc.Block())

        @block.scalar
        def _(act):
            act.wait_ge(var_ready, 1)
            act.activation(std[:, :], var[:, :], ACT.Sqrt).then_inc(std_ready, 1)
            if second_eps is not None:
                act.wait_ge(var2_ready, 1)
                act.activation(std[:, :], var[:, :], ACT.Sqrt).then_inc(std2_ready, 1)

        @block.vector
        def _(dve):
            chain = Chain(dve, step)
            dve.tensor_scalar(var[:, :], core.stat[:, :, 1], LN_EPS, None, ALU.add).then_inc(var_ready, 1)
            dve.wait_ge(std_ready, 1)
            chain.link(dve.reciprocal(rstd, std[:, :]))
            chain.link(dve.scalar_tensor_tensor(nmr, core.stat[:, :, 0], -1.0, rstd, ALU.mult, ALU.mult))
            if second_eps is not None:
                chain.link(dve.tensor_tensor(var[:, :], core.stat[:, :, 1], rstd, ALU.mult))
                chain.link(dve.tensor_tensor(var[:, :], var[:, :], rstd, ALU.mult))
                dve.tensor_scalar(var[:, :], var[:, :], second_eps, None, ALU.add).then_inc(var2_ready, 1)
                dve.wait_ge(std2_ready, 1)
                chain.link(dve.reciprocal(std[:, :], std[:, :]))
                dve.tensor_tensor(rstd2, rstd, std[:, :], ALU.mult)
                dve.tensor_tensor(nmr2, nmr, std[:, :], ALU.mult)


def softmax_attention(nc, core, dram, tag, heads_norm=False, context=None, latent=False):
    batch = core.batch
    own = context != "only"
    key_tiles = ([(SC, "ctx")] if context else []) + ([(P, "own")] if own else [])
    NK = sum(n for n, _ in key_tiles)
    CHUNK = min(BANK // NK, 4)
    NCH = HEADS // CHUNK
    K = HD + 1 if context else HD
    blocks = [(h, t) for h in range(CHUNK) for t in range(len(key_tiles))]
    scale = 1.0 if latent else float(HD) ** -0.5

    with ExitStack() as ctx:
        st = Stage(nc, ctx, tag)
        U = UNITS

        def unit_sb(name, shape, dt=F32):
            return [st.sb(f"{name}{u}", shape, dt) for u in range(U)]

        names = [n for n in (tag + "_w_qkv", tag + "_w_q", tag + "_b_q", tag + "_w_k", tag + "_w_kc", tag + "_w_v",
                             tag + "_w_vc", tag + "_aux", tag + "_w_o", tag + "_b_o", tag + "_b_v",
                             tag + "_w_kv", tag + "_w_down", tag + "_w_up_v", tag + "_gb") if n in dram]
        shared = (["rope"] if heads_norm else []) + (["decay"] if latent else [])
        w = {n: st.sb(n + "_s", list(dram[n].shape)) for n in names + shared}

        def W(n):
            return w[f"{tag}_{n}"]

        xn, xT = unit_sb("xn", [P, P]), unit_sb("xT", [P, P])
        qT, kT = unit_sb("qT", [P, GROUPS, P]), unit_sb("kT", [P, GROUPS, NK])
        v = [unit_sb(f"v_{kind}", [n, HEADS, SLOT]) for n, kind in key_tiles]
        probs = [unit_sb(f"probs{j}_", [P, CHUNK, NK]) for j in range(2)]
        pT = [unit_sb(f"pT{j}_", [P, 4, P]) for j in range(2)]
        top = unit_sb("top", [P, HEADS])
        rz = unit_sb("rz", [P, HEADS])
        accT = unit_sb("accT", [P, GROUPS, P])
        o, oT = unit_sb("o", [P, P]), unit_sb("oT", [P, P])
        bn, mv = unit_sb("bn", [P, 6]), unit_sb("mv", [P, 2])
        if heads_norm:
            qk = unit_sb("qk", [P, 2, HEADS, HD])
            sq = unit_sb("sq", [P, 2, HEADS, HD])
            rot = unit_sb("rot", [P, 2, HEADS, HD])
            hstat = unit_sb("hstat", [P, 2 * HEADS])
            hvar = unit_sb("hvar", [P, 2 * HEADS])
            hrstd = unit_sb("hrstd", [P, 2 * HEADS])
            minus_half = st.sb("minus_half", [P, 2 * HEADS])
            padded = unit_sb("padded", [P, 2, GROUPS, 4, SLOT])
            ident_b = st.sb("ident_b", [P, P], BF16)
            causal_b = st.sb("causal_b", [P, 4, P], BF16)
        if context:
            rows = st.sb("rows", [2, batch, SC])
            ctxm, ctxu = unit_sb("ctxm", [P, SC]), unit_sb("ctxu", [P, SC])
        if latent:
            kvT, latT = unit_sb("kvT", [P, P]), unit_sb("latT", [SLOT, P])

        scores = [st.ps(f"scores{u}", [P, 2, BANK]) for u in range(U)]
        ptp = [st.ps(f"ptp{j}", [P, 4, P]) for j in range(2)]
        misc = [st.ps(f"misc{u}", [P, BANK]) for u in range(U)]
        A, B2 = slice(0, P), slice(3 * P, 4 * P)

        s = {n: st.sem(n) for n in (
            "loaded", "consts", "rows_step", "rows_ready", "xn_ready", "xt_done", "xt_ready", "vec_step",
            "first_step", "last_step", "scores_done", "shifted", "probs_ready",
            "pt_done", "pt_copied", "pv_done", "acc_ready", "back_done", "o_ready", "ot_done", "ot_ready",
            "y_done", "y_added", "q_done", "q_ready", "k_done", "k_ready", "v_done", "v_ready")}
        if heads_norm:
            s |= {n: st.sem(n) for n in ("proj_done", "var_ready", "square_ready", "centred", "hrstd_ready",
                                         "padded_ready")}
        if context:
            s |= {n: st.sem(n) for n in ("mask_done", "ctxm_ready", "ctxu_ready", "kc_done", "kc_ready",
                                         "vc_done", "vc_ready")}
        if latent:
            s |= {n: st.sem(n) for n in ("kv_done", "kv_ready", "lat_done", "lat_ready")}
        n_loads = len(names) + len(shared) + (2 if context else 0) + (2 if heads_norm else 0)
        mask_raw = st.sb("mask_raw", [2, batch, SC], U8) if context == "only" else None
        len_raw = st.sb("len_raw", [2, batch], I32) if context == "past" else None
        row_c = st.sb("row_c", [2, 2 + SC]) if context else None
        stage_f = st.sb("stage_f", [P, 5 * P]) if heads_norm else None
        len_f = st.sb("len_f", [2, batch]) if context == "past" else None
        len_max = st.sb("len_max", [2, 1]) if context == "past" else None
        keep_less_fill = st.sb("keep_less_fill", [2, 1]) if context == "only" else None
        beyond = st.sb("beyond", [2, SC]) if context == "past" else None
        block = ctx.enter_context(nc.Block())

        def head_of(c, j):
            return (4 * c + j) if CHUNK == 4 else (8 * (c // 4) + 4 * (c % 2) + 2 * (c // 2 % 2) + j)

        def count(b, per=1, extra=1):
            i, at = b
            return at * per + extra if i is None else i * (U * per) + (at * per + extra)

        def number(b):
            return count(b, 1, 0)

        def neighbour(b, d):
            return (b[0], b[1] + d)

        def step_of(k):
            return k * 4 // NCH if k * 4 % NCH == 0 else None

        @block.sync
        def _(sp):
            for n in names + shared:
                sp.dma_start(w[n][tuple(slice(None) for _ in dram[n].shape)], dram[n]).then_inc(s["loaded"], 16)
            if context:
                sp.dma_start(row_c[:, :], dram["row_c"]).then_inc(s["loaded"], 16)
                if context == "only":
                    src = dram["key_mask"].rearrange("(a b) t -> a b t", a=1).broadcast_to([2, batch, SC])
                    sp.dma_start(mask_raw[:, :, :], src).then_inc(s["loaded"], 16)
                else:
                    src = dram["lens"].rearrange("(a b) -> a b", a=1).broadcast_to([2, batch])
                    sp.dma_start(len_raw[:, :], src).then_inc(s["loaded"], 16)
            if heads_norm:
                sp.dma_start(stage_f[:, 0:P], dram["ident"]).then_inc(s["loaded"], 16)
                sp.dma_start(stage_f[:, P:5 * P], dram["causal"]).then_inc(s["loaded"], 16)
            sp.wait_ge(s["loaded"], 16 * n_loads)

        @block.gpsimd
        def _(pool):
            if not heads_norm:
                return
            pool.wait_ge(s["consts"], 1)
            with pool.Fori(0, batch // U) as i:
                for u in range(U):
                    pool.wait_ge(s["var_ready"], i * U + (u + 1))
                    pool.tensor_tensor(hrstd[u][:, :], hvar[u][:, :], minus_half[:, :], ALU.pow)\
                        .then_inc(s["hrstd_ready"], 1)

        @block.vector
        def _(dve):
            once = Chain(dve, s["rows_step"])
            for tile in v:
                for u in range(U):
                    once.link(dve.memset(tile[u][:, :, :], 0.0))
                    dve.memset(tile[u][:, :, HD:HD + 1], 1.0)
            dve.wait_ge(s["loaded"], 16 * n_loads)
            if heads_norm:
                for u in range(U):
                    dve.memset(padded[u][:, :, :, :, :], 0.0)
                dve.memset(minus_half[:, :], -0.5)
                dve.tensor_copy(ident_b[:, :], stage_f[:, 0:P])
                once.link(dve.tensor_copy(causal_b[:, :, :].rearrange("p a b -> p (a b)"), stage_f[:, P:5 * P]))
            if context == "only":
                once.link(dve.tensor_tensor(keep_less_fill[:, :], row_c[:, 0:1], row_c[:, 1:2], ALU.subtract))
                once.link(dve.tensor_copy(rows[:, :, :], mask_raw[:, :, :]))
                once.link(dve.tensor_scalar(rows[:, :, :], rows[:, :, :], keep_less_fill[:, :], row_c[:, 1:2],
                                            ALU.mult, ALU.add))
            if context == "past":
                pos = row_c[:, 2:2 + SC]
                once.link(dve.tensor_copy(len_f[:, :], len_raw[:, :]))
                once.link(dve.tensor_reduce(len_max[:, :], len_f[:, :], AX.X, ALU.max))
                once.link(dve.tensor_scalar(beyond[:, :], pos, len_max[:, :], row_c[:, 1:2], ALU.is_ge, ALU.mult))
                once.link(dve.tensor_tensor(rows[:, :, :], spread(pos, 1, batch), spread(len_f[:, :], 2, SC), ALU.is_lt))
                once.link(dve.tensor_scalar(rows[:, :, :], rows[:, :, :], row_c[:, 0:1], None, ALU.mult))
                once.link(dve.tensor_tensor(rows[:, :, :], rows[:, :, :], spread(beyond[:, :], 1, batch), ALU.add))
            dve.sem_inc(s["rows_ready"], 1)
            dve.drain().then_inc(s["consts"], 1)

            def shift(chain, b, c, u):
                dve.wait_ge(s["scores_done"], count(b, NCH, c + 1))
                S = scores[u][:, c % 2, 0:CHUNK * NK].rearrange("p (h k) -> p h k", h=CHUNK)
                tp = top[u][:, c * CHUNK:(c + 1) * CHUNK]
                dst = probs[c % 2][u][:, :, :]
                if latent:
                    chain.link(dve.tensor_scalar(dst, S, -1e4, 1e4, ALU.max, ALU.min))
                    chain.link(dve.tensor_tensor(dst, dst, spread(w["decay"][:, :], 1, CHUNK), ALU.mult))
                    S = dst
                chain.link(dve.tensor_reduce(tp, S, AX.X, ALU.max))
                dve.tensor_tensor(dst, S, spread(tp, 2, NK), ALU.subtract).then_inc(s["shifted"], 1)

            def finish(chain, b, u):
                dve.wait_ge(s["back_done"], count(b))
                acc = misc[u][:, :].rearrange("p (g r f) -> p g r f", g=GROUPS, f=SLOT)
                by_group = rz[u][:, :].rearrange("p (g r) -> p g r", g=GROUPS)
                chain.link(dve.reciprocal(by_group, acc[:, :, :, HD]))
                dve.tensor_tensor(o[u][:, :].rearrange("p (r g f) -> p g r f", g=GROUPS, f=HD), acc[:, :, :, 0:HD],
                                  spread(by_group, 3, HD), ALU.mult).then_inc(s["o_ready"], 1)

            def head_norm(chain, b, u):
                acc = scores[u][:, 0, 0:2 * P].rearrange("p (a h f) -> p a h f", a=2, h=HEADS)
                hs = hstat[u][:, :].rearrange("p (a h) -> p a h", a=2)
                dve.wait_ge(s["proj_done"], count(b))
                chain.link(dve.tensor_reduce(hs, acc, AX.X, ALU.add))
                chain.link(dve.tensor_scalar(hstat[u][:, :], hstat[u][:, :], 1.0 / HD, None, ALU.mult))
                chain.link(dve.tensor_tensor(qk[u][:, :, :, :], acc, spread(hs, 3, HD), ALU.subtract))
                chain.link(dve.tensor_tensor(sq[u][:, :, :, :], qk[u][:, :, :, :], qk[u][:, :, :, :], ALU.mult))
                chain.link(dve.tensor_reduce(hs, sq[u][:, :, :, :], AX.X, ALU.add))
                dve.tensor_scalar(hvar[u][:, :], hstat[u][:, :], 1.0 / HD, LN_EPS, ALU.mult, ALU.add)\
                   .then_inc(s["var_ready"], 1)

            def rotate(chain, b, u):
                flat = qk[u][:, :, :, :].rearrange("p a h f -> p (a h) f")
                gb = W("gb")[:, :].rearrange("p (s a f) -> p s a f", s=2, a=2)
                dve.wait_ge(s["hrstd_ready"], count(b))
                chain.link(dve.tensor_tensor(flat, flat, spread(hrstd[u][:, :], 2, HD), ALU.mult))
                for a in range(2):
                    chain.link(dve.tensor_tensor(qk[u][:, a, :, :], qk[u][:, a, :, :],
                                                 spread(gb[:, 0, a, :], 1, HEADS), ALU.mult))
                    chain.link(dve.tensor_tensor(qk[u][:, a, :, :], qk[u][:, a, :, :],
                                                 spread(gb[:, 1, a, :], 1, HEADS), ALU.add))
                cos, sin = w["rope"][:, 0:HD], w["rope"][:, HD:2 * HD]
                r = rot[u][:, :, :, :].rearrange("p a h f -> p (a h) f")
                dve.tensor_tensor(r[:, :, 0:HD // 2], flat[:, :, 1:HD:2], spread(sin[:, 0:HD // 2], 1, 2 * HEADS), ALU.mult)
                dve.tensor_tensor(r[:, :, HD // 2:HD], flat[:, :, 0:HD:2], spread(sin[:, HD // 2:HD], 1, 2 * HEADS), ALU.mult)
                chain.link(dve.tensor_tensor(sq[u][:, :, :, :].rearrange("p a h f -> p (a h) f"), flat,
                                             spread(cos, 1, 2 * HEADS), ALU.mult))
                for a in range(2):
                    last = dve.tensor_tensor(padded[u][:, a, :, :, 0:HD].rearrange("p g r f -> p r g f"),
                                             sq[u][:, a, :, :].rearrange("p (r g) f -> p r g f", g=GROUPS),
                                             rot[u][:, a, :, :].rearrange("p (r g) f -> p r g f", g=GROUPS), ALU.add)
                last.then_inc(s["padded_ready"], 1)

            def residual(chain, b, u):
                dve.wait_ge(s["y_done"], count(b))
                n = number(b)
                chain.link(dve.tensor_tensor(core.x[:, n, :], core.x[:, n, :], misc[u][:, B2], ALU.add))
                take_stats(dve, chain, core, n, bn[u], mv[u]).then_inc(s["y_added"], 1)

            def mask_context(b, u):
                dve.wait_ge(s["mask_done"], count(b))
                dve.tensor_tensor(ctxm[u][:, :], scores[u][:, 1, 0:SC], core.ctxT[:, number(b), :], ALU.mult)\
                   .then_inc(s["ctxm_ready"], 1)

            def copy_q(b, u):
                dve.wait_ge(s["q_done"], count(b))
                acc = scores[u][:, 0, :].rearrange("p (g t) -> p g t", g=GROUPS)
                if context:
                    last = dve.tensor_tensor(qT[u][:, :, :], acc, spread(W("b_q")[:, :], 2, P), ALU.add)
                elif latent:
                    last = dve.tensor_scalar(qT[u][:, :, :], acc, 1.0 / (float(np.sqrt(np.float32(P))) + 1e-8), None,
                                             ALU.mult)
                else:
                    last = dve.tensor_copy(qT[u][:, :, :], acc)
                last.then_inc(s["q_ready"], 1)

            def front(chain, b, u, step):
                if step == 0 and context:
                    mask_context(b, u)
                if step == 0 and heads_norm:
                    head_norm(chain, b, u)
                if step == 1 and not heads_norm:
                    copy_q(b, u)
                if step == 3 and heads_norm:
                    rotate(chain, b, u)

            def attend(chain, b, u, tail=True, start_next=True):
                before, behind, other = neighbour(b, -1), neighbour(b, 1), 1 - u
                for c in range(NCH):
                    shift(chain, b, c, u)
                    if tail and step_of(c) == 1:
                        finish(chain, before, other)
                    if start_next:
                        front(chain, behind, other, step_of(c))
                    if tail and step_of(c) == 3:
                        residual(chain, before, other)
                if start_next and heads_norm:
                    copy_q(behind, other)

            once = Chain(dve, s["first_step"])
            for step in range(4):
                front(once, (None, 0), 0, step)
            if heads_norm:
                copy_q((None, 0), 0)
            attend(once, (None, 0), 0, tail=False)
            per_sequence = (11 if heads_norm else 0) + (3 if latent else 1) * NCH + 1 + 3
            with dve.Fori(0, batch // U - 1) as i:
                chain = Chain(dve, s["vec_step"], i, per_sequence * U)
                attend(chain, (i, 1), 1)
                attend(chain, (i, 2), 0)
                chain.close()
            once = Chain(dve, s["last_step"])
            attend(once, (None, batch - 1), 1, start_next=False)
            finish(once, (None, batch - 1), 1)
            residual(once, (None, batch - 1), 1)

        @block.scalar
        def _(act):
            act.wait_ge(s["consts"], 1)

            def begin(b, u):
                n = number(b)
                act.activation(xn[u][:, :], core.x[:, n, :], ACT.Identity, bias=core.nmr[:, n, :],
                               scale=core.rstd[:, n, :]).then_inc(s["xn_ready"], 1)
                if context:
                    act.activation(ctxu[u][:, :], core.ctxT[:, n, :], ACT.Copy).then_inc(s["ctxu_ready"], 1)
                act.wait_ge(s["xt_done"], count(b))
                act.activation(xT[u][:, :], scores[u][:, 0, A], ACT.Copy).then_inc(s["xt_ready"], 1)

            def copy_k(b, u):
                act.wait_ge(s["k_done"], count(b))
                act.activation(kT[u][:, :, NK - P:NK], scores[u][:, 1, :].rearrange("p (g t) -> p g t", g=GROUPS),
                               ACT.Copy).then_inc(s["k_ready"], 1)

            def copy_v(b, u, src):
                act.wait_ge(s["v_done"], count(b))
                act.activation(v[-1][u][:, :, 0:HD], src.rearrange("p (h f) -> p h f", h=HEADS), ACT.Copy)\
                   .then_inc(s["v_ready"], 1)

            def front(b, u, step):
                if heads_norm and step == 0:
                    copy_v(b, u, scores[u][:, 1, 0:P])
                if heads_norm and step == 3:
                    copy_k(b, u)
                if latent and step == 0:
                    act.wait_ge(s["kv_done"], count(b))
                    act.activation(kvT[u][:, :], scores[u][:, 1, 0:P], ACT.Copy).then_inc(s["kv_ready"], 1)
                if latent and step == 1:
                    act.wait_ge(s["lat_done"], count(b))
                    act.activation(latT[u][:, :], scores[u][0:SLOT, 1, P:2 * P], ACT.Copy).then_inc(s["lat_ready"], 1)
                if own and not heads_norm and step == (2 if latent else 1):
                    copy_k(b, u)
                if context and step == 2:
                    act.wait_ge(s["kc_done"], count(b))
                    act.activation(kT[u][:, :, 0:SC], misc[u][:, 0:GROUPS * SC].rearrange("p (g t) -> p g t", g=GROUPS),
                                   ACT.Copy).then_inc(s["kc_ready"], 1)
                if own and not heads_norm and step == 2:
                    copy_v(b, u, misc[u][:, B2])
                if context and step == 3:
                    act.wait_ge(s["vc_done"], count(b))
                    act.activation(v[0][u][:, :, 0:HD], scores[u][0:SC, 1, 0:P].rearrange("p (h f) -> p h f", h=HEADS),
                                   ACT.Copy).then_inc(s["vc_ready"], 1)

            def copy_acc(b, u):
                act.wait_ge(s["pv_done"], count(b, NCH, NCH))
                act.activation(accT[u][:, :, :], misc[u][:, :].rearrange("p (g t) -> p g t", g=GROUPS), ACT.Copy)\
                   .then_inc(s["acc_ready"], 1)

            def tail(b, u):
                act.wait_ge(s["ot_done"], count(b))
                act.activation(oT[u][:, :], misc[u][:, A], ACT.Copy).then_inc(s["ot_ready"], 1)

            def exps(b, c, u):
                act.wait_ge(s["shifted"], count(b, NCH, c + 1))
                act.activation(probs[c % 2][u][:, :, :], probs[c % 2][u][:, :, :], ACT.Exp, scale=scale)\
                   .then_inc(s["probs_ready"], 1)

            def copies(b, c, u):
                act.wait_ge(s["pt_done"], count(b, NCH, c + 1))
                src, dst = ptp[c % 2], pT[c % 2][u]
                if len(key_tiles) == 1:
                    m = key_tiles[0][0]
                    act.activation(dst[0:m, :, :], src[0:m, :, :], ACT.Copy).then_inc(s["pt_copied"], 1)
                else:
                    act.activation(dst[0:SC, 0:4:2, :], src[0:SC, 0:4:2, :], ACT.Copy)
                    act.activation(dst[:, 1:4:2, :], src[:, 1:4:2, :], ACT.Copy).then_inc(s["pt_copied"], 1)

            def attend(b, u, with_tail=True, start_next=True):
                if with_tail:
                    copy_acc(neighbour(b, -1), 1 - u)
                if start_next:
                    begin(neighbour(b, 1), 1 - u)
                for c in range(NCH):
                    exps(b, c, u)
                    if c:
                        copies(b, c - 1, u)
                    if with_tail and step_of(c) == 2:
                        tail(neighbour(b, -1), 1 - u)
                    if start_next and step_of(c) in (0, 1):
                        front(neighbour(b, 1), 1 - u, step_of(c))
                copies(b, NCH - 1, u)
                if start_next:
                    front(neighbour(b, 1), 1 - u, 2)
                    front(neighbour(b, 1), 1 - u, 3)

            begin((None, 0), 0)
            for step in range(4):
                front((None, 0), 0, step)
            attend((None, 0), 0, with_tail=False)
            with act.Fori(0, batch // U - 1) as i:
                attend((i, 1), 1)
                attend((i, 2), 0)
            attend((None, batch - 1), 1, start_next=False)
            copy_acc((None, batch - 1), 1)
            tail((None, batch - 1), 1)

        @block.tensor
        def _(pe):
            pe.wait_ge(s["consts"], 1)

            def mm(out, lhsT, rhs, start=True, stop=True, skip=False):
                return pe.matmul(out, lhsT, rhs, start=start, stop=stop, skip_group_check=skip)

            def begin(b, u):
                pe.wait_ge(s["xn_ready"], count(b))
                pe.transpose(scores[u][:, 0, A], xn[u][:, :], core.ident[:, :]).then_inc(s["xt_done"], 1)
                if context:
                    mm(scores[u][:, 1, 0:SC], core.ones[0:1, :], rows[0:1, number(b), :]).then_inc(s["mask_done"], 1)

            def front_0(b, u):
                pe.wait_ge(s["xt_ready"], count(b))
                if heads_norm:
                    mm(scores[u][:, 0, 0:2 * P], xT[u][:, :], W("w_qkv")[:, 0:2 * P]).then_inc(s["proj_done"], 1)
                    mm(scores[u][:, 1, 0:P], xT[u][:, :], W("w_qkv")[:, 2 * P:3 * P]).then_inc(s["v_done"], 1)
                    return
                if latent:
                    mm(scores[u][:, 1, 0:P], W("w_kv")[:, 0:P], xT[u][:, :], stop=False)
                    mm(scores[u][:, 1, 0:P], W("w_kv")[:, P:2 * P], xT[u][:, :], start=False).then_inc(s["kv_done"], 1)
                for g in range(GROUPS):
                    last = mm(scores[u][:, 0, g * P:(g + 1) * P], W("w_q")[:, g * P:(g + 1) * P], xT[u][:, :])
                last.then_inc(s["q_done"], 1)
                if context:
                    pe.wait_ge(s["ctxm_ready"], count(b))
                if own and not latent:
                    for g in range(GROUPS):
                        last = mm(scores[u][:, 1, g * P:(g + 1) * P], W("w_k")[:, g * P:(g + 1) * P], xT[u][:, :])
                    last.then_inc(s["k_done"], 1)

            def front_1(b, u):
                if latent:
                    pe.wait_ge(s["kv_ready"], count(b))
                    mm(scores[u][0:SLOT, 1, P:2 * P], W("w_down")[:, :], kvT[u][:, :]).then_inc(s["lat_done"], 1)

            def front_2(b, u):
                if latent:
                    pe.wait_ge(s["lat_ready"], count(b))
                    for g in range(GROUPS):
                        last = mm(scores[u][:, 1, g * P:(g + 1) * P], W("w_k")[:, g * P:(g + 1) * P], latT[u][:, :])
                    last.then_inc(s["k_done"], 1)
                    mm(misc[u][:, B2], latT[u][:, :], W("w_up_v")[:, :]).then_inc(s["v_done"], 1)
                if context:
                    if own:
                        mm(misc[u][:, B2], xT[u][:, :], W("w_v")[:, :]).then_inc(s["v_done"], 1)
                    for g in range(GROUPS):
                        out = misc[u][:, g * SC:(g + 1) * SC]
                        mm(out, W("w_kc")[:, g * P:(g + 1) * P], ctxm[u][:, :], stop=False)
                        last = mm(out, W("aux")[:, g * P:(g + 1) * P], rows[:, number(b), :], start=False)
                    last.then_inc(s["kc_done"], 1)

            def front_3(b, u):
                if context:
                    pe.wait_ge(s["k_ready" if own else "q_ready"], count(b))
                    src = ctxm[u] if own else ctxu[u]
                    if not own:
                        pe.wait_ge(s["ctxu_ready"], count(b))
                    out = scores[u][0:SC, 1, 0:P]
                    last = mm(out, src[:, :], W("w_vc")[:, :], stop=own)
                    if not own:
                        last = mm(out, core.ones[0:1, 0:SC], W("b_v")[0:1, :], start=False)
                    last.then_inc(s["vc_done"], 1)
                if heads_norm:
                    pe.wait_ge(s["padded_ready"], count(b))
                    pe.wait_ge(s["v_ready"], count(b))
                    for a, sem in ((0, "q_done"), (1, "k_done")):
                        for g in range(GROUPS):
                            last = pe.transpose(scores[u][:, a, g * P:(g + 1) * P],
                                                padded[u][:, a, g, :, :].rearrange("p h f -> p (h f)"), core.ident[:, :])
                        last.then_inc(s[sem], 1)

            def tail_back(b, u):
                pe.wait_ge(s["acc_ready"], count(b))
                for g in range(GROUPS):
                    last = pe.transpose(misc[u][:, g * P:(g + 1) * P], accT[u][:, g, :], core.ident[:, :])
                last.then_inc(s["back_done"], 1)

            def tail_turn(b, u):
                pe.wait_ge(s["o_ready"], count(b))
                pe.transpose(misc[u][:, A], o[u][:, :], core.ident[:, :]).then_inc(s["ot_done"], 1)

            def tail_project(b, u):
                pe.wait_ge(s["ot_ready"], count(b))
                last = mm(misc[u][:, B2], oT[u][:, :], W("w_o")[:, :], stop=latent)
                if not latent:
                    last = mm(misc[u][:, B2], core.ones[0:1, :], W("b_o")[0:1, :], start=False)
                last.then_inc(s["y_done"], 1)

            def scoring(b, c, u):
                if c == 0:
                    pe.wait_ge(s["q_ready"], count(b))
                    if own:
                        pe.wait_ge(s["k_ready"], count(b))
                        if not heads_norm:
                            pe.wait_ge(s["v_ready"], count(b))
                    if context:
                        pe.wait_ge(s["kc_ready"], count(b))
                        pe.wait_ge(s["vc_ready"], count(b))
                if c >= 2:
                    pe.wait_ge(s["shifted"], count(b, NCH, c - 1))
                if heads_norm:
                    mm(scores[u][:, c % 2, :], ident_b[:, :], causal_b[:, :, :].rearrange("p a b -> p (a b)"),
                       stop=False, skip=True)
                for j in range(CHUNK):
                    r, g = divmod(head_of(c, j), GROUPS)
                    at = r * SLOT
                    last = mm(scores[u][:, c % 2, j * NK:(j + 1) * NK], qT[u][at:at + K, g, :], kT[u][at:at + K, g, :],
                              start=not heads_norm, skip=heads_norm)
                last.then_inc(s["scores_done"], 1)

            def turn(b, c, u):
                pe.wait_ge(s["probs_ready"], count(b, NCH, c + 1))
                for at, (h, t) in enumerate(blocks):
                    k0 = sum(key_tiles[x][0] for x in range(t))
                    nk = key_tiles[t][0]
                    last = pe.transpose(ptp[c % 2][0:nk, at, :], probs[c % 2][u][:, h, k0:k0 + nk], core.ident[:, :])
                last.then_inc(s["pt_done"], 1)

            def weigh(b, c, u):
                pe.wait_ge(s["pt_copied"], count(b, NCH, c + 1))
                for at, (h, t) in enumerate(blocks):
                    hh = head_of(c, h)
                    r, g = divmod(hh, GROUPS)
                    nk = key_tiles[t][0]
                    last = mm(misc[u][r * SLOT:(r + 1) * SLOT, g * P:(g + 1) * P], v[t][u][:, hh, :],
                              pT[c % 2][u][0:nk, at, :], start=t == 0, stop=t == len(key_tiles) - 1)
                last.then_inc(s["pv_done"], 1)

            def beside(b, u, step, tail, start_next):
                before, behind = neighbour(b, -1), neighbour(b, 1)
                if step == 0:
                    if start_next:
                        front_0(behind, u)
                    if tail:
                        tail_back(before, u)
                if step == 1 and start_next:
                    front_1(behind, u)
                if step == 2 and tail:
                    tail_turn(before, u)
                if step == 3 and tail:
                    tail_project(before, u)

            def attend(b, u, tail=True, start_next=True):
                scoring(b, 0, u)
                if start_next:
                    begin(neighbour(b, 1), 1 - u)
                for c in range(NCH):
                    if c + 1 < NCH:
                        scoring(b, c + 1, u)
                    beside(b, 1 - u, step_of(c), tail, start_next)
                    turn(b, c, u)
                    if c:
                        weigh(b, c - 1, u)
                if start_next and heads_norm:
                    front_3(neighbour(b, 1), 1 - u)
                if start_next and tail:
                    pe.wait_ge(s["y_added"], count(neighbour(b, -1)))
                if start_next and not heads_norm:
                    front_2(neighbour(b, 1), 1 - u)
                    front_3(neighbour(b, 1), 1 - u)
                weigh(b, NCH - 1, u)

            begin((None, 0), 0)
            for front in (front_0, front_1, front_2, front_3):
                front((None, 0), 0)
            attend((None, 0), 0, tail=False)
            with pe.Fori(0, batch // U - 1) as i:
                attend((i, 1), 1)
                attend((i, 2), 0)
            attend((None, batch - 1), 1, start_next=False)
            tail_back((None, batch - 1), 1)
            tail_turn((None, batch - 1), 1)
            tail_project((None, batch - 1), 1)


TILE = 4


def mlp_stage(nc, core, dram, tag, kind):
    batch, T, NT = core.batch, TILE, TILE * P
    gated = kind != "plain"
    NCHK = dram[tag + "_w_d"].shape[1]
    E, EG = 32, 4
    NW = E + (16 if kind == "moe3" else 0)
    routed = [k for k in range(NCHK) if gated and k != NCHK - 1]
    with ExitStack() as ctx:
        st = Stage(nc, ctx, tag)
        s = {n: st.sem(n) for n in (
            "loaded", "consts", "once_step", "first_step", "last_step", "xn_ready", "xt_done", "xt_ready", "up_done", "act_ready",
            "hidden_ready", "down_done", "y_done", "y_read", "vec_step", "spread_done",
            "logits_done", "logits_ready", "clamped", "exp_ready", "route_ready", "rt_done", "rt_ready")}
        if gated:
            names = ["w_g", "w_u", "w_d", "w_r", "b_r", "pick"]
        else:
            names = ["w_g", "w_d", "b_g", "b_d", "ln_g", "ln_b"]
        w = {n: st.sb(n, list(dram[f"{tag}_{n}"].shape)) for n in names}
        if not gated:
            raw = {n: st.sb("raw_" + n, list(dram[f"{tag}_q_{n}"].shape), I32) for n in ("w_g", "w_d")}
            xres = [st.sb(f"xres{p}", [P, T, P]) for p in range(2)]
            hb = st.sb("half_bias", [P, NCHK])
        xn = st.sb("xn", [P, T, P])
        xT = [st.sb(f"xT{p}", [P, NT]) for p in range(2)]
        act_t = [st.sb(f"act{j}", [P, NT]) for j in range(2)]
        hid = [st.sb(f"hid{j}", [P, NT]) for j in range(2)] if gated else act_t
        bn, mv = st.sb("bn", [P, 6]), st.sb("mv", [P, 2])
        gp = [st.ps(f"g{j}", [P, NT]) for j in range(2)]
        up = [st.ps(f"u{j}", [P, NT]) for j in range(2)] if gated else None
        wb = [st.ps(f"wb{j}", [P, NT]) for j in range(2)] if gated else None
        yp = st.ps("y", [P, T, P])
        misc = st.ps("misc", [P, NT])
        if gated:
            sig = st.sb("sig", [P, T, E])
            choice = st.sb("choice", [P, T, EG, E // EG])
            best = st.sb("best", [P, T, EG, 8])
            gs = st.sb("gs", [P, T, EG])
            gt = st.sb("gt", [P, T, EG, EG])
            eq = st.sb("eq", [P, T, EG, EG])
            keep = st.sb("keep", [P, T, EG])
            top8 = st.sb("top8", [P, T, 8])
            first8 = st.sb("first8", [P, T, 8])
            marked = st.sb("marked", [P, T, E])
            tot = st.sb("tot", [P, T])
            route = st.sb("route", [P, T, P])
            rT = [st.sb(f"rT{p}", [NW, NT]) for p in range(2)]
            lower = st.sb("lower", [P, EG, EG])
        n_loads = 16 * (len(names) + (0 if gated else 2) + (1 if gated else 0))
        block = ctx.enter_context(nc.Block())
        tiles = batch // T

        def count(m, per=1, extra=1):
            i, at = m
            return at * per + extra if i is None else i * (2 * per) + (at * per + extra)

        def neighbour(m, d):
            return (m[0], m[1] + d)

        def is_first(m):
            return m[0] is None and m[1] == 0

        def buffer_of(m, k):
            return (m[1] * NCHK + k) % 2

        X_TURN, LOGITS, EXP, ROUTE, R_TURN = (1, 2, 3, 4, 12) if gated else (2, None, None, None, None)

        @block.sync
        def _(sp):
            for n in names:
                sp.dma_start(w[n][tuple(slice(None) for _ in w[n].shape)], dram[f"{tag}_{n}"]).then_inc(s["loaded"], 16)
            if gated:
                sp.dma_start(lower[:, :, :], dram["lower"]).then_inc(s["loaded"], 16)
            else:
                for n in raw:
                    sp.dma_start(raw[n][tuple(slice(None) for _ in raw[n].shape)], dram[f"{tag}_q_{n}"])\
                      .then_inc(s["loaded"], 16)
            sp.wait_ge(s["loaded"], n_loads)

        @block.vector
        def _(dve):
            dve.wait_ge(s["loaded"], n_loads)
            once = Chain(dve, s["once_step"])
            if gated:
                once.link(dve.memset(route[:, :, :], 0.0))
                once.link(dve.memset(first8[:, :, :], -1e30))
            else:
                for n in raw:
                    dst = w[n][tuple(slice(None) for _ in w[n].shape)]
                    src = raw[n][tuple(slice(None) for _ in raw[n].shape)]
                    once.link(dve.scalar_tensor_tensor(dst, src, -128.0, dst, ALU.add, ALU.mult))
            dve.sem_inc(s["consts"], 1)

            def beat():
                dve.memset(core.beat[:, :], 0.0)

            flat = choice[:, :, :, :].rearrange("p t g e -> p t (g e)") if gated else None

            def route_tokens(chain, m, part):
                if part == 0:
                    dve.wait_ge(s["logits_ready"], count(m))
                    dve.tensor_scalar(sig[:, :, :], sig[:, :, :], -1.0, 88.0, ALU.mult, ALU.min).then_inc(s["clamped"], 1)
                if part == 1:
                    dve.wait_ge(s["exp_ready"], count(m))
                    chain.link(dve.tensor_scalar(sig[:, :, :], sig[:, :, :], 1.0, None, ALU.add))
                    chain.link(dve.reciprocal(sig[:, :, :], sig[:, :, :]))
                    chain.link(dve.tensor_tensor(flat, sig[:, :, :], spread(w["b_r"][:, :], 1, T), ALU.add))
                if part == 2:
                    beat()
                    for t in range(T):
                        for g in range(EG):
                            last = dve.max(best[:, t, g, :], choice[:, t, g, :])
                    chain.link(last)
                if part == 3:
                    chain.link(dve.tensor_tensor(gs[:, :, :], best[:, :, :, 0], best[:, :, :, 1], ALU.add))
                    for t in range(T):
                        ahead, behind = spread(gs[:, t, :], 1, EG), spread(gs[:, t, :], 2, EG)
                        dve.tensor_tensor(gt[:, t, :, :], ahead, behind, ALU.is_gt)
                        last = dve.tensor_tensor(eq[:, t, :, :], ahead, behind, ALU.is_equal)
                    chain.link(last)
                    chain.link(dve.tensor_tensor(eq[:, :, :, :], eq[:, :, :, :], spread(lower[:, :, :], 1, T), ALU.mult))
                    chain.link(dve.tensor_tensor(gt[:, :, :, :], gt[:, :, :, :], eq[:, :, :, :], ALU.add))
                    chain.link(dve.tensor_reduce(keep[:, :, :], gt[:, :, :, :], AX.X, ALU.add))
                    chain.link(dve.tensor_scalar(keep[:, :, :], keep[:, :, :], 2.0, None, ALU.is_lt))
                    chain.link(dve.tensor_tensor(choice[:, :, :, :], choice[:, :, :, :], spread(keep[:, :, :], 3, E // EG), ALU.mult))
                    if kind == "moe3":
                        chain.link(dve.tensor_scalar(keep[:, :, :], keep[:, :, :], -1.0, 1e30, ALU.add, ALU.mult))
                        chain.link(dve.tensor_tensor(choice[:, :, :, :], choice[:, :, :, :],
                                                     spread(keep[:, :, :], 3, E // EG), ALU.add))
                if part == 4:
                    beat()
                    for t in range(T):
                        last = dve.max(top8[:, t, :], flat[:, t, :])
                    chain.link(last)
                    if kind == "moe3":
                        chain.link(dve.tensor_copy(first8[:, :, 0:1], top8[:, :, 0:1]))
                        chain.link(dve.memset(top8[:, :, 6:8], -1e30))
                        beat()
                        for t in range(T):
                            last = dve.match_replace(marked[:, t, :], first8[:, t, :], flat[:, t, :], 1e30)
                        chain.link(last)
                        chain.link(dve.tensor_scalar(marked[:, :, :], marked[:, :, :], 1e30, None, ALU.is_equal))
                        chain.link(dve.scalar_tensor_tensor(marked[:, :, :], flat, -1e29, marked[:, :, :], ALU.is_gt, ALU.mult))
                        chain.link(dve.tensor_tensor(route[:, :, E:NW], marked[:, :, 0:E:2], marked[:, :, 1:E:2], ALU.add))
                        chain.link(dve.tensor_scalar(route[:, :, E:NW], route[:, :, E:NW], 0.1, None, ALU.mult))
                if part == 5:
                    beat()
                    for t in range(T):
                        last = dve.match_replace(marked[:, t, :], top8[:, t, :], flat[:, t, :], 1e30)
                    chain.link(last)
                    chain.link(dve.tensor_scalar(marked[:, :, :], marked[:, :, :], 1e30, None, ALU.is_equal))
                    if kind == "moe3":
                        chain.link(dve.scalar_tensor_tensor(marked[:, :, :], flat, -1e29, marked[:, :, :], ALU.is_gt, ALU.mult))
                if part == 6:
                    chain.link(dve.tensor_tensor(marked[:, :, :], marked[:, :, :], sig[:, :, :], ALU.mult))
                    chain.link(dve.tensor_reduce(tot[:, :], marked[:, :, :], AX.X, ALU.add))
                    chain.link(dve.tensor_scalar(tot[:, :], tot[:, :], 1e-20, None, ALU.add))
                    chain.link(dve.reciprocal(tot[:, :], tot[:, :]))
                    chain.link(dve.tensor_scalar(tot[:, :], tot[:, :], 2.5 if kind == "moe0" else 0.2, None, ALU.mult))
                    dve.tensor_tensor(route[:, :, 0:E], marked[:, :, :], spread(tot[:, :], 2, E), ALU.mult)\
                       .then_inc(s["route_ready"], 1)

            def hidden(chain, m, k):
                j = buffer_of(m, k)
                dve.wait_ge(s["act_ready"], count(m, NCHK, k + 1))
                if k >= 2 or not is_first(m):
                    dve.wait_ge(s["down_done"], count(m, NCHK, k - 1))
                if k in routed:
                    chain.link(dve.tensor_tensor(hid[j][:, :], act_t[j][:, :], up[j][:, :], ALU.mult))
                    dve.wait_ge(s["spread_done"], count(m, len(routed), k + 1))
                    dve.tensor_tensor(hid[j][:, :], hid[j][:, :], wb[j][:, :], ALU.mult).then_inc(s["hidden_ready"], 1)
                else:
                    dve.tensor_tensor(hid[j][:, :], act_t[j][:, :], up[j][:, :], ALU.mult).then_inc(s["hidden_ready"], 1)

            def residual(chain, m):
                x = core.x[:, :, :].rearrange("p (i t) f -> p i t f", t=T)[:, count(m, 1, 0), :, :]
                if gated:
                    dve.wait_ge(s["down_done"], count(m, NCHK, NCHK))
                    chain.link(dve.tensor_tensor(x, x, yp[:, :, :], ALU.add))
                else:
                    dve.wait_ge(s["y_done"], count(m))
                    chain.link(dve.tensor_tensor(x, x, xres[m[1] % 2][:, :, :], ALU.add))
                    chain.link(dve.scalar_tensor_tensor(x, yp[:, :, :], 0.5, x, ALU.mult, ALU.add))
                dve.sem_inc(s["y_read"], 1)

            def statistics(chain, m, t):
                chain.link(take_stats(dve, chain, core, count(m, T, t), bn, mv))

            def experts(chain, m, before=True, behind=True):
                for k in range(NCHK):
                    if gated:
                        hidden(chain, m, k)
                    if k == 0 and before:
                        residual(chain, neighbour(m, -1))
                    if k < T and before:
                        statistics(chain, neighbour(m, -1), k)
                    if gated and behind and k == LOGITS:
                        route_tokens(chain, neighbour(m, 1), 0)
                    if gated and behind and ROUTE <= k < ROUTE + 6:
                        route_tokens(chain, neighbour(m, 1), 1 + k - ROUTE)

            once = Chain(dve, s["first_step"])
            if gated:
                for part in range(7):
                    route_tokens(once, (None, 0), part)
            experts(once, (None, 0), before=False)
            per = ((29 if kind == "moe3" else 19) + len(routed) + 1 if gated else 2) + 3 * T
            with dve.Fori(0, tiles // 2 - 1) as i:
                chain = Chain(dve, s["vec_step"], i, 2 * per)
                experts(chain, (i, 1))
                experts(chain, (i, 2))
                chain.close()
            once = Chain(dve, s["last_step"])
            experts(once, (None, tiles - 1), behind=False)
            residual(once, (None, tiles - 1))
            for t in range(T):
                statistics(once, (None, tiles - 1), t)

        @block.scalar
        def _(act):
            act.wait_ge(s["consts"], 1)

            def normalise(m):
                if not gated and m[1] >= 2:
                    act.wait_ge(s["y_read"], count(m, 1, -1))
                for t in range(T):
                    b = count(m, T, t)
                    if not gated:
                        act.activation(xres[m[1] % 2][:, t, :], core.x[:, b, :], ACT.Identity, bias=core.nmr[:, b, :],
                                       scale=core.rstd[:, b, :])
                        last = act.activation(xn[:, t, :], core.x[:, b, :], ACT.Identity, bias=core.nmr2[:, b, :],
                                              scale=core.rstd2[:, b, :])
                    else:
                        last = act.activation(xn[:, t, :], core.x[:, b, :], ACT.Identity, bias=core.nmr[:, b, :],
                                              scale=core.rstd[:, b, :])
                last.then_inc(s["xn_ready"], 1)

            def prepare(m, k):
                if k == 0:
                    normalise(m)
                if k == X_TURN:
                    act.wait_ge(s["xt_done"], count(m))
                    if gated:
                        act.activation(xT[m[1] % 2][:, :], misc[:, :], ACT.Copy).then_inc(s["xt_ready"], 1)
                    else:
                        act.activation(xT[m[1] % 2][:, :], misc[:, :], ACT.Identity, bias=w["ln_b"][:, :],
                                       scale=w["ln_g"][:, :]).then_inc(s["xt_ready"], 1)
                if k == LOGITS:
                    act.wait_ge(s["logits_done"], count(m))
                    act.activation(sig[:, :, :], misc[:, 0:T * E].rearrange("p (t e) -> p t e", t=T), ACT.Copy)\
                       .then_inc(s["logits_ready"], 1)
                if k == EXP:
                    act.wait_ge(s["clamped"], count(m))
                    act.activation(sig[:, :, :], sig[:, :, :], ACT.Exp).then_inc(s["exp_ready"], 1)
                if k == R_TURN:
                    act.wait_ge(s["rt_done"], count(m))
                    act.activation(rT[m[1] % 2][:, :], misc[0:NW, :], ACT.Copy).then_inc(s["rt_ready"], 1)

            def experts(m, behind=True):
                for k in range(NCHK):
                    j = buffer_of(m, k)
                    act.wait_ge(s["up_done"], count(m, NCHK, k + 1))
                    if k >= 2 or not is_first(m):
                        act.wait_ge(s["hidden_ready" if gated else "down_done"], count(m, NCHK, k - 1))
                    if gated:
                        act.activation(act_t[j][:, :], gp[j][:, :], ACT.Silu).then_inc(s["act_ready"], 1)
                    else:
                        act.activation(act_t[j][:, :], gp[j][:, :], ACT.Silu, bias=w["b_g"][:, k:k + 1])\
                           .then_inc(s["act_ready"], 1)
                    if behind:
                        prepare(neighbour(m, 1), k)

            for k in range(NCHK):
                prepare((None, 0), k)
            experts((None, 0))
            with act.Fori(0, tiles // 2 - 1) as i:
                experts((i, 1))
                experts((i, 2))
            experts((None, tiles - 1), behind=False)

        @block.tensor
        def _(pe):
            pe.wait_ge(s["consts"], 1)

            def down(m, k):
                j = buffer_of(m, k)
                pe.wait_ge(s["hidden_ready" if gated else "act_ready"], count(m, NCHK, k + 1))
                for t in range(T):
                    last = pe.matmul(yp[:, t, :], hid[j][:, t * P:(t + 1) * P], w["w_d"][:, k, :],
                                     start=(k == 0 and t == 0), stop=(gated and k == NCHK - 1), skip_group_check=True)
                last.then_inc(s["down_done"], 1)

            def finish(m):
                down(m, NCHK - 1)
                if not gated:
                    for t in range(T):
                        last = pe.matmul(yp[:, t, :], core.ones[0:1, :], w["b_d"][0:1, :], start=False, stop=True,
                                         skip_group_check=True)
                    last.then_inc(s["y_done"], 1)

            def prepare(m, k):
                if k == X_TURN:
                    pe.wait_ge(s["xn_ready"], count(m))
                    for t in range(T):
                        last = pe.transpose(misc[:, t * P:(t + 1) * P], xn[:, t, :], core.ident[:, :])
                    last.then_inc(s["xt_done"], 1)
                if k == LOGITS:
                    pe.wait_ge(s["xt_ready"], count(m))
                    for t in range(T):
                        last = pe.matmul(misc[:, t * E:(t + 1) * E], xT[m[1] % 2][:, t * P:(t + 1) * P], w["w_r"][:, :],
                                         start=True, stop=True)
                    last.then_inc(s["logits_done"], 1)
                if k == R_TURN:
                    pe.wait_ge(s["route_ready"], count(m))
                    for t in range(T):
                        last = pe.transpose(misc[:, t * P:(t + 1) * P], route[:, t, :], core.ident[:, :])
                    last.then_inc(s["rt_done"], 1)

            def experts(m, before=True, behind=True):
                p = m[1] % 2
                for k in range(NCHK):
                    j = buffer_of(m, k)
                    if k == 0:
                        pe.wait_ge(s["xt_ready"], count(m))
                    if k >= 2 or before:
                        pe.wait_ge(s["hidden_ready" if gated else "act_ready"], count(m, NCHK, k - 1))
                    last = pe.matmul(gp[j][:, :], w["w_g"][:, k, :], xT[p][:, :], start=True, stop=True)
                    if gated:
                        last = pe.matmul(up[j][:, :], w["w_u"][:, k, :], xT[p][:, :], start=True, stop=True)
                    last.then_inc(s["up_done"], 1)
                    if k in routed:
                        if k == 0:
                            pe.wait_ge(s["rt_ready"], count(m))
                        pe.matmul(wb[j][:, :], w["pick"][:, k, :], rT[p][:, :], start=True, stop=True)\
                          .then_inc(s["spread_done"], 1)
                    if behind:
                        prepare(neighbour(m, 1), k)
                    if k == 0 and before:
                        finish(neighbour(m, -1))
                    if k == 1 and before:
                        pe.wait_ge(s["y_read"], count(m, 1, 0))
                    if k:
                        down(m, k - 1)

            for k in range(NCHK):
                prepare((None, 0), k)
            experts((None, 0), before=False)
            with pe.Fori(0, tiles // 2 - 1) as i:
                experts((i, 1))
                experts((i, 2))
            experts((None, tiles - 1), behind=False)
            finish((None, tiles - 1))


MAGIC = 1.5 * 2.0 ** 23
QMAX = 32767.0


def quantised_mlp(nc, core, dram, tag):
    batch, T, NT, CH = core.batch, TILE, TILE * P, 3
    NI = batch // T
    with ExitStack() as ctx:
        st = Stage(nc, ctx, tag)
        wn = st.sb("w_natural", [P, 3 * CH, P])
        wT = st.sb("w", [P, 3 * CH, P])
        ws, wr = st.sb("w_scale", [P, 3 * CH * 4]), st.sb("w_inverse", [P, 3 * CH * 4])
        xi = st.sb("x_int", [P, NI, NT], I16)
        ui = st.sb("up_int", [P, NI, CH * NT], I16)
        gi = st.sb("gate_int", [P, NI, CH * NT], I16)
        high = st.sb("high", [P, 2, NI])
        top, most = st.sb("top", [P, 2]), st.sb("most", [P, 2])
        unit, scale, ratio = (st.sb(n, [P, 5]) for n in ("unit", "scale", "ratio"))
        X, G, UP, G2, OUT = range(5)
        xn = st.sb("xn", [P, T, P])
        f0, f1 = st.sb("f0", [P, CH * NT]), st.sb("f1", [P, CH * NT])
        xT = st.sb("xT", [P, NT])
        bn, mv = st.sb("bn", [P, 6]), st.sb("mv", [P, 2])
        misc = st.ps("misc", [P, NT])
        gu = [st.ps(n, [P, CH, NT]) for n in ("g", "u")]

        def col(tile, c):
            return tile[:, c:c + 1]

        def rounded(dve, chain, dst, src, mult, tmp):
            chain.link(dve.tensor_scalar(tmp, src, mult, MAGIC, ALU.mult, ALU.add))
            return dve.tensor_scalar(dst, tmp, -MAGIC, None, ALU.add)

        with ExitStack() as c2:
            st2 = Stage(nc, c2, tag + "_weights")
            loaded, step, quantised, turned, copied = (st2.sem(n) for n in ("loaded", "step", "quantised", "turned", "copied"))
            block = c2.enter_context(nc.Block())

            @block.sync
            def _(sp):
                sp.dma_start(wn[:, :, :], dram[tag + "_w"]).then_inc(loaded, 16)
                sp.wait_ge(loaded, 16)

            @block.vector
            def _(dve):
                chain = Chain(dve, step)
                blocks = wn[:, :, :].rearrange("p c (k i) -> p (c k) i", i=32)
                dve.wait_ge(loaded, 16)
                chain.link(dve.tensor_reduce(ws[:, :], blocks, AX.X, ALU.max, apply_absolute_value=True))
                chain.link(dve.tensor_scalar(ws[:, :], ws[:, :], 1.0 / 7.0, 1e-12, ALU.mult, ALU.max))
                chain.link(dve.reciprocal(wr[:, :], ws[:, :]))
                chain.link(dve.tensor_tensor(blocks, blocks, spread(wr[:, :], 2, 32), ALU.mult))
                chain.link(dve.tensor_scalar(wn[:, :, :], wn[:, :, :], MAGIC, None, ALU.add))
                chain.link(dve.tensor_scalar(wn[:, :, :], wn[:, :, :], -MAGIC, None, ALU.add))
                dve.tensor_tensor(blocks, blocks, spread(ws[:, :], 2, 32), ALU.mult).then_inc(quantised, 1)

            @block.tensor
            def _(pe):
                pe.wait_ge(quantised, 1)
                for k in range(3 * CH):
                    last = pe.transpose(gu[k // 6][:, k % 6 // 2, k % 2 * P:(k % 2 + 1) * P], wn[:, k, :], core.ident[:, :])
                last.then_inc(turned, 1)

            @block.scalar
            def _(act):
                act.wait_ge(turned, 1)
                for k in range(3 * CH):
                    act.activation(wT[:, k, :], gu[k // 6][:, k % 6 // 2, k % 2 * P:(k % 2 + 1) * P], ACT.Copy)

        def measured(name, first, n, units):
            with ExitStack() as c2:
                st2 = Stage(nc, c2, f"{tag}_{name}")
                step, top_ready, most_ready = st2.sem("step"), st2.sem("top_ready"), st2.sem("most_ready")
                block = c2.enter_context(nc.Block())

                @block.vector
                def _(dve):
                    chain = Chain(dve, step)
                    dve.tensor_reduce(top[:, 0:n], high[:, 0:n, :], AX.X, ALU.max).then_inc(top_ready, 1)
                    units(dve, chain)
                    sc, ra, un = (a[:, first:first + n] for a in (scale, ratio, unit))
                    dve.wait_ge(most_ready, 1)
                    chain.link(dve.tensor_tensor(sc, most[:, 0:n], un, ALU.mult))
                    chain.link(dve.tensor_scalar(sc, sc, 1.0 / QMAX, 1e-12, ALU.mult, ALU.max))
                    chain.link(dve.reciprocal(ra, sc))
                    dve.tensor_tensor(ra, ra, un, ALU.mult)

                @block.gpsimd
                def _(pool):
                    pool.wait_ge(top_ready, 1)
                    pool.partition_all_reduce(most[:, 0:n], top[:, 0:n], P, bass.bass_isa.ReduceOp.max)\
                        .then_inc(most_ready, 1)

        def run_pass(name, sems, vector, scalar=None, tensor=None, per=0):
            with ExitStack() as c2:
                st2 = Stage(nc, c2, f"{tag}_{name}")
                s = {n: st2.sem(n) for n in sems + ["vec_step", "tile_done"]}
                block = c2.enter_context(nc.Block())

                @block.vector
                def _(dve):
                    dve.sem_inc(s["tile_done"], 1)
                    with dve.Fori(0, NI) as i:
                        chain = Chain(dve, s["vec_step"], i, per)
                        vector(dve, s, i, chain).then_inc(s["tile_done"], 1)
                        chain.close()

                if scalar:
                    @block.scalar
                    def _(act):
                        with act.Fori(0, NI) as i:
                            scalar(act, s, i)

                if tensor:
                    @block.tensor
                    def _(pe):
                        with pe.Fori(0, NI) as i:
                            tensor(pe, s, i)

        def normalise(act, s, i):
            act.wait_ge(s["tile_done"], i + 1)
            for t in range(T):
                b = i * T + t
                last = act.activation(xn[:, t, :], core.x[:, b, :], ACT.Identity, bias=core.nmr[:, b, :],
                                      scale=core.rstd[:, b, :])
            last.then_inc(s["xn_ready"], 1)

        def max_x(dve, s, i, chain):
            dve.wait_ge(s["xn_ready"], i + 1)
            return dve.tensor_reduce(high[:, 0, i:i + 1] if isinstance(i, int) else high[:, 0, i].unsqueeze(1),
                                     xn[:, :, :], AX.XY, ALU.max, apply_absolute_value=True)

        run_pass("max_x", ["xn_ready"], max_x, scalar=normalise)
        measured("scale_x", X, 1, lambda dve, chain: chain.link(dve.memset(col(unit, X), 1.0)))

        def quantise_x(dve, s, i, chain):
            dve.wait_ge(s["xn_ready"], i + 1)
            chain.link(dve.tensor_scalar(xn[:, :, :], xn[:, :, :], col(ratio, X), MAGIC, ALU.mult, ALU.add))
            dve.tensor_scalar(xn[:, :, :], xn[:, :, :], -MAGIC, None, ALU.add).then_inc(s["xq_ready"], 1)
            dve.wait_ge(s["gu_done"], i + 1)
            for a in range(2):
                last = dve.tensor_reduce(high[:, a, i].unsqueeze(1), gu[a][:, :, :], AX.XY, ALU.max,
                                         apply_absolute_value=True)
            return last

        def copy_x(act, s, i):
            normalise(act, s, i)
            act.wait_ge(s["xt_done"], i + 1)
            act.activation(xi[:, i, :], misc[:, :], ACT.Copy)
            act.activation(xT[:, :], misc[:, :], ACT.Copy).then_inc(s["xt_ready"], 1)

        def gate_up(pe, s, i):
            pe.wait_ge(s["tile_done"], i + 1)
            pe.wait_ge(s["xt_ready"], i + 1)
            for a in range(2):
                for k in range(CH):
                    last = pe.matmul(gu[a][:, k, :], wT[:, a * CH + k, :], xT[:, :], start=True, stop=True)
            last.then_inc(s["gu_done"], 1)

        def turn_x(pe, s, i):
            pe.wait_ge(s["xq_ready"], i + 1)
            for t in range(T):
                last = pe.transpose(misc[:, t * P:(t + 1) * P], xn[:, t, :], core.ident[:, :])
            last.then_inc(s["xt_done"], 1)
            gate_up(pe, s, i)

        run_pass("max_gu", ["xn_ready", "xq_ready", "xt_done", "xt_ready", "gu_done"], quantise_x, copy_x, turn_x, per=1)

        def unit_gu(dve, chain):
            dve.tensor_copy(col(unit, G), col(scale, X))
            chain.link(dve.tensor_copy(col(unit, UP), col(scale, X)))

        measured("scale_gu", G, 2, unit_gu)

        def quantise_sigmoid(dve, s, i, chain):
            dve.wait_ge(s["sig_ready"], i + 1)
            chain.link(dve.tensor_scalar(f1[:, :], f1[:, :], 65536.0, MAGIC, ALU.mult, ALU.add))
            chain.link(dve.tensor_scalar(f1[:, :], f1[:, :], -MAGIC, 65535.0, ALU.add, ALU.min))
            chain.link(dve.tensor_tensor(f1[:, :], f1[:, :], gi[:, i, :], ALU.mult))

        def quantise_gu(dve, s, i, chain):
            dve.wait_ge(s["gu_done"], i + 1)
            g, u = (gu[a][:, :, :].rearrange("p c t -> p (c t)") for a in range(2))
            rounded(dve, chain, gi[:, i, :], g, col(ratio, G), f0[:, :]).then_inc(s["gate_ready"], 1)
            dve.wait_ge(s["gate_ready"], i + 1)
            chain.link(rounded(dve, chain, ui[:, i, :], u, col(ratio, UP), f0[:, :]))
            quantise_sigmoid(dve, s, i, chain)
            return dve.tensor_reduce(high[:, 0, i].unsqueeze(1), f1[:, :], AX.X, ALU.max, apply_absolute_value=True)

        def sigmoid(act, s, i):
            act.activation(f1[:, :], gi[:, i, :], ACT.Sigmoid, scale=col(scale, G)).then_inc(s["sig_ready"], 1)

        def widen_x(act, s, i):
            act.wait_ge(s["tile_done"], i + 1)
            act.activation(xT[:, :], xi[:, i, :], ACT.Copy).then_inc(s["xt_ready"], 1)
            act.wait_ge(s["gate_ready"], i + 1)
            sigmoid(act, s, i)

        run_pass("max_g2", ["xt_ready", "gu_done", "gate_ready", "sig_ready"], quantise_gu, widen_x, gate_up, per=6)
        measured("scale_g2", G2, 1, lambda dve, chain: chain.link(
            dve.tensor_scalar(col(unit, G2), col(scale, G), 1.0 / 65536.0, None, ALU.mult)))

        def quantise_g2(dve, s, i, chain):
            quantise_sigmoid(dve, s, i, chain)
            chain.link(rounded(dve, chain, gi[:, i, :], f1[:, :], col(ratio, G2), f1[:, :]))
            chain.link(dve.tensor_tensor(f1[:, :], gi[:, i, :], ui[:, i, :], ALU.mult))
            return dve.tensor_reduce(high[:, 0, i].unsqueeze(1), f1[:, :], AX.X, ALU.max, apply_absolute_value=True)

        def sigmoid_again(act, s, i):
            act.wait_ge(s["tile_done"], i + 1)
            sigmoid(act, s, i)

        run_pass("max_out", ["sig_ready"], quantise_g2, sigmoid_again, per=6)
        measured("scale_out", OUT, 1, lambda dve, chain: chain.link(
            dve.tensor_tensor(col(unit, OUT), col(scale, G2), col(scale, UP), ALU.mult)))

        def finish(dve, s, i, chain):
            chain.link(dve.tensor_tensor(f0[:, :], gi[:, i, :], ui[:, i, :], ALU.mult))
            rounded(dve, chain, f0[:, :], f0[:, :], col(ratio, OUT), f0[:, :]).then_inc(s["out_ready"], 1)
            dve.wait_ge(s["y_done"], i + 1)
            for t in range(T):
                b = i * T + t
                chain.link(dve.scalar_tensor_tensor(core.x[:, b, :], misc[:, t * P:(t + 1) * P], col(scale, OUT),
                                                    core.x[:, b, :], ALU.mult, ALU.add))
                last = take_stats(dve, chain, core, b, bn, mv)
            return last

        def down(pe, s, i):
            pe.wait_ge(s["out_ready"], i + 1)
            for t in range(T):
                for k in range(CH):
                    last = pe.matmul(misc[:, t * P:(t + 1) * P], f0[:, k * NT + t * P:k * NT + (t + 1) * P],
                                     wT[:, 2 * CH + k, :], start=(k == 0), stop=(k == CH - 1))
            last.then_inc(s["y_done"], 1)

        run_pass("down", ["out_ready", "y_done"], finish, None, down, per=2 + 3 * T)


def wide_cross_attention(nc, core, dram, tag):
    batch, U, H, DH, CH = core.batch, UNITS, 8, 64, 4
    INNER = H * DH
    with ExitStack() as ctx:
        st = Stage(nc, ctx, tag)

        def unit_sb(name, shape, dt=F32):
            return [st.sb(f"{name}{u}", shape, dt) for u in range(U)]

        names = ["w_q", "w_kv", "w_o", "b_o", "ln"]
        w = {n: st.sb(n, list(dram[f"{tag}_{n}"].shape)) for n in names}
        c_all = st.sb("c_all", [SC, batch, P])
        cstat = st.sb("cstat", [SC, batch, 2])
        crstd, cnmr = st.sb("crstd", [SC, batch, 1]), st.sb("cnmr", [SC, batch, 1])
        cbn, cmv = st.sb("cbn", [SC, 6]), st.sb("cmv", [SC, 2])
        xn, xT, cn, cT = unit_sb("xn", [P, P]), unit_sb("xT", [P, P]), unit_sb("cn", [SC, P]), unit_sb("cT", [P, SC])
        qT, kT, v = unit_sb("qT", [P, CH, P]), unit_sb("kT", [P, CH, SC]), unit_sb("v", [SC, INNER])
        probs = unit_sb("probs", [P, 2, CH, SC])
        pT = unit_sb("pT", [SC, 2, CH, P])
        top, z = unit_sb("top", [P, 2, CH]), unit_sb("z", [P, 2, CH])
        o, oT = unit_sb("o", [P, INNER]), unit_sb("oT", [P, CH, P])
        bn, mv = unit_sb("bn", [P, 6]), unit_sb("mv", [P, 2])
        scores = [st.ps(f"scores{u}", [P, 2, BANK]) for u in range(U)]
        ptp = [st.ps(f"ptp{a}", [P, CH, P]) for a in range(2)]
        misc = [st.ps(f"misc{u}", [P, BANK]) for u in range(U)]
        s = {n: st.sem(n) for n in (
            "loaded", "once_step", "cvar_ready", "cstd_ready", "consts", "xn_ready", "cn_ready", "xt_done", "xt_ready",
            "ct_done", "ct_ready", "q_done", "q_ready", "k_done", "k_ready", "v_done", "v_ready", "scores_done",
            "shifted", "probs_ready", "pt_done0", "pt_done1", "pt_copied0", "pt_copied1", "pv_done", "o_ready",
            "ot_done", "ot_ready", "y_done", "y_added", "vec_step")}
        n_loads = 16 * (len(names) + 1)
        block = ctx.enter_context(nc.Block())

        @block.sync
        def _(sp):
            sp.dma_start(c_all[:, :, :], dram["ctx"].rearrange("b t d -> t b d")).then_inc(s["loaded"], 16)
            for n in names:
                sp.dma_start(w[n][tuple(slice(None) for _ in w[n].shape)], dram[f"{tag}_{n}"]).then_inc(s["loaded"], 16)
            sp.wait_ge(s["loaded"], n_loads)

        @block.vector
        def _(dve):
            dve.sem_inc(s["y_added"], U)
            dve.wait_ge(s["loaded"], n_loads)
            with dve.Fori(0, batch) as b:
                once = Chain(dve, s["once_step"], b, 3)
                once.link(dve.bn_stats(cbn[:, :], c_all[:, b, :]))
                dve.memset(core.beat[:, :], 0.0)
                once.link(dve.bn_aggr(cmv[:, :], cbn[:, :]))
                once.link(dve.tensor_copy(cstat[:, b, :], cmv[:, :]))
            dve.tensor_scalar(crstd[:, :, 0], cstat[:, :, 1], LN_EPS, None, ALU.add).then_inc(s["cvar_ready"], 1)
            dve.wait_ge(s["cstd_ready"], 1)
            dve.reciprocal(crstd[:, :, 0], crstd[:, :, 0]).then_inc(s["once_step"], 1)
            dve.wait_ge(s["once_step"], 3 * batch + 1)
            dve.scalar_tensor_tensor(cnmr[:, :, 0], cstat[:, :, 0], -1.0, crstd[:, :, 0], ALU.mult, ALU.mult)\
               .then_inc(s["consts"], 1)
            with dve.Fori(0, batch // U) as i:
                chain = Chain(dve, s["vec_step"], i, 6 * U)
                for u in range(U):
                    dve.wait_ge(s["q_done"], i * U + (u + 1))
                    dve.tensor_copy(qT[u][:, :, :], scores[u][:, 0, :].rearrange("p (c t) -> p c t", c=CH))\
                       .then_inc(s["q_ready"], 1)
                for u in range(U):
                    S = scores[u][:, :, 0:CH * SC].rearrange("p a (c k) -> p a c k", c=CH)
                    dve.wait_ge(s["scores_done"], i * U + (u + 1))
                    chain.link(dve.tensor_reduce(top[u][:, :, :], S, AX.X, ALU.max))
                    dve.tensor_tensor(probs[u][:, :, :, :], S, spread(top[u][:, :, :], 3, SC), ALU.subtract)\
                       .then_inc(s["shifted"], 1)
                for u in range(U):
                    dve.wait_ge(s["probs_ready"], i * U + (u + 1))
                    chain.link(dve.tensor_reduce(z[u][:, :, :], probs[u][:, :, :, :], AX.X, ALU.add))
                    chain.link(dve.reciprocal(z[u][:, :, :], z[u][:, :, :]))
                for u in range(U):
                    dve.wait_ge(s["pv_done"], i * U + (u + 1))
                    dve.tensor_tensor(o[u][:, :].rearrange("p (c a f) -> p a c f", a=2, f=DH),
                                      misc[u][:, :].rearrange("p (c a f) -> p a c f", a=2, f=DH),
                                      spread(z[u][:, :, :], 3, DH), ALU.mult).then_inc(s["o_ready"], 1)
                for u in range(U):
                    b = i * U + u
                    dve.wait_ge(s["y_done"], i * U + (u + 1))
                    chain.link(dve.tensor_tensor(core.x[:, b, :], core.x[:, b, :], scores[u][:, 1, 0:P], ALU.add))
                    take_stats(dve, chain, core, b, bn[u], mv[u]).then_inc(s["y_added"], 1)
                chain.close()

        @block.scalar
        def _(act):
            act.wait_ge(s["cvar_ready"], 1)
            act.activation(crstd[:, :, 0], crstd[:, :, 0], ACT.Sqrt).then_inc(s["cstd_ready"], 1)
            act.wait_ge(s["consts"], 1)
            with act.Fori(0, batch // U) as i:
                def n_of(u):
                    return i * U + (u + 1)

                for u in range(U):
                    b = i * U + u
                    act.activation(xn[u][:, :], core.x[:, b, :], ACT.Identity, bias=core.nmr2[:, b, :],
                                   scale=core.rstd2[:, b, :]).then_inc(s["xn_ready"], 1)
                    act.activation(cn[u][:, :], c_all[:, b, :], ACT.Identity, bias=cnmr[:, b, :],
                                   scale=crstd[:, b, :]).then_inc(s["cn_ready"], 1)
                for u in range(U):
                    act.wait_ge(s["xt_done"], n_of(u))
                    act.activation(xT[u][:, :], misc[u][:, 0:P], ACT.Identity, bias=w["ln"][:, 1:2], scale=w["ln"][:, 0:1])\
                       .then_inc(s["xt_ready"], 1)
                    act.wait_ge(s["ct_done"], n_of(u))
                    act.activation(cT[u][:, :], scores[u][:, 1, 0:SC], ACT.Identity, bias=w["ln"][:, 3:4],
                                   scale=w["ln"][:, 2:3]).then_inc(s["ct_ready"], 1)
                for u in range(U):
                    act.wait_ge(s["v_done"], n_of(u))
                    act.activation(v[u][:, :], misc[u][0:SC, :], ACT.Copy).then_inc(s["v_ready"], 1)
                    act.wait_ge(s["k_done"], n_of(u))
                    act.activation(kT[u][:, :, :], scores[u][:, 1, 0:CH * SC].rearrange("p (c t) -> p c t", c=CH),
                                   ACT.Copy).then_inc(s["k_ready"], 1)
                for u in range(U):
                    act.wait_ge(s["shifted"], n_of(u))
                    act.activation(probs[u][:, :, :, :], probs[u][:, :, :, :], ACT.Exp, scale=float(DH) ** -0.5)\
                       .then_inc(s["probs_ready"], 1)
                for u in range(U):
                    for a in range(2):
                        act.wait_ge(s[f"pt_done{a}"], n_of(u))
                        act.activation(pT[u][:, a, :, :], ptp[a][0:SC, :, :], ACT.Copy).then_inc(s[f"pt_copied{a}"], 1)
                for u in range(U):
                    act.wait_ge(s["ot_done"], n_of(u))
                    act.activation(oT[u][:, :, :], scores[u][:, 0, :].rearrange("p (c t) -> p c t", c=CH), ACT.Copy)\
                       .then_inc(s["ot_ready"], 1)

        @block.tensor
        def _(pe):
            pe.sem_inc(s["pt_copied0"], 1)
            pe.sem_inc(s["pt_copied1"], 1)
            pe.wait_ge(s["consts"], 1)

            def mm(out, lhsT, rhs, start=True, stop=True):
                return pe.matmul(out, lhsT, rhs, start=start, stop=stop)

            with pe.Fori(0, batch // U) as i:
                def n_of(u):
                    return i * U + (u + 1)

                for u in range(U):
                    pe.wait_ge(s["y_added"], n_of(u))
                    pe.wait_ge(s["xn_ready"], n_of(u))
                    pe.transpose(misc[u][:, 0:P], xn[u][:, :], core.ident[:, :]).then_inc(s["xt_done"], 1)
                    pe.wait_ge(s["cn_ready"], n_of(u))
                    pe.transpose(scores[u][:, 1, 0:SC], cn[u][:, :], core.ident[0:SC, 0:SC]).then_inc(s["ct_done"], 1)
                for u in range(U):
                    pe.wait_ge(s["xt_ready"], n_of(u))
                    for c in range(CH):
                        last = mm(scores[u][:, 0, c * P:(c + 1) * P], w["w_q"][:, c * P:(c + 1) * P], xT[u][:, :])
                    last.then_inc(s["q_done"], 1)
                    pe.wait_ge(s["ct_ready"], n_of(u))
                    mm(misc[u][0:SC, :], cT[u][:, :], w["w_kv"][:, INNER:2 * INNER]).then_inc(s["v_done"], 1)
                    for c in range(CH):
                        last = mm(scores[u][:, 1, c * SC:(c + 1) * SC], w["w_kv"][:, c * P:(c + 1) * P], cT[u][:, :])
                    last.then_inc(s["k_done"], 1)
                for u in range(U):
                    pe.wait_ge(s["q_ready"], n_of(u))
                    pe.wait_ge(s["k_ready"], n_of(u))
                    for c in range(CH):
                        for a in range(2):
                            last = mm(scores[u][:, a, c * SC:(c + 1) * SC], qT[u][a * DH:(a + 1) * DH, c, :],
                                      kT[u][a * DH:(a + 1) * DH, c, :])
                    last.then_inc(s["scores_done"], 1)
                for u in range(U):
                    pe.wait_ge(s["probs_ready"], n_of(u))
                    for a in range(2):
                        pe.wait_ge(s[f"pt_copied{a}"], n_of(u))
                        for c in range(CH):
                            last = pe.transpose(ptp[a][0:SC, c, :], probs[u][:, a, c, :], core.ident[:, :])
                        last.then_inc(s[f"pt_done{a}"], 1)
                for u in range(U):
                    pe.wait_ge(s["v_ready"], n_of(u))
                    for a in range(2):
                        pe.wait_ge(s[f"pt_copied{a}"], n_of(u) + 1)
                        for c in range(CH):
                            h = 2 * c + a
                            last = mm(misc[u][:, h * DH:(h + 1) * DH], pT[u][:, a, c, :], v[u][:, h * DH:(h + 1) * DH])
                    last.then_inc(s["pv_done"], 1)
                for u in range(U):
                    pe.wait_ge(s["o_ready"], n_of(u))
                    for c in range(CH):
                        last = pe.transpose(scores[u][:, 0, c * P:(c + 1) * P], o[u][:, c * P:(c + 1) * P], core.ident[:, :])
                    last.then_inc(s["ot_done"], 1)
                for u in range(U):
                    pe.wait_ge(s["ot_ready"], n_of(u))
                    for c in range(CH):
                        mm(scores[u][:, 1, 0:P], oT[u][:, c, :], w["w_o"][:, c, :], start=c == 0, stop=False)
                    mm(scores[u][:, 1, 0:P], core.ones[0:1, :], w["b_o"][0:1, :], start=False).then_inc(s["y_done"], 1)


def query_softmax_attention(nc, core, dram, tag):
    batch, U = core.batch, UNITS
    CHUNK = 4
    CHUNKS = [(at, src) for at in range(0, HEADS, CHUNK) for src in range(2)]
    NCH = len(CHUNKS)
    scale = float(P) ** -0.5
    with ExitStack() as ctx:
        st = Stage(nc, ctx, tag)

        def unit_sb(name, shape, dt=F32):
            return [st.sb(f"{name}{u}", shape, dt) for u in range(U)]

        names = ["w_q", "b_q", "w_k", "b_k", "w_slot", "w_v", "b_v", "w_qt", "b_qt", "w_o", "b_o", "gb", "unslot"]
        w = {n: st.sb(n, list(dram[f"{tag}_{n}"].shape)) for n in names}
        xn, xT = unit_sb("xn", [P, P]), unit_sb("xT", [P, P])
        k12, kT = unit_sb("k12", [P, 2, SC]), unit_sb("kT", [P, GROUPS, 2 * SC])
        qT, v = unit_sb("qT", [P, GROUPS, P]), unit_sb("v", [SC, 2, HEADS, HD])
        vs = unit_sb("vs", [SC, 2, HEADS, SLOT])
        accT = unit_sb("accT", [P, GROUPS, P])
        probs = unit_sb("probs", [SC, 2, HEADS, P])
        top, z = unit_sb("top", [SC, 2, HEADS]), unit_sb("z", [SC, 2, HEADS])
        bn, mv, var, rs = (unit_sb(n, [P, k]) for n, k in (("bn", 6), ("mv", 2), ("var", 1), ("rs", 1)))
        o1, o1T, o2 = unit_sb("o1", [P, P]), unit_sb("o1T", [P, P]), unit_sb("o2", [P, P])
        minus_half = st.sb("minus_half", [P, 1])
        scores = [st.ps(f"scores{u}", [P, 2, BANK]) for u in range(U)]
        misc = [st.ps(f"misc{u}", [P, BANK]) for u in range(U)]
        extra = [st.ps(f"extra{u}", [P, BANK]) for u in range(U)]
        s = {n: st.sem(n) for n in (
            "loaded", "consts", "xn_ready", "xt_done", "xt_ready", "q_done", "q_ready", "k12_ready", "first_step", "last_step",
            "k_done", "k_ready", "v_done", "v_ready", "scores_done", "top_ready", "probs_ready", "vs_ready", "pv_done", "acc_ready", "attended",
            "var_ready", "rs_ready", "o1_ready", "o1t_done", "o1t_ready", "y_done", "y_added", "vec_step")}
        block = ctx.enter_context(nc.Block())

        def count(b, per=1, extra=1):
            i, at = b
            return at * per + extra if i is None else i * (U * per) + (at * per + extra)

        def number(b):
            return count(b, 1, 0)

        def neighbour(b, d):
            return (b[0], b[1] + d)

        def part(c):
            at, src = CHUNKS[c]
            return src, slice(at, at + CHUNK)

        @block.sync
        def _(sp):
            for n in names:
                sp.dma_start(w[n][tuple(slice(None) for _ in w[n].shape)], dram[f"{tag}_{n}"]).then_inc(s["loaded"], 16)
            sp.wait_ge(s["loaded"], 16 * len(names))

        @block.gpsimd
        def _(pool):
            pool.wait_ge(s["consts"], 1)
            with pool.Fori(0, batch // U) as i:
                for u in range(U):
                    for r in range(2):
                        pool.wait_ge(s["var_ready"], i * (2 * U) + (2 * u + r + 1))
                        pool.tensor_tensor(rs[u][:, :], var[u][:, :], minus_half[:, :], ALU.pow).then_inc(s["rs_ready"], 1)

        @block.vector
        def _(dve):
            dve.wait_ge(s["loaded"], 16 * len(names))
            for u in range(U):
                dve.memset(vs[u][:, :, :, :], 0.0)
            dve.memset(minus_half[:, :], -0.5).then_inc(s["consts"], 1)
            dve.wait_ge(s["consts"], 1)

            def maxima(chain, b, c, u):
                src, hs = part(c)
                S = scores[u][0:SC, c % 2, :].rearrange("p (h t) -> p h t", t=P)
                dve.wait_ge(s["scores_done"], count(b, NCH, c + 1))
                chain.link(dve.tensor_reduce(top[u][:, src, hs], S, AX.X, ALU.max))
                dve.tensor_scalar(top[u][:, src, hs], top[u][:, src, hs], -scale, None, ALU.mult).then_inc(s["top_ready"], 1)

            def divide(chain, b, c, u):
                src, hs = part(c)
                dve.wait_ge(s["probs_ready"], count(b, NCH, c + 1))
                chain.link(dve.reciprocal(z[u][:, src, hs], z[u][:, src, hs]))
                dve.tensor_tensor(vs[u][:, src, hs, 0:HD], v[u][:, src, hs, :], spread(z[u][:, src, hs], 2, HD), ALU.mult)\
                   .then_inc(s["vs_ready"], 1)

            def moments(chain, u, src):
                dve.memset(core.beat[:, :], 0.0)
                chain.link(dve.bn_stats(bn[u][:, :], src))
                dve.memset(core.beat[:, :], 0.0)
                chain.link(dve.bn_aggr(mv[u][:, :], bn[u][:, :]))
                dve.tensor_scalar(var[u][:, :], mv[u][:, 1:2], LN_EPS, None, ALU.add).then_inc(s["var_ready"], 1)

            def norm(chain, b, r, u, dst, src):
                dve.wait_ge(s["rs_ready"], count(b, 2, r + 1))
                chain.link(dve.tensor_scalar(dst, src, mv[u][:, 0:1], rs[u][:, :], ALU.subtract, ALU.mult))
                chain.link(dve.tensor_tensor(dst, dst, w["gb"][:, 2 * r, :], ALU.mult))
                return dve.tensor_tensor(dst, dst, w["gb"][:, 2 * r + 1, :], ALU.add)

            def tail(chain, b, u, step):
                if step == 0:
                    dve.wait_ge(s["attended"], count(b))
                    moments(chain, u, extra[u][:, 0:P])
                if step == 1:
                    norm(chain, b, 0, u, o1[u][:, :], extra[u][:, 0:P]).then_inc(s["o1_ready"], 1)
                if step == 2:
                    dve.wait_ge(s["o1_ready"], count(b))
                    dve.wait_ge(s["y_done"], count(b))
                    chain.link(dve.scalar_tensor_tensor(o2[u][:, :], misc[u][:, P:2 * P], 0.0, o1[u][:, :], ALU.max, ALU.add))
                    moments(chain, u, o2[u][:, :])
                if step == 3:
                    n = number(b)
                    chain.link(norm(chain, b, 1, u, o2[u][:, :], o2[u][:, :]))
                    chain.link(dve.tensor_tensor(core.x[:, n, :], core.x[:, n, :], o2[u][:, :], ALU.add))
                    take_stats(dve, chain, core, n, bn[u], mv[u]).then_inc(s["y_added"], 1)

            def copy_q(b, u):
                dve.wait_ge(s["q_done"], count(b))
                acc = scores[u][:, 0, :].rearrange("p (g t) -> p g t", g=GROUPS)
                dve.tensor_tensor(qT[u][:, :, :], acc, spread(w["b_q"][:, :], 2, P), ALU.add).then_inc(s["q_ready"], 1)

            def attend(chain, b, u, with_tail=True, start_next=True):
                before, behind, other = neighbour(b, -1), neighbour(b, 1), 1 - u
                for c in range(NCH):
                    maxima(chain, b, c, u)
                    if c:
                        divide(chain, b, c - 1, u)
                    if c == 1 and with_tail:
                        tail(chain, before, other, 0)
                    if c == 1 and start_next:
                        copy_q(behind, other)
                    if c == 2 and with_tail:
                        tail(chain, before, other, 1)
                    if c in (5, 7) and with_tail:
                        tail(chain, before, other, c // 2)
                divide(chain, b, NCH - 1, u)

            once = Chain(dve, s["first_step"])
            copy_q((None, 0), 0)
            attend(once, (None, 0), 0, with_tail=False)
            with dve.Fori(0, batch // U - 1) as i:
                chain = Chain(dve, s["vec_step"], i, U * (2 * NCH + 2 + 2 + 1 + 2 + 3 + 1 + 2))
                attend(chain, (i, 1), 1)
                attend(chain, (i, 2), 0)
                chain.close()
            once = Chain(dve, s["last_step"])
            attend(once, (None, batch - 1), 1, start_next=False)
            for step in range(4):
                tail(once, (None, batch - 1), 1, step)

        @block.scalar
        def _(act):
            act.wait_ge(s["consts"], 1)

            def begin(b, u):
                n = number(b)
                act.activation(xn[u][:, :], core.x[:, n, :], ACT.Identity, bias=core.nmr[:, n, :],
                               scale=core.rstd[:, n, :]).then_inc(s["xn_ready"], 1)
                act.wait_ge(s["xt_done"], count(b))
                act.activation(xT[u][:, :], scores[u][:, 0, 0:P], ACT.Copy).then_inc(s["xt_ready"], 1)
                for src in range(2):
                    last = act.activation(k12[u][:, src, :], scores[u][:, 0, P + src * SC:P + (src + 1) * SC], ACT.Identity,
                                          bias=w["b_k"][:, src:src + 1])
                last.then_inc(s["k12_ready"], 1)

            def copy_v(b, u):
                act.wait_ge(s["v_done"], count(b))
                act.activation(v[u][:, :, :, :].rearrange("p s h f -> p (s h f)"), scores[u][0:SC, 1, 0:2 * P], ACT.Copy)\
                   .then_inc(s["v_ready"], 1)

            def copy_k(b, u):
                act.wait_ge(s["k_done"], count(b))
                for a in range(2):
                    last = act.activation(kT[u][:, 2 * a:2 * a + 2, :],
                                          scores[u][:, 1 - a, 0:4 * SC].rearrange("p (g t) -> p g t", g=2), ACT.Copy)
                last.then_inc(s["k_ready"], 1)

            def copy_acc(b, u):
                act.wait_ge(s["pv_done"], count(b, NCH, NCH))
                act.activation(accT[u][:, :, :], misc[u][:, :].rearrange("p (g t) -> p g t", g=GROUPS), ACT.Copy)\
                   .then_inc(s["acc_ready"], 1)

            def tail(b, u):
                act.wait_ge(s["o1t_done"], count(b))
                act.activation(o1T[u][:, :], misc[u][:, 0:P], ACT.Copy).then_inc(s["o1t_ready"], 1)

            def attend(b, u, with_tail=True, start_next=True):
                behind, other = neighbour(b, 1), 1 - u
                if with_tail:
                    copy_acc(neighbour(b, -1), other)
                if start_next:
                    begin(behind, other)
                for c in range(NCH):
                    src, hs = part(c)
                    act.wait_ge(s["top_ready"], count(b, NCH, c + 1))
                    for j in range(CHUNK):
                        h = hs.start + j
                        last = act.activation(probs[u][:, src, h, :], scores[u][0:SC, c % 2, j * P:(j + 1) * P], ACT.Exp,
                                              scale=scale, bias=top[u][:, src, h:h + 1], accum_out=z[u][:, src, h:h + 1])
                    last.then_inc(s["probs_ready"], 1)
                    if c == 0 and start_next:
                        copy_v(behind, other)
                    if c == 2 and start_next:
                        copy_k(behind, other)
                    if c == 4 and with_tail:
                        tail(neighbour(b, -1), other)

            begin((None, 0), 0)
            copy_v((None, 0), 0)
            copy_k((None, 0), 0)
            attend((None, 0), 0, with_tail=False)
            with act.Fori(0, batch // U - 1) as i:
                attend((i, 1), 1)
                attend((i, 2), 0)
            attend((None, batch - 1), 1, start_next=False)
            copy_acc((None, batch - 1), 1)
            tail((None, batch - 1), 1)

        @block.tensor
        def _(pe):
            pe.wait_ge(s["consts"], 1)

            def mm(out, lhsT, rhs, start=True, stop=True, skip=False):
                return pe.matmul(out, lhsT, rhs, start=start, stop=stop, skip_group_check=skip)

            def begin(b, u):
                for src in range(2):
                    mm(scores[u][:, 0, P + src * SC:P + (src + 1) * SC], w["w_k"][:, src, :], core.ctxT[:, number(b), :])
                pe.wait_ge(s["xn_ready"], count(b))
                pe.transpose(scores[u][:, 0, 0:P], xn[u][:, :], core.ident[:, :]).then_inc(s["xt_done"], 1)

            def front_0(b, u):
                pe.wait_ge(s["xt_ready"], count(b))
                pe.wait_ge(s["k12_ready"], count(b))
                for g in range(GROUPS):
                    last = mm(scores[u][:, 0, g * P:(g + 1) * P], w["w_q"][:, g * P:(g + 1) * P], xT[u][:, :])
                last.then_inc(s["q_done"], 1)
                for src in range(2):
                    out = scores[u][0:SC, 1, src * P:(src + 1) * P]
                    mm(out, k12[u][:, src, :], w["w_v"][:, src, :], stop=False)
                    last = mm(out, core.ones[0:1, 0:SC], w["b_v"][0:1, src * P:(src + 1) * P], start=False)
                last.then_inc(s["v_done"], 1)

            def front_1(b, u):
                pe.wait_ge(s["v_ready"], count(b))
                pe.wait_ge(s["q_ready"], count(b))
                keys = k12[u][:, :, :].rearrange("p s t -> p (s t)")
                for g in range(GROUPS):
                    out = scores[u][:, 1 - g // 2, g % 2 * 2 * SC:(g % 2 + 1) * 2 * SC]
                    last = mm(out, w["w_slot"][:, g * P:(g + 1) * P], keys)
                last.then_inc(s["k_done"], 1)

            def front_3(b, u):
                mm(extra[u][:, 0:P], xT[u][:, :], w["w_qt"][:, :], stop=False, skip=True)
                mm(extra[u][:, 0:P], core.ones[0:1, :], w["b_qt"][0:1, :], start=False, stop=False, skip=True)

            def tail_join(b, u):
                pe.wait_ge(s["acc_ready"], count(b))
                for g in range(GROUPS):
                    last = mm(extra[u][:, 0:P], accT[u][:, g, :], w["unslot"][:, g * P:(g + 1) * P], start=False,
                              stop=(g == GROUPS - 1), skip=True)
                last.then_inc(s["attended"], 1)

            def tail_turn(b, u):
                pe.wait_ge(s["o1_ready"], count(b))
                pe.transpose(misc[u][:, 0:P], o1[u][:, :], core.ident[:, :]).then_inc(s["o1t_done"], 1)

            def tail_project(b, u):
                pe.wait_ge(s["o1t_ready"], count(b))
                mm(misc[u][:, P:2 * P], o1T[u][:, :], w["w_o"][:, :], stop=False)
                mm(misc[u][:, P:2 * P], core.ones[0:1, :], w["b_o"][0:1, :], start=False).then_inc(s["y_done"], 1)

            def scoring(b, c, u):
                if c == 0:
                    pe.wait_ge(s["q_ready"], count(b))
                    pe.wait_ge(s["k_ready"], count(b))
                if c >= 2:
                    pe.wait_ge(s["probs_ready"], count(b, NCH, c - 1))
                first, src = CHUNKS[c]
                for g in range(GROUPS):
                    at = first // GROUPS * SLOT
                    last = mm(scores[u][0:SC, c % 2, g * P:(g + 1) * P], kT[u][at:at + HD, g, src * SC:(src + 1) * SC],
                              qT[u][at:at + HD, g, :])
                last.then_inc(s["scores_done"], 1)

            def weigh(b, c, u):
                pe.wait_ge(s["vs_ready"], count(b, NCH, c + 1))
                first, src = CHUNKS[c]
                at = first // GROUPS * SLOT
                for g in range(GROUPS):
                    last = mm(misc[u][at:at + SLOT, g * P:(g + 1) * P], vs[u][:, src, first + g, :],
                              probs[u][:, src, first + g, :], start=(src == 0 and g == 0), stop=(src == 1), skip=True)
                last.then_inc(s["pv_done"], 1)

            def attend(b, u, with_tail=True, start_next=True):
                before, behind, other = neighbour(b, -1), neighbour(b, 1), 1 - u
                scoring(b, 0, u)
                if start_next:
                    begin(behind, other)
                for c in range(NCH):
                    if c + 1 < NCH:
                        scoring(b, c + 1, u)
                    if c == 0 and start_next:
                        front_0(behind, other)
                    if c == 2 and start_next:
                        front_1(behind, other)
                    if c == 1 and with_tail:
                        tail_join(before, other)
                    if c == 3 and with_tail:
                        tail_turn(before, other)
                    if c == 5 and with_tail:
                        tail_project(before, other)
                    if c == 6 and start_next:
                        front_3(behind, other)
                    if c:
                        weigh(b, c - 1, u)
                weigh(b, NCH - 1, u)
                if start_next and with_tail:
                    pe.wait_ge(s["y_added"], count(before))

            begin((None, 0), 0)
            for front in (front_0, front_1, front_3):
                front((None, 0), 0)
            attend((None, 0), 0, with_tail=False)
            with pe.Fori(0, batch // U - 1) as i:
                attend((i, 1), 1)
                attend((i, 2), 0)
            attend((None, batch - 1), 1, start_next=False)
            tail_join((None, batch - 1), 1)
            tail_turn((None, batch - 1), 1)
            tail_project((None, batch - 1), 1)


def delta_rule_attention(nc, core, dram, tag):
    batch, T, NT = core.batch, TILE, TILE * P
    NI, NJ, KC, EPS = batch // TILE, batch // 8, 4, 1e-6
    STORES = 6 * 16
    TR = KC - 1
    scratch = {n: nc.dram_tensor(f"{tag}_scratch_{n}", [batch, P, P], F32, kind="Internal").ap() for n in "qkvo"}
    small_d = nc.dram_tensor(f"{tag}_scratch_small", [3, batch, HEADS, P], F32, kind="Internal").ap()

    with ExitStack() as ctx:
        st = Stage(nc, ctx, tag + "_in")
        names = ["w_in", "b_in", "conv", "w_beta", "b_beta", "head_sum"]
        w = {n: st.sb(n, list(dram[f"{tag}_{n}"].shape)) for n in names}
        xn, xT = st.sb("xn", [P, T, P]), st.sb("xT", [P, NT])
        raw = [st.sb(f"raw_{n}", [P, T, TR + P]) for n in "qkv"]
        cv = [st.sb(f"conv_{n}", [P, T, P]) for n in "qkv"]
        sq = [st.sb(f"square_{n}", [P, NT]) for n in "qk"]
        small = st.sb("small", [HEADS, 3, NT])
        misc = st.ps("misc", [P, NT])
        proj = [st.ps(f"proj_{n}", [P, NT]) for n in "qkv"]
        sm = [st.ps(f"small{n}", [HEADS, NT]) for n in range(3)]
        s = {n: st.sem(n) for n in ("loaded", "consts", "xn_ready", "xt_done", "xt_ready", "proj_done", "raw_ready",
                                    "conv_ready", "conv_step", "square_ready", "sums_done", "small_ready", "v_ready", "stored")}
        block = ctx.enter_context(nc.Block())

        @block.sync
        def _(sp):
            for n in names:
                sp.dma_start(w[n][tuple(slice(None) for _ in w[n].shape)], dram[f"{tag}_{n}"]).then_inc(s["loaded"], 16)
            sp.wait_ge(s["loaded"], 16 * len(names))
            sp.sem_inc(s["stored"], STORES)
            with sp.Fori(0, NI) as i:
                for k, n in enumerate("qk"):
                    if k == 0:
                        sp.wait_ge(s["conv_ready"], i + 1)
                    dst = scratch[n].rearrange("(i b) p t -> i p b t", b=T)[i]
                    sp.dma_start(dst, cv[k][:, :, :]).then_inc(s["stored"], 16)
                sp.wait_ge(s["v_ready"], i + 1)
                sp.dma_start(scratch["v"].rearrange("(i b) p t -> i p b t", b=T)[i], cv[2][:, :, :]).then_inc(s["stored"], 16)
                sp.wait_ge(s["small_ready"], i + 1)
                for k in range(3):
                    dst = small_d[k].rearrange("(i b) h t -> i h b t", b=T)[i]
                    sp.dma_start(dst, small[:, k, :].rearrange("h (b t) -> h b t", b=T)).then_inc(s["stored"], 16)
            sp.wait_ge(s["stored"], STORES * (NI + 1))

        @block.vector
        def _(dve):
            dve.wait_ge(s["loaded"], 16 * len(names))
            for r in raw:
                last = dve.memset(r[:, :, 0:TR], 0.0)
            last.then_inc(s["consts"], 1)
            with dve.Fori(0, NI) as i:
                chain = Chain(dve, s["conv_step"], i, 3 * (KC - 1))
                dve.wait_ge(s["stored"], STORES * (i + 1))
                for k in range(3):
                    dve.wait_ge(s["raw_ready"], i * 3 + (k + 1))
                    c = w["conv"][:, k, :]
                    chain.link(dve.tensor_scalar(cv[k][:, :, :], raw[k][:, :, 0:P], c[:, 0:1], c[:, KC:KC + 1],
                                                 ALU.mult, ALU.add))
                    for tap in range(1, KC):
                        last = dve.scalar_tensor_tensor(cv[k][:, :, :], raw[k][:, :, tap:tap + P], c[:, tap:tap + 1],
                                                        cv[k][:, :, :], ALU.mult, ALU.add)
                        if tap < KC - 1:
                            chain.link(last)
                last.then_inc(s["conv_ready"], 1)
                chain.close()

        @block.scalar
        def _(act):
            act.wait_ge(s["consts"], 1)
            with act.Fori(0, NI) as i:
                for t in range(T):
                    b = i * T + t
                    last = act.activation(xn[:, t, :], core.x[:, b, :], ACT.Identity, bias=core.nmr[:, b, :],
                                          scale=core.rstd[:, b, :])
                last.then_inc(s["xn_ready"], 1)
                act.wait_ge(s["xt_done"], i + 1)
                act.activation(xT[:, :], misc[:, :], ACT.Copy).then_inc(s["xt_ready"], 1)
                act.wait_ge(s["proj_done"], i + 1)
                for k in range(3):
                    act.activation(raw[k][:, :, TR:], proj[k][:, :].rearrange("p (b t) -> p b t", b=T), ACT.Identity,
                                   bias=w["b_in"][:, k:k + 1]).then_inc(s["raw_ready"], 1)
                act.wait_ge(s["conv_ready"], i + 1)
                act.activation(cv[2][:, :, :], cv[2][:, :, :], ACT.Silu).then_inc(s["v_ready"], 1)
                for k in range(2):
                    last = act.activation(sq[k][:, :], cv[k][:, :, :].rearrange("p b t -> p (b t)"), ACT.Square)
                last.then_inc(s["square_ready"], 1)
                act.wait_ge(s["sums_done"], i + 1)
                for k in range(3):
                    last = act.activation(small[:, k, :], sm[k][:, :], ACT.Identity, bias=w["b_beta"][:, k:k + 1])
                last.then_inc(s["small_ready"], 1)

        @block.tensor
        def _(pe):
            pe.wait_ge(s["consts"], 1)
            with pe.Fori(0, NI) as i:
                pe.wait_ge(s["xn_ready"], i + 1)
                for t in range(T):
                    last = pe.transpose(misc[:, t * P:(t + 1) * P], xn[:, t, :], core.ident[:, :])
                last.then_inc(s["xt_done"], 1)
                pe.wait_ge(s["xt_ready"], i + 1)
                for k in range(3):
                    last = pe.matmul(proj[k][:, :], w["w_in"][:, k, :], xT[:, :], start=True, stop=True)
                last.then_inc(s["proj_done"], 1)
                pe.matmul(sm[0][:, :], w["w_beta"][:, :], xT[:, :], start=True, stop=True)
                pe.wait_ge(s["square_ready"], i + 1)
                for k in range(2):
                    last = pe.matmul(sm[1 + k][:, :], w["head_sum"][:, :], sq[k][:, :], start=True, stop=True)
                last.then_inc(s["sums_done"], 1)

    with ExitStack() as ctx:
        st = Stage(nc, ctx, tag + "_rec")
        q, k, v = (st.sb(n, [P, NJ, HD, P]) for n in "qkv")
        beta, qq, kk = (st.sb(n, [P, NJ, P]) for n in ("beta", "q_sq", "k_sq"))
        S = st.sb("S", [P, NJ, HD, HD])
        m0, m1 = st.sb("m0", [P, NJ, HD, HD]), st.sb("m1", [P, NJ, HD, HD])
        d = st.sb("d", [P, NJ, HD])
        osq = st.sb("osq", [P, HD, P])
        s = {n: st.sem(n) for n in ("loaded", "step", "clamped", "exp_ready", "norms_ready", "rms_ready", "root_ready",
                                    "rec", "token_done", "post", "o_ready", "stored")}
        block = ctx.enter_context(nc.Block())

        @block.sync
        def _(sp):
            for n, t in (("k", k), ("v", v), ("q", q)):
                sp.dma_start(t[:, :, :, :].rearrange("p j d t -> p j (d t)"),
                             scratch[n].rearrange("(j l) (h d) t -> (l h) j (d t)", l=8, h=HEADS)).then_inc(s["loaded"], 16)
            for n, t in ((0, beta), (1, qq), (2, kk)):
                sp.dma_start(t[:, :, :], small_d[n].rearrange("(j l) h t -> (l h) j t", l=8)).then_inc(s["loaded"], 16)
            sp.wait_ge(s["o_ready"], 1)
            sp.dma_start(scratch["o"].rearrange("(j l) (h d) t -> (l h) j (d t)", l=8, h=HEADS),
                         v[:, :, :, :].rearrange("p j d t -> p j (d t)")).then_inc(s["stored"], 16)
            sp.wait_ge(s["stored"], 16)

        @block.scalar
        def _(act):
            act.wait_ge(s["clamped"], 1)
            act.activation(beta[:, :, :], beta[:, :, :], ACT.Exp).then_inc(s["exp_ready"], 1)
            act.activation(kk[:, :, :], kk[:, :, :], ACT.Sqrt)
            act.activation(qq[:, :, :], qq[:, :, :], ACT.Sqrt).then_inc(s["norms_ready"], 1)
            act.wait_ge(s["rms_ready"], 1)
            act.activation(kk[:, :, :], kk[:, :, :], ACT.Sqrt).then_inc(s["root_ready"], 1)

        @block.vector
        def _(dve):
            pre = Chain(dve, s["step"])
            dve.wait_ge(s["loaded"], 16 * 6)
            dve.tensor_scalar(beta[:, :, :], beta[:, :, :], -1.0, 88.0, ALU.mult, ALU.min).then_inc(s["clamped"], 1)
            dve.memset(S[:, :, :, :], 0.0)
            dve.wait_ge(s["exp_ready"], 1)
            pre.link(dve.tensor_scalar(beta[:, :, :], beta[:, :, :], 1.0, None, ALU.add))
            pre.link(dve.reciprocal(beta[:, :, :], beta[:, :, :]))
            dve.wait_ge(s["norms_ready"], 1)
            for a in (kk, qq):
                pre.link(dve.tensor_scalar(a[:, :, :], a[:, :, :], EPS, None, ALU.add))
                pre.link(dve.reciprocal(a[:, :, :], a[:, :, :]))
            pre.link(dve.tensor_tensor(beta[:, :, :], beta[:, :, :], kk[:, :, :], ALU.mult))
            pre.link(dve.tensor_tensor(beta[:, :, :], beta[:, :, :], kk[:, :, :], ALU.mult))
            with dve.Fori(0, P) as t:
                chain = Chain(dve, s["rec"], t, 7)
                kt, qt = spread(k[:, :, :, t], 2, HD), spread(q[:, :, :, t], 2, HD)
                chain.link(dve.tensor_tensor(m0[:, :, :, :], S[:, :, :, :], kt, ALU.mult))
                chain.link(dve.tensor_reduce(d[:, :, :], m0[:, :, :, :], AX.X, ALU.add))
                chain.link(dve.tensor_tensor(d[:, :, :], v[:, :, :, t], d[:, :, :], ALU.subtract))
                chain.link(dve.tensor_tensor(d[:, :, :], d[:, :, :], spread(beta[:, :, t], 2, HD), ALU.mult))
                chain.link(dve.tensor_tensor(m1[:, :, :, :], spread(d[:, :, :], 3, HD), kt, ALU.mult))
                chain.link(dve.tensor_tensor(S[:, :, :, :], S[:, :, :, :], m1[:, :, :, :], ALU.add))
                chain.link(dve.tensor_tensor(m1[:, :, :, :], S[:, :, :, :], qt, ALU.mult))
                dve.memset(core.beat[:, :], 0.0)
                dve.tensor_reduce(v[:, :, :, t], m1[:, :, :, :], AX.X, ALU.add).then_inc(s["token_done"], 1)
                chain.close()
                dve.wait_ge(s["token_done"], t + 1)
            post = Chain(dve, s["post"])
            for j in range(NJ):
                post.link(dve.tensor_tensor(osq[:, :, :], v[:, j, :, :], v[:, j, :, :], ALU.mult))
                post.link(dve.tensor_reduce(kk[:, j, :], osq[:, :, :].rearrange("p d t -> p t d"), AX.X, ALU.add))
            post.link(dve.tensor_tensor(kk[:, :, :], kk[:, :, :], qq[:, :, :], ALU.mult))
            post.link(dve.tensor_tensor(kk[:, :, :], kk[:, :, :], qq[:, :, :], ALU.mult))
            dve.tensor_scalar(kk[:, :, :], kk[:, :, :], 1.0 / HD, 1e-6, ALU.mult, ALU.add).then_inc(s["rms_ready"], 1)
            dve.wait_ge(s["root_ready"], 1)
            post.link(dve.reciprocal(kk[:, :, :], kk[:, :, :]))
            post.link(dve.tensor_tensor(kk[:, :, :], kk[:, :, :], qq[:, :, :], ALU.mult))
            dve.tensor_tensor(v[:, :, :, :], v[:, :, :, :], spread(kk[:, :, :], 2, HD), ALU.mult).then_inc(s["o_ready"], 1)

    with ExitStack() as ctx:
        st = Stage(nc, ctx, tag + "_out")
        oT = st.sb("oT", [P, batch, P])
        ot = [st.sb(f"ot{j}", [P, T, P]) for j in range(1)]
        w_o, b_o, nw = st.sb("w_o", [P, P]), st.sb("b_o", [1, P]), st.sb("norm_w", [P, 1])
        bn, mv = st.sb("bn", [P, 6]), st.sb("mv", [P, 2])
        yp = st.ps("y", [P, T, P])
        s = {n: st.sem(n) for n in ("loaded", "consts", "ot_ready", "y_done", "y_added", "vec_step")}
        block = ctx.enter_context(nc.Block())

        @block.sync
        def _(sp):
            sp.dma_start(oT[:, :, :], scratch["o"].rearrange("b p t -> p b t")).then_inc(s["loaded"], 16)
            sp.dma_start(w_o[:, :], dram[tag + "_w_o"]).then_inc(s["loaded"], 16)
            sp.dma_start(b_o[:, :], dram[tag + "_b_o"]).then_inc(s["loaded"], 16)
            sp.dma_start(nw[:, :], dram[tag + "_norm_w"]).then_inc(s["loaded"], 16)
            sp.wait_ge(s["loaded"], 64)

        @block.scalar
        def _(act):
            act.wait_ge(s["consts"], 1)
            with act.Fori(0, NI) as i:
                act.wait_ge(s["y_added"], i + 1)
                for t in range(T):
                    last = act.activation(ot[0][:, t, :], oT[:, i * T + t, :], ACT.Copy)
                last.then_inc(s["ot_ready"], 1)

        @block.tensor
        def _(pe):
            pe.wait_ge(s["consts"], 1)
            with pe.Fori(0, NI) as i:
                pe.wait_ge(s["ot_ready"], i + 1)
                for t in range(T):
                    pe.matmul(yp[:, t, :], ot[0][:, t, :], w_o[:, :], start=True, stop=False)
                    last = pe.matmul(yp[:, t, :], core.ones[0:1, :], b_o[0:1, :], start=False, stop=True)
                last.then_inc(s["y_done"], 1)

        @block.vector
        def _(dve):
            dve.sem_inc(s["y_added"], 1)
            dve.wait_ge(s["loaded"], 64)
            dve.tensor_scalar(w_o[:, :], w_o[:, :], nw[:, :], None, ALU.mult).then_inc(s["consts"], 1)
            with dve.Fori(0, NI) as i:
                chain = Chain(dve, s["vec_step"], i, 3 * T)
                dve.wait_ge(s["y_done"], i + 1)
                for t in range(T):
                    b = i * T + t
                    chain.link(dve.tensor_tensor(core.x[:, b, :], core.x[:, b, :], yp[:, t, :], ALU.add))
                    last = take_stats(dve, chain, core, b, bn, mv)
                last.then_inc(s["y_added"], 1)
                chain.close()


def wave_attention(nc, core, dram, tag):
    batch, T, NT = core.batch, TILE, TILE * P
    NI, H, PD, NS, DH = batch // T, 8, 16, 33, 16
    W3 = 3 * H
    LINKS = 34 + 14 * T
    with ExitStack() as ctx:
        st = Stage(nc, ctx, tag)
        names = ["w_wave", "b_wave", "w_query", "b_query", "kw", "w_se1", "b_se1", "w_se2", "b_se2", "w_out"]
        w = {n: st.sb(n, list(dram[f"{tag}_{n}"].shape)) for n in names}
        tab = st.sb("tables", list(dram["wave_tables"].shape))
        grid, absgrid, J = tab[:, 0:NS], tab[:, NS:2 * NS], tab[:, 2 * NS:2 * NS + P]
        cent, half_less, A3, B3 = (tab[:, 2 * NS + P + a:2 * NS + P + b] for a, b in ((0, 1), (1, 2), (2, 5), (5, 8)))
        hb1, hb2 = st.sb("half_b_se1", [P // 4, 1]), st.sb("half_b_se2", [P, 1])
        xn, xT = st.sb("xn", [P, T, P]), st.sb("xT", [P, NT])
        th_w, th_q = st.sb("th_wave", [P, T, W3]), st.sb("th_query", [P, T, P])
        wave, wt = st.sb("wave2", [P, T, W3]), st.sb("wave_tanh", [P, T, W3])
        qk = st.sb("qk", [P, T, H])
        fpd, inv = st.sb("fpd", [P, T, 3]), st.sb("inverse", [P, T, 3])
        place, valid, hole, rel, rd, far = (st.sb(n, [P, T, NS]) for n in ("place", "valid", "hole", "rel", "rd", "far"))
        e1, e2 = st.sb("e1", [P, T, H, NS]), st.sb("e2", [P, T, H, NS])
        top, z, norm, slope, bias = (st.sb(n, [P, T, H]) for n in ("top", "z", "norm", "slope", "bias"))
        near, shift = st.sb("near", [P, T, 1]), st.sb("shift", [P, T, 1])
        smp = [st.sb(f"sample{j}", [P, 2, P]) for j in range(2)]
        off = [st.sb(f"off{j}", [P, 2, P]) for j in range(2)]
        flag = [st.sb(f"flag{j}", [P, 2, P]) for j in range(2)]
        dist = [st.sb(f"dist{j}", [P, 2, P]) for j in range(2)]
        E = [st.sb(f"E{j}", [P, H, 2, P]) for j in range(2)]
        A = [st.sb(f"A{j}", [P, H, P]) for j in range(2)]
        AT = [st.sb(f"AT{j}", [P, H, P]) for j in range(2)]
        o, oT = st.sb("o", [P, T, P]), st.sb("oT", [P, NT])
        s1, s1t = st.sb("s1", [P // 4, NT]), st.sb("s1t", [P // 4, NT])
        s2t, yt = st.sb("s2t", [P, NT]), st.sb("yt", [P, T, P])
        bn, mv = st.sb("bn", [P, 6]), st.sb("mv", [P, 2])
        misc, zw, zq, op, s1p = st.ps("misc", [P, NT]), st.ps("zw", [P, T, W3]), st.ps("zq", [P, T, P]), \
            st.ps("op", [P, T, P]), st.ps("s1p", [P // 4, NT])
        yp = st.ps("yp", [P, T, P])
        ptp = [st.ps(f"ptp{a}", [P, 4, P]) for a in range(2)]
        s = {n: st.sem(n) for n in (
            "loaded", "once", "consts", "xn_ready", "xt_done", "xt_ready", "z_done", "th_ready", "wave_ready", "wt_ready",
            "e1_ready", "e1_exp", "dist_ready", "E_ready", "A_ready", "at_done", "at_ready", "pv_done",
            "o_ready", "ot_done", "ot_ready", "s1_done", "s1_ready", "s1_used", "s2_done", "s2_ready", "g_ready",
            "y_done", "yt_ready", "y_added", "vec_step")}
        n_loads = 16 * (len(names) + 1)
        block = ctx.enter_context(nc.Block())

        @block.sync
        def _(sp):
            for n in names:
                sp.dma_start(w[n][tuple(slice(None) for _ in w[n].shape)], dram[f"{tag}_{n}"]).then_inc(s["loaded"], 16)
            sp.dma_start(tab[:, :], dram["wave_tables"]).then_inc(s["loaded"], 16)
            sp.wait_ge(s["loaded"], n_loads)

        @block.vector
        def _(dve):
            dve.sem_inc(s["y_added"], 1)
            dve.wait_ge(s["loaded"], n_loads)
            dve.tensor_scalar(hb1[:, :], w["b_se1"][:, :], 0.5, None, ALU.mult)
            dve.tensor_scalar(hb2[:, :], w["b_se2"][:, :], 0.5, None, ALU.mult).then_inc(s["consts"], 1)

            def tt(out, a, b, op):
                chain.link(dve.tensor_tensor(out, a, b, op))

            def ts(out, a, s1_, s2_, op0, op1=ALU.bypass):
                chain.link(dve.tensor_scalar(out, a, s1_, s2_, op0, op1))

            def stt(out, a, sc, b, op0, op1):
                chain.link(dve.scalar_tensor_tensor(out, a, sc, b, op0, op1))

            def flat(a):
                return a[:, :, :].rearrange("p a b -> p (a b)")

            def waves(i):
                dve.wait_ge(s["th_ready"], i + 1)
                dve.scalar_tensor_tensor(flat(wave), flat(th_w), 1.0, zw[:, :, :].rearrange("p a b -> p (a b)"),
                                         ALU.add, ALU.mult).then_inc(s["wave_ready"], 1)
                stt(flat(th_q), flat(th_q), 1.0, zq[:, :, :].rearrange("p a b -> p (a b)"), ALU.add, ALU.mult)
                q = flat(th_q).rearrange("p (x d) -> p x d", d=PD)
                tt(q, q, spread(w["kw"][:, :], 1, T * H), ALU.mult)
                chain.link(dve.tensor_reduce(flat(qk), q, AX.X, ALU.add))
                ts(qk[:, :, :], qk[:, :, :], 0.5 * PD ** -0.5, None, ALU.mult)
                dve.wait_ge(s["wt_ready"], i + 1)
                chain.link(dve.tensor_reduce(fpd[:, :, :], wt[:, :, :].rearrange("p t (a h) -> p t a h", a=3), AX.X, ALU.add))
                tt(fpd[:, :, :], fpd[:, :, :], spread(A3, 1, T), ALU.mult)
                tt(fpd[:, :, :], fpd[:, :, :], spread(B3, 1, T), ALU.add)
                ts(fpd[:, :, 2:3], fpd[:, :, 2:3], 0.1, None, ALU.max)
                chain.link(dve.reciprocal(inv[:, :, 0:3:2], fpd[:, :, 0:3:2]))

            def samples(i):
                f, ph, rdec = (spread(a, 2, NS) for a in (fpd[:, :, 0], fpd[:, :, 1], inv[:, :, 2]))
                tt(place[:, :, :], spread(grid, 1, T), f, ALU.mult)
                ts(place[:, :, :], place[:, :, :], cent, None, ALU.add)
                tt(place[:, :, :], place[:, :, :], ph, ALU.add)
                ts(hole[:, :, :], place[:, :, :], 0.0, None, ALU.is_ge)
                stt(flat(valid), flat(place), float(P), flat(hole), ALU.is_lt, ALU.mult)
                ts(hole[:, :, :], valid[:, :, :], -1.0, 1e30, ALU.add, ALU.mult)
                tt(rel[:, :, :], spread(absgrid, 1, T), f, ALU.mult)
                tt(rd[:, :, :], rel[:, :, :], rdec, ALU.mult)
                tt(far[:, :, :], rel[:, :, :], hole[:, :, :], ALU.subtract)
                chain.link(dve.tensor_reduce(near[:, :, 0], far[:, :, :], AX.X, ALU.min))
                tt(e1[:, :, :, :], spread(qk[:, :, :], 3, NS), spread(rel[:, :, :], 2, H), ALU.mult)
                tt(e1[:, :, :, :], e1[:, :, :, :], spread(hole[:, :, :], 2, H), ALU.add)
                chain.link(dve.tensor_reduce(top[:, :, :], e1[:, :, :, :], AX.X, ALU.max))
                tt(e1[:, :, :, :], e1[:, :, :, :], spread(top[:, :, :], 3, NS), ALU.subtract)
                dve.tensor_tensor(e2[:, :, :, :], e1[:, :, :, :], spread(rd[:, :, :], 2, H), ALU.subtract)\
                   .then_inc(s["e1_ready"], 1)
                tt(slope[:, :, :], qk[:, :, :], spread(inv[:, :, 2], 2, H), ALU.subtract)
                tt(bias[:, :, :], slope[:, :, :], spread(near[:, :, 0], 2, H), ALU.mult)
                tt(bias[:, :, :], bias[:, :, :], top[:, :, :], ALU.subtract)
                ts(shift[:, :, 0], fpd[:, :, 1], -1.0, half_less, ALU.mult, ALU.add)
                tt(shift[:, :, 0], shift[:, :, 0], inv[:, :, 0], ALU.mult)
                ts(shift[:, :, 0], shift[:, :, 0], -0.5, None, ALU.add)

            def sums(i):
                dve.wait_ge(s["e1_exp"], i + 1)
                chain.link(dve.tensor_reduce(z[:, :, :], e1[:, :, :, :], AX.X, ALU.add))
                chain.link(dve.tensor_reduce(norm[:, :, :], e2[:, :, :, :], AX.X, ALU.add))
                stt(flat(norm), flat(z), 1e-8, flat(norm), ALU.mult, ALU.add)
                chain.link(dve.reciprocal(norm[:, :, :], norm[:, :, :]))

            def spots(i, t):
                j = t % 2
                f, ph = fpd[:, t, 0:1], fpd[:, t, 1:2]
                ts(smp[j][:, 0, :], J, inv[:, t, 0:1], shift[:, t, :], ALU.mult, ALU.add)
                ts(smp[j][:, 0, :], smp[j][:, 0, :], MAGIC, -MAGIC, ALU.add, ALU.add)
                ts(smp[j][:, 1, :], smp[j][:, 0, :], 1.0, None, ALU.add)
                ts(off[j][:, :, :], smp[j][:, :, :], f, cent, ALU.mult, ALU.add)
                for k in range(2):
                    last = dve.scalar_tensor_tensor(off[j][:, k, :], off[j][:, k, :], ph, J, ALU.add, ALU.subtract)
                chain.link(last)
                stt(smp[j][:, :, :], smp[j][:, :, :], -1.0, smp[j][:, :, :], ALU.mult, ALU.max)
                if t >= 2:
                    dve.wait_ge(s["A_ready"], i * T + (t - 1))
                ts(flag[j][:, :, :], off[j][:, :, :], 0.0, None, ALU.is_ge)
                stt(flag[j][:, :, :], off[j][:, :, :], 1.0, flag[j][:, :, :], ALU.is_lt, ALU.mult)
                stt(flag[j][:, :, :], smp[j][:, :, :], float(NS // 2), flag[j][:, :, :], ALU.is_le, ALU.mult)
                ts(smp[j][:, :, :], smp[j][:, :, :], f, near[:, t, :], ALU.mult, ALU.subtract)
                if t >= 2:
                    dve.wait_ge(s["E_ready"], i * T + (t - 1))
                dve.tensor_tensor(dist[j][:, :, :], smp[j][:, :, :], flag[j][:, :, :], ALU.mult).then_inc(s["dist_ready"], 1)

            def matrix(i, t):
                j = t % 2
                dve.wait_ge(s["E_ready"], i * T + (t + 1))
                tt(E[j][:, :, :, :].rearrange("p h k j -> p h (k j)"), E[j][:, :, :, :].rearrange("p h k j -> p h (k j)"),
                   spread(flag[j][:, :, :].rearrange("p k j -> p (k j)"), 1, H), ALU.mult)
                if t >= 2:
                    dve.wait_ge(s["at_done"], (i * T + (t - 1)) * 2)
                dve.tensor_tensor(A[j][:, :, :], E[j][:, :, 0, :], E[j][:, :, 1, :], ALU.add).then_inc(s["A_ready"], 1)

            with dve.Fori(0, NI) as i:
                chain = Chain(dve, s["vec_step"], i, LINKS)
                waves(i)
                samples(i)
                spots(i, 0)
                spots(i, 1)
                sums(i)
                for t in range(T):
                    matrix(i, t)
                    if t + 2 < T:
                        spots(i, t + 2)
                dve.wait_ge(s["pv_done"], i * T + T)
                dve.tensor_tensor(o[:, :, :].rearrange("p t (h d) -> p (t h) d", h=H),
                                  op[:, :, :].rearrange("p t (h d) -> p (t h) d", h=H), spread(flat(norm), 2, DH), ALU.mult)\
                   .then_inc(s["o_ready"], 1)
                dve.wait_ge(s["s1_ready"], i + 1)
                dve.scalar_tensor_tensor(s1[:, :], s1t[:, :], 1.0, s1[:, :], ALU.add, ALU.mult).then_inc(s["s1_used"], 1)
                dve.wait_ge(s["s2_ready"], i + 1)
                dve.scalar_tensor_tensor(oT[:, :], s2t[:, :], 1.0, oT[:, :], ALU.add, ALU.mult).then_inc(s["g_ready"], 1)
                dve.wait_ge(s["yt_ready"], i + 1)
                stt(flat(yt), flat(yt), 1.0, yp[:, :, :].rearrange("p a b -> p (a b)"), ALU.add, ALU.mult)
                for t in range(T):
                    b = i * T + t
                    stt(core.x[:, b, :], yt[:, t, :], 0.25, core.x[:, b, :], ALU.mult, ALU.add)
                    last = take_stats(dve, chain, core, b, bn, mv)
                last.then_inc(s["y_added"], 1)
                chain.close()

        @block.scalar
        def _(act):
            act.wait_ge(s["consts"], 1)
            with act.Fori(0, NI) as i:
                act.wait_ge(s["y_added"], i + 1)
                for t in range(T):
                    b = i * T + t
                    last = act.activation(xn[:, t, :], core.x[:, b, :], ACT.Identity, bias=core.nmr[:, b, :],
                                          scale=core.rstd[:, b, :])
                last.then_inc(s["xn_ready"], 1)
                act.wait_ge(s["xt_done"], i + 1)
                act.activation(xT[:, :], misc[:, :], ACT.Copy).then_inc(s["xt_ready"], 1)
                act.wait_ge(s["z_done"], i + 1)
                act.activation(th_w[:, :, :], zw[:, :, :], ACT.Tanh, scale=0.5)
                act.activation(th_q[:, :, :], zq[:, :, :], ACT.Tanh, scale=0.5).then_inc(s["th_ready"], 1)
                act.wait_ge(s["wave_ready"], i + 1)
                w3, t3 = (a[:, :, :].rearrange("p t (a h) -> p t a h", a=3) for a in (wave, wt))
                for a, sc in ((0, 0.25), (2, 0.25), (1, 0.5)):
                    last = act.activation(t3[:, :, a, :], w3[:, :, a, :], ACT.Tanh, scale=sc)
                last.then_inc(s["wt_ready"], 1)
                act.wait_ge(s["e1_ready"], i + 1)
                act.activation(e1[:, :, :, :], e1[:, :, :, :], ACT.Exp)
                act.activation(e2[:, :, :, :], e2[:, :, :, :], ACT.Exp).then_inc(s["e1_exp"], 1)

                def exps(t):
                    j = t % 2
                    act.wait_ge(s["dist_ready"], i * T + (t + 1))
                    if t >= 2:
                        act.wait_ge(s["A_ready"], i * T + (t - 1))
                    for h in range(H):
                        last = act.activation(E[j][:, h, :, :], dist[j][:, :, :], ACT.Exp, bias=bias[:, t, h:h + 1],
                                              scale=slope[:, t, h:h + 1])
                    last.then_inc(s["E_ready"], 1)

                def copies(t):
                    j = t % 2
                    for a in range(2):
                        act.wait_ge(s["at_done"], (i * T + t) * 2 + (a + 1))
                        act.activation(AT[j][:, 4 * a:4 * a + 4, :], ptp[a][:, :, :], ACT.Copy).then_inc(s["at_ready"], 1)

                exps(0)
                for t in range(T):
                    if t + 1 < T:
                        exps(t + 1)
                    copies(t)
                act.wait_ge(s["ot_done"], i + 1)
                act.activation(oT[:, :], misc[:, :], ACT.Copy).then_inc(s["ot_ready"], 1)
                act.wait_ge(s["s1_done"], i + 1)
                act.activation(s1t[:, :], s1p[:, :], ACT.Tanh, scale=0.5, bias=hb1[:, :])
                act.activation(s1[:, :], s1p[:, :], ACT.Identity, bias=w["b_se1"][:, :]).then_inc(s["s1_ready"], 1)
                act.wait_ge(s["s2_done"], i + 1)
                act.activation(s2t[:, :], yp[:, :, :].rearrange("p a b -> p (a b)"), ACT.Tanh, scale=0.25, bias=hb2[:, :])\
                   .then_inc(s["s2_ready"], 1)
                act.wait_ge(s["y_done"], i + 1)
                act.activation(yt[:, :, :], yp[:, :, :], ACT.Tanh, scale=0.25).then_inc(s["yt_ready"], 1)

        @block.tensor
        def _(pe):
            pe.wait_ge(s["consts"], 1)

            def mm(out, lhsT, rhs, start=True, stop=True):
                return pe.matmul(out, lhsT, rhs, start=start, stop=stop)

            with pe.Fori(0, NI) as i:
                pe.wait_ge(s["xn_ready"], i + 1)
                for t in range(T):
                    last = pe.transpose(misc[:, t * P:(t + 1) * P], xn[:, t, :], core.ident[:, :])
                last.then_inc(s["xt_done"], 1)
                pe.wait_ge(s["xt_ready"], i + 1)
                for t in range(T):
                    mm(zw[:, t, :], xT[:, t * P:(t + 1) * P], w["w_wave"][:, :], stop=False)
                    mm(zw[:, t, :], core.ones[0:1, :], w["b_wave"][0:1, :], start=False)
                    mm(zq[:, t, :], xT[:, t * P:(t + 1) * P], w["w_query"][:, :], stop=False)
                    last = mm(zq[:, t, :], core.ones[0:1, :], w["b_query"][0:1, :], start=False)
                last.then_inc(s["z_done"], 1)
                for t in range(T):
                    j = t % 2
                    pe.wait_ge(s["A_ready"], i * T + (t + 1))
                    for a in range(2):
                        if t:
                            pe.wait_ge(s["at_ready"], (i * T + (t - 1)) * 2 + (a + 1))
                        for h in range(4):
                            last = pe.transpose(ptp[a][:, h, :], A[j][:, 4 * a + h, :], core.ident[:, :])
                        last.then_inc(s["at_done"], 1)
                    pe.wait_ge(s["at_ready"], (i * T + t) * 2 + 2)
                    for h in range(H):
                        last = mm(op[:, t, h * DH:(h + 1) * DH], AT[j][:, h, :], xn[:, t, h * DH:(h + 1) * DH])
                    last.then_inc(s["pv_done"], 1)
                pe.wait_ge(s["o_ready"], i + 1)
                for t in range(T):
                    last = pe.transpose(misc[:, t * P:(t + 1) * P], o[:, t, :], core.ident[:, :])
                last.then_inc(s["ot_done"], 1)
                pe.wait_ge(s["ot_ready"], i + 1)
                mm(s1p[:, :], w["w_se1"][:, :], oT[:, :]).then_inc(s["s1_done"], 1)
                pe.wait_ge(s["s1_used"], i + 1)
                mm(yp[:, :, :].rearrange("p a b -> p (a b)"), w["w_se2"][:, :], s1[:, :]).then_inc(s["s2_done"], 1)
                pe.wait_ge(s["g_ready"], i + 1)
                for t in range(T):
                    last = mm(yp[:, t, :], oT[:, t * P:(t + 1) * P], w["w_out"][:, :])
                last.then_inc(s["y_done"], 1)


STAGES = ["L0_attn", "L0_xattn", "L0_ffn", "L1_attn", "L1_xattn", "L1_ffn",
          "L2_attn", "L2_xattn", "L2_ffn", "L3_attn", "L3_xattn", "L3_ffn"]

MLP_KINDS = {"L0_ffn": "moe0", "L2_ffn": "plain", "L3_ffn": "moe3"}


def decoder_kernel(nc, dram, batch, stages=STAGES):
    with ExitStack() as ctx:
        core = Core(nc, ctx, batch)
        load_everything(nc, core, dram)
        for tag in stages:
            norm_scalars(nc, core, tag, LN_EPS if tag in ("L2_ffn", "L3_xattn") else None)
            if tag == "L0_attn":
                softmax_attention(nc, core, dram, tag, heads_norm=True)
            elif tag == "L0_xattn":
                softmax_attention(nc, core, dram, tag, context="past")
            elif tag == "L1_xattn":
                softmax_attention(nc, core, dram, tag, context="only")
            elif tag == "L3_attn":
                softmax_attention(nc, core, dram, tag, latent=True)
            elif tag == "L1_ffn":
                quantised_mlp(nc, core, dram, tag)
            elif tag == "L2_xattn":
                query_softmax_attention(nc, core, dram, tag)
            elif tag == "L3_xattn":
                wide_cross_attention(nc, core, dram, tag)
            elif tag == "L2_attn":
                delta_rule_attention(nc, core, dram, tag)
            elif tag == "L1_attn":
                wave_attention(nc, core, dram, tag)
            elif tag in MLP_KINDS:
                mlp_stage(nc, core, dram, tag, MLP_KINDS[tag])
        store_everything(nc, core, dram)


def head_slots(w):
    out = np.zeros((w.shape[0], GROUPS, 4, SLOT), w.dtype)
    out[..., :HD] = w.reshape(w.shape[0], 4, GROUPS, HD).transpose(0, 2, 1, 3)
    return out.reshape(w.shape[0], HEADS * SLOT)


def slot_column(value):
    out = np.zeros((HEADS, SLOT), np.float32)
    out[:, HD] = value
    return out.reshape(HEADS * SLOT)


def layout(x):
    a = {"x": x["x"], "ctxT": x["ctx_1024"].transpose(2, 0, 1), "ident": np.eye(P, dtype=np.float32)}
    pos, di = np.arange(P, dtype=np.float32)[:, None], np.arange(0, HD, 2, dtype=np.float32) / HD
    theta = pos * np.exp(-di * np.float32(np.log(10000.0)))
    sin = np.repeat(np.sin(theta), 2, axis=1)
    sin[:, :HD // 2] *= -1
    a["rope"] = np.concatenate([np.repeat(np.cos(theta), 2, axis=1), sin], axis=1).astype(np.float32)
    a["causal"] = np.tile(np.triu(np.full((P, P), -1e30, np.float32), 1), (1, 4))
    a["decay"] = np.exp(-0.01 * 0.01 * np.abs(pos - pos.T)).astype(np.float32)
    a["row_c"] = np.concatenate([np.eye(2, dtype=np.float32), np.tile(np.arange(SC, dtype=np.float32), (2, 1))], axis=1)
    a["lens"] = x["_lenS2"]
    a["key_mask"] = x["mask_BxS2_bf1"].view(np.uint8)

    t = "L0_attn_"
    a[t + "w_qkv"] = np.concatenate([x[t + n].T for n in ("Wq", "Wk", "Wv")], axis=1)
    a[t + "gb"] = np.tile(np.concatenate([x[t + n] for n in ("q_gamma", "k_gamma", "q_beta", "k_beta")]), (P, 1))
    a[t + "w_o"], a[t + "b_o"] = x[t + "Wo"].T, x[t + "bo"][None]

    t = "L0_xattn_"
    a[t + "w_q"], a[t + "w_k"] = head_slots(x[t + "wq"].T), head_slots(x[t + "wk"].T)
    a[t + "b_q"] = slot_column(1.0).reshape(GROUPS, P).T
    a[t + "w_kc"] = head_slots(a["ident"])
    a[t + "aux"] = np.stack([slot_column(0.0), slot_column(-1e30)])
    a[t + "w_v"], a[t + "w_vc"] = x[t + "wv"].T, a["ident"]
    a[t + "w_o"], a[t + "b_o"] = x[t + "wo"].T, x[t + "bo"][None]

    t = "L1_xattn_"
    a[t + "w_q"], a[t + "w_kc"] = head_slots(x[t + "Wq"].T), head_slots(x[t + "Wk"].T)
    bq = head_slots(x[t + "bq"][None])[0]
    bq.reshape(HEADS, SLOT)[:, HD] = 1.0
    a[t + "b_q"] = bq.reshape(GROUPS, P).T
    a[t + "aux"] = np.stack([head_slots(x[t + "bk"][None])[0], slot_column(-1e8 * HD ** 0.5)])
    a[t + "w_vc"], a[t + "b_v"] = x[t + "Wv"].T, x[t + "bv"][None]
    a[t + "w_o"], a[t + "b_o"] = x[t + "Wo"].T, x[t + "bo"][None]

    t = "L3_attn_"
    a[t + "w_q"] = head_slots(x[t + "Wq"])
    a[t + "w_kv"] = np.concatenate([x[t + "Wk"], x[t + "Wv"]], axis=1)
    a[t + "w_down"], a[t + "w_k"], a[t + "w_up_v"] = x[t + "W_down_kv"], head_slots(x[t + "W_up_k"]), x[t + "W_up_v"]
    a[t + "w_o"] = x[t + "Wo"]

    def chunks_in(*ws):
        return np.concatenate(ws, axis=1).reshape(P, -1, P)

    def chunks_out(*ws):
        return np.concatenate(ws, axis=0).reshape(-1, P, P).transpose(1, 0, 2)

    def pick(rows, groups):
        owner = np.concatenate([first + np.arange(n * width) // width for first, n, width in groups])
        return (np.arange(rows)[:, None] == owner[None, :]).astype(np.float32).reshape(rows, -1, P)

    t = "L3_xattn_"
    a["ctx"] = x["ctx_1024"]
    a[t + "w_q"], a[t + "w_kv"] = x[t + "Wq"], x[t + "Wkv"]
    a[t + "w_o"], a[t + "b_o"] = x[t + "Wout"].reshape(-1, P, P).transpose(1, 0, 2), x[t + "bout"][None]
    a[t + "ln"] = np.stack([x[t + n] for n in ("g1", "b1", "g2", "b2")], axis=1)

    t = "L2_xattn_"
    a[t + "w_q"], a[t + "b_q"] = head_slots(x[t + "Wq"]), head_slots(x[t + "bq"][None]).reshape(GROUPS, P).T
    a[t + "w_k"] = np.stack([x[t + "Wk1"], x[t + "Wk2"]], axis=1)
    a[t + "b_k"] = np.stack([x[t + "bk1"], x[t + "bk2"]], axis=1)
    a[t + "w_slot"] = head_slots(a["ident"])
    a[t + "unslot"] = a[t + "w_slot"].reshape(P, GROUPS, P).transpose(2, 1, 0).reshape(P, GROUPS * P)
    a[t + "w_v"] = np.stack([x[t + "Wv1"], x[t + "Wv2"]], axis=1)
    a[t + "b_v"] = np.concatenate([x[t + "bv1"], x[t + "bv2"]])[None]
    a[t + "w_qt"], a[t + "b_qt"] = x[t + "Wq"], x[t + "bq"][None]
    a[t + "w_o"], a[t + "b_o"] = x[t + "Wo"], x[t + "bo"][None]
    a[t + "gb"] = np.tile(np.stack([x[t + n] for n in ("g0", "beta0", "g1", "beta1")]), (P, 1, 1))

    t = "L2_attn_"
    a[t + "w_in"] = np.stack([x[t + n].T for n in ("Wq", "Wk", "Wv")], axis=1)
    a[t + "b_in"] = np.stack([x[t + n] for n in ("bq", "bk", "bv")], axis=1)
    a[t + "conv"] = np.stack([np.concatenate([x[f"{t}w{n}_conv"], x[f"{t}b{n}_conv"][:, None]], axis=1) for n in "qkv"], axis=1)
    a[t + "w_beta"] = x[t + "Wbeta"].T
    a[t + "b_beta"] = np.stack([x[t + "bbeta"], np.zeros(HEADS, np.float32), np.zeros(HEADS, np.float32)], axis=1)
    a[t + "head_sum"] = np.repeat(np.eye(HEADS, dtype=np.float32), HD, axis=0)
    a[t + "w_o"], a[t + "b_o"], a[t + "norm_w"] = x[t + "Wo"].T, x[t + "bo"][None], np.tile(x[t + "norm_w"], HEADS)[:, None]

    t = "L1_attn_"
    grid = np.arange(-16, 17, dtype=np.float32)
    tok = np.arange(P, dtype=np.float32)
    a["wave_tables"] = np.concatenate(
        [np.tile(np.concatenate([grid, np.abs(grid), tok]), (P, 1)), tok[:, None], 0.5 - tok[:, None],
         np.tile(np.float32([7.5 / 8, 2.0, 4.75 / 8, 8.5, 0.0, 5.25]), (P, 1))], axis=1).astype(np.float32)
    for n in ("w_wave", "w_query", "w_se1", "w_se2", "w_out"):
        a[t + n] = x[t + n]
    a[t + "b_wave"], a[t + "b_query"] = x[t + "b_wave"][None], x[t + "b_query"][None]
    a[t + "b_se1"], a[t + "b_se2"] = x[t + "b_se1"][:, None], x[t + "b_se2"][:, None]
    a[t + "kw"] = np.tile(x[t + "key_weight"], (P, 1))

    a["lower"] = np.tile(np.tril(np.ones((4, 4), np.float32), -1), (P, 1, 1))
    t = "L0_ffn_"
    for dst, e, sh in (("w_g", "expert_gate", "shared_gate"), ("w_u", "expert_up", "shared_up")):
        a[t + dst] = chunks_in(x[t + e].transpose(2, 0, 1).reshape(P, -1), x[t + sh].T)
    a[t + "w_d"] = chunks_out(x[t + "expert_down"].transpose(0, 2, 1).reshape(-1, P), x[t + "shared_down"].T)
    a[t + "w_r"], a[t + "b_r"] = x[t + "gate_w"].T, np.tile(x[t + "gate_bias"], (P, 1))
    a[t + "pick"] = pick(32, [(0, 32, 64)])

    t = "L3_ffn_"
    pad = np.zeros((P, P // 2), np.float32)
    for n in ("g", "u"):
        full = {"g": "gate", "u": "up"}[n]
        a[t + "w_" + n] = chunks_in(x[t + "w_" + full].transpose(1, 0, 2).reshape(P, -1),
                                    x[t + "anchor_w_" + full].transpose(1, 0, 2).reshape(P, -1),
                                    x[t + "shared_w_" + full], pad)
    a[t + "w_d"] = chunks_out(x[t + "w_down"].reshape(-1, P), x[t + "anchor_w_down"].reshape(-1, P),
                              x[t + "shared_w_down"], pad.T)
    a[t + "w_r"], a[t + "b_r"] = x[t + "gate_weight"].T, np.tile(x[t + "gate_bias"], (P, 1))
    a[t + "pick"] = pick(48, [(0, 32, 64), (32, 16, 32)])

    t = "L1_ffn_"
    a[t + "w"] = np.concatenate([x[t + "w_gate"].reshape(3, P, P).transpose(1, 0, 2),
                                 x[t + "w_up"].reshape(3, P, P).transpose(1, 0, 2), x[t + "w_down"].reshape(P, 3, P)], axis=1)

    t = "L2_ffn_"
    a[t + "q_w_g"], a[t + "q_w_d"] = chunks_in(x[t + "fc1_q"]), chunks_out(x[t + "fc2_q"])
    a[t + "w_g"] = np.tile(x[t + "fc1_scales"].reshape(1, -1, P), (P, 1, 1))
    a[t + "w_d"] = np.tile(x[t + "fc2_scales"].reshape(1, -1, P), (P, 1, 1))
    a[t + "b_g"], a[t + "b_d"] = x[t + "fc1_bias"].reshape(-1, P).T, x[t + "fc2_bias"][None]
    a[t + "ln_g"], a[t + "ln_b"] = x[t + "ln_gamma"][:, None], x[t + "ln_beta"][:, None]
    return a


def kernel(**inputs):
    import concourse.bacc as bacc
    from concourse.bass_utils import run_bass_kernel_spmd

    arrays = {n: np.ascontiguousarray(v) for n, v in layout({n: np.asarray(v) for n, v in inputs.items()}).items()}
    nc = bacc.Bacc("TRN2", target_bir_lowering=False, num_devices=1)
    dram = {n: nc.dram_tensor("in_" + n, v.shape, mybir.dt.from_np(v.dtype), kind="ExternalInput").ap()
            for n, v in arrays.items()}
    shape = inputs["x"].shape
    dram["out"] = nc.dram_tensor("out", shape, F32, kind="ExternalOutput").ap()
    decoder_kernel(nc, dram, shape[0])
    r = run_bass_kernel_spmd(nc, [{"in_" + n: v for n, v in arrays.items()}], core_ids=[0])
    return r.results[0]["out"]
```

```python
from contextlib import ExitStack

import concourse.bass as bass
import numpy as np
from concourse import mybir

F32 = mybir.dt.float32
BF16 = mybir.dt.bfloat16
I32 = mybir.dt.int32
I16 = mybir.dt.int16
U8 = mybir.dt.uint8
ALU = mybir.AluOpType
ACT = mybir.ActivationFunctionType
AX = mybir.AxisListType

P = 128
SC = 77
UNITS = 2
HEADS = 16
HD = 8
SLOT = 32
GROUPS = HEADS * SLOT // P
BANK = 512
LN_EPS = 1e-5


def spread(ap, axis, size):
    shape = list(ap.shape)
    return ap.unsqueeze(axis).broadcast_to(shape[:axis] + [size] + shape[axis:])


class Chain:

    def __init__(self, eng, sem, i=0, per_iteration=0):
        self.eng, self.sem, self.base, self.per, self.k = eng, sem, i * per_iteration, per_iteration, 0

    def link(self, ins):
        self.k += 1
        ins.then_inc(self.sem, 1)
        self.eng.wait_ge(self.sem, self.base + self.k)

    def close(self):
        assert self.k == self.per, (self.k, self.per)


class Stage:

    def __init__(self, nc, ctx, tag):
        self.nc, self.ctx, self.tag, self.sems = nc, ctx, tag, []
        ctx.callback(self.clear)

    def clear(self):
        self.nc.clear_and_free_semaphores(self.sems)
        self.nc.all_engine_barrier()

    def sb(self, name, shape, dt=F32):
        return self.ctx.enter_context(self.nc.sbuf_tensor(f"{self.tag}_{name}", shape, dt))

    def ps(self, name, shape, dt=F32):
        return self.ctx.enter_context(self.nc.psum_tensor(f"{self.tag}_{name}", shape, dt))

    def sem(self, name):
        self.sems.append(self.nc.alloc_semaphore(f"{self.tag}_{name}"))
        return self.sems[-1]


class Core:

    def __init__(self, nc, ctx, batch):
        def sb(name, shape, dt=F32):
            return ctx.enter_context(nc.sbuf_tensor(name, shape, dt))

        self.nc, self.batch = nc, batch
        self.x = sb("x_all", [P, batch, P])
        self.stat = sb("stat_all", [P, batch, 2])
        self.rstd = sb("rstd_all", [P, batch, 1])
        self.rstd2 = sb("rstd2_all", [P, batch, 1])
        self.nmr2 = sb("nmr2_all", [P, batch, 1])
        self.nmr = sb("nmr_all", [P, batch, 1])
        self.ctxT = sb("ctxT", [P, batch, SC])
        self.ident = sb("ident", [P, P])
        self.beat = sb("beat", [1, 1])
        self.ones = sb("ones", [1, P])


def load_everything(nc, core, dram):
    with ExitStack() as ctx:
        st = Stage(nc, ctx, "load")
        x_in, c_in, stats_step = st.sem("x_in"), st.sem("c_in"), st.sem("stats_step")
        bn = st.sb("bn", [P, 8, 6])
        mv = st.sb("mv", [P, 8, 2])
        block = ctx.enter_context(nc.Block())

        @block.sync
        def _(sp):
            sp.dma_start(core.x[:, :, :], dram["x"].rearrange("b t d -> t b d")).then_inc(x_in, 16)
            sp.wait_ge(x_in, 16)

        @block.scalar
        def _(act):
            act.dma_start(core.ctxT[:, :, :], dram["ctxT"]).then_inc(c_in, 16)
            act.dma_start(core.ident[:, :], dram["ident"]).then_inc(c_in, 16)
            act.dma_start(core.ones[:, :], dram["ident"][0:1, :]).then_inc(c_in, 16)
            act.wait_ge(c_in, 48)

        @block.vector
        def _(dve):
            dve.wait_ge(c_in, 48)
            nc.vector.memset(core.ones[:, :], 1.0)
            dve.wait_ge(x_in, 16)
            with dve.Fori(0, core.batch // 8) as i:
                chain = Chain(dve, stats_step, i, 3)
                take_tile_stats(dve, chain, core.x, core.stat, i, 8, bn, mv, core.beat)
                chain.close()


def store_everything(nc, core, dram):
    with ExitStack() as ctx:
        st = Stage(nc, ctx, "store")
        x_out = st.sem("x_out")
        block = ctx.enter_context(nc.Block())

        @block.sync
        def _(sp):
            sp.dma_start(dram["out"].rearrange("b t d -> t b d"), core.x[:, :, :]).then_inc(x_out, 16)
            sp.wait_ge(x_out, 16)


def take_stats(dve, chain, core, b, bn, mv):
    dve.memset(core.beat[:, :], 0.0)
    chain.link(dve.bn_stats(bn[:, :], core.x[:, b, :]))
    dve.memset(core.beat[:, :], 0.0)
    chain.link(dve.bn_aggr(mv[:, :], bn[:, :]))
    return dve.tensor_copy(core.stat[:, b, :], mv[:, :])


def take_tile_stats(dve, chain, x, stat, i, size, bn, mv, beat):
    x_tile = x[:, :, :].rearrange("p (i t) f -> p i t f", t=size)
    stat_tile = stat[:, :, :].rearrange("p (i t) s -> p i t s", t=size)
    dve.memset(beat[:, :], 0.0)
    for t in range(size):
        last = dve.bn_stats(bn[:, t, :], x_tile[:, i, t, :])
    chain.link(last)
    dve.memset(beat[:, :], 0.0)
    for t in range(size):
        last = dve.bn_aggr(mv[:, t, :], bn[:, t, :])
    chain.link(last)
    chain.link(dve.tensor_copy(stat_tile[:, i, :, :], mv[:, :, :]))


def norm_scalars(nc, core, tag, second_eps=None):
    with ExitStack() as ctx:
        st = Stage(nc, ctx, tag + "_ln")
        var_ready, std_ready, step, var2_ready, std2_ready = (
            st.sem(n) for n in ("var_ready", "std_ready", "step", "var2_ready", "std2_ready"))
        std = st.sb("std", [P, core.batch])
        var = st.sb("var", [P, core.batch])
        rstd, nmr, rstd2, nmr2 = (a[:, :, 0] for a in (core.rstd, core.nmr, core.rstd2, core.nmr2))
        block = ctx.enter_context(nc.Block())

        @block.scalar
        def _(act):
            act.wait_ge(var_ready, 1)
            act.activation(std[:, :], var[:, :], ACT.Sqrt).then_inc(std_ready, 1)
            if second_eps is not None:
                act.wait_ge(var2_ready, 1)
                act.activation(std[:, :], var[:, :], ACT.Sqrt).then_inc(std2_ready, 1)

        @block.vector
        def _(dve):
            chain = Chain(dve, step)
            dve.tensor_scalar(var[:, :], core.stat[:, :, 1], LN_EPS, None, ALU.add).then_inc(var_ready, 1)
            dve.wait_ge(std_ready, 1)
            chain.link(dve.reciprocal(rstd, std[:, :]))
            chain.link(dve.scalar_tensor_tensor(nmr, core.stat[:, :, 0], -1.0, rstd, ALU.mult, ALU.mult))
            if second_eps is not None:
                chain.link(dve.tensor_tensor(var[:, :], core.stat[:, :, 1], rstd, ALU.mult))
                chain.link(dve.tensor_tensor(var[:, :], var[:, :], rstd, ALU.mult))
                dve.tensor_scalar(var[:, :], var[:, :], second_eps, None, ALU.add).then_inc(var2_ready, 1)
                dve.wait_ge(std2_ready, 1)
                chain.link(dve.reciprocal(std[:, :], std[:, :]))
                dve.tensor_tensor(rstd2, rstd, std[:, :], ALU.mult)
                dve.tensor_tensor(nmr2, nmr, std[:, :], ALU.mult)


def softmax_attention(nc, core, dram, tag, heads_norm=False, context=None, latent=False):
    batch = core.batch
    own = context != "only"
    key_tiles = ([(SC, "ctx")] if context else []) + ([(P, "own")] if own else [])
    NK = sum(n for n, _ in key_tiles)
    CHUNK = min(BANK // NK, 4)
    NCH = HEADS // CHUNK
    K = HD + 1 if context else HD
    blocks = [(h, t) for h in range(CHUNK) for t in range(len(key_tiles))]
    copy_first = own
    scale = 1.0 if latent else float(HD) ** -0.5

    with ExitStack() as ctx:
        st = Stage(nc, ctx, tag)
        U = UNITS

        def unit_sb(name, shape, dt=F32):
            return [st.sb(f"{name}{u}", shape, dt) for u in range(U)]

        names = [n for n in (tag + "_w_qkv", tag + "_w_q", tag + "_b_q", tag + "_w_k", tag + "_w_kc", tag + "_w_v",
                             tag + "_w_vc", tag + "_aux", tag + "_w_o", tag + "_b_o", tag + "_b_v",
                             tag + "_w_kv", tag + "_w_down", tag + "_w_up_v", tag + "_gb") if n in dram]
        shared = (["rope"] if heads_norm else []) + (["decay"] if latent else [])
        w = {n: st.sb(n + "_s", list(dram[n].shape)) for n in names + shared}

        def W(n):
            return w[f"{tag}_{n}"]

        xn, xT = unit_sb("xn", [P, P]), unit_sb("xT", [P, P])
        qT, kT = unit_sb("qT", [P, GROUPS, P]), unit_sb("kT", [P, GROUPS, NK])
        v = [unit_sb(f"v_{kind}", [n, HEADS, SLOT]) for n, kind in key_tiles]
        probs = [unit_sb(f"probs{j}_", [P, CHUNK, NK]) for j in range(2)]
        pT = [unit_sb(f"pT{j}_", [P, 4, P]) for j in range(2)]
        top = unit_sb("top", [P, HEADS])
        rz = unit_sb("rz", [P, HEADS])
        accT = unit_sb("accT", [P, GROUPS, P])
        o, oT = unit_sb("o", [P, P]), unit_sb("oT", [P, P])
        bn, mv = unit_sb("bn", [P, 6]), unit_sb("mv", [P, 2])
        if heads_norm:
            qk = unit_sb("qk", [P, 2, HEADS, HD])
            sq = unit_sb("sq", [P, 2, HEADS, HD])
            rot = unit_sb("rot", [P, 2, HEADS, HD])
            hstat = unit_sb("hstat", [P, 2 * HEADS])
            hvar = unit_sb("hvar", [P, 2 * HEADS])
            hrstd = unit_sb("hrstd", [P, 2 * HEADS])
            minus_half = st.sb("minus_half", [P, 2 * HEADS])
            padded = unit_sb("padded", [P, 2, GROUPS, 4, SLOT])
            ident_b = st.sb("ident_b", [P, P], BF16)
            causal_b = st.sb("causal_b", [P, 4, P], BF16)
        if context:
            rows = st.sb("rows", [2, batch, SC])
            ctxm, ctxu = unit_sb("ctxm", [P, SC]), unit_sb("ctxu", [P, SC])
        if latent:
            kvT, latT = unit_sb("kvT", [P, P]), unit_sb("latT", [SLOT, P])

        scores = [st.ps(f"scores{u}", [P, 2, BANK]) for u in range(U)]
        ptp = [st.ps(f"ptp{j}", [P, 4, P]) for j in range(2)]
        misc = [st.ps(f"misc{u}", [P, BANK]) for u in range(U)]
        A, B2 = slice(0, P), slice(3 * P, 4 * P)

        s = {n: st.sem(n) for n in (
            "loaded", "consts", "rows_step", "rows_ready", "xn_ready", "xt_done", "xt_ready", "vec_step",
            "first_step", "last_step", "scores_done", "shifted", "probs_ready",
            "pt_done", "pt_copied", "pv_done", "acc_ready", "back_done", "o_ready", "ot_done", "ot_ready",
            "y_done", "y_added", "q_done", "q_ready", "k_done", "k_ready", "v_done", "v_ready")}
        if heads_norm:
            s |= {n: st.sem(n) for n in ("proj_done", "var_ready", "square_ready", "centred", "hrstd_ready",
                                         "padded_ready")}
        if context:
            s |= {n: st.sem(n) for n in ("mask_done", "ctxm_ready", "ctxu_ready", "kc_done", "kc_ready",
                                         "vc_done", "vc_ready")}
        if latent:
            s |= {n: st.sem(n) for n in ("kv_done", "kv_ready", "lat_done", "lat_ready")}
        n_loads = len(names) + len(shared) + (2 if context else 0) + (2 if heads_norm else 0)
        mask_raw = st.sb("mask_raw", [2, batch, SC], U8) if context == "only" else None
        len_raw = st.sb("len_raw", [2, batch], I32) if context == "past" else None
        row_c = st.sb("row_c", [2, 2 + SC]) if context else None
        stage_f = st.sb("stage_f", [P, 5 * P]) if heads_norm else None
        len_f = st.sb("len_f", [2, batch]) if context == "past" else None
        len_max = st.sb("len_max", [2, 1]) if context == "past" else None
        keep_less_fill = st.sb("keep_less_fill", [2, 1]) if context == "only" else None
        beyond = st.sb("beyond", [2, SC]) if context == "past" else None
        block = ctx.enter_context(nc.Block())

        def head_of(c, j):
            return (4 * c + j) if CHUNK == 4 else (8 * (c // 4) + 4 * (c % 2) + 2 * (c // 2 % 2) + j)

        def count(b, per=1, extra=1):
            i, at = b
            return at * per + extra if i is None else i * (U * per) + (at * per + extra)

        def number(b):
            return count(b, 1, 0)

        def neighbour(b, d):
            return (b[0], b[1] + d)

        def step_of(k):
            return k * 4 // NCH if k * 4 % NCH == 0 else None

        @block.sync
        def _(sp):
            for n in names + shared:
                sp.dma_start(w[n][tuple(slice(None) for _ in dram[n].shape)], dram[n]).then_inc(s["loaded"], 16)
            if context:
                sp.dma_start(row_c[:, :], dram["row_c"]).then_inc(s["loaded"], 16)
                if context == "only":
                    src = dram["key_mask"].rearrange("(a b) t -> a b t", a=1).broadcast_to([2, batch, SC])
                    sp.dma_start(mask_raw[:, :, :], src).then_inc(s["loaded"], 16)
                else:
                    src = dram["lens"].rearrange("(a b) -> a b", a=1).broadcast_to([2, batch])
                    sp.dma_start(len_raw[:, :], src).then_inc(s["loaded"], 16)
            if heads_norm:
                sp.dma_start(stage_f[:, 0:P], dram["ident"]).then_inc(s["loaded"], 16)
                sp.dma_start(stage_f[:, P:5 * P], dram["causal"]).then_inc(s["loaded"], 16)
            sp.wait_ge(s["loaded"], 16 * n_loads)

        @block.gpsimd
        def _(pool):
            if not heads_norm:
                return
            pool.wait_ge(s["consts"], 1)
            with pool.Fori(0, batch // U) as i:
                for u in range(U):
                    pool.wait_ge(s["var_ready"], i * U + (u + 1))
                    pool.tensor_tensor(hrstd[u][:, :], hvar[u][:, :], minus_half[:, :], ALU.pow)\
                        .then_inc(s["hrstd_ready"], 1)

        @block.vector
        def _(dve):
            once = Chain(dve, s["rows_step"])
            for tile in v:
                for u in range(U):
                    once.link(dve.memset(tile[u][:, :, :], 0.0))
                    dve.memset(tile[u][:, :, HD:HD + 1], 1.0)
            dve.wait_ge(s["loaded"], 16 * n_loads)
            if heads_norm:
                for u in range(U):
                    dve.memset(padded[u][:, :, :, :, :], 0.0)
                dve.memset(minus_half[:, :], -0.5)
                dve.tensor_copy(ident_b[:, :], stage_f[:, 0:P])
                once.link(dve.tensor_copy(causal_b[:, :, :].rearrange("p a b -> p (a b)"), stage_f[:, P:5 * P]))
            if context == "only":
                once.link(dve.tensor_tensor(keep_less_fill[:, :], row_c[:, 0:1], row_c[:, 1:2], ALU.subtract))
                once.link(dve.tensor_copy(rows[:, :, :], mask_raw[:, :, :]))
                once.link(dve.tensor_scalar(rows[:, :, :], rows[:, :, :], keep_less_fill[:, :], row_c[:, 1:2],
                                            ALU.mult, ALU.add))
            if context == "past":
                pos = row_c[:, 2:2 + SC]
                once.link(dve.tensor_copy(len_f[:, :], len_raw[:, :]))
                once.link(dve.tensor_reduce(len_max[:, :], len_f[:, :], AX.X, ALU.max))
                once.link(dve.tensor_scalar(beyond[:, :], pos, len_max[:, :], row_c[:, 1:2], ALU.is_ge, ALU.mult))
                once.link(dve.tensor_tensor(rows[:, :, :], spread(pos, 1, batch), spread(len_f[:, :], 2, SC), ALU.is_lt))
                once.link(dve.tensor_scalar(rows[:, :, :], rows[:, :, :], row_c[:, 0:1], None, ALU.mult))
                once.link(dve.tensor_tensor(rows[:, :, :], rows[:, :, :], spread(beyond[:, :], 1, batch), ALU.add))
            dve.sem_inc(s["rows_ready"], 1)
            dve.drain().then_inc(s["consts"], 1)

            def shift(chain, b, c, u):
                dve.wait_ge(s["scores_done"], count(b, NCH, c + 1))
                S = scores[u][:, c % 2, 0:CHUNK * NK].rearrange("p (h k) -> p h k", h=CHUNK)
                tp = top[u][:, c * CHUNK:(c + 1) * CHUNK]
                dst = probs[c % 2][u][:, :, :]
                if latent:
                    chain.link(dve.tensor_scalar(dst, S, -1e4, 1e4, ALU.max, ALU.min))
                    chain.link(dve.tensor_tensor(dst, dst, spread(w["decay"][:, :], 1, CHUNK), ALU.mult))
                    S = dst
                chain.link(dve.tensor_reduce(tp, S, AX.X, ALU.max))
                dve.tensor_tensor(dst, S, spread(tp, 2, NK), ALU.subtract).then_inc(s["shifted"], 1)

            def finish(chain, b, u):
                dve.wait_ge(s["back_done"], count(b))
                acc = misc[u][:, :].rearrange("p (g r f) -> p g r f", g=GROUPS, f=SLOT)
                by_group = rz[u][:, :].rearrange("p (g r) -> p g r", g=GROUPS)
                chain.link(dve.reciprocal(by_group, acc[:, :, :, HD]))
                dve.tensor_tensor(o[u][:, :].rearrange("p (r g f) -> p g r f", g=GROUPS, f=HD), acc[:, :, :, 0:HD],
                                  spread(by_group, 3, HD), ALU.mult).then_inc(s["o_ready"], 1)

            def head_norm(chain, b, u):
                acc = scores[u][:, 0, 0:2 * P].rearrange("p (a h f) -> p a h f", a=2, h=HEADS)
                hs = hstat[u][:, :].rearrange("p (a h) -> p a h", a=2)
                dve.wait_ge(s["proj_done"], count(b))
                chain.link(dve.tensor_reduce(hs, acc, AX.X, ALU.add))
                chain.link(dve.tensor_scalar(hstat[u][:, :], hstat[u][:, :], 1.0 / HD, None, ALU.mult))
                chain.link(dve.tensor_tensor(qk[u][:, :, :, :], acc, spread(hs, 3, HD), ALU.subtract))
                chain.link(dve.tensor_tensor(sq[u][:, :, :, :], qk[u][:, :, :, :], qk[u][:, :, :, :], ALU.mult))
                chain.link(dve.tensor_reduce(hs, sq[u][:, :, :, :], AX.X, ALU.add))
                dve.tensor_scalar(hvar[u][:, :], hstat[u][:, :], 1.0 / HD, LN_EPS, ALU.mult, ALU.add)\
                   .then_inc(s["var_ready"], 1)

            def rotate(chain, b, u):
                flat = qk[u][:, :, :, :].rearrange("p a h f -> p (a h) f")
                gb = W("gb")[:, :].rearrange("p (s a f) -> p s a f", s=2, a=2)
                dve.wait_ge(s["hrstd_ready"], count(b))
                chain.link(dve.tensor_tensor(flat, flat, spread(hrstd[u][:, :], 2, HD), ALU.mult))
                for a in range(2):
                    chain.link(dve.tensor_tensor(qk[u][:, a, :, :], qk[u][:, a, :, :],
                                                 spread(gb[:, 0, a, :], 1, HEADS), ALU.mult))
                    chain.link(dve.tensor_tensor(qk[u][:, a, :, :], qk[u][:, a, :, :],
                                                 spread(gb[:, 1, a, :], 1, HEADS), ALU.add))
                cos, sin = w["rope"][:, 0:HD], w["rope"][:, HD:2 * HD]
                r = rot[u][:, :, :, :].rearrange("p a h f -> p (a h) f")
                dve.tensor_tensor(r[:, :, 0:HD // 2], flat[:, :, 1:HD:2], spread(sin[:, 0:HD // 2], 1, 2 * HEADS), ALU.mult)
                dve.tensor_tensor(r[:, :, HD // 2:HD], flat[:, :, 0:HD:2], spread(sin[:, HD // 2:HD], 1, 2 * HEADS), ALU.mult)
                chain.link(dve.tensor_tensor(sq[u][:, :, :, :].rearrange("p a h f -> p (a h) f"), flat,
                                             spread(cos, 1, 2 * HEADS), ALU.mult))
                for a in range(2):
                    last = dve.tensor_tensor(padded[u][:, a, :, :, 0:HD].rearrange("p g r f -> p r g f"),
                                             sq[u][:, a, :, :].rearrange("p (r g) f -> p r g f", g=GROUPS),
                                             rot[u][:, a, :, :].rearrange("p (r g) f -> p r g f", g=GROUPS), ALU.add)
                last.then_inc(s["padded_ready"], 1)

            def residual(chain, b, u):
                dve.wait_ge(s["y_done"], count(b))
                n = number(b)
                chain.link(dve.tensor_tensor(core.x[:, n, :], core.x[:, n, :], misc[u][:, B2], ALU.add))
                take_stats(dve, chain, core, n, bn[u], mv[u]).then_inc(s["y_added"], 1)

            def mask_context(b, u):
                dve.wait_ge(s["mask_done"], count(b))
                dve.tensor_tensor(ctxm[u][:, :], scores[u][:, 1, 0:SC], core.ctxT[:, number(b), :], ALU.mult)\
                   .then_inc(s["ctxm_ready"], 1)

            def copy_q(b, u):
                dve.wait_ge(s["q_done"], count(b))
                acc = scores[u][:, 0, :].rearrange("p (g t) -> p g t", g=GROUPS)
                if context:
                    last = dve.tensor_tensor(qT[u][:, :, :], acc, spread(W("b_q")[:, :], 2, P), ALU.add)
                elif latent:
                    last = dve.tensor_scalar(qT[u][:, :, :], acc, 1.0 / (float(np.sqrt(np.float32(P))) + 1e-8), None,
                                             ALU.mult)
                else:
                    last = dve.tensor_copy(qT[u][:, :, :], acc)
                last.then_inc(s["q_ready"], 1)

            def front(chain, b, u, step):
                if step == 0 and context:
                    mask_context(b, u)
                if step == 0 and heads_norm:
                    head_norm(chain, b, u)
                if step == 1 and not heads_norm:
                    copy_q(b, u)
                if step == 3 and heads_norm:
                    rotate(chain, b, u)

            def attend(chain, b, u, tail=True, start_next=True):
                before, behind, other = neighbour(b, -1), neighbour(b, 1), 1 - u
                for c in range(NCH):
                    shift(chain, b, c, u)
                    if tail and step_of(c) == 1:
                        finish(chain, before, other)
                    if start_next:
                        front(chain, behind, other, step_of(c))
                    if tail and step_of(c) == 3:
                        residual(chain, before, other)
                if start_next and heads_norm:
                    copy_q(behind, other)

            once = Chain(dve, s["first_step"])
            for step in range(4):
                front(once, (None, 0), 0, step)
            if heads_norm:
                copy_q((None, 0), 0)
            attend(once, (None, 0), 0, tail=False)
            per_sequence = (11 if heads_norm else 0) + (3 if latent else 1) * NCH + 1 + 3
            with dve.Fori(0, batch // U - 1) as i:
                chain = Chain(dve, s["vec_step"], i, per_sequence * U)
                attend(chain, (i, 1), 1)
                attend(chain, (i, 2), 0)
                chain.close()
            once = Chain(dve, s["last_step"])
            attend(once, (None, batch - 1), 1, start_next=False)
            finish(once, (None, batch - 1), 1)
            residual(once, (None, batch - 1), 1)

        @block.scalar
        def _(act):
            act.wait_ge(s["consts"], 1)

            def begin(b, u):
                n = number(b)
                act.activation(xn[u][:, :], core.x[:, n, :], ACT.Identity, bias=core.nmr[:, n, :],
                               scale=core.rstd[:, n, :]).then_inc(s["xn_ready"], 1)
                if context:
                    act.activation(ctxu[u][:, :], core.ctxT[:, n, :], ACT.Copy).then_inc(s["ctxu_ready"], 1)
                act.wait_ge(s["xt_done"], count(b))
                act.activation(xT[u][:, :], scores[u][:, 0, A], ACT.Copy).then_inc(s["xt_ready"], 1)

            def copy_k(b, u):
                act.wait_ge(s["k_done"], count(b))
                act.activation(kT[u][:, :, NK - P:NK], scores[u][:, 1, :].rearrange("p (g t) -> p g t", g=GROUPS),
                               ACT.Copy).then_inc(s["k_ready"], 1)

            def copy_v(b, u, src):
                act.wait_ge(s["v_done"], count(b))
                act.activation(v[-1][u][:, :, 0:HD], src.rearrange("p (h f) -> p h f", h=HEADS), ACT.Copy)\
                   .then_inc(s["v_ready"], 1)

            def front(b, u, step):
                if heads_norm and step == 0:
                    copy_v(b, u, scores[u][:, 1, 0:P])
                if heads_norm and step == 3:
                    copy_k(b, u)
                if latent and step == 0:
                    act.wait_ge(s["kv_done"], count(b))
                    act.activation(kvT[u][:, :], scores[u][:, 1, 0:P], ACT.Copy).then_inc(s["kv_ready"], 1)
                if latent and step == 1:
                    act.wait_ge(s["lat_done"], count(b))
                    act.activation(latT[u][:, :], scores[u][0:SLOT, 1, P:2 * P], ACT.Copy).then_inc(s["lat_ready"], 1)
                if own and not heads_norm and step == (2 if latent else 1):
                    copy_k(b, u)
                if context and step == 2:
                    act.wait_ge(s["kc_done"], count(b))
                    act.activation(kT[u][:, :, 0:SC], misc[u][:, 0:GROUPS * SC].rearrange("p (g t) -> p g t", g=GROUPS),
                                   ACT.Copy).then_inc(s["kc_ready"], 1)
                if own and not heads_norm and step == 2:
                    copy_v(b, u, misc[u][:, B2])
                if context and step == 3:
                    act.wait_ge(s["vc_done"], count(b))
                    act.activation(v[0][u][:, :, 0:HD], scores[u][0:SC, 1, 0:P].rearrange("p (h f) -> p h f", h=HEADS),
                                   ACT.Copy).then_inc(s["vc_ready"], 1)

            def copy_acc(b, u):
                act.wait_ge(s["pv_done"], count(b, NCH, NCH))
                act.activation(accT[u][:, :, :], misc[u][:, :].rearrange("p (g t) -> p g t", g=GROUPS), ACT.Copy)\
                   .then_inc(s["acc_ready"], 1)

            def tail(b, u):
                act.wait_ge(s["ot_done"], count(b))
                act.activation(oT[u][:, :], misc[u][:, A], ACT.Copy).then_inc(s["ot_ready"], 1)

            def exps(b, c, u):
                act.wait_ge(s["shifted"], count(b, NCH, c + 1))
                act.activation(probs[c % 2][u][:, :, :], probs[c % 2][u][:, :, :], ACT.Exp, scale=scale)\
                   .then_inc(s["probs_ready"], 1)

            def copies(b, c, u):
                act.wait_ge(s["pt_done"], count(b, NCH, c + 1))
                src, dst = ptp[c % 2], pT[c % 2][u]
                if len(key_tiles) == 1:
                    m = key_tiles[0][0]
                    act.activation(dst[0:m, :, :], src[0:m, :, :], ACT.Copy).then_inc(s["pt_copied"], 1)
                else:
                    act.activation(dst[0:SC, 0:4:2, :], src[0:SC, 0:4:2, :], ACT.Copy)
                    act.activation(dst[:, 1:4:2, :], src[:, 1:4:2, :], ACT.Copy).then_inc(s["pt_copied"], 1)

            def attend(b, u, with_tail=True, start_next=True):
                if with_tail:
                    copy_acc(neighbour(b, -1), 1 - u)
                if start_next:
                    begin(neighbour(b, 1), 1 - u)
                for c in range(NCH):
                    if not copy_first:
                        exps(b, c, u)
                    if c:
                        copies(b, c - 1, u)
                    if copy_first:
                        exps(b, c, u)
                    if with_tail and step_of(c) == 2:
                        tail(neighbour(b, -1), 1 - u)
                    if start_next and step_of(c) in (0, 1):
                        front(neighbour(b, 1), 1 - u, step_of(c))
                copies(b, NCH - 1, u)
                if start_next:
                    front(neighbour(b, 1), 1 - u, 2)
                    front(neighbour(b, 1), 1 - u, 3)

            begin((None, 0), 0)
            for step in range(4):
                front((None, 0), 0, step)
            attend((None, 0), 0, with_tail=False)
            with act.Fori(0, batch // U - 1) as i:
                attend((i, 1), 1)
                attend((i, 2), 0)
            attend((None, batch - 1), 1, start_next=False)
            copy_acc((None, batch - 1), 1)
            tail((None, batch - 1), 1)

        @block.tensor
        def _(pe):
            pe.wait_ge(s["consts"], 1)

            def mm(out, lhsT, rhs, start=True, stop=True, skip=False):
                return pe.matmul(out, lhsT, rhs, start=start, stop=stop, skip_group_check=skip)

            def begin(b, u):
                pe.wait_ge(s["xn_ready"], count(b))
                pe.transpose(scores[u][:, 0, A], xn[u][:, :], core.ident[:, :]).then_inc(s["xt_done"], 1)
                if context:
                    mm(scores[u][:, 1, 0:SC], core.ones[0:1, :], rows[0:1, number(b), :]).then_inc(s["mask_done"], 1)

            def front_0(b, u):
                pe.wait_ge(s["xt_ready"], count(b))
                if heads_norm:
                    mm(scores[u][:, 0, 0:2 * P], xT[u][:, :], W("w_qkv")[:, 0:2 * P]).then_inc(s["proj_done"], 1)
                    mm(scores[u][:, 1, 0:P], xT[u][:, :], W("w_qkv")[:, 2 * P:3 * P]).then_inc(s["v_done"], 1)
                    return
                if latent:
                    mm(scores[u][:, 1, 0:P], W("w_kv")[:, 0:P], xT[u][:, :], stop=False)
                    mm(scores[u][:, 1, 0:P], W("w_kv")[:, P:2 * P], xT[u][:, :], start=False).then_inc(s["kv_done"], 1)
                for g in range(GROUPS):
                    last = mm(scores[u][:, 0, g * P:(g + 1) * P], W("w_q")[:, g * P:(g + 1) * P], xT[u][:, :])
                last.then_inc(s["q_done"], 1)
                if context:
                    pe.wait_ge(s["ctxm_ready"], count(b))
                if own and not latent:
                    for g in range(GROUPS):
                        last = mm(scores[u][:, 1, g * P:(g + 1) * P], W("w_k")[:, g * P:(g + 1) * P], xT[u][:, :])
                    last.then_inc(s["k_done"], 1)

            def front_1(b, u):
                if latent:
                    pe.wait_ge(s["kv_ready"], count(b))
                    mm(scores[u][0:SLOT, 1, P:2 * P], W("w_down")[:, :], kvT[u][:, :]).then_inc(s["lat_done"], 1)

            def front_2(b, u):
                if latent:
                    pe.wait_ge(s["lat_ready"], count(b))
                    for g in range(GROUPS):
                        last = mm(scores[u][:, 1, g * P:(g + 1) * P], W("w_k")[:, g * P:(g + 1) * P], latT[u][:, :])
                    last.then_inc(s["k_done"], 1)
                    mm(misc[u][:, B2], latT[u][:, :], W("w_up_v")[:, :]).then_inc(s["v_done"], 1)
                if context:
                    if own:
                        mm(misc[u][:, B2], xT[u][:, :], W("w_v")[:, :]).then_inc(s["v_done"], 1)
                    for g in range(GROUPS):
                        out = misc[u][:, g * SC:(g + 1) * SC]
                        mm(out, W("w_kc")[:, g * P:(g + 1) * P], ctxm[u][:, :], stop=False)
                        last = mm(out, W("aux")[:, g * P:(g + 1) * P], rows[:, number(b), :], start=False)
                    last.then_inc(s["kc_done"], 1)

            def front_3(b, u):
                if context:
                    pe.wait_ge(s["k_ready" if own else "q_ready"], count(b))
                    src = ctxm[u] if own else ctxu[u]
                    if not own:
                        pe.wait_ge(s["ctxu_ready"], count(b))
                    out = scores[u][0:SC, 1, 0:P]
                    last = mm(out, src[:, :], W("w_vc")[:, :], stop=own)
                    if not own:
                        last = mm(out, core.ones[0:1, 0:SC], W("b_v")[0:1, :], start=False)
                    last.then_inc(s["vc_done"], 1)
                if heads_norm:
                    pe.wait_ge(s["padded_ready"], count(b))
                    pe.wait_ge(s["v_ready"], count(b))
                    for a, sem in ((0, "q_done"), (1, "k_done")):
                        for g in range(GROUPS):
                            last = pe.transpose(scores[u][:, a, g * P:(g + 1) * P],
                                                padded[u][:, a, g, :, :].rearrange("p h f -> p (h f)"), core.ident[:, :])
                        last.then_inc(s[sem], 1)

            def tail_back(b, u):
                pe.wait_ge(s["acc_ready"], count(b))
                for g in range(GROUPS):
                    last = pe.transpose(misc[u][:, g * P:(g + 1) * P], accT[u][:, g, :], core.ident[:, :])
                last.then_inc(s["back_done"], 1)

            def tail_turn(b, u):
                pe.wait_ge(s["o_ready"], count(b))
                pe.transpose(misc[u][:, A], o[u][:, :], core.ident[:, :]).then_inc(s["ot_done"], 1)

            def tail_project(b, u):
                pe.wait_ge(s["ot_ready"], count(b))
                last = mm(misc[u][:, B2], oT[u][:, :], W("w_o")[:, :], stop=latent)
                if not latent:
                    last = mm(misc[u][:, B2], core.ones[0:1, :], W("b_o")[0:1, :], start=False)
                last.then_inc(s["y_done"], 1)

            def scoring(b, c, u):
                if c == 0:
                    pe.wait_ge(s["q_ready"], count(b))
                    if own:
                        pe.wait_ge(s["k_ready"], count(b))
                        if not heads_norm:
                            pe.wait_ge(s["v_ready"], count(b))
                    if context:
                        pe.wait_ge(s["kc_ready"], count(b))
                        pe.wait_ge(s["vc_ready"], count(b))
                if c >= 2:
                    pe.wait_ge(s["shifted"], count(b, NCH, c - 1))
                if heads_norm:
                    mm(scores[u][:, c % 2, :], ident_b[:, :], causal_b[:, :, :].rearrange("p a b -> p (a b)"),
                       stop=False, skip=True)
                for j in range(CHUNK):
                    r, g = divmod(head_of(c, j), GROUPS)
                    at = r * SLOT
                    last = mm(scores[u][:, c % 2, j * NK:(j + 1) * NK], qT[u][at:at + K, g, :], kT[u][at:at + K, g, :],
                              start=not heads_norm, skip=heads_norm)
                last.then_inc(s["scores_done"], 1)

            def turn(b, c, u):
                pe.wait_ge(s["probs_ready"], count(b, NCH, c + 1))
                for at, (h, t) in enumerate(blocks):
                    k0 = sum(key_tiles[x][0] for x in range(t))
                    nk = key_tiles[t][0]
                    last = pe.transpose(ptp[c % 2][0:nk, at, :], probs[c % 2][u][:, h, k0:k0 + nk], core.ident[:, :])
                last.then_inc(s["pt_done"], 1)

            def weigh(b, c, u):
                pe.wait_ge(s["pt_copied"], count(b, NCH, c + 1))
                for at, (h, t) in enumerate(blocks):
                    hh = head_of(c, h)
                    r, g = divmod(hh, GROUPS)
                    nk = key_tiles[t][0]
                    last = mm(misc[u][r * SLOT:(r + 1) * SLOT, g * P:(g + 1) * P], v[t][u][:, hh, :],
                              pT[c % 2][u][0:nk, at, :], start=t == 0, stop=t == len(key_tiles) - 1)
                last.then_inc(s["pv_done"], 1)

            def beside(b, u, step, tail, start_next):
                before, behind = neighbour(b, -1), neighbour(b, 1)
                if step == 0:
                    if start_next:
                        front_0(behind, u)
                    if tail:
                        tail_back(before, u)
                if step == 1 and start_next:
                    front_1(behind, u)
                if step == 2 and tail:
                    tail_turn(before, u)
                if step == 3 and tail:
                    tail_project(before, u)

            def attend(b, u, tail=True, start_next=True):
                scoring(b, 0, u)
                if start_next:
                    begin(neighbour(b, 1), 1 - u)
                for c in range(NCH):
                    if c + 1 < NCH:
                        scoring(b, c + 1, u)
                    beside(b, 1 - u, step_of(c), tail, start_next)
                    if not copy_first:
                        turn(b, c, u)
                    if c:
                        weigh(b, c - 1, u)
                    if copy_first:
                        turn(b, c, u)
                if start_next and heads_norm:
                    front_3(neighbour(b, 1), 1 - u)
                if start_next and tail:
                    pe.wait_ge(s["y_added"], count(neighbour(b, -1)))
                if start_next and not heads_norm:
                    front_2(neighbour(b, 1), 1 - u)
                    front_3(neighbour(b, 1), 1 - u)
                weigh(b, NCH - 1, u)

            begin((None, 0), 0)
            for front in (front_0, front_1, front_2, front_3):
                front((None, 0), 0)
            attend((None, 0), 0, tail=False)
            with pe.Fori(0, batch // U - 1) as i:
                attend((i, 1), 1)
                attend((i, 2), 0)
            attend((None, batch - 1), 1, start_next=False)
            tail_back((None, batch - 1), 1)
            tail_turn((None, batch - 1), 1)
            tail_project((None, batch - 1), 1)


TILE = 4


def mlp_stage(nc, core, dram, tag, kind):
    batch, T, NT = core.batch, TILE, TILE * P
    gated = kind != "plain"
    NCHK = dram[tag + "_w_d"].shape[1]
    E, EG = 32, 4
    NW = E + (16 if kind == "moe3" else 0)
    PER_BLOCK = min(P // NW, 3)
    BLOCKS = [range(n, min(n + PER_BLOCK, 3)) for n in range(0, 3, PER_BLOCK)]
    routed = [k for k in range(NCHK) if gated and k != NCHK - 1]
    with ExitStack() as ctx:
        st = Stage(nc, ctx, tag)
        s = {n: st.sem(n) for n in (
            "loaded", "consts", "once_step", "first_step", "last_step", "xn_ready", "xt_done", "xt_ready", "up_done", "act_ready",
            "hidden_ready", "down_done", "y_done", "y_read", "vec_step", "spread_done",
            "logits_done", "logits_ready", "clamped", "exp_ready", "route_ready", "rt_done", "rt_ready")}
        if gated:
            names = ["w_g", "w_u", "w_d", "w_r", "b_r", "pick"]
        else:
            names = ["w_g", "w_d", "b_g", "b_d", "ln_g", "ln_b"]
        w = {n: st.sb(n, list(dram[f"{tag}_{n}"].shape)) for n in names if n != "pick"}
        if not gated:
            raw = {n: st.sb("raw_" + n, list(dram[f"{tag}_q_{n}"].shape), I32) for n in ("w_g", "w_d")}
            xres = [st.sb(f"xres{p}", [P, T, P]) for p in range(2)]
            hb = st.sb("half_bias", [P, NCHK])
        xn = st.sb("xn", [P, T, P])
        xT = [st.sb(f"xT{p}", [P, NT]) for p in range(2)]
        act_t = [st.sb(f"act{j}", [P, NT]) for j in range(2)]
        hid = [st.sb(f"hid{j}", [P, NT]) for j in range(2)] if gated else act_t
        bn, mv = st.sb("bn", [P, 6]), st.sb("mv", [P, 2])
        gp = [st.ps(f"g{j}", [P, NT]) for j in range(2)]
        up = [st.ps(f"u{j}", [P, NT]) for j in range(2)] if gated else None
        wb = [st.ps(f"wb{j}", [P, NT]) for j in range(2)] if gated else None
        yp = st.ps("y", [P, T, P])
        misc = st.ps("misc", [P, NT])
        if gated:
            sig = st.sb("sig", [P, T, E])
            choice = st.sb("choice", [P, T, EG, E // EG])
            best = st.sb("best", [P, T, EG, 8])
            gs = st.sb("gs", [P, T, EG])
            gt = st.sb("gt", [P, T, EG, EG])
            eq = st.sb("eq", [P, T, EG, EG])
            keep = st.sb("keep", [P, T, EG])
            top8 = st.sb("top8", [P, T, 8])
            first8 = st.sb("first8", [P, T, 8])
            marked = st.sb("marked", [P, T, E])
            tot = st.sb("tot", [P, T])
            weight = st.sb("weight", [P, T, NW])
            part_b = st.sb("part_b", [P, T, NW], BF16)
            route = [st.sb(f"route{n}", [P, T, P]) for n in range(len(BLOCKS))]
            rT = [[st.sb(f"rT{n}_{p}", [len(BLOCKS[n]) * NW, NT], BF16) for n in range(len(BLOCKS))] for p in range(2)]
            pick_f = st.sb("pick", [PER_BLOCK * NW, NCHK - 1, P])
            pick = st.sb("pick_b", [PER_BLOCK * NW, NCHK - 1, P], BF16)
            lower = st.sb("lower", [P, EG, EG])
        n_loads = 16 * (len(w) + (PER_BLOCK + 1 if gated else 2))
        block = ctx.enter_context(nc.Block())
        tiles = batch // T

        def count(m, per=1, extra=1):
            i, at = m
            return at * per + extra if i is None else i * (2 * per) + (at * per + extra)

        def neighbour(m, d):
            return (m[0], m[1] + d)

        def is_first(m):
            return m[0] is None and m[1] == 0

        def buffer_of(m, k):
            return (m[1] * NCHK + k) % 2

        X_TURN, LOGITS, EXP, ROUTE, R_TURN = (1, 2, 3, 4, 12) if gated else (2, None, None, None, None)

        @block.sync
        def _(sp):
            for n in w:
                sp.dma_start(w[n][tuple(slice(None) for _ in w[n].shape)], dram[f"{tag}_{n}"]).then_inc(s["loaded"], 16)
            if gated:
                sp.dma_start(lower[:, :, :], dram["lower"]).then_inc(s["loaded"], 16)
                for n in range(PER_BLOCK):
                    sp.dma_start(pick_f[n * NW:(n + 1) * NW, :, :], dram[tag + "_pick"]).then_inc(s["loaded"], 16)
            else:
                for n in raw:
                    sp.dma_start(raw[n][tuple(slice(None) for _ in raw[n].shape)], dram[f"{tag}_q_{n}"])\
                      .then_inc(s["loaded"], 16)
            sp.wait_ge(s["loaded"], n_loads)

        @block.vector
        def _(dve):
            dve.wait_ge(s["loaded"], n_loads)
            once = Chain(dve, s["once_step"])
            if gated:
                for r in route:
                    once.link(dve.memset(r[:, :, :], 0.0))
                once.link(dve.tensor_copy(pick[:, :, :], pick_f[:, :, :]))
                once.link(dve.memset(first8[:, :, :], -1e30))
            else:
                for n in raw:
                    dst = w[n][tuple(slice(None) for _ in w[n].shape)]
                    src = raw[n][tuple(slice(None) for _ in raw[n].shape)]
                    once.link(dve.scalar_tensor_tensor(dst, src, -128.0, dst, ALU.add, ALU.mult))
            dve.sem_inc(s["consts"], 1)

            def beat():
                dve.memset(core.beat[:, :], 0.0)

            flat = choice[:, :, :, :].rearrange("p t g e -> p t (g e)") if gated else None

            def route_tokens(chain, m, part):
                if part == 0:
                    dve.wait_ge(s["logits_ready"], count(m))
                    dve.tensor_scalar(sig[:, :, :], sig[:, :, :], -1.0, 88.0, ALU.mult, ALU.min).then_inc(s["clamped"], 1)
                if part == 1:
                    dve.wait_ge(s["exp_ready"], count(m))
                    chain.link(dve.tensor_scalar(sig[:, :, :], sig[:, :, :], 1.0, None, ALU.add))
                    chain.link(dve.reciprocal(sig[:, :, :], sig[:, :, :]))
                    chain.link(dve.tensor_tensor(flat, sig[:, :, :], spread(w["b_r"][:, :], 1, T), ALU.add))
                if part == 2:
                    beat()
                    for t in range(T):
                        for g in range(EG):
                            last = dve.max(best[:, t, g, :], choice[:, t, g, :])
                    chain.link(last)
                if part == 3:
                    chain.link(dve.tensor_tensor(gs[:, :, :], best[:, :, :, 0], best[:, :, :, 1], ALU.add))
                    for t in range(T):
                        ahead, behind = spread(gs[:, t, :], 1, EG), spread(gs[:, t, :], 2, EG)
                        dve.tensor_tensor(gt[:, t, :, :], ahead, behind, ALU.is_gt)
                        last = dve.tensor_tensor(eq[:, t, :, :], ahead, behind, ALU.is_equal)
                    chain.link(last)
                    chain.link(dve.tensor_tensor(eq[:, :, :, :], eq[:, :, :, :], spread(lower[:, :, :], 1, T), ALU.mult))
                    chain.link(dve.tensor_tensor(gt[:, :, :, :], gt[:, :, :, :], eq[:, :, :, :], ALU.add))
                    chain.link(dve.tensor_reduce(keep[:, :, :], gt[:, :, :, :], AX.X, ALU.add))
                    chain.link(dve.tensor_scalar(keep[:, :, :], keep[:, :, :], 2.0, None, ALU.is_lt))
                    chain.link(dve.tensor_tensor(choice[:, :, :, :], choice[:, :, :, :], spread(keep[:, :, :], 3, E // EG), ALU.mult))
                    if kind == "moe3":
                        chain.link(dve.tensor_scalar(keep[:, :, :], keep[:, :, :], -1.0, 1e30, ALU.add, ALU.mult))
                        chain.link(dve.tensor_tensor(choice[:, :, :, :], choice[:, :, :, :],
                                                     spread(keep[:, :, :], 3, E // EG), ALU.add))
                if part == 4:
                    beat()
                    for t in range(T):
                        last = dve.max(top8[:, t, :], flat[:, t, :])
                    chain.link(last)
                    if kind == "moe3":
                        chain.link(dve.tensor_copy(first8[:, :, 0:1], top8[:, :, 0:1]))
                        chain.link(dve.memset(top8[:, :, 6:8], -1e30))
                        beat()
                        for t in range(T):
                            last = dve.match_replace(marked[:, t, :], first8[:, t, :], flat[:, t, :], 1e30)
                        chain.link(last)
                        chain.link(dve.tensor_scalar(marked[:, :, :], marked[:, :, :], 1e30, None, ALU.is_equal))
                        chain.link(dve.scalar_tensor_tensor(marked[:, :, :], flat, -1e29, marked[:, :, :], ALU.is_gt, ALU.mult))
                        chain.link(dve.tensor_tensor(weight[:, :, E:NW], marked[:, :, 0:E:2], marked[:, :, 1:E:2], ALU.add))
                        chain.link(dve.tensor_scalar(weight[:, :, E:NW], weight[:, :, E:NW], 0.1, None, ALU.mult))
                if part == 5:
                    beat()
                    for t in range(T):
                        last = dve.match_replace(marked[:, t, :], top8[:, t, :], flat[:, t, :], 1e30)
                    chain.link(last)
                    chain.link(dve.tensor_scalar(marked[:, :, :], marked[:, :, :], 1e30, None, ALU.is_equal))
                    if kind == "moe3":
                        chain.link(dve.scalar_tensor_tensor(marked[:, :, :], flat, -1e29, marked[:, :, :], ALU.is_gt, ALU.mult))
                if part == 6:
                    chain.link(dve.tensor_tensor(marked[:, :, :], marked[:, :, :], sig[:, :, :], ALU.mult))
                    chain.link(dve.tensor_reduce(tot[:, :], marked[:, :, :], AX.X, ALU.add))
                    chain.link(dve.tensor_scalar(tot[:, :], tot[:, :], 1e-20, None, ALU.add))
                    chain.link(dve.reciprocal(tot[:, :], tot[:, :]))
                    chain.link(dve.tensor_scalar(tot[:, :], tot[:, :], 2.5 if kind == "moe0" else 0.2, None, ALU.mult))
                    chain.link(dve.tensor_tensor(weight[:, :, 0:E], marked[:, :, :], spread(tot[:, :], 2, E), ALU.mult))
                if part == 7:
                    for n in range(3):
                        at = n % PER_BLOCK * NW
                        dst = route[n // PER_BLOCK][:, :, at:at + NW]
                        if n < 2:
                            chain.link(dve.tensor_copy(part_b[:, :, :], weight[:, :, :]))
                            dve.tensor_copy(dst, part_b[:, :, :])
                            chain.link(dve.tensor_tensor(weight[:, :, :], weight[:, :, :], part_b[:, :, :], ALU.subtract))
                        else:
                            dve.tensor_copy(dst, weight[:, :, :]).then_inc(s["route_ready"], 1)

            def hidden(chain, m, k):
                j = buffer_of(m, k)
                dve.wait_ge(s["act_ready"], count(m, NCHK, k + 1))
                if k >= 2 or not is_first(m):
                    dve.wait_ge(s["down_done"], count(m, NCHK, k - 1))
                if k in routed:
                    chain.link(dve.tensor_tensor(hid[j][:, :], act_t[j][:, :], up[j][:, :], ALU.mult))
                    dve.wait_ge(s["spread_done"], count(m, len(routed), k + 1))
                    dve.tensor_tensor(hid[j][:, :], hid[j][:, :], wb[j][:, :], ALU.mult).then_inc(s["hidden_ready"], 1)
                else:
                    dve.tensor_tensor(hid[j][:, :], act_t[j][:, :], up[j][:, :], ALU.mult).then_inc(s["hidden_ready"], 1)

            def residual(chain, m):
                x = core.x[:, :, :].rearrange("p (i t) f -> p i t f", t=T)[:, count(m, 1, 0), :, :]
                if gated:
                    dve.wait_ge(s["down_done"], count(m, NCHK, NCHK))
                    chain.link(dve.tensor_tensor(x, x, yp[:, :, :], ALU.add))
                else:
                    dve.wait_ge(s["y_done"], count(m))
                    chain.link(dve.tensor_tensor(x, x, xres[m[1] % 2][:, :, :], ALU.add))
                    chain.link(dve.scalar_tensor_tensor(x, yp[:, :, :], 0.5, x, ALU.mult, ALU.add))
                dve.sem_inc(s["y_read"], 1)

            def statistics(chain, m, t):
                chain.link(take_stats(dve, chain, core, count(m, T, t), bn, mv))

            def experts(chain, m, before=True, behind=True):
                for k in range(NCHK):
                    if gated:
                        hidden(chain, m, k)
                    if k == 0 and before:
                        residual(chain, neighbour(m, -1))
                    if k < T and before:
                        statistics(chain, neighbour(m, -1), k)
                    if gated and behind and k == LOGITS:
                        route_tokens(chain, neighbour(m, 1), 0)
                    if gated and behind and ROUTE <= k < ROUTE + 7:
                        route_tokens(chain, neighbour(m, 1), 1 + k - ROUTE)

            once = Chain(dve, s["first_step"])
            if gated:
                for part in range(8):
                    route_tokens(once, (None, 0), part)
            experts(once, (None, 0), before=False)
            per = ((34 if kind == "moe3" else 24) + len(routed) + 1 if gated else 2) + 3 * T
            with dve.Fori(0, tiles // 2 - 1) as i:
                chain = Chain(dve, s["vec_step"], i, 2 * per)
                experts(chain, (i, 1))
                experts(chain, (i, 2))
                chain.close()
            once = Chain(dve, s["last_step"])
            experts(once, (None, tiles - 1), behind=False)
            residual(once, (None, tiles - 1))
            for t in range(T):
                statistics(once, (None, tiles - 1), t)

        @block.scalar
        def _(act):
            act.wait_ge(s["consts"], 1)

            def normalise(m):
                if not gated and m[1] >= 2:
                    act.wait_ge(s["y_read"], count(m, 1, -1))
                for t in range(T):
                    b = count(m, T, t)
                    if not gated:
                        act.activation(xres[m[1] % 2][:, t, :], core.x[:, b, :], ACT.Identity, bias=core.nmr[:, b, :],
                                       scale=core.rstd[:, b, :])
                        last = act.activation(xn[:, t, :], core.x[:, b, :], ACT.Identity, bias=core.nmr2[:, b, :],
                                              scale=core.rstd2[:, b, :])
                    else:
                        last = act.activation(xn[:, t, :], core.x[:, b, :], ACT.Identity, bias=core.nmr[:, b, :],
                                              scale=core.rstd[:, b, :])
                last.then_inc(s["xn_ready"], 1)

            def prepare(m, k):
                if k == 0:
                    normalise(m)
                if k == X_TURN:
                    act.wait_ge(s["xt_done"], count(m))
                    if gated:
                        act.activation(xT[m[1] % 2][:, :], misc[:, :], ACT.Copy).then_inc(s["xt_ready"], 1)
                    else:
                        act.activation(xT[m[1] % 2][:, :], misc[:, :], ACT.Identity, bias=w["ln_b"][:, :],
                                       scale=w["ln_g"][:, :]).then_inc(s["xt_ready"], 1)
                if k == LOGITS:
                    act.wait_ge(s["logits_done"], count(m))
                    act.activation(sig[:, :, :], misc[:, 0:T * E].rearrange("p (t e) -> p t e", t=T), ACT.Copy)\
                       .then_inc(s["logits_ready"], 1)
                if k == EXP:
                    act.wait_ge(s["clamped"], count(m))
                    act.activation(sig[:, :, :], sig[:, :, :], ACT.Exp).then_inc(s["exp_ready"], 1)
                if gated and R_TURN <= k < R_TURN + len(BLOCKS):
                    n = k - R_TURN
                    act.wait_ge(s["rt_done"], count(m, len(BLOCKS), n + 1))
                    act.activation(rT[m[1] % 2][n][:, :], misc[0:len(BLOCKS[n]) * NW, :], ACT.Copy).then_inc(s["rt_ready"], 1)

            def experts(m, behind=True):
                for k in range(NCHK):
                    j = buffer_of(m, k)
                    act.wait_ge(s["up_done"], count(m, NCHK, k + 1))
                    if k >= 2 or not is_first(m):
                        act.wait_ge(s["hidden_ready" if gated else "down_done"], count(m, NCHK, k - 1))
                    if gated:
                        act.activation(act_t[j][:, :], gp[j][:, :], ACT.Silu).then_inc(s["act_ready"], 1)
                    else:
                        act.activation(act_t[j][:, :], gp[j][:, :], ACT.Silu, bias=w["b_g"][:, k:k + 1])\
                           .then_inc(s["act_ready"], 1)
                    if behind:
                        prepare(neighbour(m, 1), k)

            for k in range(NCHK):
                prepare((None, 0), k)
            experts((None, 0))
            with act.Fori(0, tiles // 2 - 1) as i:
                experts((i, 1))
                experts((i, 2))
            experts((None, tiles - 1), behind=False)

        @block.tensor
        def _(pe):
            pe.wait_ge(s["consts"], 1)

            def down(m, k):
                j = buffer_of(m, k)
                pe.wait_ge(s["hidden_ready" if gated else "act_ready"], count(m, NCHK, k + 1))
                for t in range(T):
                    last = pe.matmul(yp[:, t, :], hid[j][:, t * P:(t + 1) * P], w["w_d"][:, k, :],
                                     start=(k == 0 and t == 0), stop=(gated and k == NCHK - 1), skip_group_check=True)
                last.then_inc(s["down_done"], 1)

            def finish(m):
                down(m, NCHK - 1)
                if not gated:
                    for t in range(T):
                        last = pe.matmul(yp[:, t, :], core.ones[0:1, :], w["b_d"][0:1, :], start=False, stop=True,
                                         skip_group_check=True)
                    last.then_inc(s["y_done"], 1)

            def prepare(m, k):
                if k == X_TURN:
                    pe.wait_ge(s["xn_ready"], count(m))
                    for t in range(T):
                        last = pe.transpose(misc[:, t * P:(t + 1) * P], xn[:, t, :], core.ident[:, :])
                    last.then_inc(s["xt_done"], 1)
                if k == LOGITS:
                    pe.wait_ge(s["xt_ready"], count(m))
                    for t in range(T):
                        last = pe.matmul(misc[:, t * E:(t + 1) * E], xT[m[1] % 2][:, t * P:(t + 1) * P], w["w_r"][:, :],
                                         start=True, stop=True)
                    last.then_inc(s["logits_done"], 1)
                if gated and R_TURN <= k < R_TURN + len(BLOCKS):
                    n = k - R_TURN
                    pe.wait_ge(s["route_ready"], count(m))
                    if n:
                        pe.wait_ge(s["rt_ready"], count(m, len(BLOCKS), n))
                    for t in range(T):
                        last = pe.transpose(misc[:, t * P:(t + 1) * P], route[n][:, t, :], core.ident[:, :])
                    last.then_inc(s["rt_done"], 1)

            def experts(m, before=True, behind=True):
                p = m[1] % 2
                for k in range(NCHK):
                    j = buffer_of(m, k)
                    if k == 0:
                        pe.wait_ge(s["xt_ready"], count(m))
                    if k >= 2 or before:
                        pe.wait_ge(s["hidden_ready" if gated else "act_ready"], count(m, NCHK, k - 1))
                    last = pe.matmul(gp[j][:, :], w["w_g"][:, k, :], xT[p][:, :], start=True, stop=True)
                    if gated:
                        last = pe.matmul(up[j][:, :], w["w_u"][:, k, :], xT[p][:, :], start=True, stop=True)
                    last.then_inc(s["up_done"], 1)
                    if k in routed:
                        if k == 0:
                            pe.wait_ge(s["rt_ready"], count(m, len(BLOCKS), len(BLOCKS)))
                        for n, parts in enumerate(BLOCKS):
                            rows = len(parts) * NW
                            last = pe.matmul(wb[j][:, :], pick[0:rows, k, :], rT[p][n][:, :], start=(n == 0),
                                             stop=(n == len(BLOCKS) - 1))
                        last.then_inc(s["spread_done"], 1)
                    if behind:
                        prepare(neighbour(m, 1), k)
                    if k == 0 and before:
                        finish(neighbour(m, -1))
                    if k == 1 and before:
                        pe.wait_ge(s["y_read"], count(m, 1, 0))
                    if k:
                        down(m, k - 1)

            for k in range(NCHK):
                prepare((None, 0), k)
            experts((None, 0), before=False)
            with pe.Fori(0, tiles // 2 - 1) as i:
                experts((i, 1))
                experts((i, 2))
            experts((None, tiles - 1), behind=False)
            finish((None, tiles - 1))


MAGIC = 1.5 * 2.0 ** 23
QMAX = 32767.0


def quantised_mlp(nc, core, dram, tag):
    batch, T, NT, CH = core.batch, TILE, TILE * P, 3
    NI = batch // T
    with ExitStack() as ctx:
        st = Stage(nc, ctx, tag)
        wn = st.sb("w_natural", [P, 3 * CH, P])
        wT = st.sb("w", [P, 3 * CH, P])
        ws, wr = st.sb("w_scale", [P, 3 * CH * 4]), st.sb("w_inverse", [P, 3 * CH * 4])
        xi = st.sb("x_int", [P, NI, NT], I16)
        ui = st.sb("up_int", [P, NI, CH * NT], I16)
        gi = st.sb("gate_int", [P, NI, CH * NT], I16)
        high = st.sb("high", [P, 2, NI])
        top, most = st.sb("top", [P, 2]), st.sb("most", [P, 2])
        unit, scale, ratio = (st.sb(n, [P, 5]) for n in ("unit", "scale", "ratio"))
        X, G, UP, G2, OUT = range(5)
        xn = st.sb("xn", [P, T, P])
        f0, f1 = st.sb("f0", [P, CH * NT]), st.sb("f1", [P, CH * NT])
        xT = st.sb("xT", [P, NT])
        bn, mv = st.sb("bn", [P, T, 6]), st.sb("mv", [P, T, 2])
        misc = st.ps("misc", [P, NT])
        gu = [st.ps(n, [P, CH, NT]) for n in ("g", "u")]

        def col(tile, c):
            return tile[:, c:c + 1]

        def rounded(dve, chain, dst, src, mult, tmp):
            chain.link(dve.tensor_scalar(tmp, src, mult, MAGIC, ALU.mult, ALU.add))
            return dve.tensor_scalar(dst, tmp, -MAGIC, None, ALU.add)

        with ExitStack() as c2:
            st2 = Stage(nc, c2, tag + "_weights")
            loaded, step, quantised, turned, copied = (st2.sem(n) for n in ("loaded", "step", "quantised", "turned", "copied"))
            block = c2.enter_context(nc.Block())

            @block.sync
            def _(sp):
                sp.dma_start(wn[:, :, :], dram[tag + "_w"]).then_inc(loaded, 16)
                sp.wait_ge(loaded, 16)

            @block.vector
            def _(dve):
                chain = Chain(dve, step)
                blocks = wn[:, :, :].rearrange("p c (k i) -> p (c k) i", i=32)
                dve.wait_ge(loaded, 16)
                chain.link(dve.tensor_reduce(ws[:, :], blocks, AX.X, ALU.max, apply_absolute_value=True))
                chain.link(dve.tensor_scalar(ws[:, :], ws[:, :], 1.0 / 7.0, 1e-12, ALU.mult, ALU.max))
                chain.link(dve.reciprocal(wr[:, :], ws[:, :]))
                chain.link(dve.tensor_tensor(blocks, blocks, spread(wr[:, :], 2, 32), ALU.mult))
                chain.link(dve.tensor_scalar(wn[:, :, :], wn[:, :, :], MAGIC, None, ALU.add))
                chain.link(dve.tensor_scalar(wn[:, :, :], wn[:, :, :], -MAGIC, None, ALU.add))
                dve.tensor_tensor(blocks, blocks, spread(ws[:, :], 2, 32), ALU.mult).then_inc(quantised, 1)

            @block.tensor
            def _(pe):
                pe.wait_ge(quantised, 1)
                for k in range(3 * CH):
                    last = pe.transpose(gu[k // 6][:, k % 6 // 2, k % 2 * P:(k % 2 + 1) * P], wn[:, k, :], core.ident[:, :])
                last.then_inc(turned, 1)

            @block.scalar
            def _(act):
                act.wait_ge(turned, 1)
                for k in range(3 * CH):
                    act.activation(wT[:, k, :], gu[k // 6][:, k % 6 // 2, k % 2 * P:(k % 2 + 1) * P], ACT.Copy)

        def measured(name, first, n, units):
            with ExitStack() as c2:
                st2 = Stage(nc, c2, f"{tag}_{name}")
                step, top_ready, most_ready = st2.sem("step"), st2.sem("top_ready"), st2.sem("most_ready")
                block = c2.enter_context(nc.Block())

                @block.vector
                def _(dve):
                    chain = Chain(dve, step)
                    dve.tensor_reduce(top[:, 0:n], high[:, 0:n, :], AX.X, ALU.max).then_inc(top_ready, 1)
                    units(dve, chain)
                    sc, ra, un = (a[:, first:first + n] for a in (scale, ratio, unit))
                    dve.wait_ge(most_ready, 1)
                    chain.link(dve.tensor_tensor(sc, most[:, 0:n], un, ALU.mult))
                    chain.link(dve.tensor_scalar(sc, sc, 1.0 / QMAX, 1e-12, ALU.mult, ALU.max))
                    chain.link(dve.reciprocal(ra, sc))
                    dve.tensor_tensor(ra, ra, un, ALU.mult)

                @block.gpsimd
                def _(pool):
                    pool.wait_ge(top_ready, 1)
                    pool.partition_all_reduce(most[:, 0:n], top[:, 0:n], P, bass.bass_isa.ReduceOp.max)\
                        .then_inc(most_ready, 1)

        def run_pass(name, sems, vector, scalar, per=0):
            with ExitStack() as c2:
                st2 = Stage(nc, c2, f"{tag}_{name}")
                s = {n: st2.sem(n) for n in sems + ["vec_step", "tile_done"]}
                block = c2.enter_context(nc.Block())

                @block.vector
                def _(dve):
                    dve.sem_inc(s["tile_done"], 1)
                    with dve.Fori(0, NI) as i:
                        chain = Chain(dve, s["vec_step"], i, per)
                        vector(dve, s, i, chain).then_inc(s["tile_done"], 1)
                        chain.close()

                @block.scalar
                def _(act):
                    with act.Fori(0, NI) as i:
                        act.wait_ge(s["tile_done"], i + 1)
                        scalar(act, s, i)

        def normalise(act, s, i):
            for t in range(T):
                b = i * T + t
                last = act.activation(xn[:, t, :], core.x[:, b, :], ACT.Identity, bias=core.nmr[:, b, :],
                                      scale=core.rstd[:, b, :])
            last.then_inc(s["xn_ready"], 1)

        def max_x(dve, s, i, chain):
            dve.wait_ge(s["xn_ready"], i + 1)
            return dve.tensor_reduce(high[:, 0, i:i + 1] if isinstance(i, int) else high[:, 0, i].unsqueeze(1),
                                     xn[:, :, :], AX.XY, ALU.max, apply_absolute_value=True)

        run_pass("max_x", ["xn_ready"], max_x, scalar=normalise)
        measured("scale_x", X, 1, lambda dve, chain: chain.link(dve.memset(col(unit, X), 1.0)))

        def gate_up(pe, s, i):
            for a, name in enumerate(("g", "u")):
                pe.wait_ge(s[name + "_read"], i + 1)
                for k in range(CH):
                    last = pe.matmul(gu[a][:, k, :], wT[:, a * CH + k, :], xT[:, :], start=True, stop=True)
                last.then_inc(s[name + "_done"], 1)

        with ExitStack() as c2:
            st2 = Stage(nc, c2, f"{tag}_max_gu")
            s = {n: st2.sem(n) for n in ("xn_ready", "xq_ready", "xt_done", "xt_ready", "g_done", "u_done", "g_read",
                                         "u_read", "round_step")}
            block = c2.enter_context(nc.Block())

            @block.vector
            def _(dve):
                for name in ("g", "u"):
                    dve.sem_inc(s[name + "_read"], 1)

                def quantise_x(chain, i, d):
                    dve.wait_ge(s["xn_ready"], i + (d + 1))
                    chain.link(dve.tensor_scalar(xn[:, :, :], xn[:, :, :], col(ratio, X), MAGIC, ALU.mult, ALU.add))
                    dve.tensor_scalar(xn[:, :, :], xn[:, :, :], -MAGIC, None, ALU.add).then_inc(s["xq_ready"], 1)

                def largest(i):
                    for a, name in enumerate(("g", "u")):
                        dve.wait_ge(s[name + "_done"], i + 1)
                        dst = high[:, a, i:i + 1] if isinstance(i, int) else high[:, a, i].unsqueeze(1)
                        dve.tensor_reduce(dst, gu[a][:, :, :], AX.XY, ALU.max, apply_absolute_value=True)\
                           .then_inc(s[name + "_read"], 1)

                quantise_x(Chain(dve, s["round_step"]), 0, 0)
                with dve.Fori(0, NI - 1) as i:
                    chain = Chain(dve, s["round_step"], i + 1, 1)
                    quantise_x(chain, i, 1)
                    largest(i)
                    chain.close()
                largest(NI - 1)

            @block.scalar
            def _(act):
                with act.Fori(0, NI) as i:
                    normalise(act, s, i)
                    act.wait_ge(s["xt_done"], i + 1)
                    act.activation(xT[:, :], misc[:, :], ACT.Copy).then_inc(s["xt_ready"], 1)
                    act.activation(xi[:, i, :], misc[:, :], ACT.Copy).then_inc(s["xt_ready"], 1)

            @block.tensor
            def _(pe):
                with pe.Fori(0, NI) as i:
                    pe.wait_ge(s["xq_ready"], i + 1)
                    for t in range(T):
                        last = pe.transpose(misc[:, t * P:(t + 1) * P], xn[:, t, :], core.ident[:, :])
                    last.then_inc(s["xt_done"], 1)
                    pe.wait_ge(s["xt_ready"], i * 2 + 2)
                    gate_up(pe, s, i)

        def unit_gu(dve, chain):
            dve.tensor_copy(col(unit, G), col(scale, X))
            chain.link(dve.tensor_copy(col(unit, UP), col(scale, X)))

        measured("scale_gu", G, 2, unit_gu)

        def quantise_sigmoid(dve, s, i, chain):
            dve.wait_ge(s["sig_ready"], i + 1)
            chain.link(dve.tensor_scalar(f1[:, :], f1[:, :], 65536.0, MAGIC, ALU.mult, ALU.add))
            chain.link(dve.tensor_scalar(f1[:, :], f1[:, :], -MAGIC, 65535.0, ALU.add, ALU.min))
            chain.link(dve.tensor_tensor(f1[:, :], f1[:, :], gi[:, i, :], ALU.mult))

        def sigmoid(act, s, i):
            act.activation(f1[:, :], gi[:, i, :], ACT.Sigmoid, scale=col(scale, G)).then_inc(s["sig_ready"], 1)

        with ExitStack() as c2:
            st2 = Stage(nc, c2, f"{tag}_max_g2")
            s = {n: st2.sem(n) for n in ("xt_ready", "g_done", "u_done", "g_read", "u_read", "gate_ready", "sig_ready",
                                         "tile_done", "vec_step")}
            block = c2.enter_context(nc.Block())

            @block.vector
            def _(dve):
                for name in ("g_read", "u_read", "tile_done"):
                    dve.sem_inc(s[name], 1)
                with dve.Fori(0, NI) as i:
                    chain = Chain(dve, s["vec_step"], i, 3 + 1)
                    for a, (name, dst, c) in enumerate((("g", gi, G), ("u", ui, UP))):
                        dve.wait_ge(s[name + "_done"], i + (1 + a))
                        dve.tensor_scalar(f0[:, :], gu[a][:, :, :].rearrange("p c t -> p (c t)"), col(ratio, c), MAGIC,
                                          ALU.mult, ALU.add).then_inc(s[name + "_read"], 1)
                        dve.wait_ge(s[name + "_read"], i + 2)
                        last = dve.tensor_scalar(dst[:, i, :], f0[:, :], -MAGIC, None, ALU.add)
                        if a == 0:
                            last.then_inc(s["gate_ready"], 1)
                            dve.wait_ge(s["gate_ready"], i + 1)
                        else:
                            chain.link(last)
                    quantise_sigmoid(dve, s, i, chain)
                    dve.tensor_reduce(high[:, 0, i].unsqueeze(1), f1[:, :], AX.X, ALU.max, apply_absolute_value=True)\
                       .then_inc(s["tile_done"], 1)
                    chain.close()

            @block.scalar
            def _(act):
                with act.Fori(0, NI) as i:
                    act.wait_ge(s["u_done"], i + 1)
                    act.activation(xT[:, :], xi[:, i, :], ACT.Copy).then_inc(s["xt_ready"], 1)
                    act.wait_ge(s["gate_ready"], i + 1)
                    act.wait_ge(s["tile_done"], i + 1)
                    sigmoid(act, s, i)

            @block.tensor
            def _(pe):
                pe.sem_inc(s["u_done"], 1)
                with pe.Fori(0, NI) as i:
                    pe.wait_ge(s["xt_ready"], i + 1)
                    gate_up(pe, s, i)

        measured("scale_g2", G2, 1, lambda dve, chain: chain.link(
            dve.tensor_scalar(col(unit, G2), col(scale, G), 1.0 / 65536.0, None, ALU.mult)))

        def quantise_g2(dve, s, i, chain):
            quantise_sigmoid(dve, s, i, chain)
            chain.link(rounded(dve, chain, gi[:, i, :], f1[:, :], col(ratio, G2), f1[:, :]))
            chain.link(dve.tensor_tensor(f1[:, :], gi[:, i, :], ui[:, i, :], ALU.mult))
            return dve.tensor_reduce(high[:, 0, i].unsqueeze(1), f1[:, :], AX.X, ALU.max, apply_absolute_value=True)

        run_pass("max_out", ["sig_ready"], quantise_g2, sigmoid, per=6)
        measured("scale_out", OUT, 1, lambda dve, chain: chain.link(
            dve.tensor_tensor(col(unit, OUT), col(scale, G2), col(scale, UP), ALU.mult)))

        with ExitStack() as c2:
            st2 = Stage(nc, c2, f"{tag}_down")
            s = {n: st2.sem(n) for n in ("out_ready", "y_done", "first_step", "vec_step", "last_step")}
            block = c2.enter_context(nc.Block())
            out, yp = (f0, f1), (misc[:, :], gu[0][:, 0, :])

            def count(m, per=1, extra=1):
                i, at = m
                return at * per + extra if i is None else i * (2 * per) + (at * per + extra)

            @block.vector
            def _(dve):
                tile_of = core.x[:, :, :].rearrange("p (i t) f -> p i t f", t=T)

                def product(chain, m):
                    n, dst = count(m, 1, 0), out[m[1] % 2][:, :]
                    chain.link(dve.tensor_tensor(dst, gi[:, n, :], ui[:, n, :], ALU.mult))
                    rounded(dve, chain, dst, dst, col(ratio, OUT), dst).then_inc(s["out_ready"], 1)

                def residual(chain, m):
                    x = tile_of[:, count(m, 1, 0), :, :]
                    dve.wait_ge(s["y_done"], count(m))
                    chain.link(dve.scalar_tensor_tensor(x, yp[m[1] % 2].rearrange("p (t f) -> p t f", t=T), col(scale, OUT),
                                                        x, ALU.mult, ALU.add))
                    take_tile_stats(dve, chain, core.x, core.stat, count(m, 1, 0), T, bn, mv, core.beat)

                def tile(chain, m, start_next=True):
                    if start_next:
                        product(chain, (m[0], m[1] + 1))
                    residual(chain, m)

                once = Chain(dve, s["first_step"])
                product(once, (None, 0))
                tile(once, (None, 0))
                with dve.Fori(0, NI // 2 - 1) as i:
                    chain = Chain(dve, s["vec_step"], i, 2 * (3 + 3))
                    tile(chain, (i, 1))
                    tile(chain, (i, 2))
                    chain.close()
                tile(Chain(dve, s["last_step"]), (None, NI - 1), start_next=False)

            @block.tensor
            def _(pe):
                with pe.Fori(0, NI // 2) as i:
                    for p in range(2):
                        pe.wait_ge(s["out_ready"], i * 2 + (p + 1))
                        for t in range(T):
                            for k in range(CH):
                                last = pe.matmul(yp[p][:, t * P:(t + 1) * P], out[p][:, k * NT + t * P:k * NT + (t + 1) * P],
                                                 wT[:, 2 * CH + k, :], start=(k == 0), stop=(k == CH - 1))
                        last.then_inc(s["y_done"], 1)


def wide_cross_attention(nc, core, dram, tag):
    batch, U, H, DH, CH = core.batch, UNITS, 8, 64, 4
    INNER = H * DH
    with ExitStack() as ctx:
        st = Stage(nc, ctx, tag)

        def unit_sb(name, shape, dt=F32):
            return [st.sb(f"{name}{u}", shape, dt) for u in range(U)]

        names = ["w_q", "w_kv", "w_o", "b_o", "ln"]
        w = {n: st.sb(n, list(dram[f"{tag}_{n}"].shape)) for n in names}
        c_all = st.sb("c_all", [SC, batch, P])
        cstat = st.sb("cstat", [SC, batch, 2])
        crstd, cnmr = st.sb("crstd", [SC, batch, 1]), st.sb("cnmr", [SC, batch, 1])
        cbn, cmv = st.sb("cbn", [SC, 8, 6]), st.sb("cmv", [SC, 8, 2])
        xn, xT, cn, cT = unit_sb("xn", [P, P]), unit_sb("xT", [P, P]), unit_sb("cn", [SC, P]), unit_sb("cT", [P, SC])
        qT, kT, v = unit_sb("qT", [P, CH, P]), unit_sb("kT", [P, CH, SC]), unit_sb("v", [SC, INNER])
        probs = unit_sb("probs", [P, 2, CH, SC])
        pT = unit_sb("pT", [SC, 2, CH, P])
        top, z = unit_sb("top", [P, 2, CH]), unit_sb("z", [P, 2, CH])
        o, oT = unit_sb("o", [P, INNER]), unit_sb("oT", [P, CH, P])
        bn, mv = unit_sb("bn", [P, 6]), unit_sb("mv", [P, 2])
        scores = [st.ps(f"scores{u}", [P, 2, BANK]) for u in range(U)]
        ptp = [st.ps(f"ptp{a}", [P, CH, P]) for a in range(2)]
        misc = [st.ps(f"misc{u}", [P, BANK]) for u in range(U)]
        s = {n: st.sem(n) for n in (
            "loaded", "once_step", "cvar_ready", "cstd_ready", "consts", "xn_ready", "cn_ready", "xt_done", "xt_ready",
            "ct_done", "ct_ready", "q_done", "q_ready", "k_done", "k_ready", "v_done", "v_ready", "scores_done",
            "shifted", "probs_ready", "pt_done0", "pt_done1", "pt_copied0", "pt_copied1", "pv_done", "o_ready",
            "ot_done", "ot_ready", "y_done", "y_added", "vec_step")}
        n_loads = 16 * (len(names) + 1)
        block = ctx.enter_context(nc.Block())

        @block.sync
        def _(sp):
            sp.dma_start(c_all[:, :, :], dram["ctx"].rearrange("b t d -> t b d")).then_inc(s["loaded"], 16)
            for n in names:
                sp.dma_start(w[n][tuple(slice(None) for _ in w[n].shape)], dram[f"{tag}_{n}"]).then_inc(s["loaded"], 16)
            sp.wait_ge(s["loaded"], n_loads)

        @block.vector
        def _(dve):
            dve.sem_inc(s["y_added"], U)
            dve.wait_ge(s["loaded"], n_loads)
            with dve.Fori(0, batch // 8) as i:
                once = Chain(dve, s["once_step"], i, 3)
                take_tile_stats(dve, once, c_all, cstat, i, 8, cbn, cmv, core.beat)
            dve.tensor_scalar(crstd[:, :, 0], cstat[:, :, 1], LN_EPS, None, ALU.add).then_inc(s["cvar_ready"], 1)
            dve.wait_ge(s["cstd_ready"], 1)
            dve.reciprocal(crstd[:, :, 0], crstd[:, :, 0]).then_inc(s["once_step"], 1)
            dve.wait_ge(s["once_step"], 3 * (batch // 8) + 1)
            dve.scalar_tensor_tensor(cnmr[:, :, 0], cstat[:, :, 0], -1.0, crstd[:, :, 0], ALU.mult, ALU.mult)\
               .then_inc(s["consts"], 1)
            with dve.Fori(0, batch // U) as i:
                chain = Chain(dve, s["vec_step"], i, 6 * U)
                for u in range(U):
                    dve.wait_ge(s["q_done"], i * U + (u + 1))
                    dve.tensor_copy(qT[u][:, :, :], scores[u][:, 0, :].rearrange("p (c t) -> p c t", c=CH))\
                       .then_inc(s["q_ready"], 1)
                for u in range(U):
                    S = scores[u][:, :, 0:CH * SC].rearrange("p a (c k) -> p a c k", c=CH)
                    dve.wait_ge(s["scores_done"], i * U + (u + 1))
                    chain.link(dve.tensor_reduce(top[u][:, :, :], S, AX.X, ALU.max))
                    dve.tensor_tensor(probs[u][:, :, :, :], S, spread(top[u][:, :, :], 3, SC), ALU.subtract)\
                       .then_inc(s["shifted"], 1)
                for u in range(U):
                    dve.wait_ge(s["probs_ready"], i * U + (u + 1))
                    chain.link(dve.tensor_reduce(z[u][:, :, :], probs[u][:, :, :, :], AX.X, ALU.add))
                    chain.link(dve.reciprocal(z[u][:, :, :], z[u][:, :, :]))
                for u in range(U):
                    dve.wait_ge(s["pv_done"], i * U + (u + 1))
                    dve.tensor_tensor(o[u][:, :].rearrange("p (c a f) -> p a c f", a=2, f=DH),
                                      misc[u][:, :].rearrange("p (c a f) -> p a c f", a=2, f=DH),
                                      spread(z[u][:, :, :], 3, DH), ALU.mult).then_inc(s["o_ready"], 1)
                for u in range(U):
                    b = i * U + u
                    dve.wait_ge(s["y_done"], i * U + (u + 1))
                    chain.link(dve.tensor_tensor(core.x[:, b, :], core.x[:, b, :], scores[u][:, 1, 0:P], ALU.add))
                    take_stats(dve, chain, core, b, bn[u], mv[u]).then_inc(s["y_added"], 1)
                chain.close()

        @block.scalar
        def _(act):
            act.wait_ge(s["cvar_ready"], 1)
            act.activation(crstd[:, :, 0], crstd[:, :, 0], ACT.Sqrt).then_inc(s["cstd_ready"], 1)
            act.wait_ge(s["consts"], 1)
            with act.Fori(0, batch // U) as i:
                def n_of(u):
                    return i * U + (u + 1)

                for u in range(U):
                    b = i * U + u
                    act.activation(xn[u][:, :], core.x[:, b, :], ACT.Identity, bias=core.nmr2[:, b, :],
                                   scale=core.rstd2[:, b, :]).then_inc(s["xn_ready"], 1)
                    act.activation(cn[u][:, :], c_all[:, b, :], ACT.Identity, bias=cnmr[:, b, :],
                                   scale=crstd[:, b, :]).then_inc(s["cn_ready"], 1)
                for u in range(U):
                    act.wait_ge(s["xt_done"], n_of(u))
                    act.activation(xT[u][:, :], misc[u][:, 0:P], ACT.Identity, bias=w["ln"][:, 1:2], scale=w["ln"][:, 0:1])\
                       .then_inc(s["xt_ready"], 1)
                    act.wait_ge(s["ct_done"], n_of(u))
                    act.activation(cT[u][:, :], scores[u][:, 1, 0:SC], ACT.Identity, bias=w["ln"][:, 3:4],
                                   scale=w["ln"][:, 2:3]).then_inc(s["ct_ready"], 1)
                for u in range(U):
                    act.wait_ge(s["v_done"], n_of(u))
                    act.activation(v[u][:, :], misc[u][0:SC, :], ACT.Copy).then_inc(s["v_ready"], 1)
                    act.wait_ge(s["k_done"], n_of(u))
                    act.activation(kT[u][:, :, :], scores[u][:, 1, 0:CH * SC].rearrange("p (c t) -> p c t", c=CH),
                                   ACT.Copy).then_inc(s["k_ready"], 1)
                for u in range(U):
                    act.wait_ge(s["shifted"], n_of(u))
                    act.activation(probs[u][:, :, :, :], probs[u][:, :, :, :], ACT.Exp, scale=float(DH) ** -0.5)\
                       .then_inc(s["probs_ready"], 1)
                for u in range(U):
                    for a in range(2):
                        act.wait_ge(s[f"pt_done{a}"], n_of(u))
                        act.activation(pT[u][:, a, :, :], ptp[a][0:SC, :, :], ACT.Copy).then_inc(s[f"pt_copied{a}"], 1)
                for u in range(U):
                    act.wait_ge(s["ot_done"], n_of(u))
                    act.activation(oT[u][:, :, :], scores[u][:, 0, :].rearrange("p (c t) -> p c t", c=CH), ACT.Copy)\
                       .then_inc(s["ot_ready"], 1)

        @block.tensor
        def _(pe):
            pe.sem_inc(s["pt_copied0"], 1)
            pe.sem_inc(s["pt_copied1"], 1)
            pe.wait_ge(s["consts"], 1)

            def mm(out, lhsT, rhs, start=True, stop=True):
                return pe.matmul(out, lhsT, rhs, start=start, stop=stop)

            with pe.Fori(0, batch // U) as i:
                def n_of(u):
                    return i * U + (u + 1)

                for u in range(U):
                    pe.wait_ge(s["y_added"], n_of(u))
                    pe.wait_ge(s["xn_ready"], n_of(u))
                    pe.transpose(misc[u][:, 0:P], xn[u][:, :], core.ident[:, :]).then_inc(s["xt_done"], 1)
                    pe.wait_ge(s["cn_ready"], n_of(u))
                    pe.transpose(scores[u][:, 1, 0:SC], cn[u][:, :], core.ident[0:SC, 0:SC]).then_inc(s["ct_done"], 1)
                for u in range(U):
                    pe.wait_ge(s["xt_ready"], n_of(u))
                    for c in range(CH):
                        last = mm(scores[u][:, 0, c * P:(c + 1) * P], w["w_q"][:, c * P:(c + 1) * P], xT[u][:, :])
                    last.then_inc(s["q_done"], 1)
                    pe.wait_ge(s["ct_ready"], n_of(u))
                    mm(misc[u][0:SC, :], cT[u][:, :], w["w_kv"][:, INNER:2 * INNER]).then_inc(s["v_done"], 1)
                    for c in range(CH):
                        last = mm(scores[u][:, 1, c * SC:(c + 1) * SC], w["w_kv"][:, c * P:(c + 1) * P], cT[u][:, :])
                    last.then_inc(s["k_done"], 1)
                for u in range(U):
                    pe.wait_ge(s["q_ready"], n_of(u))
                    pe.wait_ge(s["k_ready"], n_of(u))
                    for c in range(CH):
                        for a in range(2):
                            last = mm(scores[u][:, a, c * SC:(c + 1) * SC], qT[u][a * DH:(a + 1) * DH, c, :],
                                      kT[u][a * DH:(a + 1) * DH, c, :])
                    last.then_inc(s["scores_done"], 1)
                for u in range(U):
                    pe.wait_ge(s["probs_ready"], n_of(u))
                    for a in range(2):
                        pe.wait_ge(s[f"pt_copied{a}"], n_of(u))
                        for c in range(CH):
                            last = pe.transpose(ptp[a][0:SC, c, :], probs[u][:, a, c, :], core.ident[:, :])
                        last.then_inc(s[f"pt_done{a}"], 1)
                for u in range(U):
                    pe.wait_ge(s["v_ready"], n_of(u))
                    for a in range(2):
                        pe.wait_ge(s[f"pt_copied{a}"], n_of(u) + 1)
                        for c in range(CH):
                            h = 2 * c + a
                            last = mm(misc[u][:, h * DH:(h + 1) * DH], pT[u][:, a, c, :], v[u][:, h * DH:(h + 1) * DH])
                    last.then_inc(s["pv_done"], 1)
                for u in range(U):
                    pe.wait_ge(s["o_ready"], n_of(u))
                    for c in range(CH):
                        last = pe.transpose(scores[u][:, 0, c * P:(c + 1) * P], o[u][:, c * P:(c + 1) * P], core.ident[:, :])
                    last.then_inc(s["ot_done"], 1)
                for u in range(U):
                    pe.wait_ge(s["ot_ready"], n_of(u))
                    for c in range(CH):
                        mm(scores[u][:, 1, 0:P], oT[u][:, c, :], w["w_o"][:, c, :], start=c == 0, stop=False)
                    mm(scores[u][:, 1, 0:P], core.ones[0:1, :], w["b_o"][0:1, :], start=False).then_inc(s["y_done"], 1)


def query_softmax_attention(nc, core, dram, tag):
    batch, U = core.batch, UNITS
    CHUNK = 4
    CHUNKS = [(at, src) for at in range(0, HEADS, CHUNK) for src in range(2)]
    NCH = len(CHUNKS)
    scale = float(P) ** -0.5
    with ExitStack() as ctx:
        st = Stage(nc, ctx, tag)

        def unit_sb(name, shape, dt=F32):
            return [st.sb(f"{name}{u}", shape, dt) for u in range(U)]

        names = ["w_q", "b_q", "w_k", "b_k", "w_slot", "w_v", "b_v", "w_qt", "b_qt", "w_o", "b_o", "gb", "unslot"]
        w = {n: st.sb(n, list(dram[f"{tag}_{n}"].shape)) for n in names}
        xn, xT = unit_sb("xn", [P, P]), unit_sb("xT", [P, P])
        k12, kT = unit_sb("k12", [P, 2, SC]), unit_sb("kT", [P, GROUPS, 2 * SC])
        qT, v = unit_sb("qT", [P, GROUPS, P]), unit_sb("v", [SC, 2, HEADS, HD])
        vs = unit_sb("vs", [SC, 2, HEADS, SLOT])
        accT = unit_sb("accT", [P, GROUPS, P])
        probs = unit_sb("probs", [SC, 2, HEADS, P])
        top, z = unit_sb("top", [SC, 2, HEADS]), unit_sb("z", [SC, 2, HEADS])
        bn, mv, var, rs = (unit_sb(n, [P, k]) for n, k in (("bn", 6), ("mv", 2), ("var", 1), ("rs", 1)))
        o1, o1T, o2 = unit_sb("o1", [P, P]), unit_sb("o1T", [P, P]), unit_sb("o2", [P, P])
        minus_half = st.sb("minus_half", [P, 1])
        scores = [st.ps(f"scores{u}", [P, 2, BANK]) for u in range(U)]
        misc = [st.ps(f"misc{u}", [P, BANK]) for u in range(U)]
        extra = [st.ps(f"extra{u}", [P, BANK]) for u in range(U)]
        s = {n: st.sem(n) for n in (
            "loaded", "consts", "xn_ready", "xt_done", "xt_ready", "q_done", "q_ready", "k12_ready", "first_step", "last_step",
            "k_done", "k_ready", "v_done", "v_ready", "scores_done", "top_ready", "probs_ready", "vs_ready", "pv_done", "acc_ready", "attended",
            "var_ready", "rs_ready", "o1_ready", "o1t_done", "o1t_ready", "y_done", "y_added", "vec_step")}
        block = ctx.enter_context(nc.Block())

        def count(b, per=1, extra=1):
            i, at = b
            return at * per + extra if i is None else i * (U * per) + (at * per + extra)

        def number(b):
            return count(b, 1, 0)

        def neighbour(b, d):
            return (b[0], b[1] + d)

        def part(c):
            at, src = CHUNKS[c]
            return src, slice(at, at + CHUNK)

        @block.sync
        def _(sp):
            for n in names:
                sp.dma_start(w[n][tuple(slice(None) for _ in w[n].shape)], dram[f"{tag}_{n}"]).then_inc(s["loaded"], 16)
            sp.wait_ge(s["loaded"], 16 * len(names))

        @block.gpsimd
        def _(pool):
            pool.wait_ge(s["consts"], 1)
            with pool.Fori(0, batch // U) as i:
                for u in range(U):
                    for r in range(2):
                        pool.wait_ge(s["var_ready"], i * (2 * U) + (2 * u + r + 1))
                        pool.tensor_tensor(rs[u][:, :], var[u][:, :], minus_half[:, :], ALU.pow).then_inc(s["rs_ready"], 1)

        @block.vector
        def _(dve):
            dve.wait_ge(s["loaded"], 16 * len(names))
            for u in range(U):
                dve.memset(vs[u][:, :, :, :], 0.0)
            dve.memset(minus_half[:, :], -0.5).then_inc(s["consts"], 1)
            dve.wait_ge(s["consts"], 1)

            def maxima(chain, b, c, u):
                src, hs = part(c)
                S = scores[u][0:SC, c % 2, :].rearrange("p (h t) -> p h t", t=P)
                dve.wait_ge(s["scores_done"], count(b, NCH, c + 1))
                chain.link(dve.tensor_reduce(top[u][:, src, hs], S, AX.X, ALU.max))
                dve.tensor_scalar(top[u][:, src, hs], top[u][:, src, hs], -scale, None, ALU.mult).then_inc(s["top_ready"], 1)

            def divide(chain, b, c, u):
                src, hs = part(c)
                dve.wait_ge(s["probs_ready"], count(b, NCH, c + 1))
                chain.link(dve.reciprocal(z[u][:, src, hs], z[u][:, src, hs]))
                dve.tensor_tensor(vs[u][:, src, hs, 0:HD], v[u][:, src, hs, :], spread(z[u][:, src, hs], 2, HD), ALU.mult)\
                   .then_inc(s["vs_ready"], 1)

            def moments(chain, u, src):
                dve.memset(core.beat[:, :], 0.0)
                chain.link(dve.bn_stats(bn[u][:, :], src))
                dve.memset(core.beat[:, :], 0.0)
                chain.link(dve.bn_aggr(mv[u][:, :], bn[u][:, :]))
                dve.tensor_scalar(var[u][:, :], mv[u][:, 1:2], LN_EPS, None, ALU.add).then_inc(s["var_ready"], 1)

            def norm(chain, b, r, u, dst, src):
                dve.wait_ge(s["rs_ready"], count(b, 2, r + 1))
                chain.link(dve.tensor_scalar(dst, src, mv[u][:, 0:1], rs[u][:, :], ALU.subtract, ALU.mult))
                chain.link(dve.tensor_tensor(dst, dst, w["gb"][:, 2 * r, :], ALU.mult))
                return dve.tensor_tensor(dst, dst, w["gb"][:, 2 * r + 1, :], ALU.add)

            def tail(chain, b, u, step):
                if step == 0:
                    dve.wait_ge(s["attended"], count(b))
                    moments(chain, u, extra[u][:, 0:P])
                if step == 1:
                    norm(chain, b, 0, u, o1[u][:, :], extra[u][:, 0:P]).then_inc(s["o1_ready"], 1)
                if step == 2:
                    dve.wait_ge(s["o1_ready"], count(b))
                    dve.wait_ge(s["y_done"], count(b))
                    chain.link(dve.scalar_tensor_tensor(o2[u][:, :], misc[u][:, P:2 * P], 0.0, o1[u][:, :], ALU.max, ALU.add))
                    moments(chain, u, o2[u][:, :])
                if step == 3:
                    n = number(b)
                    chain.link(norm(chain, b, 1, u, o2[u][:, :], o2[u][:, :]))
                    chain.link(dve.tensor_tensor(core.x[:, n, :], core.x[:, n, :], o2[u][:, :], ALU.add))
                    take_stats(dve, chain, core, n, bn[u], mv[u]).then_inc(s["y_added"], 1)

            def copy_q(b, u):
                dve.wait_ge(s["q_done"], count(b))
                acc = scores[u][:, 0, :].rearrange("p (g t) -> p g t", g=GROUPS)
                dve.tensor_tensor(qT[u][:, :, :], acc, spread(w["b_q"][:, :], 2, P), ALU.add).then_inc(s["q_ready"], 1)

            def attend(chain, b, u, with_tail=True, start_next=True):
                before, behind, other = neighbour(b, -1), neighbour(b, 1), 1 - u
                for c in range(NCH):
                    maxima(chain, b, c, u)
                    if c:
                        divide(chain, b, c - 1, u)
                    if c == 1 and with_tail:
                        tail(chain, before, other, 0)
                    if c == 1 and start_next:
                        copy_q(behind, other)
                    if c == 2 and with_tail:
                        tail(chain, before, other, 1)
                    if c in (5, 7) and with_tail:
                        tail(chain, before, other, c // 2)
                divide(chain, b, NCH - 1, u)

            once = Chain(dve, s["first_step"])
            copy_q((None, 0), 0)
            attend(once, (None, 0), 0, with_tail=False)
            with dve.Fori(0, batch // U - 1) as i:
                chain = Chain(dve, s["vec_step"], i, U * (2 * NCH + 2 + 2 + 1 + 2 + 3 + 1 + 2))
                attend(chain, (i, 1), 1)
                attend(chain, (i, 2), 0)
                chain.close()
            once = Chain(dve, s["last_step"])
            attend(once, (None, batch - 1), 1, start_next=False)
            for step in range(4):
                tail(once, (None, batch - 1), 1, step)

        @block.scalar
        def _(act):
            act.wait_ge(s["consts"], 1)

            def begin(b, u):
                n = number(b)
                act.activation(xn[u][:, :], core.x[:, n, :], ACT.Identity, bias=core.nmr[:, n, :],
                               scale=core.rstd[:, n, :]).then_inc(s["xn_ready"], 1)
                act.wait_ge(s["xt_done"], count(b))
                act.activation(xT[u][:, :], scores[u][:, 0, 0:P], ACT.Copy).then_inc(s["xt_ready"], 1)
                for src in range(2):
                    last = act.activation(k12[u][:, src, :], scores[u][:, 0, P + src * SC:P + (src + 1) * SC], ACT.Identity,
                                          bias=w["b_k"][:, src:src + 1])
                last.then_inc(s["k12_ready"], 1)

            def copy_v(b, u):
                act.wait_ge(s["v_done"], count(b))
                act.activation(v[u][:, :, :, :].rearrange("p s h f -> p (s h f)"), scores[u][0:SC, 1, 0:2 * P], ACT.Copy)\
                   .then_inc(s["v_ready"], 1)

            def copy_k(b, u):
                act.wait_ge(s["k_done"], count(b))
                for a in range(2):
                    last = act.activation(kT[u][:, 2 * a:2 * a + 2, :],
                                          scores[u][:, 1 - a, 0:4 * SC].rearrange("p (g t) -> p g t", g=2), ACT.Copy)
                last.then_inc(s["k_ready"], 1)

            def copy_acc(b, u):
                act.wait_ge(s["pv_done"], count(b, NCH, NCH))
                act.activation(accT[u][:, :, :], misc[u][:, :].rearrange("p (g t) -> p g t", g=GROUPS), ACT.Copy)\
                   .then_inc(s["acc_ready"], 1)

            def tail(b, u):
                act.wait_ge(s["o1t_done"], count(b))
                act.activation(o1T[u][:, :], misc[u][:, 0:P], ACT.Copy).then_inc(s["o1t_ready"], 1)

            def attend(b, u, with_tail=True, start_next=True):
                behind, other = neighbour(b, 1), 1 - u
                if with_tail:
                    copy_acc(neighbour(b, -1), other)
                if start_next:
                    begin(behind, other)
                for c in range(NCH):
                    src, hs = part(c)
                    act.wait_ge(s["top_ready"], count(b, NCH, c + 1))
                    for j in range(CHUNK):
                        h = hs.start + j
                        last = act.activation(probs[u][:, src, h, :], scores[u][0:SC, c % 2, j * P:(j + 1) * P], ACT.Exp,
                                              scale=scale, bias=top[u][:, src, h:h + 1], accum_out=z[u][:, src, h:h + 1])
                    last.then_inc(s["probs_ready"], 1)
                    if c == 0 and start_next:
                        copy_v(behind, other)
                    if c == 2 and start_next:
                        copy_k(behind, other)
                    if c == 4 and with_tail:
                        tail(neighbour(b, -1), other)

            begin((None, 0), 0)
            copy_v((None, 0), 0)
            copy_k((None, 0), 0)
            attend((None, 0), 0, with_tail=False)
            with act.Fori(0, batch // U - 1) as i:
                attend((i, 1), 1)
                attend((i, 2), 0)
            attend((None, batch - 1), 1, start_next=False)
            copy_acc((None, batch - 1), 1)
            tail((None, batch - 1), 1)

        @block.tensor
        def _(pe):
            pe.wait_ge(s["consts"], 1)

            def mm(out, lhsT, rhs, start=True, stop=True, skip=False):
                return pe.matmul(out, lhsT, rhs, start=start, stop=stop, skip_group_check=skip)

            def begin(b, u):
                for src in range(2):
                    mm(scores[u][:, 0, P + src * SC:P + (src + 1) * SC], w["w_k"][:, src, :], core.ctxT[:, number(b), :])
                pe.wait_ge(s["xn_ready"], count(b))
                pe.transpose(scores[u][:, 0, 0:P], xn[u][:, :], core.ident[:, :]).then_inc(s["xt_done"], 1)

            def front_0(b, u):
                pe.wait_ge(s["xt_ready"], count(b))
                pe.wait_ge(s["k12_ready"], count(b))
                for g in range(GROUPS):
                    last = mm(scores[u][:, 0, g * P:(g + 1) * P], w["w_q"][:, g * P:(g + 1) * P], xT[u][:, :])
                last.then_inc(s["q_done"], 1)
                for src in range(2):
                    out = scores[u][0:SC, 1, src * P:(src + 1) * P]
                    mm(out, k12[u][:, src, :], w["w_v"][:, src, :], stop=False)
                    last = mm(out, core.ones[0:1, 0:SC], w["b_v"][0:1, src * P:(src + 1) * P], start=False)
                last.then_inc(s["v_done"], 1)

            def front_1(b, u):
                pe.wait_ge(s["v_ready"], count(b))
                pe.wait_ge(s["q_ready"], count(b))
                keys = k12[u][:, :, :].rearrange("p s t -> p (s t)")
                for g in range(GROUPS):
                    out = scores[u][:, 1 - g // 2, g % 2 * 2 * SC:(g % 2 + 1) * 2 * SC]
                    last = mm(out, w["w_slot"][:, g * P:(g + 1) * P], keys)
                last.then_inc(s["k_done"], 1)

            def front_3(b, u):
                mm(extra[u][:, 0:P], xT[u][:, :], w["w_qt"][:, :], stop=False, skip=True)
                mm(extra[u][:, 0:P], core.ones[0:1, :], w["b_qt"][0:1, :], start=False, stop=False, skip=True)

            def tail_join(b, u):
                pe.wait_ge(s["acc_ready"], count(b))
                for g in range(GROUPS):
                    last = mm(extra[u][:, 0:P], accT[u][:, g, :], w["unslot"][:, g * P:(g + 1) * P], start=False,
                              stop=(g == GROUPS - 1), skip=True)
                last.then_inc(s["attended"], 1)

            def tail_turn(b, u):
                pe.wait_ge(s["o1_ready"], count(b))
                pe.transpose(misc[u][:, 0:P], o1[u][:, :], core.ident[:, :]).then_inc(s["o1t_done"], 1)

            def tail_project(b, u):
                pe.wait_ge(s["o1t_ready"], count(b))
                mm(misc[u][:, P:2 * P], o1T[u][:, :], w["w_o"][:, :], stop=False)
                mm(misc[u][:, P:2 * P], core.ones[0:1, :], w["b_o"][0:1, :], start=False).then_inc(s["y_done"], 1)

            def scoring(b, c, u):
                if c == 0:
                    pe.wait_ge(s["q_ready"], count(b))
                    pe.wait_ge(s["k_ready"], count(b))
                if c >= 2:
                    pe.wait_ge(s["probs_ready"], count(b, NCH, c - 1))
                first, src = CHUNKS[c]
                for g in range(GROUPS):
                    at = first // GROUPS * SLOT
                    last = mm(scores[u][0:SC, c % 2, g * P:(g + 1) * P], kT[u][at:at + HD, g, src * SC:(src + 1) * SC],
                              qT[u][at:at + HD, g, :])
                last.then_inc(s["scores_done"], 1)

            def weigh(b, c, u):
                pe.wait_ge(s["vs_ready"], count(b, NCH, c + 1))
                first, src = CHUNKS[c]
                at = first // GROUPS * SLOT
                for g in range(GROUPS):
                    last = mm(misc[u][at:at + SLOT, g * P:(g + 1) * P], vs[u][:, src, first + g, :],
                              probs[u][:, src, first + g, :], start=(src == 0 and g == 0), stop=(src == 1), skip=True)
                last.then_inc(s["pv_done"], 1)

            def attend(b, u, with_tail=True, start_next=True):
                before, behind, other = neighbour(b, -1), neighbour(b, 1), 1 - u
                scoring(b, 0, u)
                if start_next:
                    begin(behind, other)
                for c in range(NCH):
                    if c + 1 < NCH:
                        scoring(b, c + 1, u)
                    if c == 0 and start_next:
                        front_0(behind, other)
                    if c == 2 and start_next:
                        front_1(behind, other)
                    if c == 1 and with_tail:
                        tail_join(before, other)
                    if c == 3 and with_tail:
                        tail_turn(before, other)
                    if c == 5 and with_tail:
                        tail_project(before, other)
                    if c == 6 and start_next:
                        front_3(behind, other)
                    if c:
                        weigh(b, c - 1, u)
                weigh(b, NCH - 1, u)
                if start_next and with_tail:
                    pe.wait_ge(s["y_added"], count(before))

            begin((None, 0), 0)
            for front in (front_0, front_1, front_3):
                front((None, 0), 0)
            attend((None, 0), 0, with_tail=False)
            with pe.Fori(0, batch // U - 1) as i:
                attend((i, 1), 1)
                attend((i, 2), 0)
            attend((None, batch - 1), 1, start_next=False)
            tail_join((None, batch - 1), 1)
            tail_turn((None, batch - 1), 1)
            tail_project((None, batch - 1), 1)


def delta_rule_attention(nc, core, dram, tag):
    batch, T, NT = core.batch, TILE, TILE * P
    NI, NJ, KC, EPS = batch // TILE, batch // 8, 4, 1e-6
    STORES = 3 * 16
    TR = KC - 1
    scratch = {n: nc.dram_tensor(f"{tag}_scratch_{n}", [batch, P, P], F32, kind="Internal").ap() for n in "qkvo"}
    small_d = nc.dram_tensor(f"{tag}_scratch_small", [3, batch, HEADS, P], F32, kind="Internal").ap()

    with ExitStack() as ctx:
        st = Stage(nc, ctx, tag + "_in")
        names = ["w_in", "b_in", "conv", "w_beta", "b_beta", "head_sum"]
        w = {n: st.sb(n, list(dram[f"{tag}_{n}"].shape)) for n in names}
        xn, xT = st.sb("xn", [P, T, P]), st.sb("xT", [P, NT])
        raw = [st.sb(f"raw_{n}", [P, T, TR + P]) for n in "qkv"]
        cv = [st.sb(f"conv_{n}", [P, T, P]) for n in "qkv"]
        sq = [st.sb(f"square_{n}", [P, NT]) for n in "qk"]
        small = st.sb("small", [HEADS, 3, NT])
        misc = st.ps("misc", [P, NT])
        proj = [st.ps(f"proj_{n}", [P, NT]) for n in "qkv"]
        sm = [st.ps(f"small{n}", [HEADS, NT]) for n in range(3)]
        s = {n: st.sem(n) for n in ("loaded", "consts", "xn_ready", "xt_done", "xt_ready", "proj_done", "raw_ready",
                                    "conv_ready", "conv_step", "square_ready", "sums_done", "small_ready", "v_ready", "stored", "small_stored")}
        block = ctx.enter_context(nc.Block())

        @block.sync
        def _(sp):
            for n in names:
                sp.dma_start(w[n][tuple(slice(None) for _ in w[n].shape)], dram[f"{tag}_{n}"]).then_inc(s["loaded"], 16)
            sp.wait_ge(s["loaded"], 16 * len(names))
            sp.sem_inc(s["stored"], STORES)
            sp.sem_inc(s["small_stored"], STORES)
            with sp.Fori(0, NI) as i:
                for k, n in enumerate("qk"):
                    if k == 0:
                        sp.wait_ge(s["conv_ready"], i + 1)
                    dst = scratch[n].rearrange("(i b) p t -> i p b t", b=T)[i]
                    sp.dma_start(dst, cv[k][:, :, :]).then_inc(s["stored"], 16)
                sp.wait_ge(s["v_ready"], i + 1)
                sp.dma_start(scratch["v"].rearrange("(i b) p t -> i p b t", b=T)[i], cv[2][:, :, :]).then_inc(s["stored"], 16)
                sp.wait_ge(s["small_ready"], i + 1)
                for k in range(3):
                    dst = small_d[k].rearrange("(i b) h t -> i h b t", b=T)[i]
                    sp.dma_start(dst, small[:, k, :].rearrange("h (b t) -> h b t", b=T)).then_inc(s["small_stored"], 16)
            sp.wait_ge(s["stored"], STORES * (NI + 1))
            sp.wait_ge(s["small_stored"], STORES * (NI + 1))

        @block.vector
        def _(dve):
            dve.wait_ge(s["loaded"], 16 * len(names))
            for r in raw:
                last = dve.memset(r[:, :, 0:TR], 0.0)
            last.then_inc(s["consts"], 1)
            with dve.Fori(0, NI) as i:
                chain = Chain(dve, s["conv_step"], i, 3 * (KC - 1))
                dve.wait_ge(s["stored"], STORES * (i + 1))
                for k in range(3):
                    dve.wait_ge(s["raw_ready"], i * 3 + (k + 1))
                    c = w["conv"][:, k, :]
                    chain.link(dve.tensor_scalar(cv[k][:, :, :], raw[k][:, :, 0:P], c[:, 0:1], c[:, KC:KC + 1],
                                                 ALU.mult, ALU.add))
                    for tap in range(1, KC):
                        last = dve.scalar_tensor_tensor(cv[k][:, :, :], raw[k][:, :, tap:tap + P], c[:, tap:tap + 1],
                                                        cv[k][:, :, :], ALU.mult, ALU.add)
                        if tap < KC - 1:
                            chain.link(last)
                last.then_inc(s["conv_ready"], 1)
                chain.close()

        @block.scalar
        def _(act):
            act.wait_ge(s["consts"], 1)

            def normalise(i, d):
                for t in range(T):
                    b = i * T + (d * T + t)
                    last = act.activation(xn[:, t, :], core.x[:, b, :], ACT.Identity, bias=core.nmr[:, b, :],
                                          scale=core.rstd[:, b, :])
                last.then_inc(s["xn_ready"], 1)
                act.wait_ge(s["xt_done"], i + (d + 1))
                act.activation(xT[:, :], misc[:, :], ACT.Copy).then_inc(s["xt_ready"], 1)

            def copy_projections(i, d):
                act.wait_ge(s["proj_done"], i + (d + 1))
                for k in range(3):
                    act.activation(raw[k][:, :, TR:], proj[k][:, :].rearrange("p (b t) -> p b t", b=T), ACT.Identity,
                                   bias=w["b_in"][:, k:k + 1]).then_inc(s["raw_ready"], 1)

            def silu_v(i):
                act.wait_ge(s["conv_ready"], i + 1)
                act.activation(cv[2][:, :, :], cv[2][:, :, :], ACT.Silu).then_inc(s["v_ready"], 1)

            def squares(i):
                for k in range(2):
                    last = act.activation(sq[k][:, :], cv[k][:, :, :].rearrange("p b t -> p (b t)"), ACT.Square)
                last.then_inc(s["square_ready"], 1)

            def copy_small(i):
                act.wait_ge(s["sums_done"], i + 1)
                act.wait_ge(s["small_stored"], STORES * (i + 1))
                for k in range(3):
                    last = act.activation(small[:, k, :], sm[k][:, :], ACT.Identity, bias=w["b_beta"][:, k:k + 1])
                last.then_inc(s["small_ready"], 1)

            normalise(0, 0)
            copy_projections(0, 0)
            with act.Fori(0, NI - 1) as i:
                normalise(i, 1)
                silu_v(i)
                squares(i)
                copy_projections(i, 1)
                copy_small(i)
            silu_v(NI - 1)
            squares(NI - 1)
            copy_small(NI - 1)

        @block.tensor
        def _(pe):
            pe.wait_ge(s["consts"], 1)

            def project(i, d):
                pe.wait_ge(s["xn_ready"], i + (d + 1))
                for t in range(T):
                    last = pe.transpose(misc[:, t * P:(t + 1) * P], xn[:, t, :], core.ident[:, :])
                last.then_inc(s["xt_done"], 1)
                pe.wait_ge(s["xt_ready"], i + (d + 1))
                if d:
                    pe.wait_ge(s["raw_ready"], i * 3 + 3)
                for k in range(3):
                    last = pe.matmul(proj[k][:, :], w["w_in"][:, k, :], xT[:, :], start=True, stop=True)
                last.then_inc(s["proj_done"], 1)

            def beta_logits(i, d):
                if d:
                    pe.wait_ge(s["small_ready"], i + 1)
                pe.matmul(sm[0][:, :], w["w_beta"][:, :], xT[:, :], start=True, stop=True)

            def sums(i):
                pe.wait_ge(s["square_ready"], i + 1)
                for k in range(2):
                    last = pe.matmul(sm[1 + k][:, :], w["head_sum"][:, :], sq[k][:, :], start=True, stop=True)
                last.then_inc(s["sums_done"], 1)

            project(0, 0)
            beta_logits(0, 0)
            with pe.Fori(0, NI - 1) as i:
                project(i, 1)
                sums(i)
                beta_logits(i, 1)
            sums(NI - 1)

    with ExitStack() as ctx:
        st = Stage(nc, ctx, tag + "_rec")
        q, k, v = (st.sb(n, [P, NJ, HD, P]) for n in "qkv")
        beta, qq, kk = (st.sb(n, [P, NJ, P]) for n in ("beta", "q_sq", "k_sq"))
        S = [st.sb(f"S{p}", [P, NJ, HD, HD]) for p in range(2)]
        sq_t = st.sb("state_times_q", [P, NJ, HD, HD])
        m0, m1 = st.sb("m0", [P, NJ, HD, HD]), st.sb("m1", [P, NJ, HD, HD])
        d = st.sb("d", [P, NJ, HD])
        osq = st.sb("osq", [P, HD, P])
        s = {n: st.sem(n) for n in ("loaded", "step", "clamped", "exp_ready", "norms_ready", "rms_ready", "root_ready",
                                    "rec", "state_ready", "product_step", "output_ready", "post", "o_ready", "stored")}
        block = ctx.enter_context(nc.Block())

        @block.sync
        def _(sp):
            for n, t in (("k", k), ("v", v), ("q", q)):
                sp.dma_start(t[:, :, :, :].rearrange("p j d t -> p j (d t)"),
                             scratch[n].rearrange("(j l) (h d) t -> (l h) j (d t)", l=8, h=HEADS)).then_inc(s["loaded"], 16)
            for n, t in ((0, beta), (1, qq), (2, kk)):
                sp.dma_start(t[:, :, :], small_d[n].rearrange("(j l) h t -> (l h) j t", l=8)).then_inc(s["loaded"], 16)
            sp.wait_ge(s["o_ready"], 1)
            sp.dma_start(scratch["o"].rearrange("(j l) (h d) t -> (l h) j (d t)", l=8, h=HEADS),
                         v[:, :, :, :].rearrange("p j d t -> p j (d t)")).then_inc(s["stored"], 16)
            sp.wait_ge(s["stored"], 16)

        @block.gpsimd
        def _(pool):
            pool.sem_inc(s["output_ready"], 2)
            pool.wait_ge(s["loaded"], 16 * 6)
            with pool.Fori(0, P // 2) as i:
                chain = Chain(pool, s["product_step"], i, 2 * 3)
                for at in range(2):
                    t = i * 2 + at
                    pool.wait_ge(s["state_ready"], i * 2 + (at + 1))
                    chain.link(pool.tensor_tensor(sq_t[:, :, :, :], S[at][:, :, :, :], spread(q[:, :, :, t], 2, HD), ALU.mult))
                    for half in (HD // 2, HD // 4):
                        chain.link(pool.tensor_tensor(sq_t[:, :, :, 0:half], sq_t[:, :, :, 0:half],
                                                      sq_t[:, :, :, half:2 * half], ALU.add))
                    pool.tensor_tensor(v[:, :, :, t], sq_t[:, :, :, 0], sq_t[:, :, :, 1], ALU.add).then_inc(s["output_ready"], 1)
                    pool.wait_ge(s["output_ready"], i * 2 + (at + 3))
                chain.close()

        @block.scalar
        def _(act):
            act.wait_ge(s["clamped"], 1)
            act.activation(beta[:, :, :], beta[:, :, :], ACT.Exp).then_inc(s["exp_ready"], 1)
            act.activation(kk[:, :, :], kk[:, :, :], ACT.Sqrt)
            act.activation(qq[:, :, :], qq[:, :, :], ACT.Sqrt).then_inc(s["norms_ready"], 1)
            act.wait_ge(s["rms_ready"], 1)
            act.activation(kk[:, :, :], kk[:, :, :], ACT.Sqrt).then_inc(s["root_ready"], 1)

        @block.vector
        def _(dve):
            pre = Chain(dve, s["step"])
            dve.wait_ge(s["loaded"], 16 * 6)
            dve.tensor_scalar(beta[:, :, :], beta[:, :, :], -1.0, 88.0, ALU.mult, ALU.min).then_inc(s["clamped"], 1)
            dve.memset(S[1][:, :, :, :], 0.0)
            dve.wait_ge(s["exp_ready"], 1)
            pre.link(dve.tensor_scalar(beta[:, :, :], beta[:, :, :], 1.0, None, ALU.add))
            pre.link(dve.reciprocal(beta[:, :, :], beta[:, :, :]))
            dve.wait_ge(s["norms_ready"], 1)
            for a in (kk, qq):
                pre.link(dve.tensor_scalar(a[:, :, :], a[:, :, :], EPS, None, ALU.add))
                pre.link(dve.reciprocal(a[:, :, :], a[:, :, :]))
            pre.link(dve.tensor_tensor(beta[:, :, :], beta[:, :, :], kk[:, :, :], ALU.mult))
            pre.link(dve.tensor_tensor(beta[:, :, :], beta[:, :, :], kk[:, :, :], ALU.mult))
            with dve.Fori(0, P // 2) as i:
                chain = Chain(dve, s["rec"], i, 2 * 5)
                for at in range(2):
                    t = i * 2 + at
                    old, new = S[1 - at], S[at]
                    kt = spread(k[:, :, :, t], 2, HD)
                    chain.link(dve.tensor_tensor(m0[:, :, :, :], old[:, :, :, :], kt, ALU.mult))
                    chain.link(dve.tensor_reduce(d[:, :, :], m0[:, :, :, :], AX.X, ALU.add))
                    chain.link(dve.tensor_tensor(d[:, :, :], v[:, :, :, t], d[:, :, :], ALU.subtract))
                    chain.link(dve.tensor_tensor(d[:, :, :], d[:, :, :], spread(beta[:, :, t], 2, HD), ALU.mult))
                    chain.link(dve.tensor_tensor(m1[:, :, :, :], spread(d[:, :, :], 3, HD), kt, ALU.mult))
                    dve.wait_ge(s["output_ready"], i * 2 + (at + 1))
                    dve.tensor_tensor(new[:, :, :, :], old[:, :, :, :], m1[:, :, :, :], ALU.add).then_inc(s["state_ready"], 1)
                    dve.wait_ge(s["state_ready"], i * 2 + (at + 1))
                chain.close()
            dve.wait_ge(s["output_ready"], P + 2)
            post = Chain(dve, s["post"])
            for j in range(NJ):
                post.link(dve.tensor_tensor(osq[:, :, :], v[:, j, :, :], v[:, j, :, :], ALU.mult))
                post.link(dve.tensor_reduce(kk[:, j, :], osq[:, :, :].rearrange("p d t -> p t d"), AX.X, ALU.add))
            post.link(dve.tensor_tensor(kk[:, :, :], kk[:, :, :], qq[:, :, :], ALU.mult))
            post.link(dve.tensor_tensor(kk[:, :, :], kk[:, :, :], qq[:, :, :], ALU.mult))
            dve.tensor_scalar(kk[:, :, :], kk[:, :, :], 1.0 / HD, 1e-6, ALU.mult, ALU.add).then_inc(s["rms_ready"], 1)
            dve.wait_ge(s["root_ready"], 1)
            post.link(dve.reciprocal(kk[:, :, :], kk[:, :, :]))
            post.link(dve.tensor_tensor(kk[:, :, :], kk[:, :, :], qq[:, :, :], ALU.mult))
            dve.tensor_tensor(v[:, :, :, :], v[:, :, :, :], spread(kk[:, :, :], 2, HD), ALU.mult).then_inc(s["o_ready"], 1)

    with ExitStack() as ctx:
        st = Stage(nc, ctx, tag + "_out")
        oT = st.sb("oT", [P, batch, P])
        ot = [st.sb(f"ot{p}", [P, T, P]) for p in range(2)]
        w_o, b_o, nw = st.sb("w_o", [P, P]), st.sb("b_o", [1, P]), st.sb("norm_w", [P, 1])
        bn, mv = st.sb("bn", [P, T, 6]), st.sb("mv", [P, T, 2])
        yp = [st.ps(f"y{p}", [P, T, P]) for p in range(2)]
        s = {n: st.sem(n) for n in ("loaded", "consts", "ot_ready", "y_done", "y_read", "vec_step")}
        block = ctx.enter_context(nc.Block())

        @block.sync
        def _(sp):
            sp.dma_start(oT[:, :, :], scratch["o"].rearrange("b p t -> p b t")).then_inc(s["loaded"], 16)
            sp.dma_start(w_o[:, :], dram[tag + "_w_o"]).then_inc(s["loaded"], 16)
            sp.dma_start(b_o[:, :], dram[tag + "_b_o"]).then_inc(s["loaded"], 16)
            sp.dma_start(nw[:, :], dram[tag + "_norm_w"]).then_inc(s["loaded"], 16)
            sp.wait_ge(s["loaded"], 64)

        @block.scalar
        def _(act):
            act.wait_ge(s["consts"], 1)
            tile_of = oT[:, :, :].rearrange("p (i t) f -> p i t f", t=T)
            with act.Fori(0, NI // 2) as i:
                for p in range(2):
                    act.wait_ge(s["y_done"], i * 2 + (p + 1))
                    act.activation(ot[p][:, :, :], tile_of[:, i * 2 + p, :, :], ACT.Copy).then_inc(s["ot_ready"], 1)

        @block.tensor
        def _(pe):
            pe.sem_inc(s["y_done"], 2)
            pe.wait_ge(s["consts"], 1)
            with pe.Fori(0, NI // 2) as i:
                for p in range(2):
                    pe.wait_ge(s["ot_ready"], i * 2 + (p + 1))
                    pe.wait_ge(s["y_read"], i * 2 + (p + 1))
                    for t in range(T):
                        pe.matmul(yp[p][:, t, :], ot[p][:, t, :], w_o[:, :], start=True, stop=False)
                        last = pe.matmul(yp[p][:, t, :], core.ones[0:1, :], b_o[0:1, :], start=False, stop=True)
                    last.then_inc(s["y_done"], 1)

        @block.vector
        def _(dve):
            dve.sem_inc(s["y_read"], 2)
            dve.wait_ge(s["loaded"], 64)
            dve.tensor_scalar(w_o[:, :], w_o[:, :], nw[:, :], None, ALU.mult).then_inc(s["consts"], 1)
            tile_of = core.x[:, :, :].rearrange("p (i t) f -> p i t f", t=T)
            with dve.Fori(0, NI // 2) as i:
                chain = Chain(dve, s["vec_step"], i, 2 * (1 + 3))
                for p in range(2):
                    x = tile_of[:, i * 2 + p, :, :]
                    dve.wait_ge(s["y_done"], i * 2 + (p + 3))
                    chain.link(dve.tensor_tensor(x, x, yp[p][:, :, :], ALU.add))
                    dve.sem_inc(s["y_read"], 1)
                    take_tile_stats(dve, chain, core.x, core.stat, i * 2 + p, T, bn, mv, core.beat)
                chain.close()


def wave_attention(nc, core, dram, tag):
    batch, T, NT = core.batch, TILE, TILE * P
    NI, H, PD, NS, DH = batch // T, 8, 16, 33, 16
    W3 = 3 * H
    LINKS = 30 + 13 * T
    with ExitStack() as ctx:
        st = Stage(nc, ctx, tag)
        names = ["w_wave", "b_wave", "w_query", "b_query", "kw", "w_se1", "b_se1", "w_se2", "b_se2", "w_out"]
        w = {n: st.sb(n, list(dram[f"{tag}_{n}"].shape)) for n in names}
        tab = st.sb("tables", list(dram["wave_tables"].shape))
        grid, absgrid, J = tab[:, 0:NS], tab[:, NS:2 * NS], tab[:, 2 * NS:2 * NS + P]
        cent, half_less, A3, B3 = (tab[:, 2 * NS + P + a:2 * NS + P + b] for a, b in ((0, 1), (1, 2), (2, 5), (5, 8)))
        hb1, hb2 = st.sb("half_b_se1", [P // 4, 1]), st.sb("half_b_se2", [P, 1])
        xn = [st.sb(f"xn{p}", [P, T, P]) for p in range(2)]
        xT = st.sb("xT", [P, NT])
        th_w, th_q = st.sb("th_wave", [P, T, W3]), st.sb("th_query", [P, T, P])
        wave, wt = st.sb("wave2", [P, T, W3]), st.sb("wave_tanh", [P, T, W3])
        qk = st.sb("qk", [P, T, H])
        fpd, inv = st.sb("fpd", [P, T, 3]), st.sb("inverse", [P, T, 3])
        place, valid, hole, rel, rd, far = (st.sb(n, [P, T, NS]) for n in ("place", "valid", "hole", "rel", "rd", "far"))
        e1, e2 = st.sb("e1", [P, T, H, NS]), st.sb("e2", [P, T, H, NS])
        top, z, norm, slope, bias = (st.sb(n, [P, T, H]) for n in ("top", "z", "norm", "slope", "bias"))
        near, shift = st.sb("near", [P, T, 1]), st.sb("shift", [P, T, 1])
        smp = [st.sb(f"sample{j}", [P, 2, P]) for j in range(2)]
        off = [st.sb(f"off{j}", [P, 2, P]) for j in range(2)]
        flag = [st.sb(f"flag{j}", [P, 2, P]) for j in range(2)]
        dist = [st.sb(f"dist{j}", [P, 2, P]) for j in range(2)]
        E = [st.sb(f"E{j}", [P, H, 2, P]) for j in range(2)]
        A = [st.sb(f"A{j}", [P, H, P]) for j in range(2)]
        AT = [st.sb(f"AT{j}", [P, H, P]) for j in range(2)]
        o, oT = st.sb("o", [P, T, P]), st.sb("oT", [P, NT])
        s1, s1t = st.sb("s1", [P // 4, NT]), st.sb("s1t", [P // 4, NT])
        s2t, yt = st.sb("s2t", [P, NT]), st.sb("yt", [P, T, P])
        bn, mv = st.sb("bn", [P, T, 6]), st.sb("mv", [P, T, 2])
        misc, zw, zq, op, s1p = st.ps("misc", [P, NT]), st.ps("zw", [P, T, W3]), st.ps("zq", [P, T, P]), \
            st.ps("op", [P, T, P]), st.ps("s1p", [P // 4, NT])
        yp = st.ps("yp", [P, T, P])
        ptp = [st.ps(f"ptp{a}", [P, 4, P]) for a in range(2)]
        s = {n: st.sem(n) for n in (
            "loaded", "once", "consts", "xn_ready", "xt_done", "xt_ready", "z_done", "th_ready", "wave_ready", "wt_ready",
            "e1_ready", "e1_exp", "dist_ready", "E_ready", "A_ready", "at_done", "at_ready", "pv_done",
            "o_ready", "ot_done", "ot_ready", "s1_done", "s1_ready", "s1_used", "s2_done", "s2_ready", "g_ready",
            "y_done", "yt_ready", "vec_step", "first_step", "last_step")}
        n_loads = 16 * (len(names) + 1)
        block = ctx.enter_context(nc.Block())

        def count(m, per=1, extra=1):
            i, at = m
            return at * per + extra if i is None else i * (2 * per) + (at * per + extra)

        def after(m):
            return (m[0], m[1] + 1)

        @block.sync
        def _(sp):
            for n in names:
                sp.dma_start(w[n][tuple(slice(None) for _ in w[n].shape)], dram[f"{tag}_{n}"]).then_inc(s["loaded"], 16)
            sp.dma_start(tab[:, :], dram["wave_tables"]).then_inc(s["loaded"], 16)
            sp.wait_ge(s["loaded"], n_loads)

        @block.vector
        def _(dve):
            dve.wait_ge(s["loaded"], n_loads)
            dve.tensor_scalar(hb1[:, :], w["b_se1"][:, :], 0.5, None, ALU.mult)
            dve.tensor_scalar(hb2[:, :], w["b_se2"][:, :], 0.5, None, ALU.mult).then_inc(s["consts"], 1)

            chains = []

            def link(ins):
                chains[-1].link(ins)

            def tt(out, a, b, op):
                link(dve.tensor_tensor(out, a, b, op))

            def ts(out, a, s1_, s2_, op0, op1=ALU.bypass):
                link(dve.tensor_scalar(out, a, s1_, s2_, op0, op1))

            def stt(out, a, sc, b, op0, op1):
                link(dve.scalar_tensor_tensor(out, a, sc, b, op0, op1))

            def flat(a):
                return a[:, :, :].rearrange("p a b -> p (a b)")

            def waves(m):
                dve.wait_ge(s["th_ready"], count(m))
                dve.scalar_tensor_tensor(flat(wave), flat(th_w), 1.0, zw[:, :, :].rearrange("p a b -> p (a b)"),
                                         ALU.add, ALU.mult).then_inc(s["wave_ready"], 1)
                stt(flat(th_q), flat(th_q), 1.0, zq[:, :, :].rearrange("p a b -> p (a b)"), ALU.add, ALU.mult)
                q = flat(th_q).rearrange("p (x d) -> p x d", d=PD)
                tt(q, q, spread(w["kw"][:, :], 1, T * H), ALU.mult)
                link(dve.tensor_reduce(flat(qk), q, AX.X, ALU.add))
                ts(qk[:, :, :], qk[:, :, :], 0.5 * PD ** -0.5, None, ALU.mult)
                dve.wait_ge(s["wt_ready"], count(m))
                link(dve.tensor_reduce(fpd[:, :, :], wt[:, :, :].rearrange("p t (a h) -> p t a h", a=3), AX.X, ALU.add))
                tt(fpd[:, :, :], fpd[:, :, :], spread(A3, 1, T), ALU.mult)
                tt(fpd[:, :, :], fpd[:, :, :], spread(B3, 1, T), ALU.add)
                ts(fpd[:, :, 2:3], fpd[:, :, 2:3], 0.1, None, ALU.max)
                link(dve.reciprocal(inv[:, :, 0:3:2], fpd[:, :, 0:3:2]))

            def samples(m, part):
                f, ph, rdec = (spread(a, 2, NS) for a in (fpd[:, :, 0], fpd[:, :, 1], inv[:, :, 2]))
                if part == 0:
                    tt(place[:, :, :], spread(grid, 1, T), f, ALU.mult)
                    ts(place[:, :, :], place[:, :, :], cent, None, ALU.add)
                    tt(place[:, :, :], place[:, :, :], ph, ALU.add)
                    ts(hole[:, :, :], place[:, :, :], 0.0, None, ALU.is_ge)
                    stt(flat(valid), flat(place), float(P), flat(hole), ALU.is_lt, ALU.mult)
                    ts(hole[:, :, :], valid[:, :, :], -1.0, 1e30, ALU.add, ALU.mult)
                    tt(rel[:, :, :], spread(absgrid, 1, T), f, ALU.mult)
                    tt(rd[:, :, :], rel[:, :, :], rdec, ALU.mult)
                    tt(far[:, :, :], rel[:, :, :], hole[:, :, :], ALU.subtract)
                    link(dve.tensor_reduce(near[:, :, 0], far[:, :, :], AX.X, ALU.min))
                if part == 1:
                    tt(e1[:, :, :, :], spread(qk[:, :, :], 3, NS), spread(rel[:, :, :], 2, H), ALU.mult)
                    tt(e1[:, :, :, :], e1[:, :, :, :], spread(hole[:, :, :], 2, H), ALU.add)
                if part == 2:
                    link(dve.tensor_reduce(top[:, :, :], e1[:, :, :, :], AX.X, ALU.max))
                    tt(e1[:, :, :, :], e1[:, :, :, :], spread(top[:, :, :], 3, NS), ALU.subtract)
                    dve.tensor_tensor(e2[:, :, :, :], e1[:, :, :, :], spread(rd[:, :, :], 2, H), ALU.subtract)\
                       .then_inc(s["e1_ready"], 1)
                    tt(slope[:, :, :], qk[:, :, :], spread(inv[:, :, 2], 2, H), ALU.subtract)
                    tt(bias[:, :, :], slope[:, :, :], spread(near[:, :, 0], 2, H), ALU.mult)
                    tt(bias[:, :, :], bias[:, :, :], top[:, :, :], ALU.subtract)
                    ts(shift[:, :, 0], fpd[:, :, 1], -1.0, half_less, ALU.mult, ALU.add)
                    tt(shift[:, :, 0], shift[:, :, 0], inv[:, :, 0], ALU.mult)
                    ts(shift[:, :, 0], shift[:, :, 0], -0.5, None, ALU.add)

            def sums(m):
                dve.wait_ge(s["e1_exp"], count(m))
                link(dve.tensor_reduce(z[:, :, :], e1[:, :, :, :], AX.X, ALU.add))
                link(dve.tensor_reduce(norm[:, :, :], e2[:, :, :, :], AX.X, ALU.add))
                stt(flat(norm), flat(z), 1e-8, flat(norm), ALU.mult, ALU.add)
                link(dve.reciprocal(norm[:, :, :], norm[:, :, :]))

            def spots(m, t):
                j = t % 2
                f, ph = fpd[:, t, 0:1], fpd[:, t, 1:2]
                ts(smp[j][:, 0, :], J, inv[:, t, 0:1], shift[:, t, :], ALU.mult, ALU.add)
                ts(smp[j][:, 0, :], smp[j][:, 0, :], MAGIC, -MAGIC, ALU.add, ALU.add)
                ts(smp[j][:, 1, :], smp[j][:, 0, :], 1.0, None, ALU.add)
                ts(off[j][:, :, :], smp[j][:, :, :], f, cent, ALU.mult, ALU.add)
                for k in range(2):
                    last = dve.scalar_tensor_tensor(off[j][:, k, :], off[j][:, k, :], ph, J, ALU.add, ALU.subtract)
                link(last)
                stt(smp[j][:, :, :], smp[j][:, :, :], -1.0, smp[j][:, :, :], ALU.mult, ALU.max)
                if t >= 2:
                    dve.wait_ge(s["A_ready"], count(m, T, t - 1))
                ts(flag[j][:, :, :], off[j][:, :, :], 0.0, None, ALU.is_ge)
                stt(flag[j][:, :, :], off[j][:, :, :], 1.0, flag[j][:, :, :], ALU.is_lt, ALU.mult)
                stt(flag[j][:, :, :], smp[j][:, :, :], float(NS // 2), flag[j][:, :, :], ALU.is_le, ALU.mult)
                ts(smp[j][:, :, :], smp[j][:, :, :], f, near[:, t, :], ALU.mult, ALU.subtract)
                if t >= 2:
                    dve.wait_ge(s["E_ready"], count(m, T, t - 1))
                dve.tensor_tensor(dist[j][:, :, :], smp[j][:, :, :], flag[j][:, :, :], ALU.mult).then_inc(s["dist_ready"], 1)

            def matrix(m, t):
                j = t % 2
                dve.wait_ge(s["E_ready"], count(m, T, t + 1))
                tt(E[j][:, :, :, :].rearrange("p h k j -> p h (k j)"), E[j][:, :, :, :].rearrange("p h k j -> p h (k j)"),
                   spread(flag[j][:, :, :].rearrange("p k j -> p (k j)"), 1, H), ALU.mult)
                if t >= 2:
                    dve.wait_ge(s["at_done"], count(m, 2 * T, 2 * (t - 1)))
                dve.tensor_tensor(A[j][:, :, :], E[j][:, :, 0, :], E[j][:, :, 1, :], ALU.add).then_inc(s["A_ready"], 1)

            def attended(m):
                dve.wait_ge(s["pv_done"], count(m, T, T))
                dve.tensor_tensor(o[:, :, :].rearrange("p t (h d) -> p (t h) d", h=H),
                                  op[:, :, :].rearrange("p t (h d) -> p (t h) d", h=H), spread(flat(norm), 2, DH), ALU.mult)\
                   .then_inc(s["o_ready"], 1)

            def squeeze(m):
                dve.wait_ge(s["s1_ready"], count(m))
                dve.scalar_tensor_tensor(s1[:, :], s1t[:, :], 1.0, s1[:, :], ALU.add, ALU.mult).then_inc(s["s1_used"], 1)

            def excite(m):
                dve.wait_ge(s["s2_ready"], count(m))
                dve.scalar_tensor_tensor(oT[:, :], s2t[:, :], 1.0, oT[:, :], ALU.add, ALU.mult).then_inc(s["g_ready"], 1)

            def residual(m):
                dve.wait_ge(s["yt_ready"], count(m))
                stt(flat(yt), flat(yt), 1.0, yp[:, :, :].rearrange("p a b -> p (a b)"), ALU.add, ALU.mult)
                x = core.x[:, :, :].rearrange("p (i t) f -> p i t f", t=T)[:, count(m, 1, 0), :, :]
                stt(x, yt[:, :, :], 0.25, x, ALU.mult, ALU.add)
                take_tile_stats(dve, chains[-1], core.x, core.stat, count(m, 1, 0), T, bn, mv, core.beat)

            def tile(m, start_next=True):
                spots(m, 0)
                spots(m, 1)
                sums(m)
                for t in range(T):
                    matrix(m, t)
                    if t + 2 < T:
                        spots(m, t + 2)
                if start_next:
                    waves(after(m))
                attended(m)
                if start_next:
                    samples(after(m), 0)
                squeeze(m)
                if start_next:
                    samples(after(m), 1)
                excite(m)
                if start_next:
                    samples(after(m), 2)
                residual(m)

            chains.append(Chain(dve, s["first_step"]))
            waves((None, 0))
            for part in range(3):
                samples((None, 0), part)
            tile((None, 0))
            with dve.Fori(0, NI // 2 - 1) as i:
                chains.append(Chain(dve, s["vec_step"], i, 2 * LINKS))
                tile((i, 1))
                tile((i, 2))
                chains[-1].close()
            chains.append(Chain(dve, s["last_step"]))
            tile((None, NI - 1), start_next=False)

        @block.scalar
        def _(act):
            act.wait_ge(s["consts"], 1)

            def begin(m):
                for t in range(T):
                    b = count(m, T, t)
                    last = act.activation(xn[m[1] % 2][:, t, :], core.x[:, b, :], ACT.Identity, bias=core.nmr[:, b, :],
                                          scale=core.rstd[:, b, :])
                last.then_inc(s["xn_ready"], 1)
                act.wait_ge(s["xt_done"], count(m))
                act.activation(xT[:, :], misc[:, :], ACT.Copy).then_inc(s["xt_ready"], 1)
                act.wait_ge(s["z_done"], count(m))
                act.activation(th_w[:, :, :], zw[:, :, :], ACT.Tanh, scale=0.5)
                act.activation(th_q[:, :, :], zq[:, :, :], ACT.Tanh, scale=0.5).then_inc(s["th_ready"], 1)

            def waves(m):
                act.wait_ge(s["wave_ready"], count(m))
                w3, t3 = (a[:, :, :].rearrange("p t (a h) -> p t a h", a=3) for a in (wave, wt))
                for a, sc in ((0, 0.25), (2, 0.25), (1, 0.5)):
                    last = act.activation(t3[:, :, a, :], w3[:, :, a, :], ACT.Tanh, scale=sc)
                last.then_inc(s["wt_ready"], 1)

            def samples(m):
                act.wait_ge(s["e1_ready"], count(m))
                act.activation(e1[:, :, :, :], e1[:, :, :, :], ACT.Exp)
                act.activation(e2[:, :, :, :], e2[:, :, :, :], ACT.Exp).then_inc(s["e1_exp"], 1)

            def exps(m, t):
                j = t % 2
                act.wait_ge(s["dist_ready"], count(m, T, t + 1))
                if t >= 2:
                    act.wait_ge(s["A_ready"], count(m, T, t - 1))
                for h in range(H):
                    last = act.activation(E[j][:, h, :, :], dist[j][:, :, :], ACT.Exp, bias=bias[:, t, h:h + 1],
                                          scale=slope[:, t, h:h + 1])
                last.then_inc(s["E_ready"], 1)

            def copies(m, t):
                j = t % 2
                for a in range(2):
                    act.wait_ge(s["at_done"], count(m, 2 * T, 2 * t + a + 1))
                    act.activation(AT[j][:, 4 * a:4 * a + 4, :], ptp[a][:, :, :], ACT.Copy).then_inc(s["at_ready"], 1)

            def finish(m):
                act.wait_ge(s["ot_done"], count(m))
                act.activation(oT[:, :], misc[:, :], ACT.Copy).then_inc(s["ot_ready"], 1)
                act.wait_ge(s["s1_done"], count(m))
                act.activation(s1t[:, :], s1p[:, :], ACT.Tanh, scale=0.5, bias=hb1[:, :])
                act.activation(s1[:, :], s1p[:, :], ACT.Identity, bias=w["b_se1"][:, :]).then_inc(s["s1_ready"], 1)
                act.wait_ge(s["s2_done"], count(m))
                act.activation(s2t[:, :], yp[:, :, :].rearrange("p a b -> p (a b)"), ACT.Tanh, scale=0.25, bias=hb2[:, :])\
                   .then_inc(s["s2_ready"], 1)
                act.wait_ge(s["y_done"], count(m))
                act.activation(yt[:, :, :], yp[:, :, :], ACT.Tanh, scale=0.25).then_inc(s["yt_ready"], 1)

            def tile(m, start_next=True):
                exps(m, 0)
                for t in range(T):
                    if t + 1 < T:
                        exps(m, t + 1)
                    copies(m, t)
                    if t == 1 and start_next:
                        begin(after(m))
                if start_next:
                    waves(after(m))
                finish(m)
                if start_next:
                    samples(after(m))

            begin((None, 0))
            waves((None, 0))
            samples((None, 0))
            tile((None, 0))
            with act.Fori(0, NI // 2 - 1) as i:
                tile((i, 1))
                tile((i, 2))
            tile((None, NI - 1), start_next=False)

        @block.tensor
        def _(pe):
            pe.wait_ge(s["consts"], 1)

            def mm(out, lhsT, rhs, start=True, stop=True):
                return pe.matmul(out, lhsT, rhs, start=start, stop=stop)

            def begin(m):
                pe.wait_ge(s["xn_ready"], count(m))
                for t in range(T):
                    last = pe.transpose(misc[:, t * P:(t + 1) * P], xn[m[1] % 2][:, t, :], core.ident[:, :])
                last.then_inc(s["xt_done"], 1)
                pe.wait_ge(s["xt_ready"], count(m))
                for t in range(T):
                    mm(zw[:, t, :], xT[:, t * P:(t + 1) * P], w["w_wave"][:, :], stop=False)
                    mm(zw[:, t, :], core.ones[0:1, :], w["b_wave"][0:1, :], start=False)
                    mm(zq[:, t, :], xT[:, t * P:(t + 1) * P], w["w_query"][:, :], stop=False)
                    last = mm(zq[:, t, :], core.ones[0:1, :], w["b_query"][0:1, :], start=False)
                last.then_inc(s["z_done"], 1)

            def tile(m, start_next=True):
                for t in range(T):
                    j = t % 2
                    pe.wait_ge(s["A_ready"], count(m, T, t + 1))
                    for a in range(2):
                        if t:
                            pe.wait_ge(s["at_ready"], count(m, 2 * T, 2 * (t - 1) + a + 1))
                        for h in range(4):
                            last = pe.transpose(ptp[a][:, h, :], A[j][:, 4 * a + h, :], core.ident[:, :])
                        last.then_inc(s["at_done"], 1)
                    pe.wait_ge(s["at_ready"], count(m, 2 * T, 2 * t + 2))
                    for h in range(H):
                        last = mm(op[:, t, h * DH:(h + 1) * DH], AT[j][:, h, :], xn[m[1] % 2][:, t, h * DH:(h + 1) * DH])
                    last.then_inc(s["pv_done"], 1)
                    if t == 1 and start_next:
                        begin(after(m))
                pe.wait_ge(s["o_ready"], count(m))
                for t in range(T):
                    last = pe.transpose(misc[:, t * P:(t + 1) * P], o[:, t, :], core.ident[:, :])
                last.then_inc(s["ot_done"], 1)
                pe.wait_ge(s["ot_ready"], count(m))
                mm(s1p[:, :], w["w_se1"][:, :], oT[:, :]).then_inc(s["s1_done"], 1)
                pe.wait_ge(s["s1_used"], count(m))
                mm(yp[:, :, :].rearrange("p a b -> p (a b)"), w["w_se2"][:, :], s1[:, :]).then_inc(s["s2_done"], 1)
                pe.wait_ge(s["g_ready"], count(m))
                for t in range(T):
                    last = mm(yp[:, t, :], oT[:, t * P:(t + 1) * P], w["w_out"][:, :])
                last.then_inc(s["y_done"], 1)

            begin((None, 0))
            tile((None, 0))
            with pe.Fori(0, NI // 2 - 1) as i:
                tile((i, 1))
                tile((i, 2))
            tile((None, NI - 1), start_next=False)


STAGES = ["L0_attn", "L0_xattn", "L0_ffn", "L1_attn", "L1_xattn", "L1_ffn",
          "L2_attn", "L2_xattn", "L2_ffn", "L3_attn", "L3_xattn", "L3_ffn"]

MLP_KINDS = {"L0_ffn": "moe0", "L2_ffn": "plain", "L3_ffn": "moe3"}


def decoder_kernel(nc, dram, batch, stages=STAGES):
    with ExitStack() as ctx:
        core = Core(nc, ctx, batch)
        load_everything(nc, core, dram)
        for tag in stages:
            norm_scalars(nc, core, tag, LN_EPS if tag in ("L2_ffn", "L3_xattn") else None)
            if tag == "L0_attn":
                softmax_attention(nc, core, dram, tag, heads_norm=True)
            elif tag == "L0_xattn":
                softmax_attention(nc, core, dram, tag, context="past")
            elif tag == "L1_xattn":
                softmax_attention(nc, core, dram, tag, context="only")
            elif tag == "L3_attn":
                softmax_attention(nc, core, dram, tag, latent=True)
            elif tag == "L1_ffn":
                quantised_mlp(nc, core, dram, tag)
            elif tag == "L2_xattn":
                query_softmax_attention(nc, core, dram, tag)
            elif tag == "L3_xattn":
                wide_cross_attention(nc, core, dram, tag)
            elif tag == "L2_attn":
                delta_rule_attention(nc, core, dram, tag)
            elif tag == "L1_attn":
                wave_attention(nc, core, dram, tag)
            elif tag in MLP_KINDS:
                mlp_stage(nc, core, dram, tag, MLP_KINDS[tag])
        store_everything(nc, core, dram)


def head_slots(w):
    out = np.zeros((w.shape[0], GROUPS, 4, SLOT), w.dtype)
    out[..., :HD] = w.reshape(w.shape[0], 4, GROUPS, HD).transpose(0, 2, 1, 3)
    return out.reshape(w.shape[0], HEADS * SLOT)


def slot_column(value):
    out = np.zeros((HEADS, SLOT), np.float32)
    out[:, HD] = value
    return out.reshape(HEADS * SLOT)


def layout(x):
    a = {"x": x["x"], "ctxT": x["ctx_1024"].transpose(2, 0, 1), "ident": np.eye(P, dtype=np.float32)}
    pos, di = np.arange(P, dtype=np.float32)[:, None], np.arange(0, HD, 2, dtype=np.float32) / HD
    theta = pos * np.exp(-di * np.float32(np.log(10000.0)))
    sin = np.repeat(np.sin(theta), 2, axis=1)
    sin[:, :HD // 2] *= -1
    a["rope"] = np.concatenate([np.repeat(np.cos(theta), 2, axis=1), sin], axis=1).astype(np.float32)
    a["causal"] = np.tile(np.triu(np.full((P, P), -1e30, np.float32), 1), (1, 4))
    a["decay"] = np.exp(-0.01 * 0.01 * np.abs(pos - pos.T)).astype(np.float32)
    a["row_c"] = np.concatenate([np.eye(2, dtype=np.float32), np.tile(np.arange(SC, dtype=np.float32), (2, 1))], axis=1)
    a["lens"] = x["_lenS2"]
    a["key_mask"] = x["mask_BxS2_bf1"].view(np.uint8)

    t = "L0_attn_"
    a[t + "w_qkv"] = np.concatenate([x[t + n].T for n in ("Wq", "Wk", "Wv")], axis=1)
    a[t + "gb"] = np.tile(np.concatenate([x[t + n] for n in ("q_gamma", "k_gamma", "q_beta", "k_beta")]), (P, 1))
    a[t + "w_o"], a[t + "b_o"] = x[t + "Wo"].T, x[t + "bo"][None]

    t = "L0_xattn_"
    a[t + "w_q"], a[t + "w_k"] = head_slots(x[t + "wq"].T), head_slots(x[t + "wk"].T)
    a[t + "b_q"] = slot_column(1.0).reshape(GROUPS, P).T
    a[t + "w_kc"] = head_slots(a["ident"])
    a[t + "aux"] = np.stack([slot_column(0.0), slot_column(-1e30)])
    a[t + "w_v"], a[t + "w_vc"] = x[t + "wv"].T, a["ident"]
    a[t + "w_o"], a[t + "b_o"] = x[t + "wo"].T, x[t + "bo"][None]

    t = "L1_xattn_"
    a[t + "w_q"], a[t + "w_kc"] = head_slots(x[t + "Wq"].T), head_slots(x[t + "Wk"].T)
    bq = head_slots(x[t + "bq"][None])[0]
    bq.reshape(HEADS, SLOT)[:, HD] = 1.0
    a[t + "b_q"] = bq.reshape(GROUPS, P).T
    a[t + "aux"] = np.stack([head_slots(x[t + "bk"][None])[0], slot_column(-1e8 * HD ** 0.5)])
    a[t + "w_vc"], a[t + "b_v"] = x[t + "Wv"].T, x[t + "bv"][None]
    a[t + "w_o"], a[t + "b_o"] = x[t + "Wo"].T, x[t + "bo"][None]

    t = "L3_attn_"
    a[t + "w_q"] = head_slots(x[t + "Wq"])
    a[t + "w_kv"] = np.concatenate([x[t + "Wk"], x[t + "Wv"]], axis=1)
    a[t + "w_down"], a[t + "w_k"], a[t + "w_up_v"] = x[t + "W_down_kv"], head_slots(x[t + "W_up_k"]), x[t + "W_up_v"]
    a[t + "w_o"] = x[t + "Wo"]

    def chunks_in(*ws):
        return np.concatenate(ws, axis=1).reshape(P, -1, P)

    def chunks_out(*ws):
        return np.concatenate(ws, axis=0).reshape(-1, P, P).transpose(1, 0, 2)

    def pick(rows, groups):
        owner = np.concatenate([first + np.arange(n * width) // width for first, n, width in groups])
        return (np.arange(rows)[:, None] == owner[None, :]).astype(np.float32).reshape(rows, -1, P)

    t = "L3_xattn_"
    a["ctx"] = x["ctx_1024"]
    a[t + "w_q"], a[t + "w_kv"] = x[t + "Wq"], x[t + "Wkv"]
    a[t + "w_o"], a[t + "b_o"] = x[t + "Wout"].reshape(-1, P, P).transpose(1, 0, 2), x[t + "bout"][None]
    a[t + "ln"] = np.stack([x[t + n] for n in ("g1", "b1", "g2", "b2")], axis=1)

    t = "L2_xattn_"
    a[t + "w_q"], a[t + "b_q"] = head_slots(x[t + "Wq"]), head_slots(x[t + "bq"][None]).reshape(GROUPS, P).T
    a[t + "w_k"] = np.stack([x[t + "Wk1"], x[t + "Wk2"]], axis=1)
    a[t + "b_k"] = np.stack([x[t + "bk1"], x[t + "bk2"]], axis=1)
    a[t + "w_slot"] = head_slots(a["ident"])
    a[t + "unslot"] = a[t + "w_slot"].reshape(P, GROUPS, P).transpose(2, 1, 0).reshape(P, GROUPS * P)
    a[t + "w_v"] = np.stack([x[t + "Wv1"], x[t + "Wv2"]], axis=1)
    a[t + "b_v"] = np.concatenate([x[t + "bv1"], x[t + "bv2"]])[None]
    a[t + "w_qt"], a[t + "b_qt"] = x[t + "Wq"], x[t + "bq"][None]
    a[t + "w_o"], a[t + "b_o"] = x[t + "Wo"], x[t + "bo"][None]
    a[t + "gb"] = np.tile(np.stack([x[t + n] for n in ("g0", "beta0", "g1", "beta1")]), (P, 1, 1))

    t = "L2_attn_"
    a[t + "w_in"] = np.stack([x[t + n].T for n in ("Wq", "Wk", "Wv")], axis=1)
    a[t + "b_in"] = np.stack([x[t + n] for n in ("bq", "bk", "bv")], axis=1)
    a[t + "conv"] = np.stack([np.concatenate([x[f"{t}w{n}_conv"], x[f"{t}b{n}_conv"][:, None]], axis=1) for n in "qkv"], axis=1)
    a[t + "w_beta"] = x[t + "Wbeta"].T
    a[t + "b_beta"] = np.stack([x[t + "bbeta"], np.zeros(HEADS, np.float32), np.zeros(HEADS, np.float32)], axis=1)
    a[t + "head_sum"] = np.repeat(np.eye(HEADS, dtype=np.float32), HD, axis=0)
    a[t + "w_o"], a[t + "b_o"], a[t + "norm_w"] = x[t + "Wo"].T, x[t + "bo"][None], np.tile(x[t + "norm_w"], HEADS)[:, None]

    t = "L1_attn_"
    grid = np.arange(-16, 17, dtype=np.float32)
    tok = np.arange(P, dtype=np.float32)
    a["wave_tables"] = np.concatenate(
        [np.tile(np.concatenate([grid, np.abs(grid), tok]), (P, 1)), tok[:, None], 0.5 - tok[:, None],
         np.tile(np.float32([7.5 / 8, 2.0, 4.75 / 8, 8.5, 0.0, 5.25]), (P, 1))], axis=1).astype(np.float32)
    for n in ("w_wave", "w_query", "w_se1", "w_se2", "w_out"):
        a[t + n] = x[t + n]
    a[t + "b_wave"], a[t + "b_query"] = x[t + "b_wave"][None], x[t + "b_query"][None]
    a[t + "b_se1"], a[t + "b_se2"] = x[t + "b_se1"][:, None], x[t + "b_se2"][:, None]
    a[t + "kw"] = np.tile(x[t + "key_weight"], (P, 1))

    a["lower"] = np.tile(np.tril(np.ones((4, 4), np.float32), -1), (P, 1, 1))
    t = "L0_ffn_"
    for dst, e, sh in (("w_g", "expert_gate", "shared_gate"), ("w_u", "expert_up", "shared_up")):
        a[t + dst] = chunks_in(x[t + e].transpose(2, 0, 1).reshape(P, -1), x[t + sh].T)
    a[t + "w_d"] = chunks_out(x[t + "expert_down"].transpose(0, 2, 1).reshape(-1, P), x[t + "shared_down"].T)
    a[t + "w_r"], a[t + "b_r"] = x[t + "gate_w"].T, np.tile(x[t + "gate_bias"], (P, 1))
    a[t + "pick"] = pick(32, [(0, 32, 64)])

    t = "L3_ffn_"
    pad = np.zeros((P, P // 2), np.float32)
    for n in ("g", "u"):
        full = {"g": "gate", "u": "up"}[n]
        a[t + "w_" + n] = chunks_in(x[t + "w_" + full].transpose(1, 0, 2).reshape(P, -1),
                                    x[t + "anchor_w_" + full].transpose(1, 0, 2).reshape(P, -1),
                                    x[t + "shared_w_" + full], pad)
    a[t + "w_d"] = chunks_out(x[t + "w_down"].reshape(-1, P), x[t + "anchor_w_down"].reshape(-1, P),
                              x[t + "shared_w_down"], pad.T)
    a[t + "w_r"], a[t + "b_r"] = x[t + "gate_weight"].T, np.tile(x[t + "gate_bias"], (P, 1))
    a[t + "pick"] = pick(48, [(0, 32, 64), (32, 16, 32)])

    t = "L1_ffn_"
    a[t + "w"] = np.concatenate([x[t + "w_gate"].reshape(3, P, P).transpose(1, 0, 2),
                                 x[t + "w_up"].reshape(3, P, P).transpose(1, 0, 2), x[t + "w_down"].reshape(P, 3, P)], axis=1)

    t = "L2_ffn_"
    a[t + "q_w_g"], a[t + "q_w_d"] = chunks_in(x[t + "fc1_q"]), chunks_out(x[t + "fc2_q"])
    a[t + "w_g"] = np.tile(x[t + "fc1_scales"].reshape(1, -1, P), (P, 1, 1))
    a[t + "w_d"] = np.tile(x[t + "fc2_scales"].reshape(1, -1, P), (P, 1, 1))
    a[t + "b_g"], a[t + "b_d"] = x[t + "fc1_bias"].reshape(-1, P).T, x[t + "fc2_bias"][None]
    a[t + "ln_g"], a[t + "ln_b"] = x[t + "ln_gamma"][:, None], x[t + "ln_beta"][:, None]
    return a


def kernel(**inputs):
    import concourse.bacc as bacc
    from concourse.bass_utils import run_bass_kernel_spmd

    arrays = {n: np.ascontiguousarray(v) for n, v in layout({n: np.asarray(v) for n, v in inputs.items()}).items()}
    nc = bacc.Bacc("TRN2", target_bir_lowering=False, num_devices=1)
    dram = {n: nc.dram_tensor("in_" + n, v.shape, mybir.dt.from_np(v.dtype), kind="ExternalInput").ap()
            for n, v in arrays.items()}
    shape = inputs["x"].shape
    dram["out"] = nc.dram_tensor("out", shape, F32, kind="ExternalOutput").ap()
    decoder_kernel(nc, dram, shape[0])
    r = run_bass_kernel_spmd(nc, [{"in_" + n: v for n, v in arrays.items()}], core_ids=[0])
    return r.results[0]["out"]
```
